# Optimizing a Trainium2 kernel written in Bass

```python
import numpy as np
import jax
import jax.numpy as jnp

def _softmax(x, axis=-1):
    return jax.nn.softmax(x, axis=axis)

def _gelu(x):
    return jax.nn.gelu(x, approximate=True)

def _silu(x):
    return jax.nn.silu(x)

def _sigmoid(x):
    return jax.nn.sigmoid(x)

def _layernorm(x, axis=-1, eps=1e-05):
    m = jnp.mean(x, axis=axis, keepdims=True)
    v = jnp.var(x, axis=axis, keepdims=True)
    return (x - m) / jnp.sqrt(v + eps)

def _scatter_add(tgt, idx, src, axis=0):
    return tgt.at[idx].add(src)

def _segment_sum(src, seg, n):
    return jax.ops.segment_sum(src, seg, n)
kernel_name = 'mk_recurrent_d4_jaxref_r8_ac92a5'

def setup_inputs(seed: int=0):
    np.random.seed(seed)
    _w = jnp.asarray

    def _L0_attn_setup():
        import jax, jax.numpy as jnp
        import numpy as np
        B, L, D, H, W = (2, 512, 128, 16, 128)
        E = D // H

        def _ln(x, g, b):
            m = jnp.mean(x, axis=-1, keepdims=True)
            v = jnp.mean((x - m) ** 2, axis=-1, keepdims=True)
            return (x - m) / jnp.sqrt(v + 1e-05) * g + b

        def _swa(xn, Wqkv, bqkv, Wp, bp):
            b_, l_, d_ = xn.shape
            nb = l_ // W
            qkv = xn @ Wqkv + bqkv
            q, k, v = jnp.split(qkv, 3, axis=-1)

            def heads(t):
                return t.reshape(b_, l_, H, E).transpose(0, 2, 1, 3)
            q, k, v = (heads(q), heads(k), heads(v))

            def blk(t):
                return t.reshape(b_, H, nb, W, E)
            qb, kb, vb = (blk(q), blk(k), blk(v))
            kprev = jnp.pad(kb, ((0, 0), (0, 0), (1, 0), (0, 0), (0, 0)))[:, :, :nb]
            vprev = jnp.pad(vb, ((0, 0), (0, 0), (1, 0), (0, 0), (0, 0)))[:, :, :nb]
            kc = jnp.concatenate([kprev, kb], axis=3)
            vc = jnp.concatenate([vprev, vb], axis=3)
            scores = jnp.einsum('bhnre,bhnse->bhnrs', qb, kc) / np.float32(np.sqrt(E))
            r = jnp.arange(W)[:, None]
            s = jnp.arange(2 * W)[None, :]
            band = (s >= r + 1) & (s <= r + W)
            first = band & (s >= W)
            mask = jnp.concatenate([first[None], jnp.broadcast_to(band, (nb - 1, W, 2 * W))], axis=0)
            scores = jnp.where(mask[None, None], scores, jnp.float32(-1e+30))
            attn = jax.nn.softmax(scores, axis=-1)
            out = jnp.einsum('bhnrs,bhnse->bhnre', attn, vc)
            out = out.reshape(b_, H, l_, E).transpose(0, 2, 1, 3).reshape(b_, l_, d_)
            return out @ Wp + bp

        def _linattn(xn, Wqkv, bqkv, Wo, bo):
            b_, l_, d_ = xn.shape
            C = 128
            nc = l_ // C
            qkv = xn @ Wqkv + bqkv
            q, k, v = jnp.split(qkv, 3, axis=-1)
            q = q.reshape(b_, l_, H, E)
            k = k.reshape(b_, l_, H, E)
            v = v.reshape(b_, l_, H, E)
            q = jax.nn.elu(q * np.float32(E ** (-0.5))) + np.float32(1.0001)
            k = jax.nn.elu(k) + np.float32(1.0001)

            def chunks(t):
                return t.reshape(b_, nc, C, H, E).transpose(1, 0, 3, 2, 4)
            qc, kc, vc = (chunks(q), chunks(k), chunks(v))
            tril = jnp.tril(jnp.ones((C, C), jnp.float32))

            def step(carry, inp):
                S, z = carry
                qi, ki, vi = inp
                A = jnp.einsum('bhce,bhde->bhcd', qi, ki) * tril
                num = jnp.einsum('bhce,bhef->bhcf', qi, S) + jnp.einsum('bhcd,bhdf->bhcf', A, vi)
                den = jnp.einsum('bhce,bhe->bhc', qi, z) + A.sum(-1)
                o = num / (den[..., None] + 1e-06)
                S = S + jnp.einsum('bhce,bhcf->bhef', ki, vi)
                z = z + ki.sum(2)
                return ((S, z), o)
            S0 = jnp.zeros((b_, H, E, E), jnp.float32)
            z0 = jnp.zeros((b_, H, E), jnp.float32)
            _, out = jax.lax.scan(step, (S0, z0), (qc, kc, vc))
            out = out.transpose(1, 0, 3, 2, 4).reshape(b_, l_, d_)
            return out @ Wo + bo
        key = jax.random.key(seed)
        ks = jax.random.split(key, 9)

        def w(k, shape, s=0.02):
            return jax.random.normal(k, shape, jnp.float32) * s
        return {'x': jax.random.normal(ks[0], (B, L, D), jnp.float32), 'g1': jnp.ones((D,), jnp.float32), 'b1': jnp.zeros((D,), jnp.float32), 'Wqkv_a': w(ks[1], (D, 3 * D)), 'bqkv_a': jnp.zeros((3 * D,), jnp.float32), 'Wp_a': w(ks[2], (D, D)), 'bp_a': jnp.zeros((D,), jnp.float32), 'Wqkv_s': w(ks[3], (D, 3 * D)), 'bqkv_s': jnp.zeros((3 * D,), jnp.float32), 'Wo_s': w(ks[4], (D, D)), 'bo_s': jnp.zeros((D,), jnp.float32), 'Wo': w(ks[5], (D, D)), 'bo': jnp.zeros((D,), jnp.float32), 'gm': jnp.ones((D,), jnp.float32), 'bm': jnp.zeros((D,), jnp.float32), 'W1': w(ks[6], (D, 4 * D)), 'b1m': jnp.zeros((4 * D,), jnp.float32), 'W2': w(ks[7], (4 * D, D)), 'b2m': jnp.zeros((D,), jnp.float32)}
    _L0_attn_in = _L0_attn_setup()

    def _L0_ffn_setup():
        import jax, jax.numpy as jnp
        import numpy as np
        NUM_EXPERTS = 8
        TOP_K = 2
        key = jax.random.key(seed)
        ks = jax.random.split(key, 5)
        B, S, D, F, E = (4, 256, 128, 512, NUM_EXPERTS)
        x = jax.random.normal(ks[0], (B, S, D), dtype=jnp.float32)
        router_w = jax.random.normal(ks[1], (D, E), dtype=jnp.float32) * 0.02
        router_b = jnp.zeros((E,), dtype=jnp.float32)
        w1 = jax.random.normal(ks[2], (E, D, F), dtype=jnp.float32) * 0.02
        b1 = jnp.zeros((E, F), dtype=jnp.float32)
        w2 = jax.random.normal(ks[3], (E, F, D), dtype=jnp.float32) * 0.02
        b2 = jnp.zeros((E, D), dtype=jnp.float32)
        return {'x': x, 'router_w': router_w, 'router_b': router_b, 'w1': w1, 'b1': b1, 'w2': w2, 'b2': b2}
    _L0_ffn_in = _L0_ffn_setup()

    def _L1_attn_setup():
        import jax, jax.numpy as jnp
        import numpy as np
        B, L, DIM = (4, 512, 128)
        H, DQK, DV, DINNER, CHUNK = (16, 64, 64, 64, 64)
        BASE_LR, BASE_WD = (0.001, 0.9)
        key = jax.random.key(seed)
        ks = jax.random.split(key, 9)

        def s(k, shape, scale):
            return jax.random.normal(k, shape, jnp.float32) * scale
        return {'x': jax.random.normal(ks[0], (B, L, DIM), jnp.float32), 'Wq': s(ks[1], (H * DQK, DIM), DIM ** (-0.5)), 'Wk': s(ks[2], (H * DQK, DIM), DIM ** (-0.5)), 'Wv': s(ks[3], (H * DV, DIM), DIM ** (-0.5)), 'Wlr': s(ks[4], (2 * H, DIM), DIM ** (-0.5)), 'Wbeta': s(ks[5], (2 * H, DIM), DIM ** (-0.5)), 'Wo': s(ks[6], (DIM, H * DV), (H * DV) ** (-0.5)), 'W_in_init': s(ks[7], (1, DINNER, H, DQK), DQK ** (-0.5)), 'W_out_init': s(ks[8], (1, DINNER, H, DV), DINNER ** (-0.5))}
    _L1_attn_in = _L1_attn_setup()

    def _L1_ffn_setup():
        import jax, jax.numpy as jnp
        import numpy as np
        HIDDEN = 128
        FF = 512
        N_EXPERTS = 8
        CAP_FACTOR = 1.0
        B, S = (4, 256)
        STD = 0.02

        def _gelu(x):
            return x * 0.5 * (1.0 + jax.lax.erf(x / 1.41421))
        key = jax.random.key(seed)
        ks = jax.random.split(key, 6)
        x = jax.random.normal(ks[0], (B, S, HIDDEN), dtype=jnp.float32)
        W_sw = jax.random.normal(ks[1], (HIDDEN, N_EXPERTS), dtype=jnp.float32) * STD
        b_sw = jnp.zeros((N_EXPERTS,), dtype=jnp.float32)
        W1 = jax.random.normal(ks[2], (N_EXPERTS, HIDDEN, FF), dtype=jnp.float32) * STD
        b1 = jnp.zeros((N_EXPERTS, FF), dtype=jnp.float32)
        W2 = jax.random.normal(ks[3], (N_EXPERTS, FF, HIDDEN), dtype=jnp.float32) * STD
        b2 = jnp.zeros((N_EXPERTS, HIDDEN), dtype=jnp.float32)
        return {'x': x, 'W_sw': W_sw, 'b_sw': b_sw, 'W1': W1, 'b1': b1, 'W2': W2, 'b2': b2}
    _L1_ffn_in = _L1_ffn_setup()

    def _L2_attn_setup():
        import jax, jax.numpy as jnp
        import numpy as np
        N_SCALES = 11
        N_TAPS = 4
        OFFSETS = [(1 << j) * tau for j in range(N_SCALES) for tau in range(N_TAPS)]

        def _shift(a, off):
            N = a.shape[2]
            return jnp.pad(a[:, :, :N - off], ((0, 0), (0, 0), (off, 0), (0, 0)))
        key = jax.random.key(seed)
        ks = jax.random.split(key, 8)
        B, N, D, H = (4, 512, 128, 16)
        w_scale = 0.02
        return {'x': jax.random.normal(ks[0], (B, N, D), jnp.float32), 'w_qkv': jax.random.normal(ks[1], (D, 3 * D), jnp.float32) * w_scale, 'b_qkv': jnp.zeros((3 * D,), jnp.float32), 'w_out': jax.random.normal(ks[2], (D, D), jnp.float32) * w_scale, 'b_out': jnp.zeros((D,), jnp.float32), 'w_gate': jax.random.normal(ks[3], (D, D), jnp.float32) * w_scale, 'b_gate': 2.0 * jnp.ones((D,), jnp.float32), 'pos_bias': jax.random.normal(ks[4], (len(OFFSETS), H), jnp.float32) * 0.1}
    _L2_attn_in = _L2_attn_setup()

    def _L2_ffn_setup():
        import jax, jax.numpy as jnp
        import numpy as np
        DIM = 128
        N_HEADS = 16
        N_KV_HEADS = 4
        HEAD_DIM = DIM // N_HEADS
        N_REP = N_HEADS // N_KV_HEADS
        N_EXPERTS = 4
        TOP_K = 2
        HIDDEN = 3 * DIM
        EPS = 1.1920928955078125e-07

        def _rmsnorm(x, g):
            var = jnp.mean(jnp.square(x), axis=-1, keepdims=True)
            return x * jax.lax.rsqrt(var + EPS) * g

        def _rotate_half(x):
            x1, x2 = jnp.split(x, 2, axis=-1)
            return jnp.concatenate([-x2, x1], axis=-1)

        def _rope_tables(S):
            inv_freq = 1.0 / 10000.0 ** (jnp.arange(0, HEAD_DIM, 2, dtype=jnp.float32) / HEAD_DIM)
            freqs = jnp.arange(S, dtype=jnp.float32)[:, None] * inv_freq[None, :]
            emb = jnp.concatenate([freqs, freqs], axis=-1)
            return (jnp.cos(emb), jnp.sin(emb))

        def _attention(x, wq, wk, wv, wo):
            B, S, D = x.shape
            q = (x @ wq).reshape(B, S, N_HEADS, HEAD_DIM).transpose(0, 2, 1, 3)
            k = (x @ wk).reshape(B, S, N_KV_HEADS, HEAD_DIM).transpose(0, 2, 1, 3)
            v = (x @ wv).reshape(B, S, N_KV_HEADS, HEAD_DIM).transpose(0, 2, 1, 3)
            cos, sin = _rope_tables(S)
            q = q * cos + _rotate_half(q) * sin
            k = k * cos + _rotate_half(k) * sin
            k = jnp.repeat(k, N_REP, axis=1)
            v = jnp.repeat(v, N_REP, axis=1)
            scores = jnp.einsum('bhqd,bhkd->bhqk', q, k) / jnp.sqrt(jnp.float32(HEAD_DIM))
            causal = jnp.tril(jnp.ones((S, S), dtype=bool))
            scores = jnp.where(causal, scores, -jnp.inf)
            attn = jax.nn.softmax(scores, axis=-1)
            out = jnp.einsum('bhqk,bhkd->bhqd', attn, v)
            return out.transpose(0, 2, 1, 3).reshape(B, S, D) @ wo

        def _moe(x, gate, w1, w2, w3):
            B, S, D = x.shape
            xf = x.reshape(-1, D)
            probs = jax.nn.softmax(xf @ gate, axis=-1)
            w, idx = jax.lax.top_k(probs, TOP_K)
            w = w / jnp.sum(w, axis=-1, keepdims=True)
            oh = jax.nn.one_hot(idx, N_EXPERTS, dtype=xf.dtype)
            comb = jnp.einsum('nk,nke->ne', w, oh)
            out = jnp.zeros_like(xf)
            for e in range(N_EXPERTS):
                h = jax.nn.silu(xf @ w1[e]) * (xf @ w3[e])
                out = out + comb[:, e:e + 1] * (h @ w2[e])
            return out.reshape(B, S, D)
        key = jax.random.key(seed)
        ks = jax.random.split(key, 12)
        s = 0.02
        B, S = (2, 256)
        return {'x': jax.random.normal(ks[0], (B, S, DIM), jnp.float32), 'g1': jnp.ones((DIM,), jnp.float32), 'g2': jnp.ones((DIM,), jnp.float32), 'wq': jax.random.normal(ks[1], (DIM, N_HEADS * HEAD_DIM), jnp.float32) * s, 'wk': jax.random.normal(ks[2], (DIM, N_KV_HEADS * HEAD_DIM), jnp.float32) * s, 'wv': jax.random.normal(ks[3], (DIM, N_KV_HEADS * HEAD_DIM), jnp.float32) * s, 'wo': jax.random.normal(ks[4], (N_HEADS * HEAD_DIM, DIM), jnp.float32) * s, 'gate': jax.random.normal(ks[5], (DIM, N_EXPERTS), jnp.float32) * s, 'w1': jax.random.normal(ks[6], (N_EXPERTS, DIM, HIDDEN), jnp.float32) * s, 'w2': jax.random.normal(ks[7], (N_EXPERTS, HIDDEN, DIM), jnp.float32) * s, 'w3': jax.random.normal(ks[8], (N_EXPERTS, DIM, HIDDEN), jnp.float32) * s}
    _L2_ffn_in = _L2_ffn_setup()

    def _L3_attn_setup():
        import jax, jax.numpy as jnp
        import numpy as np
        K = 128
        HEADS = 16
        key = jax.random.key(seed)
        ks = jax.random.split(key, 6)
        x = jax.random.normal(ks[0], (2, 256, K), dtype=jnp.float32)
        sc = 1.0 / np.sqrt(K)
        Wq = jax.random.normal(ks[1], (K, K), dtype=jnp.float32) * sc
        Wk = jax.random.normal(ks[2], (K, K), dtype=jnp.float32) * sc
        Wv = jax.random.normal(ks[3], (K, K), dtype=jnp.float32) * sc
        Wu = jax.random.normal(ks[4], (K, K), dtype=jnp.float32) * sc
        bu = jax.random.normal(ks[5], (K,), dtype=jnp.float32) * 0.01
        return {'x': x, 'Wq': Wq, 'Wk': Wk, 'Wv': Wv, 'Wu': Wu, 'bu': bu}
    _L3_attn_in = _L3_attn_setup()

    def _L3_ffn_setup():
        import jax, jax.numpy as jnp
        import numpy as np
        B, L, D = (2, 256, 128)
        E = 15
        H = D * 1
        K = 3
        T = 1.0
        key = jax.random.key(seed)
        ks = jax.random.split(key, 12)
        s = 0.02
        return {'x': jax.random.normal(ks[0], (B, L, D), dtype=jnp.float32), 'router_W': jax.random.normal(ks[1], (D, E), dtype=jnp.float32) * s, 'router_b': jnp.zeros((E,), dtype=jnp.float32), 'sW1': jax.random.normal(ks[2], (D, H), dtype=jnp.float32) * s, 'sb1': jnp.zeros((H,), dtype=jnp.float32), 'sW2': jax.random.normal(ks[3], (H, D), dtype=jnp.float32) * s, 'sb2': jnp.zeros((D,), dtype=jnp.float32), 'eW1': jax.random.normal(ks[4], (E, D, H), dtype=jnp.float32) * s, 'eb1': jnp.zeros((E, H), dtype=jnp.float32), 'eW2': jax.random.normal(ks[5], (E, H, D), dtype=jnp.float32) * s, 'eb2': jnp.zeros((E, D), dtype=jnp.float32)}
    _L3_ffn_in = _L3_ffn_setup()
    _d = {'L0_attn_x': _L0_attn_in['x'], 'L0_attn_g1': _L0_attn_in['g1'], 'L0_attn_b1': _L0_attn_in['b1'], 'L0_attn_Wqkv_a': _L0_attn_in['Wqkv_a'], 'L0_attn_bqkv_a': _L0_attn_in['bqkv_a'], 'L0_attn_Wp_a': _L0_attn_in['Wp_a'], 'L0_attn_bp_a': _L0_attn_in['bp_a'], 'L0_attn_Wqkv_s': _L0_attn_in['Wqkv_s'], 'L0_attn_bqkv_s': _L0_attn_in['bqkv_s'], 'L0_attn_Wo_s': _L0_attn_in['Wo_s'], 'L0_attn_bo_s': _L0_attn_in['bo_s'], 'L0_attn_Wo': _L0_attn_in['Wo'], 'L0_attn_bo': _L0_attn_in['bo'], 'L0_attn_gm': _L0_attn_in['gm'], 'L0_attn_bm': _L0_attn_in['bm'], 'L0_attn_W1': _L0_attn_in['W1'], 'L0_attn_b1m': _L0_attn_in['b1m'], 'L0_attn_W2': _L0_attn_in['W2'], 'L0_attn_b2m': _L0_attn_in['b2m'], 'L0_ffn_router_w': _L0_ffn_in['router_w'], 'L0_ffn_router_b': _L0_ffn_in['router_b'], 'L0_ffn_w1': _L0_ffn_in['w1'], 'L0_ffn_b1': _L0_ffn_in['b1'], 'L0_ffn_w2': _L0_ffn_in['w2'], 'L0_ffn_b2': _L0_ffn_in['b2'], 'L1_attn_Wq': _L1_attn_in['Wq'], 'L1_attn_Wk': _L1_attn_in['Wk'], 'L1_attn_Wv': _L1_attn_in['Wv'], 'L1_attn_Wlr': _L1_attn_in['Wlr'], 'L1_attn_Wbeta': _L1_attn_in['Wbeta'], 'L1_attn_Wo': _L1_attn_in['Wo'], 'L1_attn_W_in_init': _L1_attn_in['W_in_init'], 'L1_attn_W_out_init': _L1_attn_in['W_out_init'], 'L1_ffn_W_sw': _L1_ffn_in['W_sw'], 'L1_ffn_b_sw': _L1_ffn_in['b_sw'], 'L1_ffn_W1': _L1_ffn_in['W1'], 'L1_ffn_b1': _L1_ffn_in['b1'], 'L1_ffn_W2': _L1_ffn_in['W2'], 'L1_ffn_b2': _L1_ffn_in['b2'], 'L2_attn_w_qkv': _L2_attn_in['w_qkv'], 'L2_attn_b_qkv': _L2_attn_in['b_qkv'], 'L2_attn_w_out': _L2_attn_in['w_out'], 'L2_attn_b_out': _L2_attn_in['b_out'], 'L2_attn_w_gate': _L2_attn_in['w_gate'], 'L2_attn_b_gate': _L2_attn_in['b_gate'], 'L2_attn_pos_bias': _L2_attn_in['pos_bias'], 'L2_ffn_g1': _L2_ffn_in['g1'], 'L2_ffn_g2': _L2_ffn_in['g2'], 'L2_ffn_wq': _L2_ffn_in['wq'], 'L2_ffn_wk': _L2_ffn_in['wk'], 'L2_ffn_wv': _L2_ffn_in['wv'], 'L2_ffn_wo': _L2_ffn_in['wo'], 'L2_ffn_gate': _L2_ffn_in['gate'], 'L2_ffn_w1': _L2_ffn_in['w1'], 'L2_ffn_w2': _L2_ffn_in['w2'], 'L2_ffn_w3': _L2_ffn_in['w3'], 'L3_attn_Wq': _L3_attn_in['Wq'], 'L3_attn_Wk': _L3_attn_in['Wk'], 'L3_attn_Wv': _L3_attn_in['Wv'], 'L3_attn_Wu': _L3_attn_in['Wu'], 'L3_attn_bu': _L3_attn_in['bu'], 'L3_ffn_router_W': _L3_ffn_in['router_W'], 'L3_ffn_router_b': _L3_ffn_in['router_b'], 'L3_ffn_sW1': _L3_ffn_in['sW1'], 'L3_ffn_sb1': _L3_ffn_in['sb1'], 'L3_ffn_sW2': _L3_ffn_in['sW2'], 'L3_ffn_sb2': _L3_ffn_in['sb2'], 'L3_ffn_eW1': _L3_ffn_in['eW1'], 'L3_ffn_eb1': _L3_ffn_in['eb1'], 'L3_ffn_eW2': _L3_ffn_in['eW2'], 'L3_ffn_eb2': _L3_ffn_in['eb2']}
    _x0 = _d['L0_attn_x']
    _d['L0_attn_x'] = jax.random.normal(jax.random.fold_in(jax.random.key(seed), 1), (2, 1024, 128), dtype=_x0.dtype)
    del _x0
    return _d

def reference(L0_attn_x, L0_attn_g1, L0_attn_b1, L0_attn_Wqkv_a, L0_attn_bqkv_a, L0_attn_Wp_a, L0_attn_bp_a, L0_attn_Wqkv_s, L0_attn_bqkv_s, L0_attn_Wo_s, L0_attn_bo_s, L0_attn_Wo, L0_attn_bo, L0_attn_gm, L0_attn_bm, L0_attn_W1, L0_attn_b1m, L0_attn_W2, L0_attn_b2m, L0_ffn_router_w, L0_ffn_router_b, L0_ffn_w1, L0_ffn_b1, L0_ffn_w2, L0_ffn_b2, L1_attn_Wq, L1_attn_Wk, L1_attn_Wv, L1_attn_Wlr, L1_attn_Wbeta, L1_attn_Wo, L1_attn_W_in_init, L1_attn_W_out_init, L1_ffn_W_sw, L1_ffn_b_sw, L1_ffn_W1, L1_ffn_b1, L1_ffn_W2, L1_ffn_b2, L2_attn_w_qkv, L2_attn_b_qkv, L2_attn_w_out, L2_attn_b_out, L2_attn_w_gate, L2_attn_b_gate, L2_attn_pos_bias, L2_ffn_g1, L2_ffn_g2, L2_ffn_wq, L2_ffn_wk, L2_ffn_wv, L2_ffn_wo, L2_ffn_gate, L2_ffn_w1, L2_ffn_w2, L2_ffn_w3, L3_attn_Wq, L3_attn_Wk, L3_attn_Wv, L3_attn_Wu, L3_attn_bu, L3_ffn_router_W, L3_ffn_router_b, L3_ffn_sW1, L3_ffn_sb1, L3_ffn_sW2, L3_ffn_sb2, L3_ffn_eW1, L3_ffn_eb1, L3_ffn_eW2, L3_ffn_eb2):

    def _L0_attn_ref(x, g1, b1, Wqkv_a, bqkv_a, Wp_a, bp_a, Wqkv_s, bqkv_s, Wo_s, bo_s, Wo, bo, gm, bm, W1, b1m, W2, b2m):
        import jax, jax.numpy as jnp
        import numpy as np
        B, L, D, H, W = (2, 512, 128, 16, 128)
        E = D // H

        def _ln(x, g, b):
            m = jnp.mean(x, axis=-1, keepdims=True)
            v = jnp.mean((x - m) ** 2, axis=-1, keepdims=True)
            return (x - m) / jnp.sqrt(v + 1e-05) * g + b

        def _swa(xn, Wqkv, bqkv, Wp, bp):
            b_, l_, d_ = xn.shape
            nb = l_ // W
            qkv = xn @ Wqkv + bqkv
            q, k, v = jnp.split(qkv, 3, axis=-1)

            def heads(t):
                return t.reshape(b_, l_, H, E).transpose(0, 2, 1, 3)
            q, k, v = (heads(q), heads(k), heads(v))

            def blk(t):
                return t.reshape(b_, H, nb, W, E)
            qb, kb, vb = (blk(q), blk(k), blk(v))
            kprev = jnp.pad(kb, ((0, 0), (0, 0), (1, 0), (0, 0), (0, 0)))[:, :, :nb]
            vprev = jnp.pad(vb, ((0, 0), (0, 0), (1, 0), (0, 0), (0, 0)))[:, :, :nb]
            kc = jnp.concatenate([kprev, kb], axis=3)
            vc = jnp.concatenate([vprev, vb], axis=3)
            scores = jnp.einsum('bhnre,bhnse->bhnrs', qb, kc) / np.float32(np.sqrt(E))
            r = jnp.arange(W)[:, None]
            s = jnp.arange(2 * W)[None, :]
            band = (s >= r + 1) & (s <= r + W)
            first = band & (s >= W)
            mask = jnp.concatenate([first[None], jnp.broadcast_to(band, (nb - 1, W, 2 * W))], axis=0)
            scores = jnp.where(mask[None, None], scores, jnp.float32(-1e+30))
            attn = jax.nn.softmax(scores, axis=-1)
            out = jnp.einsum('bhnrs,bhnse->bhnre', attn, vc)
            out = out.reshape(b_, H, l_, E).transpose(0, 2, 1, 3).reshape(b_, l_, d_)
            return out @ Wp + bp

        def _linattn(xn, Wqkv, bqkv, Wo, bo):
            b_, l_, d_ = xn.shape
            C = 128
            nc = l_ // C
            qkv = xn @ Wqkv + bqkv
            q, k, v = jnp.split(qkv, 3, axis=-1)
            q = q.reshape(b_, l_, H, E)
            k = k.reshape(b_, l_, H, E)
            v = v.reshape(b_, l_, H, E)
            q = jax.nn.elu(q * np.float32(E ** (-0.5))) + np.float32(1.0001)
            k = jax.nn.elu(k) + np.float32(1.0001)

            def chunks(t):
                return t.reshape(b_, nc, C, H, E).transpose(1, 0, 3, 2, 4)
            qc, kc, vc = (chunks(q), chunks(k), chunks(v))
            tril = jnp.tril(jnp.ones((C, C), jnp.float32))

            def step(carry, inp):
                S, z = carry
                qi, ki, vi = inp
                A = jnp.einsum('bhce,bhde->bhcd', qi, ki) * tril
                num = jnp.einsum('bhce,bhef->bhcf', qi, S) + jnp.einsum('bhcd,bhdf->bhcf', A, vi)
                den = jnp.einsum('bhce,bhe->bhc', qi, z) + A.sum(-1)
                o = num / (den[..., None] + 1e-06)
                S = S + jnp.einsum('bhce,bhcf->bhef', ki, vi)
                z = z + ki.sum(2)
                return ((S, z), o)
            S0 = jnp.zeros((b_, H, E, E), jnp.float32)
            z0 = jnp.zeros((b_, H, E), jnp.float32)
            _, out = jax.lax.scan(step, (S0, z0), (qc, kc, vc))
            out = out.transpose(1, 0, 3, 2, 4).reshape(b_, l_, d_)
            return out @ Wo + bo
        xn = _ln(x, g1, b1)
        attn_out = _swa(xn, Wqkv_a, bqkv_a, Wp_a, bp_a)
        ssm_out = _linattn(xn, Wqkv_s, bqkv_s, Wo_s, bo_s)
        mixed = (attn_out + ssm_out) @ Wo + bo
        x1 = x + mixed
        h = _ln(x1, gm, bm)
        mlp = jax.nn.gelu(h @ W1 + b1m, approximate=False) @ W2 + b2m
        return x1 + mlp

    def _L0_ffn_ref(x, router_w, router_b, w1, b1, w2, b2):
        import jax, jax.numpy as jnp
        import numpy as np
        NUM_EXPERTS = 8
        TOP_K = 2
        B, S, D = x.shape
        E = router_w.shape[1]
        x_flat = x.reshape(-1, D)
        router_probs = jax.nn.softmax(x_flat @ router_w + router_b, axis=-1)
        topk_probs, topk_idx = jax.lax.top_k(router_probs, TOP_K)
        topk_probs = topk_probs / jnp.sum(topk_probs, axis=-1, keepdims=True)
        cw = jnp.sum(topk_probs[..., None] * jax.nn.one_hot(topk_idx, E, dtype=x.dtype), axis=1)
        out = jnp.zeros_like(x_flat)
        for e in range(E):
            h = jax.nn.gelu(x_flat @ w1[e] + b1[e], approximate=False)
            out = out + cw[:, e:e + 1] * (h @ w2[e] + b2[e])
        return out.reshape(B, S, D)

    def _L1_attn_ref(x, Wq, Wk, Wv, Wlr, Wbeta, Wo, W_in_init, W_out_init):
        import jax, jax.numpy as jnp
        import numpy as np
        B, L, DIM = (4, 512, 128)
        H, DQK, DV, DINNER, CHUNK = (16, 64, 64, 64, 64)
        BASE_LR, BASE_WD = (0.001, 0.9)
        b, l, _ = x.shape
        nc = l // CHUNK
        q = jax.nn.silu(x @ Wq.T).reshape(b, l, H, DQK)
        k = jax.nn.silu(x @ Wk.T).reshape(b, l, H, DQK)
        v = (x @ Wv.T).reshape(b, l, H, DV)
        lr = jax.nn.sigmoid(x @ Wlr.T) * BASE_LR
        wd = jax.nn.sigmoid(x @ Wbeta.T) * BASE_WD

        def chunked(t):
            return jnp.moveaxis(t.reshape(b, nc, CHUNK, *t.shape[2:]), 1, 0)
        qc, kc, vc = (chunked(q), chunked(k), chunked(v))
        lr_c = chunked(lr).mean(axis=2)
        wd_c = chunked(wd).mean(axis=2)
        lr_in, lr_out = (lr_c[..., :H], lr_c[..., H:])
        wd_in, wd_out = (wd_c[..., :H], wd_c[..., H:])
        W_in0 = jnp.broadcast_to(W_in_init, (b, DINNER, H, DQK))
        W_out0 = jnp.broadcast_to(W_out_init, (b, DINNER, H, DV))

        def step(carry, xs):
            W_in, W_out = carry
            qi, ki, vi, li, lo, wi, wo = xs
            p_q = jax.nn.softmax(jnp.einsum('bnhd,bDhd->bnhD', qi, W_in), axis=1)
            o = jnp.einsum('bnhD,bDhd->bnhd', p_q, W_out)
            p = jax.nn.softmax(jnp.einsum('bnhd,bDhd->bnhD', ki, W_in), axis=1)
            grad_out = jnp.einsum('bnhD,bnhd->bDhd', -p, vi)
            a = jnp.einsum('bDhd,bnhd->bnhD', W_out, vi)
            s = jnp.sum(p * a, axis=-1, keepdims=True)
            g_z = -(p * a - p * s)
            grad_in = jnp.einsum('bnhd,bnhD->bDhd', ki, g_z)
            W_in = wi[:, None, :, None] * W_in - li[:, None, :, None] * grad_in
            W_out = wo[:, None, :, None] * W_out - lo[:, None, :, None] * grad_out
            return ((W_in, W_out), o)
        _, outs = jax.lax.scan(step, (W_in0, W_out0), (qc, kc, vc, lr_in, lr_out, wd_in, wd_out))
        o = jnp.moveaxis(outs, 0, 1).reshape(b, l, H * DV)
        return o @ Wo.T

    def _L1_ffn_ref(x, W_sw, b_sw, W1, b1, W2, b2):
        import jax, jax.numpy as jnp
        import numpy as np
        HIDDEN = 128
        FF = 512
        N_EXPERTS = 8
        CAP_FACTOR = 1.0
        B, S = (4, 256)
        STD = 0.02

        def _gelu(x):
            return x * 0.5 * (1.0 + jax.lax.erf(x / 1.41421))
        Bb, Ss, D = x.shape
        T = Bb * Ss
        E = W1.shape[0]
        capacity = int(CAP_FACTOR * T / E)
        xf = x.reshape(T, D)
        logits = xf @ W_sw + b_sw
        probs = jax.nn.softmax(logits, axis=-1)
        pmax = jnp.max(probs, axis=-1)
        routes = jnp.argmax(probs, axis=-1)
        factor = pmax / jax.lax.stop_gradient(pmax)
        xs = xf * factor[:, None]
        onehot = jax.nn.one_hot(routes, E, dtype=jnp.int32)
        pos = jnp.cumsum(onehot, axis=0) - 1
        pos_tok = jnp.take_along_axis(pos, routes[:, None], axis=1)[:, 0]
        keep = pos_tok < capacity
        pos_safe = jnp.where(keep, pos_tok, capacity)
        buf = jnp.zeros((E, capacity + 1, D), dtype=xs.dtype)
        buf = buf.at[routes, pos_safe].set(xs)
        buf = buf[:, :capacity]
        h = _gelu(jnp.einsum('ecd,edf->ecf', buf, W1) + b1[:, None, :])
        expert_out = jnp.einsum('ecf,efd->ecd', h, W2) + b2[:, None, :]
        gathered = expert_out[routes, jnp.minimum(pos_tok, capacity - 1)]
        final = jnp.where(keep[:, None], gathered, xs)
        return final.reshape(Bb, Ss, D)

    def _L2_attn_ref(x, w_qkv, b_qkv, w_out, b_out, w_gate, b_gate, pos_bias):
        import jax, jax.numpy as jnp
        import numpy as np
        N_SCALES = 11
        N_TAPS = 4
        OFFSETS = [(1 << j) * tau for j in range(N_SCALES) for tau in range(N_TAPS)]

        def _shift(a, off):
            N = a.shape[2]
            return jnp.pad(a[:, :, :N - off], ((0, 0), (0, 0), (off, 0), (0, 0)))
        B, N, D = x.shape
        H = pos_bias.shape[1]
        HD = D // H
        scale = HD ** (-0.5)
        qkv = x @ w_qkv + b_qkv
        q, k, v = jnp.split(qkv, 3, axis=-1)
        q = q.reshape(B, N, H, HD).transpose(0, 2, 1, 3)
        k = k.reshape(B, N, H, HD).transpose(0, 2, 1, 3)
        v = v.reshape(B, N, H, HD).transpose(0, 2, 1, 3)
        scores = []
        for off in OFFSETS:
            if off == 0:
                ks_ = k
            elif off >= N:
                ks_ = jnp.zeros_like(k)
            else:
                ks_ = _shift(k, off)
            scores.append(jnp.einsum('bhnd,bhnd->bhn', q, ks_) * scale)
        scores = jnp.stack(scores, axis=-1)
        scores = scores + pos_bias.T[None, :, None, :]
        attn = jax.nn.softmax(scores, axis=-1)
        out = jnp.zeros_like(q)
        for i, off in enumerate(OFFSETS):
            if off >= N:
                continue
            vs = v if off == 0 else _shift(v, off)
            out = out + attn[..., i:i + 1] * vs
        gathered = out.transpose(0, 2, 1, 3).reshape(B, N, D)
        gate = jax.nn.sigmoid(x @ w_gate + b_gate)
        return gathered * gate @ w_out + b_out

    def _L2_ffn_ref(x, g1, g2, wq, wk, wv, wo, gate, w1, w2, w3):
        import jax, jax.numpy as jnp
        import numpy as np
        DIM = 128
        N_HEADS = 16
        N_KV_HEADS = 4
        HEAD_DIM = DIM // N_HEADS
        N_REP = N_HEADS // N_KV_HEADS
        N_EXPERTS = 4
        TOP_K = 2
        HIDDEN = 3 * DIM
        EPS = 1.1920928955078125e-07

        def _rmsnorm(x, g):
            var = jnp.mean(jnp.square(x), axis=-1, keepdims=True)
            return x * jax.lax.rsqrt(var + EPS) * g

        def _rotate_half(x):
            x1, x2 = jnp.split(x, 2, axis=-1)
            return jnp.concatenate([-x2, x1], axis=-1)

        def _rope_tables(S):
            inv_freq = 1.0 / 10000.0 ** (jnp.arange(0, HEAD_DIM, 2, dtype=jnp.float32) / HEAD_DIM)
            freqs = jnp.arange(S, dtype=jnp.float32)[:, None] * inv_freq[None, :]
            emb = jnp.concatenate([freqs, freqs], axis=-1)
            return (jnp.cos(emb), jnp.sin(emb))

        def _attention(x, wq, wk, wv, wo):
            B, S, D = x.shape
            q = (x @ wq).reshape(B, S, N_HEADS, HEAD_DIM).transpose(0, 2, 1, 3)
            k = (x @ wk).reshape(B, S, N_KV_HEADS, HEAD_DIM).transpose(0, 2, 1, 3)
            v = (x @ wv).reshape(B, S, N_KV_HEADS, HEAD_DIM).transpose(0, 2, 1, 3)
            cos, sin = _rope_tables(S)
            q = q * cos + _rotate_half(q) * sin
            k = k * cos + _rotate_half(k) * sin
            k = jnp.repeat(k, N_REP, axis=1)
            v = jnp.repeat(v, N_REP, axis=1)
            scores = jnp.einsum('bhqd,bhkd->bhqk', q, k) / jnp.sqrt(jnp.float32(HEAD_DIM))
            causal = jnp.tril(jnp.ones((S, S), dtype=bool))
            scores = jnp.where(causal, scores, -jnp.inf)
            attn = jax.nn.softmax(scores, axis=-1)
            out = jnp.einsum('bhqk,bhkd->bhqd', attn, v)
            return out.transpose(0, 2, 1, 3).reshape(B, S, D) @ wo

        def _moe(x, gate, w1, w2, w3):
            B, S, D = x.shape
            xf = x.reshape(-1, D)
            probs = jax.nn.softmax(xf @ gate, axis=-1)
            w, idx = jax.lax.top_k(probs, TOP_K)
            w = w / jnp.sum(w, axis=-1, keepdims=True)
            oh = jax.nn.one_hot(idx, N_EXPERTS, dtype=xf.dtype)
            comb = jnp.einsum('nk,nke->ne', w, oh)
            out = jnp.zeros_like(xf)
            for e in range(N_EXPERTS):
                h = jax.nn.silu(xf @ w1[e]) * (xf @ w3[e])
                out = out + comb[:, e:e + 1] * (h @ w2[e])
            return out.reshape(B, S, D)
        x = x + _attention(_rmsnorm(x, g1), wq, wk, wv, wo)
        x = x + _moe(_rmsnorm(x, g2), gate, w1, w2, w3)
        return x

    def _L3_attn_ref(x, Wq, Wk, Wv, Wu, bu):
        import jax, jax.numpy as jnp
        import numpy as np
        K = 128
        HEADS = 16
        b, t, k = x.shape
        h = HEADS
        s = k // h
        q = (x @ Wq.T).reshape(b, t, h, s)
        kk = (x @ Wk.T).reshape(b, t, h, s)
        v = (x @ Wv.T).reshape(b, t, h, s)
        dot = jnp.einsum('bqhs,bkhs->bhqk', q, kk) / jnp.sqrt(jnp.float32(k))
        attn = jax.nn.softmax(dot, axis=-1)
        out = jnp.einsum('bhqk,bkhs->bqhs', attn, v).reshape(b, t, k)
        return out @ Wu.T + bu

    def _L3_ffn_ref(x, router_W, router_b, sW1, sb1, sW2, sb2, eW1, eb1, eW2, eb2):
        import jax, jax.numpy as jnp
        import numpy as np
        B, L, D = (2, 256, 128)
        E = 15
        H = D * 1
        K = 3
        T = 1.0
        b, l, d = x.shape
        n = b * l
        xt = x.reshape(n, d)
        shared = jax.nn.relu(xt @ sW1 + sb1) @ sW2 + sb2
        logits = xt @ router_W + router_b
        probs = jax.nn.softmax(logits / T, axis=-1)
        top_p, top_i = jax.lax.top_k(probs, K)
        cw = jnp.zeros((n, E), dtype=probs.dtype)
        cw = cw.at[jnp.arange(n)[:, None], top_i].set(top_p)
        h = jax.nn.relu(jnp.einsum('nd,edh->neh', xt, eW1) + eb1)
        ye = jnp.einsum('neh,ehd->ned', h, eW2) + eb2
        routed = jnp.einsum('ned,ne->nd', ye, cw)
        return (shared + routed).reshape(b, l, d)
    x = L0_attn_x
    xn = _layernorm(x, axis=-1)
    s = _L0_attn_ref(xn, L0_attn_g1, L0_attn_b1, L0_attn_Wqkv_a, L0_attn_bqkv_a, L0_attn_Wp_a, L0_attn_bp_a, L0_attn_Wqkv_s, L0_attn_bqkv_s, L0_attn_Wo_s, L0_attn_bo_s, L0_attn_Wo, L0_attn_bo, L0_attn_gm, L0_attn_bm, L0_attn_W1, L0_attn_b1m, L0_attn_W2, L0_attn_b2m)
    g = _silu(_L0_ffn_ref(xn, L0_ffn_router_w, L0_ffn_router_b, L0_ffn_w1, L0_ffn_b1, L0_ffn_w2, L0_ffn_b2))
    x = x + s * g
    xn = _layernorm(x, axis=-1)
    s = _L1_attn_ref(xn, L1_attn_Wq, L1_attn_Wk, L1_attn_Wv, L1_attn_Wlr, L1_attn_Wbeta, L1_attn_Wo, L1_attn_W_in_init, L1_attn_W_out_init)
    g = _silu(_L1_ffn_ref(xn, L1_ffn_W_sw, L1_ffn_b_sw, L1_ffn_W1, L1_ffn_b1, L1_ffn_W2, L1_ffn_b2))
    x = x + s * g
    xn = _layernorm(x, axis=-1)
    s = _L2_attn_ref(xn, L2_attn_w_qkv, L2_attn_b_qkv, L2_attn_w_out, L2_attn_b_out, L2_attn_w_gate, L2_attn_b_gate, L2_attn_pos_bias)
    g = _silu(_L2_ffn_ref(xn, L2_ffn_g1, L2_ffn_g2, L2_ffn_wq, L2_ffn_wk, L2_ffn_wv, L2_ffn_wo, L2_ffn_gate, L2_ffn_w1, L2_ffn_w2, L2_ffn_w3))
    x = x + s * g
    xn = _layernorm(x, axis=-1)
    s = _L3_attn_ref(xn, L3_attn_Wq, L3_attn_Wk, L3_attn_Wv, L3_attn_Wu, L3_attn_bu)
    g = _silu(_L3_ffn_ref(xn, L3_ffn_router_W, L3_ffn_router_b, L3_ffn_sW1, L3_ffn_sb1, L3_ffn_sW2, L3_ffn_sb2, L3_ffn_eW1, L3_ffn_eb1, L3_ffn_eW2, L3_ffn_eb2))
    x = x + s * g
    return x

_drawn_inputs = setup_inputs


def setup_inputs(seed=0):
    import zlib

    import numpy as np

    out = dict(_drawn_inputs(seed))
    spreads = {'L0_attn_g1': (1.0, 0.6),
     'L0_attn_b1': (0.0, 0.8),
     'L0_attn_bqkv_a': (0.0, 0.8),
     'L0_attn_bp_a': (0.0, 0.8),
     'L0_attn_bqkv_s': (0.0, 0.8),
     'L0_attn_bo_s': (0.0, 0.8),
     'L0_attn_bo': (0.0, 0.8),
     'L0_attn_gm': (1.0, 0.6),
     'L0_attn_bm': (0.0, 0.8),
     'L0_attn_b1m': (0.0, 0.8),
     'L0_attn_b2m': (0.0, 0.8),
     'L0_ffn_router_b': (0.0, 0.359),
     'L0_ffn_b1': (0.0, 0.8),
     'L0_ffn_b2': (0.0, 0.1),
     'L1_ffn_b_sw': (0.0, 0.8),
     'L1_ffn_b1': (0.0, 0.8),
     'L1_ffn_b2': (0.0, 0.8),
     'L2_attn_b_qkv': (0.0, 0.8),
     'L2_attn_b_out': (0.0, 0.1),
     'L2_attn_b_gate': (2.0, 0.6),
     'L2_ffn_g1': (1.0, 0.6),
     'L2_ffn_g2': (1.0, 0.6),
     'L3_ffn_router_b': (0.0, 0.8),
     'L3_ffn_sb1': (0.0, 0.8),
     'L3_ffn_sb2': (0.0, 0.8),
     'L3_ffn_eb1': (0.0, 0.8),
     'L3_ffn_eb2': (0.0, 0.8)}
    factors = {'L0_attn_Wqkv_a': 8.0,
     'L0_attn_Wp_a': 8.0,
     'L0_attn_Wqkv_s': 8.0,
     'L0_attn_Wo_s': 8.0,
     'L0_attn_Wo': 8.0,
     'L0_attn_W1': 8.0,
     'L0_attn_W2': 8.0,
     'L0_ffn_w1': 2.949,
     'L0_ffn_w2': 2.687,
     'L1_attn_Wq': 8.0,
     'L1_attn_Wk': 8.0,
     'L1_attn_Wv': 8.0,
     'L1_attn_Wlr': 8.0,
     'L1_attn_Wbeta': 8.0,
     'L1_attn_Wo': 8.0,
     'L1_attn_W_in_init': 8.0,
     'L1_attn_W_out_init': 8.0,
     'L1_ffn_W_sw': 8.0,
     'L1_ffn_W1': 8.0,
     'L1_ffn_W2': 8.0,
     'L2_attn_w_qkv': 7.397,
     'L2_attn_w_out': 4.6,
     'L2_attn_w_gate': 8.0,
     'L2_attn_pos_bias': 8.0,
     'L2_ffn_wq': 8.0,
     'L2_ffn_wk': 8.0,
     'L2_ffn_wv': 8.0,
     'L2_ffn_wo': 8.0,
     'L2_ffn_gate': 8.0,
     'L2_ffn_w1': 8.0,
     'L2_ffn_w2': 8.0,
     'L2_ffn_w3': 8.0,
     'L3_attn_Wq': 8.0,
     'L3_attn_Wk': 8.0,
     'L3_attn_Wv': 8.0,
     'L3_attn_Wu': 8.0,
     'L3_attn_bu': 200.0,
     'L3_ffn_router_W': 8.0,
     'L3_ffn_sW1': 8.0,
     'L3_ffn_sW2': 8.0,
     'L3_ffn_eW1': 8.0,
     'L3_ffn_eW2': 8.0}
    for name, (base, spread) in spreads.items():
        noise = np.random.default_rng([zlib.crc32(name.encode()), seed]).standard_normal(out[name].shape)
        drawn = base * np.exp(spread * noise) if base else spread * noise
        out[name] = jnp.asarray(drawn.astype(out[name].dtype))
    for name, factor in factors.items():
        out[name] = (out[name] * factor).astype(out[name].dtype)
    return out
```

```python
from contextlib import ExitStack
import numpy as np
import concourse.bass as bass
from concourse import mybir

F32 = mybir.dt.float32
BF16 = mybir.dt.bfloat16
ACT = mybir.ActivationFunctionType
ALU = mybir.AluOpType
AX = mybir.AxisListType

P = 128
T = 2048
SL = 512
NS = T // SL
N = 1024




class Kit:
    pass


def layer_norm(nc, tag, kit, src, dst, gain_dram=None, rms=False):
    tiles = T // P
    with nc.cleanup_on_exit(), ExitStack() as ctx:
        sb = lambda name, shape: ctx.enter_context(nc.sbuf_tensor(f"{tag}_{name}", shape, F32))
        sq = sb("sq", [P, T])
        gain = sb("gain", [P, 2])
        var, inv, tmp = (sb(n, [P, tiles]) for n in ("var", "inv", "tmp"))
        diag = sb("diag", [P, tiles, P])
        ps = [ctx.enter_context(nc.psum_tensor(f"{tag}_ps{s}", [P, SL], F32)) for s in range(NS)]
        ps_var = ctx.enter_context(nc.psum_tensor(f"{tag}_psvar", [P, tiles], F32))
        sem = lambda name: nc.alloc_semaphore(f"{tag}_{name}")
        loaded, mean_ready, centered, squared, var_ready = (sem(n) for n in ("loaded", "mean_ready", "centered", "squared", "var_ready"))
        chain, var_in, std_ready, diag_ready, spread, scaled = (sem(n) for n in (
            "chain", "var_in", "std_ready", "diag_ready", "spread", "scaled"))
        loads = int(gain_dram is not None)
        n_gain = gain_dram.shape[1] if loads else 0
        base = src if rms else dst
        eps = 1.1920928955078125e-07 if rms else 1e-5
        with nc.Block() as block:

            if loads:
                @block.sync
                def _(sp):
                    sp.dma_start(gain[:, 0:n_gain], gain_dram).then_inc(loaded, 16)
                    sp.wait_ge(loaded, 16)

            @block.tensor
            def _(pe):
                if not rms:
                    for s in range(NS):
                        pe.matmul(ps[s][:, :], kit.mean[:, :], src[:, s * SL:(s + 1) * SL], start=True, stop=True).then_inc(mean_ready, 1)
                for t in range(tiles):
                    if t % 4 == 0:
                        pe.wait_ge(squared, t // 4 + 1)
                    mm = pe.matmul(ps_var[:, t:t + 1], sq[:, t * P:(t + 1) * P], kit.mean[:, 0:1], start=True, stop=True)
                mm.then_inc(var_ready, 1)
                for s in range(NS):
                    pe.wait_ge(diag_ready, s + 1)
                    pe.matmul(ps[s][:, :], kit.ones[:, :], diag[:, 4 * s:4 * s + 4, :], start=True, stop=True).then_inc(spread, 1)

            @block.scalar
            def _(ac):
                for s in range(NS):
                    if not rms:
                        ac.wait_ge(centered, s + 1)
                    ac.activation(sq[:, s * SL:(s + 1) * SL], base[:, s * SL:(s + 1) * SL], ACT.Square).then_inc(squared, 1)
                ac.wait_ge(var_in, 1)
                ac.activation(inv[:, :], var[:, :], ACT.Sqrt).then_inc(std_ready, 1)

            @block.vector
            def _(ve):
                done = [0]

                def link(ins):
                    done[0] += 1
                    ins.then_inc(chain, 1)
                    ve.wait_ge(chain, done[0])

                if not rms:
                    for s in range(NS):
                        ve.wait_ge(mean_ready, s + 1)
                        ve.tensor_tensor(dst[:, s * SL:(s + 1) * SL], src[:, s * SL:(s + 1) * SL], ps[s][:, :], ALU.subtract).then_inc(centered, 1)
                ve.wait_ge(var_ready, 1)
                ve.tensor_scalar(var[:, :], ps_var[:, :], eps, None, ALU.add).then_inc(var_in, 1)
                ve.wait_ge(std_ready, 1)
                link(ve.reciprocal(inv[:, :], inv[:, :]))
                link(ve.tensor_tensor(tmp[:, :], inv[:, :], inv[:, :], ALU.mult))
                link(ve.tensor_tensor(tmp[:, :], tmp[:, :], var[:, :], ALU.mult))
                link(ve.tensor_scalar(tmp[:, :], tmp[:, :], -0.5, 1.5, ALU.mult, ALU.add))
                link(ve.tensor_tensor(inv[:, :], inv[:, :], tmp[:, :], ALU.mult))
                for s in range(NS):
                    ve.tensor_tensor(diag[:, 4 * s:4 * s + 4, :], kit.ident[:, :].unsqueeze(1).broadcast_to([P, 4, P]),
                                     inv[:, 4 * s:4 * s + 4].unsqueeze(2).broadcast_to([P, 4, P]), ALU.mult).then_inc(diag_ready, 1)
                if loads:
                    ve.wait_ge(loaded, 16)
                for s in range(NS):
                    part = slice(s * SL, (s + 1) * SL)
                    ve.wait_ge(spread, s + 1)
                    if gain_dram is None:
                        ve.tensor_tensor(dst[:, part], base[:, part], ps[s][:, :], ALU.mult).then_inc(scaled, 1)
                    else:
                        ve.scalar_tensor_tensor(dst[:, part], base[:, part], gain[:, 0:1], ps[s][:, :], ALU.mult, ALU.mult).then_inc(scaled, 1)
                    if n_gain == 2:
                        ve.wait_ge(scaled, s + 1)
                        ve.tensor_scalar(dst[:, part], dst[:, part], gain[:, 1:2], None, ALU.add).then_inc(centered, 1)


def project(nc, tag, jobs, ins, w_dram, columns_dram):
    n_w = w_dram.shape[1]
    with nc.cleanup_on_exit(), ExitStack() as ctx:
        w = ctx.enter_context(nc.sbuf_tensor(f"{tag}_w", [P, n_w, P], F32))
        cols = ctx.enter_context(nc.sbuf_tensor(f"{tag}_cols", [P, columns_dram.shape[1]], F32))
        ps = [ctx.enter_context(nc.psum_tensor(f"{tag}_ps{s}", [P, SL], F32)) for s in range(NS)]
        sem = lambda name: nc.alloc_semaphore(f"{tag}_{name}")
        loaded, product_ready, emptied, added = sem("loaded"), sem("product_ready"), sem("emptied"), sem("added")
        adds = [False]
        with nc.Block() as block:

            @block.sync
            def _(sp):
                sp.dma_start(w[:, :, :], w_dram).then_inc(loaded, 16)
                sp.dma_start(cols[:, :], columns_dram).then_inc(loaded, 16)
                sp.wait_ge(loaded, 32)

            @block.tensor
            def _(pe):
                pe.wait_ge(loaded, 32)
                for n, (terms, bias, act, rows, out, add) in enumerate(jobs):
                    for s in range(NS):
                        if n:
                            pe.wait_ge(emptied, (n - 1) * NS + s + 1)
                        for i, (k, src) in enumerate(terms):
                            mm = pe.matmul(ps[s][0:rows, :], w[:, k, 0:rows], ins[src](s),
                                           start=i == 0, stop=i == len(terms) - 1)
                        mm.then_inc(product_ready, 1)

            @block.scalar
            def _(ac):
                ac.wait_ge(loaded, 32)
                for n, (terms, bias, act, rows, out, add) in enumerate(jobs):
                    for s in range(NS):
                        ac.wait_ge(product_ready, n * NS + s + 1)
                        target = ps[s][0:rows, :] if add else out[:, s * SL:(s + 1) * SL]
                        if bias is None:
                            ins_ = ac.activation(target, ps[s][0:rows, :], ACT.Copy if act is None else act)
                        else:
                            ins_ = ac.activation(target, ps[s][0:rows, :], ACT.Identity if act is None else act,
                                                 bias=cols[0:rows, bias:bias + 1])
                        ins_.then_inc(added if add else emptied, 1)

            if any(j[5] for j in jobs):
                @block.vector
                def _(ve):
                    k = 0
                    for n, (terms, bias, act, rows, out, add) in enumerate(jobs):
                        if add:
                            for s in range(NS):
                                k += 1
                                ve.wait_ge(added, k)
                                part = out[:, s * SL:(s + 1) * SL]
                                ve.tensor_tensor(part, ps[s][0:rows, :], part, ALU.add).then_inc(emptied, 1)


def slices_of(a):
    return lambda s: a[:, s * SL:(s + 1) * SL]


def heads_of(out_all, g):
    return lambda s: out_all[:, (s // 2) * 4 + g, (s % 2) * SL:(s % 2 + 1) * SL]


def values(nc, tag, kit, xin, wv_dram, bias_dram, key_heads, v_all, function=None):
    nv = 4 * key_heads * E8
    with nc.cleanup_on_exit(), ExitStack() as ctx:
        w = ctx.enter_context(nc.sbuf_tensor(f"{tag}_w", [P, nv], F32))
        bias = ctx.enter_context(nc.sbuf_tensor(f"{tag}_b", [P, nv], F32))
        ps = [ctx.enter_context(nc.psum_tensor(f"{tag}_ps{i}", [P, 4, nv], F32)) for i in range(4)]
        sem = lambda name: nc.alloc_semaphore(f"{tag}_{name}")
        loaded, filled, product_ready, placed = sem("loaded"), sem("filled"), sem("product_ready"), sem("placed")
        with nc.Block() as block:

            @block.sync
            def _(sp):
                sp.dma_start(w[:, :], wv_dram).then_inc(loaded, 16)
                sp.dma_start(bias[:, :], bias_dram.broadcast_to([P, nv])).then_inc(loaded, 16)
                sp.wait_ge(loaded, 32)

            @block.gpsimd
            def _(po):
                po.memset(v_all[:, :, :, :, 9:32], 0.0).then_inc(filled, 1)
                po.memset(v_all[:, :, :, :, 8:9], 1.0).then_inc(filled, 1)

            @block.tensor
            def _(pe):
                pe.wait_ge(loaded, 32)
                for i in range(4):
                    for k in range(4):
                        t = 4 * i + k
                        mm = pe.matmul(ps[i][:, k, :], xin[:, t * P:(t + 1) * P], w[:, :], start=True, stop=True)
                    mm.then_inc(product_ready, 1)

            @block.vector
            def _(ve):
                ve.wait_ge(loaded, 32)
                for t in range(16):
                    if t % 4 == 0:
                        ve.wait_ge(product_ready, t // 4 + 1)
                    b, kt = t // 8, t % 8
                    ve.tensor_tensor(v_all[:, b * 4:b * 4 + 4, kt, :, 0:8],
                                     ps[t // 4][:, t % 4, :].rearrange("p (g h e) -> p g h e", g=4, h=key_heads),
                                     bias[:, :].rearrange("p (g h e) -> p g h e", g=4, h=key_heads), ALU.add).then_inc(placed, 1)


def query_parts(nc, tag, kit, xin, w_dram, bias_dram, rows, slots, dest, rope_dram=None):
    nw = 2 if rope_dram is not None else 1
    with nc.cleanup_on_exit(), ExitStack() as ctx:
        sb = lambda name, shape, dt=F32: ctx.enter_context(nc.sbuf_tensor(f"{tag}_{name}", shape, dt))
        w = sb("w", [P, nw * rows])
        bias = sb("bias", [rows, 1])
        full = sb("full", [rows, T])
        rest = sb("rest", [rows, T])
        part = [sb(f"part{i}", [rows, T], BF16) for i in range(3)]
        rope = [sb(f"rope{i}", [rows, N]) for i in range(2)] if nw == 2 else []
        ps = [ctx.enter_context(nc.psum_tensor(f"{tag}_ps{s}", [rows, SL], F32)) for s in range(NS * nw)]
        sem = lambda name: nc.alloc_semaphore(f"{tag}_{name}")
        loaded, product_ready, whole, split, stored = (sem(n) for n in ("loaded", "product_ready", "whole", "split", "stored"))
        turned = sem("turned")
        loads = 1 + (2 if nw == 2 else 0) + (bias_dram is not None)
        with nc.Block() as block:

            @block.sync
            def _(sp):
                sp.dma_start(w[:, :], w_dram).then_inc(loaded, 16)
                if bias_dram is not None:
                    sp.dma_start(bias[:, :], bias_dram).then_inc(loaded, 16)
                for i, r in enumerate(rope):
                    sp.dma_start(r[:, :], rope_dram[i, 0:rows]).then_inc(loaded, 16)
                for i, p in enumerate(slots):
                    sp.wait_ge(split, (1, 3, 4)[p])
                    sp.dma_start(dest[:, i * E8:(i + 1) * E8, :, :].rearrange("b e h n -> (e h) b n"),
                                 part[p][:, :].rearrange("r (b n) -> r b n", b=2)).then_inc(stored, 16)
                sp.wait_ge(stored, 16 * len(slots))

            @block.tensor
            def _(pe):
                pe.wait_ge(loaded, 16 * loads)
                for k in range(nw):
                    for s in range(NS):
                        pe.matmul(ps[k * NS + s][:, :], w[:, k * rows:(k + 1) * rows], xin[:, s * SL:(s + 1) * SL],
                                  start=True, stop=True).then_inc(product_ready, 1)

            if nw == 1:
                @block.scalar
                def _(ac):
                    for s in range(NS):
                        ac.wait_ge(product_ready, s + 1)
                        if bias_dram is None:
                            ac.activation(full[:, s * SL:(s + 1) * SL], ps[s][:, :], ACT.Copy).then_inc(whole, 1)
                        else:
                            ac.activation(full[:, s * SL:(s + 1) * SL], ps[s][:, :], ACT.Identity, bias=bias[:, 0:1]).then_inc(whole, 1)

            @block.vector
            def _(ve):
                if nw == 2:
                    for s in range(NS):
                        ve.wait_ge(product_ready, NS + s + 1)
                        a, r = slice(s * SL, (s + 1) * SL), slice((s % 2) * SL, (s % 2 + 1) * SL)
                        ve.tensor_tensor(full[:, a], ps[s][:, :], rope[0][:, r], ALU.mult).then_inc(turned, 1)
                        ve.tensor_tensor(rest[:, a], ps[NS + s][:, :], rope[1][:, r], ALU.mult).then_inc(turned, 1)
                        ve.wait_ge(turned, 2 * s + 2)
                        ve.tensor_tensor(full[:, a], full[:, a], rest[:, a], ALU.add).then_inc(whole, 1)
                ve.wait_ge(whole, NS)
                ve.tensor_copy(part[0][:, :], full[:, :]).then_inc(split, 1)
                ve.wait_ge(split, 1)
                ve.tensor_tensor(rest[:, :], full[:, :], part[0][:, :], ALU.subtract).then_inc(split, 1)
                ve.wait_ge(split, 2)
                ve.tensor_copy(part[1][:, :], rest[:, :]).then_inc(split, 1)
                ve.wait_ge(split, 3)
                ve.tensor_tensor(part[2][:, :], rest[:, :], part[1][:, :], ALU.subtract).then_inc(split, 1)


def route(nc, tag, kit, xn, router_dram, bias_dram, experts, top, mode, gates, gate_dram, total, capacity=None):
    E = experts
    tiles = T // P
    with nc.cleanup_on_exit(), ExitStack() as ctx:
        sb = lambda name, shape, dt=F32: ctx.enter_context(nc.sbuf_tensor(f"{tag}_{name}", shape, dt))
        w = sb("w", [P, E])
        bias = sb("bias", [P, E])
        p = sb("p", [P, tiles, E])
        big = [sb(f"big{i}", [P, tiles, E, E]) for i in range(2)]
        col = sb("col", [P, tiles])
        rank = sb("rank", [P, tiles, E])
        out = sb("out", [P, tiles, total])
        ps_l = ctx.enter_context(nc.psum_tensor(f"{tag}_l", [P, tiles, E], F32))
        ps_c = ctx.enter_context(nc.psum_tensor(f"{tag}_c", [P, tiles, E], F32))
        ps_t = [ctx.enter_context(nc.psum_tensor(f"{tag}_t{s}", [total, SL], F32)) for s in range(NS)]
        sem = lambda name: nc.alloc_semaphore(f"{tag}_{name}")
        loaded, logits_ready, shifted, exp_done, chain, gates_ready, turned, gates_in, stored = (sem(n) for n in (
            "loaded", "logits_ready", "shifted", "exp_done", "chain", "gates_ready", "turned", "gates_in", "stored"))
        chosen, counted, filled = sem("chosen"), sem("counted"), sem("filled")

        with nc.Block() as block:

            @block.sync
            def _(sp):
                sp.dma_start(w[:, :], router_dram).then_inc(loaded, 16)
                sp.dma_start(bias[:, :], bias_dram.broadcast_to([P, E])).then_inc(loaded, 16)
                sp.wait_ge(gates_in, NS)
                sp.dma_start(gate_dram, gates[0:total, :]).then_inc(stored, 16)
                sp.wait_ge(stored, 16)

            @block.tensor
            def _(pe):
                pe.wait_ge(loaded, 32)
                for t in range(tiles):
                    mm = pe.matmul(ps_l[:, t, :], xn[:, t * P:(t + 1) * P], w[:, :], start=True, stop=True)
                mm.then_inc(logits_ready, 1)
                if mode == "capacity":
                    pe.wait_ge(chosen, 1)
                    pe.matmul(ps_c[:, :, :], kit.upto[:, :], rank[:, :, :], start=True, stop=False, skip_group_check=True)
                    for t in range(tiles - 1):
                        mm = pe.matmul(ps_c[:, t + 1:, :], kit.ones[:, :],
                                       rank[:, t, :].unsqueeze(1).broadcast_to([P, tiles - 1 - t, E]), start=False,
                                       stop=t == tiles - 2, skip_group_check=True)
                    mm.then_inc(counted, 1)
                pe.wait_ge(gates_ready, 1)
                for s in range(NS):
                    for k in range(4):
                        mm = pe.transpose(ps_t[s][:, k * P:(k + 1) * P], out[:, 4 * s + k, :], kit.ident[:, :])
                    mm.then_inc(turned, 1)

            @block.scalar
            def _(ac):
                ac.wait_ge(shifted, 1)
                ac.activation(p[:, :, :], p[:, :, :], ACT.Exp).then_inc(exp_done, 1)
                for s in range(NS):
                    ac.wait_ge(turned, s + 1)
                    ac.activation(gates[0:total, s * SL:(s + 1) * SL], ps_t[s][:, :], ACT.Copy).then_inc(gates_in, 1)

            @block.vector
            def _(ve):
                done = [0]

                def link(ins):
                    done[0] += 1
                    ins.then_inc(chain, 1)
                    ve.wait_ge(chain, done[0])

                def across(a):
                    return a.unsqueeze(2).broadcast_to([P, tiles, E])

                ve.wait_ge(loaded, 32)
                ve.wait_ge(logits_ready, 1)
                link(ve.tensor_tensor(p[:, :, :], ps_l[:, :, :], bias[:, :].unsqueeze(1).broadcast_to([P, tiles, E]), ALU.add))
                link(ve.tensor_reduce(col[:, :], p[:, :, :], AX.X, ALU.max))
                ve.tensor_tensor(p[:, :, :], p[:, :, :], across(col[:, :]), ALU.subtract).then_inc(shifted, 1)
                ve.wait_ge(exp_done, 1)
                link(ve.tensor_reduce(col[:, :], p[:, :, :], AX.X, ALU.add))
                link(ve.reciprocal(col[:, :], col[:, :]))
                link(ve.tensor_tensor(p[:, :, :], p[:, :, :], across(col[:, :]), ALU.mult))
                other = p[:, :, :].unsqueeze(2).broadcast_to([P, tiles, E, E])
                own = p[:, :, :].unsqueeze(3).broadcast_to([P, tiles, E, E])
                ve.tensor_tensor(big[0][:, :, :, :], other, own, ALU.is_gt).then_inc(filled, 1)
                link(ve.tensor_tensor(big[1][:, :, :, :], other, own, ALU.is_equal))
                lower = kit.lower[:, :, :][:, 0:E, 0:E].unsqueeze(1).broadcast_to([P, tiles, E, E])
                link(ve.tensor_tensor(big[1][:, :, :, :], big[1][:, :, :, :], lower, ALU.mult))
                ve.wait_ge(filled, 1)
                link(ve.tensor_tensor(big[0][:, :, :, :], big[0][:, :, :, :], big[1][:, :, :, :], ALU.add))
                link(ve.tensor_reduce(rank[:, :, :], big[0][:, :, :, :], AX.X, ALU.add))
                link(ve.tensor_scalar(rank[:, :, :], rank[:, :, :], top - 0.5, None, ALU.is_lt))
                if mode == "capacity":
                    ve.sem_inc(chosen, 1)
                    ve.wait_ge(counted, 1)
                    link(ve.tensor_scalar(p[:, :, :], ps_c[:, :, :], capacity + 0.5, None, ALU.is_lt))
                    link(ve.tensor_tensor(out[:, :, 0:E], p[:, :, :], rank[:, :, :], ALU.mult))
                    link(ve.tensor_reduce(col[:, :], out[:, :, 0:E], AX.X, ALU.add))
                    ve.tensor_scalar(out[:, :, E:E + 1], col[:, :].unsqueeze(2), -1.0, 1.0, ALU.mult, ALU.add).then_inc(gates_ready, 1)
                elif mode == "share":
                    link(ve.tensor_tensor(p[:, :, :], p[:, :, :], rank[:, :, :], ALU.mult))
                    link(ve.tensor_reduce(col[:, :], p[:, :, :], AX.X, ALU.add))
                    link(ve.reciprocal(col[:, :], col[:, :]))
                    ve.tensor_tensor(out[:, :, :], p[:, :, :], across(col[:, :]), ALU.mult).then_inc(gates_ready, 1)
                else:
                    link(ve.memset(out[:, :, E:E + 1], 1.0))
                    ve.tensor_tensor(out[:, :, 0:E], p[:, :, :], rank[:, :, :], ALU.mult).then_inc(gates_ready, 1)


def residual(nc, tag, x, s_out, result, plus=None, dropped_dram=None, xn=None):
    with nc.cleanup_on_exit(), ExitStack() as ctx:
        drop = ctx.enter_context(nc.sbuf_tensor(f"{tag}_drop", [P, T], F32))
        sem = lambda name: nc.alloc_semaphore(f"{tag}_{name}")
        loaded, complete, silu_done, multiplied, updated = (sem(n) for n in ("loaded", "complete", "silu_done", "multiplied", "updated"))
        masked = sem("masked")
        with nc.Block() as block:

            if dropped_dram is not None:
                @block.sync
                def _(sp):
                    sp.dma_start(drop[:, :], dropped_dram.broadcast_to([P, T])).then_inc(loaded, 16)
                    sp.wait_ge(loaded, 16)

            @block.scalar
            def _(ac):
                for s in range(NS):
                    part = slice(s * SL, (s + 1) * SL)
                    if plus is not None or dropped_dram is not None:
                        ac.wait_ge(complete, s + 1)
                    ac.activation(result[:, part], result[:, part], ACT.Silu).then_inc(silu_done, 1)

            @block.vector
            def _(ve):
                if dropped_dram is not None:
                    ve.wait_ge(loaded, 16)
                for s in range(NS):
                    part = slice(s * SL, (s + 1) * SL)
                    if dropped_dram is not None:
                        ve.tensor_tensor(drop[:, part], drop[:, part], xn[:, part], ALU.mult).then_inc(masked, 1)
                        ve.wait_ge(masked, s + 1)
                        ve.tensor_tensor(result[:, part], result[:, part], drop[:, part], ALU.add).then_inc(complete, 1)
                    elif plus is not None:
                        ve.tensor_tensor(result[:, part], result[:, part], plus[:, part], ALU.add).then_inc(complete, 1)
                for s in range(NS):
                    part = slice(s * SL, (s + 1) * SL)
                    ve.wait_ge(silu_done, s + 1)
                    ve.tensor_tensor(s_out[:, part], s_out[:, part], result[:, part], ALU.mult).then_inc(multiplied, 1)
                    ve.wait_ge(multiplied, s + 1)
                    ve.tensor_tensor(x[:, part], x[:, part], s_out[:, part], ALU.add).then_inc(updated, 1)


def add_to(nc, tag, a, b, out):
    with nc.cleanup_on_exit():
        added = nc.alloc_semaphore(f"{tag}_added")
        with nc.Block() as block:

            @block.vector
            def _(ve):
                for s in range(NS):
                    part = slice(s * SL, (s + 1) * SL)
                    ve.tensor_tensor(out[:, part], a[:, part], b[:, part], ALU.add).then_inc(added, 1)


def linear_attention(nc, tag, kit, xin, w_dram, cols_dram, v_all, out_all):
    chunks = N // P
    with nc.cleanup_on_exit(), ExitStack() as ctx:
        sb = lambda name, shape, dt=F32: ctx.enter_context(nc.sbuf_tensor(f"{tag}_{name}", shape, dt))
        w = sb("w", [P, 2, P])
        cols = sb("cols", [P, 2])
        qk = [sb(f"qk{i}", [P, T]) for i in range(2)]
        low = sb("low", [P, T])
        qm = sb("qm", [P, 4, P])
        a_sb = sb("a", [P, 4, 4, P])
        ktok = sb("ktok", [P, P])
        num = sb("num", [P, SL])
        rec = sb("rec", [P, SL])
        state = sb("state", [P, 4, P])
        upd = sb("upd", [P, 4, P])
        ps_a = [ctx.enter_context(nc.psum_tensor(f"{tag}_a{g}", [P, 4, P], F32)) for g in range(4)]
        ps_o = ctx.enter_context(nc.psum_tensor(f"{tag}_o", [P, 4, P], F32))
        ps_d = ctx.enter_context(nc.psum_tensor(f"{tag}_d", [P, SL], F32))
        ps_u = ctx.enter_context(nc.psum_tensor(f"{tag}_u", [P, 4, P], F32))
        ps_k = ctx.enter_context(nc.psum_tensor(f"{tag}_k", [P, P], F32))
        sem = lambda name: nc.alloc_semaphore(f"{tag}_{name}")
        loaded, product_ready, biased, clipped, exp_done, feature = (sem(n) for n in (
            "loaded", "product_ready", "biased", "clipped", "exp_done", "feature"))
        split_ready, a_ready, masked, turned, ktok_in, num_ready, num_in, den_ready, u_ready, chain, state_ready = (
            sem(n) for n in ("split_ready", "a_ready", "masked", "turned", "ktok_in", "num_ready", "num_in",
                             "den_ready", "u_ready", "chain", "state_ready"))
        clipped_high, updated, inverted = sem("clipped_high"), sem("updated"), sem("inverted")
        with nc.Block() as block:

            @block.sync
            def _(sp):
                sp.dma_start(w[:, :, :], w_dram).then_inc(loaded, 16)
                sp.dma_start(cols[:, :], cols_dram).then_inc(loaded, 16)
                sp.wait_ge(loaded, 32)

            @block.tensor
            def _(pe):
                pe.wait_ge(loaded, 32)
                for k in range(2):
                    for s in range(NS):
                        if k:
                            pe.wait_ge(biased, s + 1)
                        pe.matmul(ps_a[s][:, :, :], w[:, k, :], xin[:, s * SL:(s + 1) * SL], start=True, stop=True).then_inc(product_ready, 1)
                pe.wait_ge(feature, 2)
                for t in range(2 * chunks):
                    b, kt = t // chunks, t % chunks
                    tok = slice(t * P, (t + 1) * P)
                    pe.wait_ge(split_ready, t + 1)
                    if t:
                        pe.wait_ge(masked, t)
                    for g in range(4):
                        r = slice(32 * g, 32 * g + 32)
                        mm = pe.matmul(ps_a[g][:, :, :], qk[1][r, tok], qm[r, :, :], start=True, stop=True, tile_position=(32 * g, 0))
                    mm.then_inc(a_ready, 1)
                    if t:
                        pe.wait_ge(ktok_in, t)
                    pe.transpose(ps_k[:, :], qk[1][:, tok], kit.ident[:, :]).then_inc(turned, 1)
                    if t:
                        pe.wait_ge(num_in, t)
                    pe.wait_ge(state_ready, t + 1)
                    pe.wait_ge(masked, t + 1)
                    for g in range(4):
                        pe.matmul(ps_o[:, g, :], state[:, g, :], qk[0][:, tok], start=True, stop=False, skip_group_check=True)
                        for j in range(4):
                            mm = pe.matmul(ps_o[32 * j:32 * j + 32, g, :], v_all[:, b * 4 + g, kt, j, :], a_sb[:, g, j, :],
                                           start=False, stop=True, skip_group_check=True)
                    mm.then_inc(num_ready, 1)
                    pe.wait_ge(ktok_in, t + 1)
                    if t:
                        pe.wait_ge(updated, t)
                    pe.matmul(ps_u[:, :, :], ktok[:, :], v_all[:, b * 4:b * 4 + 4, kt, :, :].rearrange("p g h c -> p g (h c)"),
                              start=True, stop=True).then_inc(u_ready, 1)
                    pe.wait_ge(num_in, t + 1)
                    if t:
                        pe.wait_ge(inverted, 2 * t)
                    pe.matmul(ps_d[:, :], kit.den_sel[:, :], num[:, :], start=True, stop=True).then_inc(den_ready, 1)

            @block.scalar
            def _(ac):
                ac.wait_ge(loaded, 32)
                for k in range(2):
                    for s in range(NS):
                        ac.wait_ge(product_ready, k * NS + s + 1)
                        ac.activation(qk[k][:, s * SL:(s + 1) * SL], ps_a[s][:, :, :].rearrange("p a n -> p (a n)"), ACT.Identity,
                                      bias=cols[:, k:k + 1]).then_inc(biased, 1)
                for k in range(2):
                    ac.wait_ge(clipped, k + 1)
                    ac.activation(low[:, :], low[:, :], ACT.Exp).then_inc(exp_done, 1)
                for t in range(2 * chunks):
                    ac.wait_ge(turned, t + 1)
                    if t:
                        ac.wait_ge(u_ready, t)
                    ac.activation(ktok[:, :], ps_k[:, :], ACT.Copy).then_inc(ktok_in, 1)
                    ac.wait_ge(num_ready, t + 1)
                    if t:
                        ac.wait_ge(chain, t)
                    ac.activation(num[:, :], ps_o[:, :, :].rearrange("p g n -> p (g n)"), ACT.Copy).then_inc(num_in, 1)

            @block.vector
            def _(ve):
                for k in range(2):
                    ve.wait_ge(biased, NS * (k + 1))
                    if k:
                        ve.wait_ge(feature, 1)
                    ve.tensor_scalar(low[:, :], qk[k][:, :], 0.0, E8 ** -0.5 if k == 0 else 1.0, ALU.min, ALU.mult).then_inc(clipped, 1)
                    ve.wait_ge(clipped, k + 1)
                    ve.tensor_scalar(qk[k][:, :], qk[k][:, :], 0.0, E8 ** -0.5 if k == 0 else 1.0, ALU.max, ALU.mult).then_inc(clipped_high, 1)
                    ve.wait_ge(exp_done, k + 1)
                    ve.wait_ge(clipped_high, k + 1)
                    ve.scalar_tensor_tensor(qk[k][:, :], low[:, :], 1.0001 - 1.0, qk[k][:, :], ALU.add, ALU.add).then_inc(feature, 1)
                ve.wait_ge(feature, 2)
                for t in range(2 * chunks):
                    b, kt = t // chunks, t % chunks
                    tok = slice(t * P, (t + 1) * P)
                    if t:
                        ve.wait_ge(a_ready, t)
                    ve.tensor_tensor(qm[:, :, :], qk[0][:, tok].unsqueeze(1).broadcast_to([P, 4, P]),
                                     kit.head4[:, :].unsqueeze(2).broadcast_to([P, 4, P]), ALU.mult).then_inc(split_ready, 1)
                    if kt == 0:
                        if t:
                            ve.wait_ge(num_ready, t)
                            ve.wait_ge(state_ready, t)
                        ve.memset(state[:, :, :], 0.0).then_inc(state_ready, 1)
                    ve.wait_ge(a_ready, t + 1)
                    if t:
                        ve.wait_ge(num_ready, t)
                    for g in range(4):
                        mk = ve.tensor_tensor(a_sb[:, g, :, :], ps_a[g][:, :, :], kit.upto[:, :].unsqueeze(1).broadcast_to([P, 4, P]), ALU.mult)
                    mk.then_inc(masked, 1)
                    if kt < chunks - 1:
                        ve.wait_ge(u_ready, t + 1)
                        ve.tensor_tensor(upd[:, :, :], ps_u[:, :, :], kit.blocks[:, :, :], ALU.mult).then_inc(updated, 1)
                        ve.wait_ge(updated, t + 1)
                        ve.wait_ge(num_ready, t + 1)
                        ve.tensor_tensor(state[:, :, :], state[:, :, :], upd[:, :, :], ALU.add).then_inc(state_ready, 1)
                    else:
                        ve.wait_ge(u_ready, t + 1)
                        ve.sem_inc(updated, 1)
                    ve.wait_ge(den_ready, t + 1)
                    ve.tensor_scalar(rec[:, :], ps_d[:, :], 1e-6, None, ALU.add).then_inc(inverted, 1)
                    ve.wait_ge(inverted, 2 * t + 1)
                    ve.reciprocal(rec[:, :], rec[:, :]).then_inc(inverted, 1)
                    ve.wait_ge(inverted, 2 * t + 2)
                    ve.tensor_tensor(out_all[:, b * 4:b * 4 + 4, kt * P:(kt + 1) * P], num[:, :].rearrange("p (g n) -> p g n", g=4),
                                     rec[:, :].rearrange("p (g n) -> p g n", g=4), ALU.mult).then_inc(chain, 1)


def mixture(nc, tag, xn, gates, w1_dram, w2_dram, b2_dram, gate_dram, result, experts, chunks, act,
            act_scale=1.0, group=2, gated_unit=False):
    step_count = group * NS * chunks
    ring = 2 if gated_unit else 4
    lag = 1 if gated_unit else 2
    kinds = 2 if gated_unit else 1
    turns = experts // group
    F = chunks * P
    with nc.cleanup_on_exit(), ExitStack() as ctx:
        sb = lambda name, shape, dt=F32: ctx.enter_context(nc.sbuf_tensor(f"{tag}_{name}", shape, dt))
        w1 = [sb(f"w1_{u}", [P, kinds * F + (0 if gated_unit else chunks)]) for u in range(group)]
        w2 = [sb(f"w2_{u}", [P, F]) for u in range(group)]
        gate = [sb(f"gate_{u}", [P, T]) for u in range(group)]
        b2 = sb("b2", [experts, P])
        hidden = sb("hidden", [P, ring, SL])
        ps_h = [ctx.enter_context(nc.psum_tensor(f"{tag}_psh{r}", [P, SL], F32)) for r in range(4)]
        ps_o = [ctx.enter_context(nc.psum_tensor(f"{tag}_pso{s}", [P, SL], F32)) for s in range(NS)]
        sem = lambda name: nc.alloc_semaphore(f"{tag}_{name}")
        expert_in = [sem(f"expert_in{u}") for u in range(group)]
        b2_in = sem("b2_in")
        scaled = sem("scaled")
        h_ready = sem("h_ready")
        act_done = sem("act_done")
        lifted = sem("lifted")
        gated = sem("gated")
        added = sem("added")
        evacuated = sem("evacuated")
        passed = sem("passed")
        steps = [(u, s, c) for u in range(group) for s in range(NS) for c in range(chunks)]
        per = NS * chunks
        with nc.Block() as block:

            def load(sp, u, e):
                sp.dma_start(w1[u][:, :], w1_dram[bass.ds(e, 1), :, :].rearrange("e p n -> (e p) n")).then_inc(expert_in[u], 16)
                sp.dma_start(w2[u][:, :], w2_dram[bass.ds(e, 1), :, :].rearrange("e p n -> (e p) n")).then_inc(expert_in[u], 16)
                sp.dma_start(gate[u][:, :], gate_dram[bass.ds(e, 1), :].broadcast_to([P, T])).then_inc(expert_in[u], 16)

            @block.sync
            def _(sp):
                sp.dma_start(b2[:, :], b2_dram).then_inc(b2_in, 16)
                for u in range(group):
                    load(sp, u, u)
                if turns > 1:
                    with sp.Fori(0, turns - 1) as it:
                        for u in range(group):
                            sp.wait_ge(added, it * step_count + ((u + 1) * per + 1))
                            load(sp, u, it * group + (u + group))
                sp.wait_ge(b2_in, 16)
                for u in range(group):
                    sp.wait_ge(expert_in[u], 48 * turns)

            @block.tensor
            def _(pe):
                pe.wait_ge(b2_in, 16)
                for s in range(NS):
                    mm = pe.matmul(ps_o[s][:, :], b2[:, :], gates[0:experts, s * SL:(s + 1) * SL], start=True, stop=False, skip_group_check=True)
                mm.then_inc(added, 1)
                with pe.Fori(0, turns) as it:
                    for k in range(step_count + lag):
                        if k < step_count:
                            u, s, c = steps[k]
                            if s == 0 and c == 0:
                                pe.wait_ge(expert_in[u], it * 48 + 48)
                            if k >= ring:
                                pe.wait_ge(lifted if gated_unit else act_done, it * step_count + (k - ring + 1))
                            elif gated_unit:
                                pe.wait_ge(added, it * step_count + 1)
                            for m in range(kinds):
                                mm = pe.matmul(ps_h[(k % ring) * kinds + m][:, :], w1[u][:, m * F + c * P:m * F + (c + 1) * P],
                                               xn[:, s * SL:(s + 1) * SL], start=True, stop=True)
                            mm.then_inc(h_ready, 1)
                        if k >= lag:
                            u, s, c = steps[k - lag]
                            pe.wait_ge(gated, it * step_count + (k - lag + 1))
                            pe.matmul(ps_o[s][:, :], w2[u][:, c * P:(c + 1) * P], hidden[:, (k - lag) % ring, :],
                                      start=False, stop=False, skip_group_check=True).then_inc(added, 1)

            @block.scalar
            def _(ac):
                with ac.Fori(0, turns) as it:
                    for k, (u, s, c) in enumerate(steps):
                        ac.wait_ge(h_ready, it * step_count + (k + 1))
                        if act_scale != 1.0 and s == 0 and c == 0:
                            ac.wait_ge(scaled, it * (2 * group) + (2 * u + 1))
                        ac.wait_ge(added, it * step_count + (max(k - ring + 1, 0) + 1))
                        out, src = hidden[:, k % ring, :], ps_h[(k % ring) * kinds][:, :]
                        if gated_unit:
                            ac.activation(out, src, act).then_inc(act_done, 1)
                        else:
                            ac.activation(out, src, act, bias=w1[u][:, F + c:F + c + 1], scale=act_scale).then_inc(act_done, 1)

            if act_scale != 1.0:
                @block.gpsimd
                def _(po):
                    with po.Fori(0, turns) as it:
                        for u in range(group):
                            po.wait_ge(expert_in[u], it * 48 + 48)
                            po.sem_inc(passed, 1)
                            po.tensor_scalar(w1[u][:, F:F + chunks], w1[u][:, F:F + chunks], act_scale, None, ALU.mult).then_inc(scaled, 1)
                            po.tensor_scalar(gate[u][:, :], gate[u][:, :], 1.0 / act_scale, None, ALU.mult).then_inc(scaled, 1)

            @block.vector
            def _(ve):
                with ve.Fori(0, turns) as it:
                    for k, (u, s, c) in enumerate(steps):
                        ve.wait_ge(act_done, it * step_count + (k + 1))
                        if act_scale != 1.0 and s == 0 and c == 0:
                            ve.wait_ge(scaled, it * (2 * group) + (2 * u + 2))
                        part = hidden[:, k % ring, :]
                        if gated_unit:
                            ve.tensor_tensor(part, ps_h[(k % ring) * kinds + 1][:, :], part, ALU.mult).then_inc(lifted, 1)
                            ve.wait_ge(lifted, it * step_count + (k + 1))
                        ve.tensor_tensor(part, part, gate[u][:, s * SL:(s + 1) * SL], ALU.mult).then_inc(gated, 1)
                ve.wait_ge(added, turns * step_count + 1)
                for s in range(NS):
                    ve.tensor_copy(result[:, s * SL:(s + 1) * SL], ps_o[s][:, :]).then_inc(evacuated, 1)


GH = 4
E8 = 8
ROWS = 48
PARTS_Q = (0, 0, 1, 1, 0, 2)
PARTS_K = (0, 1, 0, 1, 2, 0)


def score_steps(mode):
    out = []
    for s in range(N // SL):
        if mode == "full":
            out += [(s, kt, 0, SL, None) for kt in range(8)]
        elif mode == "causal":
            for kt in range(4 * (s + 1)):
                off = max(0, kt * P - s * SL)
                out.append((s, kt, off, SL - off, (0, P) if kt >= 4 * s else None))
        else:
            for kt in range(max(0, 4 * s - 1), 4 * s + 4):
                if kt == 4 * s - 1:
                    out.append((s, kt, 0, P, (P, P)))
                elif kt == 4 * s + 3:
                    out.append((s, kt, kt * P - s * SL, P, (0, P)))
                else:
                    out.append((s, kt, kt * P - s * SL, 2 * P, (0, 2 * P)))
    return out


def max_uses(mode):
    out = []
    for h in range(GH):
        for qt in range(8):
            if mode == "full":
                out += [[(h, qt, c * SL, SL, None, c)] for c in range(2)]
            elif mode == "causal":
                keys = (qt + 1) * P
                for c in range((keys + SL - 1) // SL):
                    n = min(SL, keys - c * SL)
                    last = (c + 1) * SL >= keys
                    out.append([(h, qt, c * SL, n, (P, P) if last else None, c)])
    if mode == "window":
        for h in range(GH):
            for qt in range(0, 8, 2):
                out.append([(h, q, max(0, q - 1) * P, P if q == 0 else 2 * P, (P, P) if q == 0 else (0, 2 * P), 0)
                            for q in (qt, qt + 1)])
    return out


def attend(nc, tag, mode, scale, q_dram, k_dram, v_all, key_heads, out_all, kit, slots=4):
    groups = 8
    nparts = 1 if mode == "window" else 2
    hw = 4 if mode == "window" else 2
    width = 1024 // hw
    steps = score_steps(mode)
    uses = max_uses(mode)
    blocks = GH // hw
    nst = len(steps)
    nexp = nst * blocks
    small = len(uses) + 1 + 2
    start = len(uses) + 1
    slice_end = [max(k for k, st in enumerate(steps) if st[0] == s) for s in range(2)]
    spread = max(1, int(nst * 0.85))
    plan, given = [], 0
    for k in range(nst):
        upto = min(len(uses), (len(uses) * (k + 1) + spread - 1) // spread)
        row = [("max", i) for i in range(given, upto)]
        given = upto
        if k == spread:
            row.append(("turn", 0))
        if k == slice_end[0] + 2:
            row.append(("den", 0))
        plan.append(row)
    plan.append([("den", 1)])
    order = [x for row in plan for x in row]
    turn_at = order.index(("turn", 0))
    assert len(order) == small

    with nc.cleanup_on_exit(), ExitStack() as ctx:
        sb = lambda name, shape, dt=F32: ctx.enter_context(nc.sbuf_tensor(f"{tag}_{name}", shape, dt))
        sem = lambda name: nc.alloc_semaphore(f"{tag}_{name}")
        qst = [sb(f"qst{u}", [P, GH * N], BF16) for u in range(slots)]
        kst = [sb(f"kst{u}", [P, key_heads, N], BF16) for u in range(slots)]
        val = [sb(f"val{u}", [P, 8, key_heads, 32]) for u in range(slots)]
        prob = [sb(f"prob{r}", [P, GH, width]) for r in range(2)]
        mpart = sb("mpart", [P, GH * 8, nparts])
        mcol = sb("mcol", [P, GH * 8])
        mhl = sb("mhl", [GH * 8, 2, P], BF16)
        osb = sb("osb", [P, SL])
        rec = sb("rec", [P, SL])
        ps_st = [ctx.enter_context(nc.psum_tensor(f"{tag}_st{r}", [P, hw, width], F32)) for r in range(2)]
        ps_o = ctx.enter_context(nc.psum_tensor(f"{tag}_o", [P, SL], F32))
        ps_s = [ctx.enter_context(nc.psum_tensor(f"{tag}_s{r}", [P, SL], F32)) for r in range(3)]
        cleared = sem("cleared")
        staged = [sem(f"staged{u}") for u in range(slots)]
        shift_in = [sem(f"shift_in{u}") for u in range(slots)]
        small_ready = sem("small_ready")
        small_free = sem("small_free")
        hi_done = sem("hi_done")
        column_done = sem("column_done")
        scores_ready = sem("scores_ready")
        probs_ready = sem("probs_ready")
        probs_used = sem("probs_used")
        o_copied = sem("o_copied")
        osb_free = sem("osb_free")

        def small_of(it, u, n):
            return it * (slots * small) + (start + u * small + n)

        def small_bank(pe, it, u, n):
            pe.wait_ge(small_free, small_of(it, u, n - 2 if n >= 3 else 0))
            return n % 3

        def steps_of(it, u, k):
            return it * (slots * nst) + (u * nst + k)

        def exps_of(it, u, e):
            return it * (slots * nexp) + (u * nexp + e)

        def slices_of(it, u, s):
            return it * (slots * 2) + (u * 2 + s)

        with nc.Block() as block:

            def load(sp, u, b):
                sp.dma_start(qst[u][0:ROWS, :].rearrange("r (h n) -> r h n", h=GH),
                             q_dram[bass.ds(b, 1), :, GH * u:GH * u + GH, :].rearrange("b r h n -> (b r) h n")).then_inc(staged[u], 16)
                sp.dma_start(kst[u][0:ROWS, :, :],
                             k_dram[bass.ds(b, 1), :, key_heads * u:key_heads * (u + 1), :].rearrange("b r h n -> (b r) h n")).then_inc(staged[u], 16)
                sp.dma_start(val[u][:, :, :, :], v_all[:, bass.ds(b * 4 + u, 1), :, :, :].rearrange("p g t h c -> p (g t) h c")).then_inc(staged[u], 16)

            def shift(sp, u, count):
                sp.wait_ge(small_free, count)
                for part in range(2):
                    sp.dma_start(qst[u][ROWS + part:ROWS + part + 1, :], mhl[:, part, :]).then_inc(shift_in[u], 16)

            @block.sync
            def _(sp):
                sp.wait_ge(cleared, 3 * slots)
                for u in range(slots):
                    load(sp, u, 0)
                shift(sp, 0, start)
                with sp.Fori(0, groups // slots) as it:
                    for u in range(slots):
                        shift(sp, (u + 1) % slots, small_of(it, u, turn_at + 1))
                        sp.wait_ge(probs_used, steps_of(it, u, nst + 2))
                        load(sp, u, (it + 1) % 2)
                for u in range(slots):
                    sp.wait_ge(staged[u], 48 * (groups // slots + 1))
                    sp.wait_ge(shift_in[u], 32 * (groups // slots + (u == 0)))

            @block.gpsimd
            def _(po):
                for u in range(slots):
                    po.memset(qst[u][:, :], 0.0).then_inc(cleared, 1)
                    po.memset(kst[u][:, :, :], 0.0).then_inc(cleared, 1)
                po.wait_ge(cleared, 2 * slots)
                for u in range(slots):
                    po.memset(kst[u][32:64, :, :], 1.0).then_inc(cleared, 1)

            def max_matmuls(pe, u, use, bank):
                col = 0
                for h, qt, k0, nk, mask, part in use:
                    kh = h if key_heads == GH else 0
                    mm = pe.matmul(ps_s[bank][:, col:col + nk], qst[u][0:ROWS, h * N + qt * P:h * N + (qt + 1) * P],
                                   kst[u][0:ROWS, kh, k0:k0 + nk], start=True, stop=mask is None, skip_group_check=True)
                    if mask is not None:
                        mm = pe.matmul(ps_s[bank][:, col + nk - mask[1]:col + nk], kit.ident_bf[:, :],
                                       kit.mask_qk[:, mask[0]:mask[0] + mask[1]], start=False, stop=True,
                                       skip_group_check=True)
                    col += 2 * P
                return mm

            @block.tensor
            def _(pe):
                pe.sem_inc(probs_used, 2)
                pe.wait_ge(cleared, 3 * slots)
                pe.wait_ge(staged[0], 48)
                for n, use in enumerate(uses):
                    if n >= 3:
                        pe.wait_ge(small_free, n - 2)
                    max_matmuls(pe, 0, use, n % 3).then_inc(small_ready, 1)
                pe.wait_ge(column_done, 1)
                pe.transpose(ps_s[len(uses) % 3][0:GH * 8, 0:P], mcol[:, :], kit.ident[:, :]).then_inc(small_ready, 1)
                with pe.Fori(0, groups // slots) as it:
                    for u in range(slots):
                        nu = (u + 1) % slots
                        pe.wait_ge(staged[nu], it * 48 + (96 if nu == 0 else 48))
                        pe.wait_ge(shift_in[u], it * 32 + 32)
                        e = n = 0
                        for k in range(nst + 1):
                            if k < nst:
                                s, kt, off, w, mask = steps[k]
                                c0 = 0 if mode == "window" else off
                                for blk in range(blocks):
                                    if e == 0:
                                        pe.wait_ge(probs_ready, exps_of(it, u, 1))
                                    elif e >= 2:
                                        pe.wait_ge(probs_ready, exps_of(it, u, e))
                                    for jj in range(hw):
                                        j = blk * hw + jj
                                        kh = j if key_heads == GH else 0
                                        mm = pe.matmul(ps_st[e % 2][:, jj, c0:c0 + w], kst[u][:, kh, kt * P:(kt + 1) * P],
                                                       qst[u][:, j * N + s * SL + off:j * N + s * SL + off + w],
                                                       start=True, stop=mask is None, skip_group_check=True)
                                        if mask is not None:
                                            mm = pe.matmul(ps_st[e % 2][:, jj, c0:c0 + mask[1]], kit.ident_bf[:, :],
                                                           kit.mask_kq[:, mask[0]:mask[0] + mask[1]], start=False,
                                                           stop=True, skip_group_check=True)
                                    mm.then_inc(scores_ready, 1)
                                    e += 1
                            if k >= 1:
                                s, kt, off, w, mask = steps[k - 1]
                                c0 = 0 if mode == "window" else off
                                first = k == 1 or steps[k - 2][0] != s
                                if first:
                                    pe.wait_ge(o_copied, slices_of(it, u, s + 1))
                                pe.wait_ge(probs_ready, exps_of(it, u, k * blocks + 1))
                                for j in range(GH):
                                    kh = j if key_heads == GH else 0
                                    mm = pe.matmul(ps_o[32 * j:32 * j + 32, off:off + w], val[u][:, kt, kh, :],
                                                   prob[(k - 1) % 2][:, j, c0:c0 + w], start=first,
                                                   stop=k - 1 in slice_end, skip_group_check=True)
                                mm.then_inc(probs_used, 1)
                            for what, i in plan[k]:
                                if what == "max":
                                    bank = small_bank(pe, it, u, n)
                                    max_matmuls(pe, nu, uses[i], bank).then_inc(small_ready, 1)
                                elif what == "turn":
                                    bank = small_bank(pe, it, u, n)
                                    pe.wait_ge(column_done, it * slots + (u + 2))
                                    pe.transpose(ps_s[bank][0:GH * 8, 0:P], mcol[:, :], kit.ident[:, :]).then_inc(small_ready, 1)
                                else:
                                    bank = small_bank(pe, it, u, n)
                                    pe.wait_ge(o_copied, slices_of(it, u, i + 2))
                                    pe.matmul(ps_s[bank][:, :], kit.den_sel[:, :], osb[:, :], start=True, stop=True).then_inc(small_ready, 1)
                                n += 1

            @block.scalar
            def _(ac):
                ac.sem_inc(probs_ready, 1)
                ac.sem_inc(o_copied, 1)

                def copy_out(it, u, s):
                    ac.wait_ge(probs_used, steps_of(it, u, slice_end[s] + 3))
                    ac.wait_ge(osb_free, slices_of(it, u, s + 1))
                    ac.activation(osb[:, :], ps_o[:, :], ACT.Copy).then_inc(o_copied, 1)

                with ac.Fori(0, groups // slots) as it:
                    for u in range(slots):
                        e = 0
                        for k, (s, kt, off, w, mask) in enumerate(steps):
                            c0 = 0 if mode == "window" else off
                            for blk in range(blocks):
                                ac.wait_ge(scores_ready, exps_of(it, u, e + 1))
                                if blk == 0 and k == 0:
                                    ac.wait_ge(probs_used, steps_of(it, u, 2))
                                elif blk == 0 and k >= 2:
                                    ac.wait_ge(probs_used, steps_of(it, u, k + 1))
                                ac.activation(prob[k % 2][:, blk * hw:(blk + 1) * hw, c0:c0 + w],
                                              ps_st[e % 2][:, :, c0:c0 + w], ACT.Exp, scale=scale).then_inc(probs_ready, 1)
                                e += 1
                            if k == slice_end[0] + 1:
                                copy_out(it, u, 0)
                        copy_out(it, u, 1)

            def reduce_use(ve, use, bank):
                h, qt, k0, nk, mask, part = use[0]
                i = h * 8 + qt
                if len(use) == 1:
                    return ve.tensor_reduce(mpart[:, i, part:part + 1], ps_s[bank][:, 0:nk], AX.X, ALU.max)
                if qt == 0:
                    ve.tensor_reduce(mpart[:, i, 0:1], ps_s[bank][:, 0:P], AX.X, ALU.max)
                    return ve.tensor_reduce(mpart[:, i + 1, 0:1], ps_s[bank][:, 2 * P:4 * P], AX.X, ALU.max)
                return ve.tensor_reduce(mpart[:, i:i + 2, 0], ps_s[bank][:, :].rearrange("p (a k) -> p a k", a=2), AX.X, ALU.max)

            def split_max(ve, bank, hi_count):
                ve.tensor_scalar(mhl[:, 0, :], ps_s[bank][0:GH * 8, 0:P], -1.0, None, ALU.mult).then_inc(hi_done, 1)
                ve.wait_ge(hi_done, hi_count)
                ve.scalar_tensor_tensor(mhl[:, 1, :], ps_s[bank][0:GH * 8, 0:P], -1.0, mhl[:, 0, :], ALU.mult,
                                        ALU.subtract).then_inc(small_free, 1)

            @block.vector
            def _(ve):
                ve.sem_inc(osb_free, 1)
                ve.memset(mpart[:, :, :], -3.0e38).then_inc(hi_done, 1)
                ve.wait_ge(hi_done, 1)
                for n, use in enumerate(uses):
                    ve.wait_ge(small_ready, n + 1)
                    reduce_use(ve, use, n % 3).then_inc(small_free, 1)
                ve.wait_ge(small_free, len(uses))
                ve.tensor_reduce(mcol[:, :], mpart[:, :, :], AX.X, ALU.max).then_inc(column_done, 1)
                ve.wait_ge(small_ready, start)
                split_max(ve, len(uses) % 3, 2)
                with ve.Fori(0, groups // slots) as it:
                    for u in range(slots):
                        for n, (what, i) in enumerate(order):
                            bank = n % 3
                            ve.wait_ge(small_ready, small_of(it, u, n + 1))
                            if what == "max":
                                reduce_use(ve, uses[i], bank).then_inc(small_free, 1)
                                if i == len(uses) - 1:
                                    ve.wait_ge(small_free, small_of(it, u, n + 1))
                                    ve.tensor_reduce(mcol[:, :], mpart[:, :, :], AX.X, ALU.max).then_inc(column_done, 1)
                            elif what == "turn":
                                ve.wait_ge(shift_in[u], it * 32 + 32)
                                split_max(ve, bank, it * slots + (u + 3))
                            else:
                                ve.reciprocal(rec[:, :], ps_s[bank][:, :]).then_inc(small_free, 1)
                                ve.wait_ge(small_free, small_of(it, u, n + 1))
                                ve.tensor_tensor(out_all[:, bass.ds(it * slots + u, 1), i * SL:(i + 1) * SL].rearrange("p g n -> p (g n)"),
                                                 osb[:, :], rec[:, :], ALU.mult).then_inc(osb_free, 1)


CH = 64
NC = N // CH
HP = 8
F = 64


def fast_weights(nc, tag, xn, wqk, wv, wo, win0, wout0, woutT0, decay_in, decay_out, rate_in, rate_out, y, ident):
    with nc.cleanup_on_exit(), ExitStack() as ctx:
        sb = lambda name, shape, dt=F32: ctx.enter_context(nc.sbuf_tensor(f"{tag}_{name}", shape, dt))
        sem = lambda name: nc.alloc_semaphore(f"{tag}_{name}")
        win, wout, woutT = (win0, wout0, woutT0)
        qk = [sb(f"qk{i}", [P, HP, 2, 2, CH]) for i in range(2)]
        vT = [sb(f"vT{i}", [P, HP, 2, CH]) for i in range(2)]
        ktok = [sb(f"ktok{i}", [P, HP, 2, F]) for i in range(2)]
        vtok = [sb(f"vtok{i}", [P, HP, 2, F]) for i in range(2)]
        prob = [sb(f"prob{g}", [P, 4, 2, 2, CH]) for g in range(2)]
        mx = [sb(f"mx{g}", [P, 16]) for g in range(2)]
        sm = [sb(f"sm{g}", [P, 16]) for g in range(2)]
        ptok = [sb(f"ptok{g}", [P, 4, 2, F]) for g in range(2)]
        pa = [sb(f"pa{g}", [P, 4, 2, F]) for g in range(2)]
        ssum = [sb(f"ssum{g}", [P, 2, 4]) for g in range(2)]
        oT = [sb(f"oT{g}", [P, 4, 2, CH]) for g in range(2)]
        ps_z = [ctx.enter_context(nc.psum_tensor(f"{tag}_z{g}", [P, 2, 512], F32)) for g in range(2)]
        ps_g = ctx.enter_context(nc.psum_tensor(f"{tag}_g", [P, 2, 512], F32))
        ps_m = [ctx.enter_context(nc.psum_tensor(f"{tag}_m{g}", [P, 512], F32)) for g in range(2)]
        z_ready, a_ready, go_ready, gi_ready = sem("z_ready"), sem("a_ready"), sem("go_ready"), sem("gi_ready")
        misc_ready = sem("misc_ready")
        act_free = sem("act_free")
        ve_free = sem("ve_free")
        shifted = sem("shifted")
        exp_done = sem("exp_done")
        normed = sem("normed")
        gz_done = sem("gz_done")
        win_new, wout_new = sem("win_new"), sem("wout_new")
        win_decayed, wout_decayed = sem("win_decayed"), sem("wout_decayed")
        ve_chain = sem("ve_chain")
        passed = sem("passed")

        next_qkv = [("qk", i, "act") for i in range(4)] + [("v", i, "act") for i in range(2)]
        next_tok = [("kt", i, "ve") for i in range(2)] + [("vt", i, "ve") for i in range(2)]
        chunk = (next_qkv + [("pt", 0, "act"), ("ot", 0, "act"), ("pt", 1, "act"), ("ot", 1, "act")]
                 + next_tok + [("y", 0, "act")])
        lead = next_qkv + next_tok
        nm = len(chunk)
        na = sum(w == "act" for *_, w in chunk)
        nv = nm - na
        la, lv = 6, 4

        def reads_before(n, who):
            return sum(w == who for *_, w in (chunk + chunk)[:n])

        def misc_wait(pe, it, n):
            if n < 2:
                pe.wait_ge(act_free, it * 2 * na + la)
                pe.wait_ge(ve_free, it * 2 * nv + lv)
            else:
                who = (chunk + chunk)[n - 2][2]
                if who == "act":
                    pe.wait_ge(act_free, it * 2 * na + (la + reads_before(n - 1, "act")))
                else:
                    pe.wait_ge(ve_free, it * 2 * nv + (lv + reads_before(n - 1, "ve")))
            return ps_m[n % 2]

        def misc_at(it, n):
            return it * 2 * nm + (len(lead) + n + 1)

        with nc.Block() as block:

            def tokens(c):
                return xn.rearrange("p (b n) -> p b n", b=2)[:, :, bass.ds(c * CH, CH)]

            def project_qk(pe, bank, i, c):
                for j in range(2):
                    for w in range(2):
                        mm = pe.matmul(bank[:, j * 256 + w * 128:j * 256 + w * 128 + 128].rearrange("p (b n) -> p b n", b=2),
                                       wqk[:, w, 2 * i + j, :], tokens(c), start=True, stop=True)
                return mm

            def project_v(pe, bank, i, c):
                for j in range(4):
                    mm = pe.matmul(bank[:, j * 128:(j + 1) * 128].rearrange("p (b n) -> p b n", b=2),
                                   wv[:, 4 * i + j, :], tokens(c), start=True, stop=True)
                return mm

            def turn(pe, bank, sources):
                for j, src in enumerate(sources):
                    mm = pe.transpose(bank[:, j * 128:(j + 1) * 128], src, ident[:, :])
                return mm

            def make(pe, what, i, bank, nxt, cn, cur, it):
                if what == "qk":
                    return project_qk(pe, bank, i, cn)
                if what == "v":
                    return project_v(pe, bank, i, cn)
                if what == "kt":
                    return turn(pe, bank, [qk[nxt][:, 4 * i + j, 1, :, :].rearrange("p b n -> p (b n)") for j in range(4)])
                if what == "vt":
                    return turn(pe, bank, [vT[nxt][:, 4 * i + j, :, :].rearrange("p b n -> p (b n)") for j in range(4)])
                if what == "pt":
                    return turn(pe, bank, [prob[i][:, j, 1, :, :].rearrange("p b n -> p (b n)") for j in range(4)])
                if what == "ot":
                    for j in range(4):
                        for b in range(2):
                            for h in range(2):
                                r = slice(64 * h, 64 * h + 64)
                                mm = pe.matmul(bank[r, (j * 2 + b) * 64:(j * 2 + b + 1) * 64], wout[r, 4 * i + j, b, :],
                                               prob[i][r, j, 0, b, :], start=True, stop=True, skip_group_check=True)
                    return mm
                if what == "y":
                    for j in range(HP):
                        mm = pe.matmul(bank[:, 0:128], wo[:, j, :], oT[j // 4][:, j % 4, :, :].rearrange("p b n -> p (b n)"),
                                       start=j == 0, stop=j == HP - 1)
                    return mm

            @block.tensor
            def _(pe):
                for n, (what, i, who) in enumerate(lead):
                    if n >= 2:
                        w2 = lead[n - 2][2]
                        pe.wait_ge(act_free if w2 == "act" else ve_free, sum(x[2] == w2 for x in lead[:n - 1]))
                    if n == 6:
                        pe.wait_ge(act_free, 6)
                    make(pe, what, i, ps_m[n % 2], 0, 0, 0, None).then_inc(misc_ready, 1)
                with pe.Fori(0, NC // 2) as it:
                    n = 0
                    for cc in range(2):
                        cur, nxt = cc, 1 - cc
                        cn = (it * 2 + (cc + 1)) % NC
                        act0 = la + cc * na
                        ve0 = lv + cc * nv
                        for g in range(2):
                            pe.wait_ge(win_new, it * 4 + (2 * cc + g + 1))
                            if g == 0:
                                pe.wait_ge(act_free, it * 2 * na + act0)
                            pe.sem_inc(passed, 1)
                            for j in range(4):
                                for b in range(2):
                                    for h in range(2):
                                        r = slice(64 * h, 64 * h + 64)
                                        mm = pe.matmul(ps_z[g][r, j // 2, (j % 2) * 256:(j % 2) * 256 + 256].rearrange("p (w b n) -> p w b n", w=2, b=2)[:, :, b, :],
                                                       win[r, 4 * g + j, b, :], qk[cur][r, 4 * g + j, :, b, :],
                                                       start=True, stop=True, skip_group_check=True)
                            mm.then_inc(z_ready, 1)

                        def misc(what, i):
                            nonlocal n
                            bank = misc_wait(pe, it, n)
                            if what == "ot":
                                pe.sem_inc(passed, 1)
                            make(pe, what, i, bank, nxt, cn, cur, it).then_inc(misc_ready, 1)
                            n += 1

                        for i in range(4):
                            misc("qk", i)
                        for i in range(2):
                            misc("v", i)
                        for g in range(2):
                            pe.wait_ge(normed, it * 4 + (2 * cc + g + 1))
                            if g == 0:
                                pe.wait_ge(wout_new, it * 4 + (2 * cc + 2))
                            misc("pt", g)
                            misc("ot", g)
                            for j in range(4):
                                for b in range(2):
                                    for h in range(2):
                                        r = slice(64 * h, 64 * h + 64)
                                        mm = pe.matmul(ps_z[g][64 * b:64 * b + 64, h, j * 64:(j + 1) * 64], vT[cur][r, 4 * g + j, b, :],
                                                       woutT[r, 4 * g + j, b, :], start=True, stop=True, skip_group_check=True)
                            mm.then_inc(a_ready, 1)

                        def grad_out(g):
                            pe.wait_ge(act_free, it * 2 * na + (act0 + 6 + 2 * g + 1))
                            if g == 0:
                                pe.wait_ge(ve_free, it * 2 * nv + ve0)
                            pe.wait_ge(wout_new, it * 4 + (2 * cc + g + 2))
                            pe.sem_inc(passed, 1)
                            for j in range(4):
                                for h in range(2):
                                    for b in range(2):
                                        r = slice(64 * b, 64 * b + 64)
                                        pe.matmul(ps_g[64 * h:64 * h + 64, b, j * 64:(j + 1) * 64], ptok[g][r, j, h, :],
                                                  vtok[cur][r, 4 * g + j, h, :], start=True, stop=True, skip_group_check=True)
                                        mm = pe.matmul(ps_g[64 * h:64 * h + 64, b, 256 + j * 64:256 + (j + 1) * 64],
                                                       vtok[cur][r, 4 * g + j, h, :], ptok[g][r, j, h, :],
                                                       start=True, stop=True, skip_group_check=True)
                            mm.then_inc(go_ready, 1)

                        def grad_in(g):
                            pe.wait_ge(gz_done, it * 4 + (2 * cc + g + 1))
                            pe.sem_inc(passed, 1)
                            for j in range(4):
                                for h in range(2):
                                    for b in range(2):
                                        r = slice(64 * b, 64 * b + 64)
                                        mm = pe.matmul(ps_z[g][64 * h:64 * h + 64, b, j * 64:(j + 1) * 64], ktok[cur][r, 4 * g + j, h, :],
                                                       pa[g][r, j, h, :], start=True, stop=True, skip_group_check=True)
                            mm.then_inc(gi_ready, 1)

                        grad_out(0)
                        pe.wait_ge(act_free, it * 2 * na + (act0 + 6))
                        for i in range(2):
                            misc("kt", i)
                        for i in range(2):
                            misc("vt", i)
                        grad_in(0)
                        grad_out(1)
                        pe.wait_ge(act_free, it * 2 * na + (act0 + 10))
                        misc("y", 0)
                        grad_in(1)

            def read_act(ac, what, i, bank, nxt, c, cur):
                if what == "qk":
                    return ac.activation(qk[nxt][:, 2 * i:2 * i + 2, :, :, :].rearrange("p a b w n -> p (a b w n)"), bank[:, :], ACT.Silu)
                if what == "v":
                    return ac.activation(vT[nxt][:, 4 * i:4 * i + 4, :, :].rearrange("p a b n -> p (a b n)"), bank[:, :], ACT.Copy)
                if what == "pt":
                    return ac.activation(ptok[i][:, :, :, :].rearrange("p a h n -> p (a h n)"), bank[:, :], ACT.Copy)
                if what == "ot":
                    return ac.activation(oT[i][:, :, :, :].rearrange("p a h n -> p (a h n)"), bank[:, :], ACT.Copy)
                if what == "y":
                    return ac.activation(y.rearrange("p (b n) -> p b n", b=2)[:, :, bass.ds(c * CH, CH)],
                                         bank[:, 0:128].rearrange("p (b n) -> p b n", b=2), ACT.Copy)

            @block.scalar
            def _(ac):
                for n, (what, i, who) in enumerate(lead):
                    if who == "act":
                        ac.wait_ge(misc_ready, n + 1)
                        read_act(ac, what, i, ps_m[n % 2], 0, 0, 0).then_inc(act_free, 1)
                with ac.Fori(0, NC // 2) as it:
                    for cc in range(2):
                        cur, nxt = cc, 1 - cc
                        for k, (what, i, who) in enumerate(chunk):
                            n = cc * nm + k
                            if k == 0:
                                if cc:
                                    ac.wait_ge(gi_ready, it * 4 + 2 * cc)
                            if k == 6:
                                for g in range(2):
                                    ac.wait_ge(shifted, it * 4 + (2 * cc + g + 1))
                                    ac.activation(prob[g][:, :, :, :, :].rearrange("p a b w n -> p (a b w n)"),
                                                  prob[g][:, :, :, :, :].rearrange("p a b w n -> p (a b w n)"), ACT.Exp).then_inc(exp_done, 1)
                            if who == "act":
                                ac.wait_ge(misc_ready, misc_at(it, n))
                                read_act(ac, what, i, ps_m[n % 2], nxt, it * 2 + cc, cur).then_inc(act_free, 1)

            def segments(t):
                return t[:, :, :, :, :].rearrange("p a b w n -> p (a b w) n")

            def read_ve(ve, what, i, bank, nxt, cn):
                dst = (ktok if what == "kt" else vtok)[nxt][:, 4 * i:4 * i + 4, :, :].rearrange("p a h d -> p (a h) d")
                rate = (rate_in if what == "kt" else rate_out)[:, bass.ds(cn, 1), 8 * i:8 * i + 8].rearrange("p c h -> p (c h)")
                return ve.tensor_tensor(dst, bank[:, :].rearrange("p (a d) -> p a d", d=F),
                                        rate.unsqueeze(2).broadcast_to([P, 8, F]), ALU.mult)

            @block.vector
            def _(ve):
                ve.sem_inc(win_new, 2)
                ve.sem_inc(wout_new, 2)
                for n, (what, i, who) in enumerate(lead):
                    if who == "ve":
                        ve.wait_ge(misc_ready, n + 1)
                        read_ve(ve, what, i, ps_m[n % 2], 0, 0).then_inc(ve_free, 1)
                links = 12
                with ve.Fori(0, NC // 2) as it:
                    done = [0]

                    def link(ins):
                        done[0] += 1
                        ins.then_inc(ve_chain, 1)
                        ve.wait_ge(ve_chain, it * 2 * links + done[0])

                    for cc in range(2):
                        cur, nxt = cc, 1 - cc
                        cn = (it * 2 + (cc + 1)) % NC
                        for g in range(2):
                            ve.wait_ge(z_ready, it * 4 + (2 * cc + g + 1))
                            z = ps_z[g][:, :, :].rearrange("p k (s n) -> p (k s) n", n=CH)
                            link(ve.tensor_reduce(mx[g][:, :], z, AX.X, ALU.max))
                            ve.tensor_tensor(segments(prob[g]), z, mx[g][:, :].unsqueeze(2).broadcast_to([P, 16, CH]),
                                             ALU.subtract).then_inc(shifted, 1)
                        for g in range(2):
                            ve.wait_ge(exp_done, it * 4 + (2 * cc + g + 1))
                            link(ve.tensor_reduce(sm[g][:, :], segments(prob[g]), AX.X, ALU.add))
                            link(ve.reciprocal(mx[g][:, :], sm[g][:, :]))
                            ve.tensor_tensor(segments(prob[g]), segments(prob[g]), mx[g][:, :].unsqueeze(2).broadcast_to([P, 16, CH]),
                                             ALU.mult).then_inc(normed, 1)
                        for g in range(2):
                            ve.wait_ge(a_ready, it * 4 + (2 * cc + g + 1))
                            ve.wait_ge(act_free, it * 2 * na + (la + cc * na + 6 + 2 * g + 1))
                            a = ps_z[g][:, :, 0:256].rearrange("p h (a d) -> p h a d", d=F)
                            pt = ptok[g][:, :, :, :].rearrange("p a h d -> p h a d")
                            out = pa[g][:, :, :, :].rearrange("p a h d -> p h a d")
                            link(ve.tensor_tensor(out, a, pt, ALU.mult))
                            link(ve.tensor_reduce(ssum[g][:, :, :], out, AX.X, ALU.add))
                            link(ve.tensor_tensor(out, a, ssum[g][:, :, :].unsqueeze(3).broadcast_to([P, 2, 4, F]), ALU.subtract))
                            ve.tensor_tensor(pa[g][:, :, :, :], pa[g][:, :, :, :], ptok[g][:, :, :, :], ALU.mult).then_inc(gz_done, 1)

                        def update_out(g):
                            ve.wait_ge(go_ready, it * 4 + (2 * cc + g + 1))
                            ve.wait_ge(wout_decayed, it * 8 + (4 * cc + 2 * g + 2))
                            for m, w in enumerate((wout, woutT)):
                                wv_ = w[:, 4 * g:4 * g + 4, :, :].rearrange("p a b d -> p b a d")
                                ins = ve.tensor_tensor(wv_, ps_g[:, :, 256 * m:256 * m + 256].rearrange("p b (a d) -> p b a d", d=F), wv_, ALU.add)
                            ins.then_inc(wout_new, 1)

                        def update_in(g):
                            ve.wait_ge(gi_ready, it * 4 + (2 * cc + g + 1))
                            ve.wait_ge(win_decayed, it * 4 + (2 * cc + g + 1))
                            wv_ = win[:, 4 * g:4 * g + 4, :, :].rearrange("p a b d -> p b a d")
                            ve.tensor_tensor(wv_, ps_z[g][:, :, 0:256].rearrange("p b (a d) -> p b a d", d=F), wv_, ALU.add).then_inc(win_new, 1)

                        update_out(0)
                        for k, (what, i, who) in enumerate(chunk):
                            if who == "ve":
                                ve.wait_ge(misc_ready, misc_at(it, cc * nm + k))
                                read_ve(ve, what, i, ps_m[(cc * nm + k) % 2], nxt, cn).then_inc(ve_free, 1)
                        update_in(0)
                        update_out(1)
                        update_in(1)
                    assert done[0] == 2 * links, done

            @block.gpsimd
            def _(po):
                def decay(w, g, d, c):
                    v = w[:, 4 * g:4 * g + 4, :, :].rearrange("p a b d -> p (a b) d")
                    k = d[:, bass.ds(c, 1), 4 * g:4 * g + 4, :].rearrange("p c a b -> p (c a b)")
                    return po.tensor_tensor(v, v, k.unsqueeze(2).broadcast_to([P, 8, F]), ALU.mult)

                with po.Fori(0, NC // 2) as it:
                    for cc in range(2):
                        c = it * 2 + cc
                        for g in range(2):
                            po.wait_ge(z_ready, it * 4 + (2 * cc + g + 1))
                            decay(win, g, decay_in, c).then_inc(win_decayed, 1)
                        for g in range(2):
                            po.wait_ge(a_ready, it * 4 + (2 * cc + g + 1))
                            decay(wout, g, decay_out, c).then_inc(wout_decayed, 1)
                            decay(woutT, g, decay_out, c).then_inc(wout_decayed, 1)


SHIFTS = [0] + [2 << j for j in range(9)] + [1] + [3 << j for j in range(9)]
PAIRED = 9
ZERO_TAPS = 11
FAR_TAPS = 5
PAD = 768


def dilated_attention(nc, tag, kit, xin, w_dram, cols_dram, taps_dram, y):
    n_in = len(SHIFTS)
    n_slots = n_in + 1
    H = 16
    taps = ZERO_TAPS + 2 * PAIRED + 1 + 9 + FAR_TAPS
    with nc.cleanup_on_exit(), ExitStack() as ctx:
        sb = lambda name, shape, dt=F32: ctx.enter_context(nc.sbuf_tensor(f"{tag}_{name}", shape, dt))
        w = sb("w", [P, 5, P])
        cols = sb("cols", [P, 5])
        q = sb("q", [P, T])
        kpad = sb("kpad", [P, 2, PAD + N])
        vpad = sb("vpad", [P, 2, PAD + N])
        pb = sb("pb", [P, taps, H])
        pbm = sb("pbm", [P, n_slots, H])
        bias = sb("bias", [P, n_slots, H])
        prod = [sb(f"prod{i}", [P, SL]) for i in range(3)]
        att = sb("att", [P, 4, n_slots, H])
        stat = sb("stat", [P, 4, H])
        attT = sb("attT", [P, 3, SL])
        wv = [sb(f"wv{i}", [P, SL]) for i in range(2)]
        acc = sb("acc", [P, SL])
        gate = sb("gate", [P, SL])
        ps_sc = ctx.enter_context(nc.psum_tensor(f"{tag}_sc", [P, 4, SL], F32))
        ps_w = [ctx.enter_context(nc.psum_tensor(f"{tag}_w{i}", [P, SL], F32)) for i in range(2)]
        ps_x = [ctx.enter_context(nc.psum_tensor(f"{tag}_x{i}", [P, SL], F32)) for i in range(2)]
        sem = lambda name: nc.alloc_semaphore(f"{tag}_{name}")
        loaded, padded, projected, placed = sem("loaded"), sem("padded"), sem("projected"), sem("placed")
        chain, tap_shifted, tap_exp, tap_sum, tap_ln = (sem(n) for n in ("chain", "tap_shifted", "tap_exp", "tap_sum", "tap_ln"))
        multiplied, used, scores_ready, shifted, exp_done, probs_ready = (sem(n) for n in (
            "multiplied", "used", "scores_ready", "shifted", "exp_done", "probs_ready"))
        turned, turned_in, spread, weighted, added, gate_ready, gated, out_ready, out_in = (sem(n) for n in (
            "turned", "turned_in", "spread", "weighted", "added", "gate_ready", "gated", "out_ready", "out_in"))
        gate_in = sem("gate_in")
        groups = ((0, 0, 1, ZERO_TAPS), (ZERO_TAPS, 1, PAIRED, 2), (taps - FAR_TAPS, n_in, 1, FAR_TAPS))
        singles = (ZERO_TAPS + 2 * PAIRED, 1 + PAIRED, 10)
        rows3 = (P, P, 5 * H)
        with nc.Block() as block:

            @block.sync
            def _(sp):
                sp.dma_start(w[:, :, :], w_dram).then_inc(loaded, 16)
                sp.dma_start(cols[:, :], cols_dram).then_inc(loaded, 16)
                sp.dma_start(pb[:, :, :], taps_dram.broadcast_to([P, taps, H])).then_inc(loaded, 16)
                sp.wait_ge(loaded, 48)

            @block.gpsimd
            def _(po):
                po.memset(kpad[:, :, 0:PAD], 0.0).then_inc(padded, 1)
                po.memset(vpad[:, :, 0:PAD], 0.0).then_inc(padded, 1)
                for s in range(NS):
                    for i in range(n_in):
                        k = s * n_in + i
                        po.wait_ge(weighted, k + 1)
                        if i == 0:
                            if s:
                                po.wait_ge(gated, s)
                            po.tensor_copy(acc[:, :], wv[k % 2][:, :]).then_inc(added, 1)
                        else:
                            po.wait_ge(added, k)
                            po.tensor_tensor(acc[:, :], acc[:, :], wv[k % 2][:, :], ALU.add).then_inc(added, 1)

            @block.tensor
            def _(pe):
                pe.wait_ge(loaded, 48)
                banks = [ps_sc[:, i, :] for i in range(4)]
                for n in range(12):
                    k, s = n // NS, n % NS
                    if n >= 4:
                        pe.wait_ge(placed, n - 3)
                    pe.matmul(banks[s], w[:, k, :], xin[:, s * SL:(s + 1) * SL], start=True, stop=True).then_inc(projected, 1)
                for s in range(NS):
                    if s:
                        pe.wait_ge(shifted, s)
                    else:
                        pe.wait_ge(placed, 12)
                    for i in range(n_in):
                        k = s * n_in + i
                        pe.wait_ge(multiplied, k + 1)
                        for t in range(4):
                            mm = pe.matmul(ps_sc[:, t, i * H:(i + 1) * H], prod[k % 3][:, t * P:(t + 1) * P], kit.heads[:, :],
                                           start=True, stop=True, skip_group_check=True)
                        mm.then_inc(used, 1)
                    sem_ = pe.wait_ge(probs_ready, s + 1)
                    for g in range(3):
                        n = 3 * s + g
                        if n >= 2:
                            pe.wait_ge(turned_in, n - 1)
                        if s and g < 2:
                            pe.wait_ge(out_in, s)
                            pe.wait_ge(gate_in, s)
                        for t in range(4):
                            mm = pe.transpose(ps_x[n % 2][0:rows3[g], t * P:(t + 1) * P],
                                              att[:, t, :, :].rearrange("p s h -> p (s h)")[:, g * P:g * P + rows3[g]], kit.ident[:, :])
                        mm.then_inc(turned, 1)
                    pe.wait_ge(turned_in, 3 * s + 3)
                    for i in range(n_in):
                        k = s * n_in + i
                        if k >= 2:
                            pe.wait_ge(weighted, k - 1)
                        r = rows3[i // 8]
                        pe.matmul(ps_w[k % 2][:, :], kit.spread[0:r, i % 8, :], attT[0:r, i // 8, :], start=True, stop=True).then_inc(spread, 1)
                    pe.matmul(ps_x[0][:, :], w[:, 3, :], xin[:, s * SL:(s + 1) * SL], start=True, stop=True).then_inc(gate_ready, 1)
                    pe.wait_ge(gated, s + 1)
                    pe.matmul(ps_x[1][:, :], w[:, 4, :], wv[0][:, :], start=True, stop=True).then_inc(out_ready, 1)

            @block.scalar
            def _(ac):
                ac.wait_ge(tap_shifted, 1)
                ac.activation(pb[:, :, :], pb[:, :, :], ACT.Exp).then_inc(tap_exp, 1)
                ac.wait_ge(tap_sum, 1)
                ac.activation(bias[:, :, :], bias[:, :, :], ACT.Ln).then_inc(tap_ln, 1)
                ac.wait_ge(loaded, 48)
                for n in range(12):
                    k, s = n // NS, n % NS
                    ac.wait_ge(projected, n + 1)
                    b, c = s // 2, (s % 2) * SL
                    dst = q[:, s * SL:(s + 1) * SL] if k == 0 else (kpad if k == 1 else vpad)[:, b, PAD + c:PAD + c + SL]
                    ac.activation(dst, ps_sc[:, s, :], ACT.Identity, bias=cols[:, k:k + 1]).then_inc(placed, 1)
                for s in range(NS):
                    ac.wait_ge(shifted, s + 1)
                    ac.activation(att[:, :, :, :], att[:, :, :, :], ACT.Exp).then_inc(exp_done, 1)
                    for g in range(3):
                        n = 3 * s + g
                        ac.wait_ge(turned, n + 1)
                        if s:
                            ac.wait_ge(spread, s * n_in)
                        ac.activation(attT[0:rows3[g], g, :], ps_x[n % 2][0:rows3[g], :], ACT.Copy).then_inc(turned_in, 1)
                    ac.wait_ge(gate_ready, s + 1)
                    if s:
                        ac.wait_ge(gated, s)
                    ac.activation(gate[:, :], ps_x[0][:, :], ACT.Sigmoid, bias=cols[:, 3:4]).then_inc(gate_in, 1)
                    ac.wait_ge(out_ready, s + 1)
                    ac.activation(y[:, s * SL:(s + 1) * SL], ps_x[1][:, :], ACT.Identity, bias=cols[:, 4:5]).then_inc(out_in, 1)

            @block.vector
            def _(ve):
                done = [0]

                def link(ins):
                    done[0] += 1
                    ins.then_inc(chain, 1)
                    ve.wait_ge(chain, done[0])

                ve.wait_ge(loaded, 48)
                f0, s0, m0 = singles
                for a, slot, n, each in groups:
                    link(ve.tensor_reduce(pbm[:, slot:slot + n, :], pb[:, a:a + n * each, :].rearrange("p (n k) h -> p n h k", k=each), AX.X, ALU.max))
                link(ve.tensor_copy(pbm[:, s0:s0 + m0, :], pb[:, f0:f0 + m0, :]))
                for a, slot, n, each in groups:
                    view = pb[:, a:a + n * each, :].rearrange("p (n k) h -> p n k h", k=each)
                    link(ve.tensor_tensor(view, view, pbm[:, slot:slot + n, :].unsqueeze(2).broadcast_to([P, n, each, H]), ALU.subtract))
                ve.tensor_tensor(pb[:, f0:f0 + m0, :], pb[:, f0:f0 + m0, :], pbm[:, s0:s0 + m0, :], ALU.subtract).then_inc(tap_shifted, 1)
                ve.wait_ge(tap_exp, 1)
                for a, slot, n, each in groups:
                    link(ve.tensor_reduce(bias[:, slot:slot + n, :], pb[:, a:a + n * each, :].rearrange("p (n k) h -> p n h k", k=each), AX.X, ALU.add))
                ve.tensor_copy(bias[:, s0:s0 + m0, :], pb[:, f0:f0 + m0, :]).then_inc(tap_sum, 1)
                ve.wait_ge(tap_ln, 1)
                link(ve.tensor_tensor(bias[:, :, :], bias[:, :, :], pbm[:, :, :], ALU.add))
                ve.wait_ge(padded, 2)
                ve.wait_ge(placed, 12)
                for s in range(NS):
                    b, c = s // 2, (s % 2) * SL
                    for i, off in enumerate(SHIFTS):
                        k = s * n_in + i
                        if k >= 3:
                            ve.wait_ge(used, k - 2)
                        ve.tensor_tensor(prod[k % 3][:, :], q[:, s * SL:(s + 1) * SL], kpad[:, b, PAD + c - off:PAD + c - off + SL],
                                         ALU.mult).then_inc(multiplied, 1)
                    ve.wait_ge(used, (s + 1) * n_in)
                    if s:
                        ve.wait_ge(turned, 3 * s)
                    ve.tensor_copy(att[:, :, n_in, :], bias[:, n_in, :].unsqueeze(1).broadcast_to([P, 4, H])).then_inc(scores_ready, 1)
                    link(ve.tensor_tensor(att[:, :, 0:n_in, :].rearrange("p t s h -> p t (s h)"), ps_sc[:, :, 0:n_in * H],
                                          bias[:, 0:n_in, :].rearrange("p s h -> p (s h)").unsqueeze(1).broadcast_to([P, 4, n_in * H]), ALU.add))
                    ve.wait_ge(scores_ready, s + 1)
                    by_head = att[:, :, :, :].rearrange("p t s h -> p t h s")
                    across = stat[:, :, :].unsqueeze(2).broadcast_to([P, 4, n_slots, H])
                    link(ve.tensor_reduce(stat[:, :, :], by_head, AX.X, ALU.max))
                    ve.tensor_tensor(att[:, :, :, :], att[:, :, :, :], across, ALU.subtract).then_inc(shifted, 1)
                    ve.wait_ge(exp_done, s + 1)
                    link(ve.tensor_reduce(stat[:, :, :], by_head, AX.X, ALU.add))
                    link(ve.reciprocal(stat[:, :, :], stat[:, :, :]))
                    ve.tensor_tensor(att[:, :, :, :], att[:, :, :, :], across, ALU.mult).then_inc(probs_ready, 1)
                    for i, off in enumerate(SHIFTS):
                        k = s * n_in + i
                        ve.wait_ge(spread, k + 1)
                        if i >= 2:
                            ve.wait_ge(added, k - 1)
                        elif s:
                            ve.wait_ge(out_ready, s)
                            ve.wait_ge(added, k - 1)
                        ve.tensor_tensor(wv[k % 2][:, :], ps_w[k % 2][:, :], vpad[:, b, PAD + c - off:PAD + c - off + SL],
                                         ALU.mult).then_inc(weighted, 1)
                    ve.wait_ge(added, (s + 1) * n_in)
                    ve.wait_ge(gate_in, s + 1)
                    ve.tensor_tensor(wv[0][:, :], acc[:, :], gate[:, :], ALU.mult).then_inc(gated, 1)


def chunk_rates(nc, tag, kit, xin, w_dram, rate_dram, decay_dram, decay_in, decay_out, rate_in, rate_out):
    K4 = 64
    chunks = N // 64
    with nc.cleanup_on_exit(), ExitStack() as ctx:
        sb = lambda name, shape, dt=F32: ctx.enter_context(nc.sbuf_tensor(f"{tag}_{name}", shape, dt))
        w = sb("w", [P, K4])
        sig = sb("sig", [K4, T])
        mean = sb("mean", [K4, 2, chunks])
        ps = [ctx.enter_context(nc.psum_tensor(f"{tag}_ps{s}", [K4, SL], F32)) for s in range(NS)]
        sem = lambda name: nc.alloc_semaphore(f"{tag}_{name}")
        loaded, ready, sigmoid_done, summed, scaled, stored, spread = (sem(n) for n in (
            "loaded", "ready", "sigmoid_done", "summed", "scaled", "stored", "spread"))
        with nc.Block() as block:

            @block.sync
            def _(sp):
                sp.dma_start(w[:, :], w_dram).then_inc(loaded, 16)
                sp.wait_ge(scaled, 1)
                with nc.allow_non_contiguous_dma(reason="one small array is stored in another order"):
                    for kind in range(2):
                        for b in range(2):
                            sp.dma_start(rate_dram[kind, b].rearrange("c h -> h c"), mean[16 * kind:16 * kind + 16, b, :]).then_inc(stored, 16)
                            for par in range(2):
                                r = 32 + kind * 16 + par * 8
                                sp.dma_start(decay_dram[kind, par, :, :, b].rearrange("c a -> a c"), mean[r:r + 8, b, :]).then_inc(stored, 16)
                sp.wait_ge(stored, 16 * 12)
                for kind in range(2):
                    rate, decay = ((rate_in, decay_in), (rate_out, decay_out))[kind]
                    for half in range(2):
                        r = slice(64 * half, 64 * half + 64)
                        sp.dma_start(rate[r, :, :], rate_dram[kind, half:half + 1].broadcast_to([64, chunks, 16])).then_inc(spread, 16)
                        sp.dma_start(decay[r, :, :, :], decay_dram[kind, half:half + 1].broadcast_to([64, chunks, 8, 2])).then_inc(spread, 16)
                sp.wait_ge(spread, 16 * 8)

            @block.tensor
            def _(pe):
                pe.wait_ge(loaded, 16)
                for s in range(NS):
                    pe.matmul(ps[s][:, :], w[:, :], xin[:, s * SL:(s + 1) * SL], start=True, stop=True).then_inc(ready, 1)

            @block.scalar
            def _(ac):
                for s in range(NS):
                    ac.wait_ge(ready, s + 1)
                    ac.activation(sig[:, s * SL:(s + 1) * SL], ps[s][:, :], ACT.Sigmoid).then_inc(sigmoid_done, 1)

            @block.vector
            def _(ve):
                ve.wait_ge(sigmoid_done, NS)
                ve.tensor_reduce(mean[:, :, :], sig[:, :].rearrange("p (b c n) -> p b c n", b=2, c=chunks), AX.X, ALU.add).then_inc(summed, 1)
                ve.wait_ge(summed, 1)
                ve.tensor_scalar(mean[:, :, :], mean[:, :, :], kit.columns[0:K4, 2:3], None, ALU.mult).then_inc(scaled, 1)


def load_constants(nc, ctx, kit, a):
    sb = lambda name, shape, dt=F32: ctx.enter_context(nc.sbuf_tensor(f"const_{name}", shape, dt))
    kit.ident, kit.den_sel, kit.mean, kit.ones, kit.upto = (sb(n, [P, P]) for n in ("ident", "den_sel", "mean", "ones", "upto"))
    kit.blocks, kit.head4, kit.heads = sb("blocks", [P, 4, P]), sb("head4", [P, 4]), sb("heads", [P, 16])
    kit.columns, kit.lower = sb("columns", [P, 3]), sb("lower", [P, 16, 16])
    kit.ident_bf, kit.mask_kq, kit.mask_qk = sb("ident_bf", [P, P], BF16), sb("mask_kq", [P, 2 * P], BF16), sb("mask_qk", [P, 2 * P], BF16)
    loads = dict(ident=kit.ident, den_sel=kit.den_sel, mean=kit.mean, ones=kit.ones, upto=kit.upto, blocks=kit.blocks,
                 head4=kit.head4, heads=kit.heads, columns=kit.columns, lower=kit.lower)
    with nc.cleanup_on_exit(), ExitStack() as inner:
        masks = inner.enter_context(nc.sbuf_tensor("const_masks", [P, 4 * P], F32))
        loaded, converted = nc.alloc_semaphore("const_loaded"), nc.alloc_semaphore("const_converted")
        with nc.Block() as block:

            @block.sync
            def _(sp):
                for name, tile in loads.items():
                    sp.dma_start(tile[:], a["c_" + name]).then_inc(loaded, 16)
                sp.dma_start(masks[:, :], a["c_masks"]).then_inc(loaded, 16)
                sp.wait_ge(loaded, 16 * (len(loads) + 1))

            @block.vector
            def _(ve):
                ve.wait_ge(loaded, 16 * (len(loads) + 1))
                ve.tensor_copy(kit.ident_bf[:, :], kit.ident[:, :]).then_inc(converted, 1)
                ve.tensor_copy(kit.mask_kq[:, :], masks[:, 0:2 * P]).then_inc(converted, 1)
                ve.tensor_copy(kit.mask_qk[:, :], masks[:, 2 * P:4 * P]).then_inc(converted, 1)


def move(nc, tag, pairs):
    with nc.cleanup_on_exit():
        moved = nc.alloc_semaphore(f"{tag}_moved")
        with nc.Block() as block:

            @block.sync
            def _(sp):
                for dst, src in pairs:
                    sp.dma_start(dst, src).then_inc(moved, 16)
                sp.wait_ge(moved, 16 * len(pairs))


class Buffers:
    pass


def layer0_attention(nc, kit, a, m):
    h = m.g
    layer_norm(nc, "l0n1", kit, m.xn, h, a["l0_ln1"])
    with ExitStack() as ctx:
        v_all = ctx.enter_context(nc.sbuf_tensor("l0_v", [P, 8, 8, GH, 32], F32))
        out_all = ctx.enter_context(nc.sbuf_tensor("l0_out", [P, 8, N], F32))
        query_parts(nc, "l0q", kit, h, a["l0_wq"], a["l0_bq"], P, PARTS_Q, kit.q_dram)
        query_parts(nc, "l0k", kit, h, a["l0_wk"], a["l0_bk"], P, PARTS_K, kit.k_dram)
        values(nc, "l0v", kit, h, a["l0_wv"], a["l0_bv"], GH, v_all)
        attend(nc, "l0a", "window", E8 ** -0.5, kit.q_dram, kit.k_dram, v_all, GH, out_all, kit)
        outs = [heads_of(out_all, g) for g in range(4)]
        terms = [(g, g) for g in range(4)]
        project(nc, "l0p", [(terms, 0, None, P, m.s, False)], outs, a["l0_wp"], a["l0_bp"])
        values(nc, "l0sv", kit, h, a["l0_wsv"], a["l0_bsv"], GH, v_all)
        linear_attention(nc, "l0s", kit, h, a["l0_wsqk"], a["l0_bsqk"], v_all, out_all)
        project(nc, "l0sp", [(terms, 0, None, P, m.s, True)], outs, a["l0_wos"], a["l0_bos"])
    project(nc, "l0m", [([(0, 0)], 0, None, P, m.g, False)], [slices_of(m.s)], a["l0_wo"], a["l0_bo"])
    add_to(nc, "l0x", m.g, m.xn, m.s)
    layer_norm(nc, "l0n2", kit, m.s, m.g, a["l0_ln2"])
    with ExitStack() as ctx:
        mlp = ctx.enter_context(nc.sbuf_tensor("l0_mlp", [P, T], F32))
        one = ctx.enter_context(nc.sbuf_tensor("l0_one", [1, T], F32))
        move(nc, "l0one", [(one[:, :], a["c_one_row"])])
        mixture(nc, "l0mlp", m.g, one, a["l0_w1"], a["l0_w2"], a["l0_b2"], a["c_one_row"], mlp, 1, 4, ACT.Gelu, group=1)
        add_to(nc, "l0y", m.s, mlp, m.s)


def layer0_ffn(nc, kit, a, m):
    with ExitStack() as ctx:
        gates = ctx.enter_context(nc.sbuf_tensor("f0_gates", [16, T], F32))
        route(nc, "f0r", kit, m.xn, a["f0_router"], a["f0_router_b"], 8, 2, "share", gates, kit.gate_dram[0:8, :], 8)
        mixture(nc, "f0", m.xn, gates, a["f0_w1"], a["f0_w2"], a["f0_b2"], kit.gate_dram, m.g, 8, 4, ACT.Gelu)
    residual(nc, "f0x", m.x, m.s, m.g)


def layer1_attention(nc, kit, a, m):
    with ExitStack() as ctx:
        sb = lambda name, shape: ctx.enter_context(nc.sbuf_tensor(f"l1_{name}", shape, F32))
        decay_in, decay_out = (sb(f"decay_{n}", [P, NC, HP, 2]) for n in ("in", "out"))
        rate_in, rate_out = (sb(f"rate_{n}", [P, NC, 2 * HP]) for n in ("in", "out"))
        wqk, wv, wo = sb("wqk", [P, 2, HP, P]), sb("wv", [P, HP, P]), sb("wo", [P, HP, P])
        win, wout, wout_t = (sb(n, [P, HP, 2, F]) for n in ("win", "wout", "wout_t"))
        chunk_rates(nc, "l1r", kit, m.xn, a["l1_wrates"], kit.rate_dram, kit.decay_dram, decay_in, decay_out, rate_in, rate_out)
        move(nc, "l1w", [(wqk[:, :, :, :], a["l1_wqk"]), (wv[:, :, :], a["l1_wv"]), (wo[:, :, :], a["l1_wo"]),
                         (win[:, :, :, :], a["l1_win"]), (wout[:, :, :, :], a["l1_wout"]), (wout_t[:, :, :, :], a["l1_wout_t"])])
        fast_weights(nc, "l1", m.xn[:, :], wqk, wv, wo, win, wout, wout_t, decay_in, decay_out, rate_in, rate_out, m.s[:, :], kit.ident)


def layer1_ffn(nc, kit, a, m):
    with ExitStack() as ctx:
        gates = ctx.enter_context(nc.sbuf_tensor("f1_gates", [16, T], F32))
        route(nc, "f1r", kit, m.xn, a["f1_router"], a["f1_router_b"], 8, 1, "capacity", gates, kit.gate_dram[0:9, :], 9, T // 8)
        mixture(nc, "f1", m.xn, gates, a["f1_w1"], a["f1_w2"], a["f1_b2"], kit.gate_dram, m.g, 8, 4, ACT.Gelu,
                act_scale=2.0 ** 0.5 / 1.41421)
    residual(nc, "f1x", m.x, m.s, m.g, dropped_dram=kit.gate_dram[8:9, :], xn=m.xn)


def layer2_attention(nc, kit, a, m):
    with ExitStack() as ctx:
        kit.spread = ctx.enter_context(nc.sbuf_tensor("l2_spread", [P, 8, P], F32))
        move(nc, "l2c", [(kit.spread[:, :, :], a["c_spread"])])
        dilated_attention(nc, "l2", kit, m.xn, a["l2_w"], a["l2_cols"], a["l2_taps"], m.s)


def layer2_ffn(nc, kit, a, m):
    layer_norm(nc, "f2n1", kit, m.xn, m.g, a["f2_g1"], rms=True)
    with ExitStack() as ctx:
        v_all = ctx.enter_context(nc.sbuf_tensor("f2_v", [P, 8, 8, 1, 32], F32))
        out_all = ctx.enter_context(nc.sbuf_tensor("f2_out", [P, 8, N], F32))
        query_parts(nc, "f2q", kit, m.g, a["f2_wq"], None, P, PARTS_Q, kit.q_dram, a["c_rope_q"])
        query_parts(nc, "f2k", kit, m.g, a["f2_wk"], None, 32, PARTS_K, kit.k4_dram, a["c_rope_k"])
        values(nc, "f2v", kit, m.g, a["f2_wv"], a["c_zero_row"][:, 0:32], 1, v_all)
        attend(nc, "f2a", "causal", E8 ** -0.5, kit.q_dram, kit.k4_dram, v_all, 1, out_all, kit)
        project(nc, "f2p", [([(g, g) for g in range(4)], 0, None, P, m.g, False)], [heads_of(out_all, g) for g in range(4)],
                a["f2_wo"], a["c_zero_col"])
    add_to(nc, "f2x", m.g, m.xn, m.g)
    with ExitStack() as ctx:
        norm = ctx.enter_context(nc.sbuf_tensor("f2_norm", [P, T], F32))
        moe = ctx.enter_context(nc.sbuf_tensor("f2_moe", [P, T], F32))
        gates = ctx.enter_context(nc.sbuf_tensor("f2_gates", [16, T], F32))
        layer_norm(nc, "f2n2", kit, m.g, norm, a["f2_g2"], rms=True)
        route(nc, "f2r", kit, norm, a["f2_router"], a["c_zero_row"][:, 0:4], 4, 2, "share", gates, kit.gate_dram[0:4, :], 4)
        mixture(nc, "f2", norm, gates, a["f2_w13"], a["f2_w2"], a["c_zero_4"], kit.gate_dram, moe, 4, 3, ACT.Silu, gated_unit=True)
        residual(nc, "f2y", m.x, m.s, moe, plus=m.g)


def layer3_attention(nc, kit, a, m):
    with ExitStack() as ctx:
        v_all = ctx.enter_context(nc.sbuf_tensor("l3_v", [P, 8, 8, GH, 32], F32))
        out_all = ctx.enter_context(nc.sbuf_tensor("l3_out", [P, 8, N], F32))
        query_parts(nc, "l3q", kit, m.xn, a["l3_wq"], None, P, PARTS_Q, kit.q_dram)
        query_parts(nc, "l3k", kit, m.xn, a["l3_wk"], None, P, PARTS_K, kit.k_dram)
        values(nc, "l3v", kit, m.xn, a["l3_wv"], a["c_zero_row"][:, 0:P], GH, v_all)
        attend(nc, "l3a", "full", P ** -0.5, kit.q_dram, kit.k_dram, v_all, GH, out_all, kit)
        project(nc, "l3p", [([(g, g) for g in range(4)], 0, None, P, m.s, False)], [heads_of(out_all, g) for g in range(4)],
                a["l3_wu"], a["l3_bu"])


def layer3_ffn(nc, kit, a, m):
    with ExitStack() as ctx:
        gates = ctx.enter_context(nc.sbuf_tensor("f3_gates", [16, T], F32))
        route(nc, "f3r", kit, m.xn, a["f3_router"], a["f3_router_b"], 15, 3, "plain", gates, kit.gate_dram[0:16, :], 16)
        mixture(nc, "f3", m.xn, gates, a["f3_w1"], a["f3_w2"], a["f3_b2"], kit.gate_dram, m.g, 16, 1, ACT.Relu)
    residual(nc, "f3x", m.x, m.s, m.g)


LAYERS = ((layer0_attention, layer0_ffn), (layer1_attention, layer1_ffn), (layer2_attention, layer2_ffn),
          (layer3_attention, layer3_ffn))


def network(nc, a, out, layers=(0, 1, 2, 3), s_out=None):
    kit, m = Kit(), Buffers()
    scratch = lambda name, shape, dt: nc.dram_tensor(name, shape, dt).ap()
    kit.q_dram = scratch("q_parts", [2, ROWS, 16, N], BF16)
    kit.k_dram = scratch("k_parts", [2, ROWS, 16, N], BF16)
    kit.k4_dram = scratch("k4_parts", [2, ROWS, 4, N], BF16)
    kit.gate_dram = scratch("gate_rows", [16, T], F32)
    kit.rate_dram = scratch("rates", [2, 2, NC, 2 * HP], F32)
    kit.decay_dram = scratch("decays", [2, 2, NC, HP, 2], F32)
    with ExitStack() as ctx:
        m.x, m.xn, m.s, m.g = (ctx.enter_context(nc.sbuf_tensor(n, [P, T], F32)) for n in ("resid", "normed", "mixer_out", "ffn_out"))
        load_constants(nc, ctx, kit, a)
        move(nc, "x", [(m.x[:, :], a["x"])])
        for i in layers:
            attention, ffn = LAYERS[i]
            layer_norm(nc, f"n{i}", kit, m.x, m.xn)
            attention(nc, kit, a, m)
            if s_out is not None:
                move(nc, f"dbg{i}", [(s_out, m.s[:, :])])
            ffn(nc, kit, a, m)
        move(nc, "y", [(out, m.x[:, :])])



def shape_constants():
    f = np.float32
    c = {}
    c["ident"] = np.eye(P, dtype=f)
    p = np.arange(P)
    c["den_sel"] = (p[:, None] == 32 * (p[None] // 32) + E8).astype(f)
    c["mean"] = np.full((P, P), 1.0 / P, f)
    c["ones"] = np.ones((P, P), f)
    c["upto"] = (p[:, None] <= p[None]).astype(f)
    col = p[None, None]
    head = 4 * np.arange(4)[None, :, None] + col // 32
    c["blocks"] = ((p[:, None, None] // E8 == head) & (col % 32 <= E8)).astype(f)
    c["head4"] = ((p[:, None] // E8) % 4 == np.arange(4)[None]).astype(f)
    c["heads"] = ((p[:, None] // E8 == np.arange(16)[None]) * f(E8 ** -0.5)).astype(f)
    scale = np.where(p < 32, 0.001 / 64, 0.9 / 64)
    c["columns"] = np.stack([np.full(P, 1e-5), np.full(P, 1.1920928955078125e-07), scale], 1).astype(f)
    lower = np.arange(16)[None, :] < np.arange(16)[:, None]
    c["lower"] = np.broadcast_to(lower.astype(f), (P, 16, 16))
    diag = np.where(p[:, None] <= p[None], 0, -1e30)
    prev = np.where(p[:, None] > p[None], 0, -1e30)
    c["masks"] = np.concatenate([diag, prev, prev.T, diag.T], 1).astype(f)
    k = np.arange(8)[None, :, None]
    c["spread"] = ((p[:, None, None] // 16 == k) & (p[:, None, None] % 16 == col // E8)).astype(f)
    inv_freq = (1.0 / 10000.0 ** (np.arange(0, E8, 2, dtype=f) / f(E8))).astype(f)
    freqs = np.arange(N, dtype=f)[:, None] * inv_freq[None]
    emb = np.concatenate([freqs, freqs], 1).astype(f)
    sign = np.where(np.arange(E8) < E8 // 2, -1.0, 1.0)[:, None]
    cos, sin = np.cos(emb).T.astype(f), (np.sin(emb).T * sign).astype(f)
    c["rope_q"] = np.stack([np.repeat(cos, 16, 0), np.repeat(sin, 16, 0)])
    c["rope_k"] = np.stack([np.repeat(cos, 4, 0), np.repeat(sin, 4, 0)])
    c["one_row"] = np.ones((1, T), f)
    c["zero_row"] = np.zeros((1, P), f)
    c["zero_col"] = np.zeros((P, 1), f)
    c["zero_4"] = np.zeros((4, P), f)
    return {"c_" + n: np.ascontiguousarray(v, dtype=f) for n, v in c.items()}


def lay_out(i):
    a = shape_constants()
    col = lambda *v: np.stack(v, 1)

    def by_dim(w, heads=16):
        return w.reshape(w.shape[:-1] + (heads, E8)).swapaxes(-1, -2).reshape(w.shape)

    def rotated(w, heads=16):
        r = w.reshape(w.shape[:-1] + (heads, E8))
        return np.concatenate([r[..., E8 // 2:], r[..., :E8 // 2]], -1).reshape(w.shape)

    def from_heads(w):
        out = np.zeros((4, 32, 4, P), w.dtype)
        out[:, :E8] = w.reshape(4, 4, E8, P).transpose(1, 2, 0, 3)
        return out.reshape(P, 4, P)

    def experts1(w, b):
        e, _, f = w.shape
        return np.concatenate([w, b.reshape(e, f // P, P).transpose(0, 2, 1)], 2)

    def experts2(w):
        e, f, _ = w.shape
        return w.reshape(e, f // P, P, P).transpose(0, 2, 1, 3).reshape(e, P, f)

    a["x"] = i["L0_attn_x"].reshape(T, P).T
    g = lambda n: i["L0_attn_" + n]
    a["l0_ln1"], a["l0_ln2"] = col(g("g1"), g("b1")), col(g("gm"), g("bm"))
    wq, wk, wv = np.split(g("Wqkv_a"), 3, 1)
    bq, bk, bv = np.split(g("bqkv_a"), 3)
    sq, sk, sv = np.split(g("Wqkv_s"), 3, 1)
    cq, ck, cv = np.split(g("bqkv_s"), 3)
    a["l0_wq"], a["l0_wk"], a["l0_wv"], a["l0_bv"] = by_dim(wq), by_dim(wk), wv, bv[None]
    a["l0_bq"], a["l0_bk"], a["l0_bsqk"] = by_dim(bq)[:, None], by_dim(bk)[:, None], col(cq, ck)
    a["l0_wp"], a["l0_bp"] = from_heads(g("Wp_a")), g("bp_a")[:, None]
    a["l0_wsv"], a["l0_bsv"], a["l0_wsqk"] = sv, cv[None], np.stack([sq, sk], 1)
    a["l0_wos"], a["l0_bos"] = from_heads(g("Wo_s")), g("bo_s")[:, None]
    a["l0_wo"], a["l0_bo"] = g("Wo")[:, None], g("bo")[:, None]
    a["l0_w1"], a["l0_w2"] = experts1(g("W1")[None], g("b1m")[None]), experts2(g("W2")[None])
    a["l0_b2"] = g("b2m")[None]
    g = lambda n: i["L0_ffn_" + n]
    a["f0_router"], a["f0_router_b"] = g("router_w"), g("router_b")[None]
    a["f0_w1"], a["f0_w2"], a["f0_b2"] = experts1(g("w1"), g("b1")), experts2(g("w2")), g("b2")
    g = lambda n: i["L1_attn_" + n]
    a["l1_wqk"] = np.stack([g("Wq").T.reshape(P, HP, P), g("Wk").T.reshape(P, HP, P)], 1)
    a["l1_wv"] = g("Wv").T.reshape(P, HP, P)
    a["l1_wo"] = g("Wo").T.reshape(HP, P, P).transpose(1, 0, 2)

    def pairs(w):
        return np.broadcast_to(w.reshape(HP, 2, F, F).transpose(1, 2, 0, 3).reshape(P, HP, 1, F), (P, HP, 2, F))
    a["l1_win"] = pairs(g("W_in_init")[0].transpose(1, 2, 0))
    a["l1_wout"] = pairs(g("W_out_init")[0].transpose(1, 0, 2))
    a["l1_wout_t"] = pairs(g("W_out_init")[0].transpose(1, 2, 0))
    by_parity = lambda w: w.reshape(2, HP, 2, P).transpose(0, 2, 1, 3).reshape(32, P)
    a["l1_wrates"] = np.concatenate([g("Wlr"), by_parity(g("Wbeta"))], 0).T
    g = lambda n: i["L1_ffn_" + n]
    a["f1_router"], a["f1_router_b"] = g("W_sw"), g("b_sw")[None]
    a["f1_w1"], a["f1_w2"], a["f1_b2"] = experts1(g("W1"), g("b1")), experts2(g("W2")), g("b2")
    g = lambda n: i["L2_attn_" + n]
    a["l2_w"] = np.stack(np.split(g("w_qkv"), 3, 1) + [g("w_gate"), g("w_out")], 1)
    a["l2_cols"] = col(*np.split(g("b_qkv"), 3), g("b_gate"), g("b_out"))
    offsets = [(1 << j) * tap for j in range(11) for tap in range(4)]
    order = [t for s in SHIFTS for t in range(44) if offsets[t] == s] + [t for t in range(44) if offsets[t] >= N]
    a["l2_taps"] = g("pos_bias")[order][None]
    g = lambda n: i["L2_ffn_" + n]
    a["f2_g1"], a["f2_g2"] = g("g1")[:, None], g("g2")[:, None]
    a["f2_wq"] = np.concatenate([by_dim(g("wq")), by_dim(rotated(g("wq")))], 1)
    a["f2_wk"] = np.concatenate([by_dim(g("wk"), 4), by_dim(rotated(g("wk"), 4), 4)], 1)
    a["f2_wv"], a["f2_wo"], a["f2_router"] = g("wv"), from_heads(g("wo")), g("gate")
    a["f2_w13"], a["f2_w2"] = np.concatenate([g("w1"), g("w3")], 2), experts2(g("w2"))
    g = lambda n: i["L3_attn_" + n]
    a["l3_wq"], a["l3_wk"], a["l3_wv"] = by_dim(g("Wq").T), by_dim(g("Wk").T), g("Wv").T
    a["l3_wu"], a["l3_bu"] = from_heads(g("Wu").T), g("bu")[:, None]
    g = lambda n: i["L3_ffn_" + n]
    a["f3_router"], a["f3_router_b"] = g("router_W"), g("router_b")[None]
    a["f3_w1"] = experts1(np.concatenate([g("eW1"), g("sW1")[None]]), np.concatenate([g("eb1"), g("sb1")[None]]))
    a["f3_w2"] = experts2(np.concatenate([g("eW2"), g("sW2")[None]]))
    a["f3_b2"] = np.concatenate([g("eb2"), g("sb2")[None]])
    return {n: np.ascontiguousarray(v) for n, v in a.items()}



def kernel(**inputs):
    import concourse.bacc as _bacc
    from concourse.bass_utils import run_bass_kernel_spmd as _run

    nc = _bacc.Bacc("TRN2", target_bir_lowering=False, num_devices=1)
    laid = lay_out({name: np.asarray(v) for name, v in inputs.items()})
    arrays, a = {}, {}
    for name, v in laid.items():
        arrays[f"in_{name}_dram"] = v
        a[name] = nc.dram_tensor(f"in_{name}_dram", v.shape, mybir.dt.from_np(v.dtype), kind="ExternalInput").ap()
    out = nc.dram_tensor("out_dram", (P, T), F32, kind="ExternalOutput").ap()
    network(nc, a, out)
    r = _run(nc, [arrays], core_ids=[0])
    return np.ascontiguousarray(r.results[0]["out_dram"].T).reshape(2, N, P)
```

```python
from contextlib import ExitStack
import numpy as np
import concourse.bass as bass
from concourse import mybir

F32 = mybir.dt.float32
BF16 = mybir.dt.bfloat16
ACT = mybir.ActivationFunctionType
ALU = mybir.AluOpType
AX = mybir.AxisListType

P = 128
T = 2048
SL = 512
NS = T // SL
N = 1024




class Kit:
    pass


def layer_norm(nc, tag, kit, src, dst, gain_dram=None, rms=False):
    tiles = T // P
    with nc.cleanup_on_exit(), ExitStack() as ctx:
        sb = lambda name, shape: ctx.enter_context(nc.sbuf_tensor(f"{tag}_{name}", shape, F32))
        sq = sb("sq", [P, T])
        gain = sb("gain", [P, 2])
        var, inv, tmp = (sb(n, [P, tiles]) for n in ("var", "inv", "tmp"))
        diag = sb("diag", [P, tiles, P])
        ps = [ctx.enter_context(nc.psum_tensor(f"{tag}_ps{s}", [P, SL], F32)) for s in range(NS)]
        ps_var = ctx.enter_context(nc.psum_tensor(f"{tag}_psvar", [P, tiles], F32))
        sem = lambda name: nc.alloc_semaphore(f"{tag}_{name}")
        loaded, mean_ready, centered, squared, var_ready = (sem(n) for n in ("loaded", "mean_ready", "centered", "squared", "var_ready"))
        chain, var_in, std_ready, diag_ready, spread, scaled = (sem(n) for n in (
            "chain", "var_in", "std_ready", "diag_ready", "spread", "scaled"))
        loads = int(gain_dram is not None)
        n_gain = gain_dram.shape[1] if loads else 0
        base = src if rms else dst
        eps = 1.1920928955078125e-07 if rms else 1e-5
        with nc.Block() as block:

            if loads:
                @block.sync
                def _(sp):
                    sp.dma_start(gain[:, 0:n_gain], gain_dram).then_inc(loaded, 16)
                    sp.wait_ge(loaded, 16)

            @block.tensor
            def _(pe):
                if not rms:
                    for s in range(NS):
                        pe.matmul(ps[s][:, :], kit.mean[:, :], src[:, s * SL:(s + 1) * SL], start=True, stop=True).then_inc(mean_ready, 1)
                for t in range(tiles):
                    if t % 4 == 0:
                        pe.wait_ge(squared, t // 4 + 1)
                    mm = pe.matmul(ps_var[:, t:t + 1], sq[:, t * P:(t + 1) * P], kit.mean[:, 0:1], start=True, stop=True)
                mm.then_inc(var_ready, 1)
                for s in range(NS):
                    pe.wait_ge(diag_ready, s + 1)
                    pe.matmul(ps[s][:, :], kit.ones[:, :], diag[:, 4 * s:4 * s + 4, :], start=True, stop=True).then_inc(spread, 1)

            @block.scalar
            def _(ac):
                for s in range(NS):
                    if not rms:
                        ac.wait_ge(centered, s + 1)
                    ac.activation(sq[:, s * SL:(s + 1) * SL], base[:, s * SL:(s + 1) * SL], ACT.Square).then_inc(squared, 1)
                ac.wait_ge(var_in, 1)
                ac.activation(inv[:, :], var[:, :], ACT.Sqrt).then_inc(std_ready, 1)

            @block.vector
            def _(ve):
                done = [0]

                def link(ins):
                    done[0] += 1
                    ins.then_inc(chain, 1)
                    ve.wait_ge(chain, done[0])

                if not rms:
                    for s in range(NS):
                        ve.wait_ge(mean_ready, s + 1)
                        ve.tensor_tensor(dst[:, s * SL:(s + 1) * SL], src[:, s * SL:(s + 1) * SL], ps[s][:, :], ALU.subtract).then_inc(centered, 1)
                ve.wait_ge(var_ready, 1)
                ve.tensor_scalar(var[:, :], ps_var[:, :], eps, None, ALU.add).then_inc(var_in, 1)
                ve.wait_ge(std_ready, 1)
                link(ve.reciprocal(inv[:, :], inv[:, :]))
                link(ve.tensor_tensor(tmp[:, :], inv[:, :], inv[:, :], ALU.mult))
                link(ve.tensor_tensor(tmp[:, :], tmp[:, :], var[:, :], ALU.mult))
                link(ve.tensor_scalar(tmp[:, :], tmp[:, :], -0.5, 1.5, ALU.mult, ALU.add))
                link(ve.tensor_tensor(inv[:, :], inv[:, :], tmp[:, :], ALU.mult))
                for s in range(NS):
                    ve.tensor_tensor(diag[:, 4 * s:4 * s + 4, :], kit.ident[:, :].unsqueeze(1).broadcast_to([P, 4, P]),
                                     inv[:, 4 * s:4 * s + 4].unsqueeze(2).broadcast_to([P, 4, P]), ALU.mult).then_inc(diag_ready, 1)
                if loads:
                    ve.wait_ge(loaded, 16)
                for s in range(NS):
                    part = slice(s * SL, (s + 1) * SL)
                    ve.wait_ge(spread, s + 1)
                    if gain_dram is None:
                        ve.tensor_tensor(dst[:, part], base[:, part], ps[s][:, :], ALU.mult).then_inc(scaled, 1)
                    else:
                        ve.scalar_tensor_tensor(dst[:, part], base[:, part], gain[:, 0:1], ps[s][:, :], ALU.mult, ALU.mult).then_inc(scaled, 1)
                    if n_gain == 2:
                        ve.wait_ge(scaled, s + 1)
                        ve.tensor_scalar(dst[:, part], dst[:, part], gain[:, 1:2], None, ALU.add).then_inc(centered, 1)


def project(nc, tag, jobs, ins, w_dram, columns_dram):
    n_w = w_dram.shape[1]
    with nc.cleanup_on_exit(), ExitStack() as ctx:
        w = ctx.enter_context(nc.sbuf_tensor(f"{tag}_w", [P, n_w, P], F32))
        cols = ctx.enter_context(nc.sbuf_tensor(f"{tag}_cols", [P, columns_dram.shape[1]], F32))
        ps = [ctx.enter_context(nc.psum_tensor(f"{tag}_ps{s}", [P, SL], F32)) for s in range(NS)]
        sem = lambda name: nc.alloc_semaphore(f"{tag}_{name}")
        loaded, product_ready, emptied, added = sem("loaded"), sem("product_ready"), sem("emptied"), sem("added")
        adds = [False]
        with nc.Block() as block:

            @block.sync
            def _(sp):
                sp.dma_start(w[:, :, :], w_dram).then_inc(loaded, 16)
                sp.dma_start(cols[:, :], columns_dram).then_inc(loaded, 16)
                sp.wait_ge(loaded, 32)

            @block.tensor
            def _(pe):
                pe.wait_ge(loaded, 32)
                for n, (terms, bias, act, rows, out, add) in enumerate(jobs):
                    for s in range(NS):
                        if n:
                            pe.wait_ge(emptied, (n - 1) * NS + s + 1)
                        for i, (k, src) in enumerate(terms):
                            mm = pe.matmul(ps[s][0:rows, :], w[:, k, 0:rows], ins[src](s),
                                           start=i == 0, stop=i == len(terms) - 1)
                        mm.then_inc(product_ready, 1)

            @block.scalar
            def _(ac):
                ac.wait_ge(loaded, 32)
                for n, (terms, bias, act, rows, out, add) in enumerate(jobs):
                    for s in range(NS):
                        ac.wait_ge(product_ready, n * NS + s + 1)
                        target = ps[s][0:rows, :] if add else out[:, s * SL:(s + 1) * SL]
                        if bias is None:
                            ins_ = ac.activation(target, ps[s][0:rows, :], ACT.Copy if act is None else act)
                        else:
                            ins_ = ac.activation(target, ps[s][0:rows, :], ACT.Identity if act is None else act,
                                                 bias=cols[0:rows, bias:bias + 1])
                        ins_.then_inc(added if add else emptied, 1)

            if any(j[5] for j in jobs):
                @block.vector
                def _(ve):
                    k = 0
                    for n, (terms, bias, act, rows, out, add) in enumerate(jobs):
                        if add:
                            for s in range(NS):
                                k += 1
                                ve.wait_ge(added, k)
                                part = out[:, s * SL:(s + 1) * SL]
                                ve.tensor_tensor(part, ps[s][0:rows, :], part, ALU.add).then_inc(emptied, 1)


def slices_of(a):
    return lambda s: a[:, s * SL:(s + 1) * SL]


def heads_of(out_all, g):
    return lambda s: out_all[:, (s // 2) * 4 + g, (s % 2) * SL:(s % 2 + 1) * SL]


def values(nc, tag, kit, xin, wv_dram, bias_dram, key_heads, v_all, function=None):
    nv = 4 * key_heads * E8
    with nc.cleanup_on_exit(), ExitStack() as ctx:
        w = ctx.enter_context(nc.sbuf_tensor(f"{tag}_w", [P, nv], F32))
        bias = ctx.enter_context(nc.sbuf_tensor(f"{tag}_b", [P, nv], F32))
        ps = [ctx.enter_context(nc.psum_tensor(f"{tag}_ps{i}", [P, 4, nv], F32)) for i in range(4)]
        sem = lambda name: nc.alloc_semaphore(f"{tag}_{name}")
        loaded, filled, product_ready, placed = sem("loaded"), sem("filled"), sem("product_ready"), sem("placed")
        with nc.Block() as block:

            @block.sync
            def _(sp):
                sp.dma_start(w[:, :], wv_dram).then_inc(loaded, 16)
                sp.dma_start(bias[:, :], bias_dram.broadcast_to([P, nv])).then_inc(loaded, 16)
                sp.wait_ge(loaded, 32)

            @block.gpsimd
            def _(po):
                po.memset(v_all[:, :, :, :, 9:32], 0.0).then_inc(filled, 1)
                po.memset(v_all[:, :, :, :, 8:9], 1.0).then_inc(filled, 1)

            @block.tensor
            def _(pe):
                pe.wait_ge(loaded, 32)
                for i in range(4):
                    for k in range(4):
                        t = 4 * i + k
                        mm = pe.matmul(ps[i][:, k, :], xin[:, t * P:(t + 1) * P], w[:, :], start=True, stop=True)
                    mm.then_inc(product_ready, 1)

            @block.vector
            def _(ve):
                ve.wait_ge(loaded, 32)
                for t in range(16):
                    if t % 4 == 0:
                        ve.wait_ge(product_ready, t // 4 + 1)
                    b, kt = t // 8, t % 8
                    ve.tensor_tensor(v_all[:, b * 4:b * 4 + 4, kt, :, 0:8],
                                     ps[t // 4][:, t % 4, :].rearrange("p (g h e) -> p g h e", g=4, h=key_heads),
                                     bias[:, :].rearrange("p (g h e) -> p g h e", g=4, h=key_heads), ALU.add).then_inc(placed, 1)


def query_parts(nc, tag, kit, xin, w_dram, bias_dram, rows, slots, dest, rope_dram=None):
    nw = 2 if rope_dram is not None else 1
    with nc.cleanup_on_exit(), ExitStack() as ctx:
        sb = lambda name, shape, dt=F32: ctx.enter_context(nc.sbuf_tensor(f"{tag}_{name}", shape, dt))
        w = sb("w", [P, nw * rows])
        bias = sb("bias", [rows, 1])
        full = sb("full", [rows, T])
        rest = sb("rest", [rows, T])
        part = [sb(f"part{i}", [rows, T], BF16) for i in range(3)]
        rope = [sb(f"rope{i}", [rows, N]) for i in range(2)] if nw == 2 else []
        ps = [ctx.enter_context(nc.psum_tensor(f"{tag}_ps{s}", [rows, SL], F32)) for s in range(NS * nw)]
        sem = lambda name: nc.alloc_semaphore(f"{tag}_{name}")
        loaded, product_ready, whole, split, stored = (sem(n) for n in ("loaded", "product_ready", "whole", "split", "stored"))
        turned = sem("turned")
        loads = 1 + (2 if nw == 2 else 0) + (bias_dram is not None)
        with nc.Block() as block:

            @block.sync
            def _(sp):
                sp.dma_start(w[:, :], w_dram).then_inc(loaded, 16)
                if bias_dram is not None:
                    sp.dma_start(bias[:, :], bias_dram).then_inc(loaded, 16)
                for i, r in enumerate(rope):
                    sp.dma_start(r[:, :], rope_dram[i, 0:rows]).then_inc(loaded, 16)
                for i, p in enumerate(slots):
                    sp.wait_ge(split, (1, 3, 4)[p])
                    sp.dma_start(dest[:, i * E8:(i + 1) * E8, :, :].rearrange("b e h n -> (e h) b n"),
                                 part[p][:, :].rearrange("r (b n) -> r b n", b=2)).then_inc(stored, 16)
                sp.wait_ge(stored, 16 * len(slots))

            @block.tensor
            def _(pe):
                pe.wait_ge(loaded, 16 * loads)
                for k in range(nw):
                    for s in range(NS):
                        pe.matmul(ps[k * NS + s][:, :], w[:, k * rows:(k + 1) * rows], xin[:, s * SL:(s + 1) * SL],
                                  start=True, stop=True).then_inc(product_ready, 1)

            if nw == 1:
                @block.scalar
                def _(ac):
                    for s in range(NS):
                        ac.wait_ge(product_ready, s + 1)
                        if bias_dram is None:
                            ac.activation(full[:, s * SL:(s + 1) * SL], ps[s][:, :], ACT.Copy).then_inc(whole, 1)
                        else:
                            ac.activation(full[:, s * SL:(s + 1) * SL], ps[s][:, :], ACT.Identity, bias=bias[:, 0:1]).then_inc(whole, 1)

            @block.vector
            def _(ve):
                if nw == 2:
                    for s in range(NS):
                        ve.wait_ge(product_ready, NS + s + 1)
                        a, r = slice(s * SL, (s + 1) * SL), slice((s % 2) * SL, (s % 2 + 1) * SL)
                        ve.tensor_tensor(full[:, a], ps[s][:, :], rope[0][:, r], ALU.mult).then_inc(turned, 1)
                        ve.tensor_tensor(rest[:, a], ps[NS + s][:, :], rope[1][:, r], ALU.mult).then_inc(turned, 1)
                        ve.wait_ge(turned, 2 * s + 2)
                        ve.tensor_tensor(full[:, a], full[:, a], rest[:, a], ALU.add).then_inc(whole, 1)
                ve.wait_ge(whole, NS)
                ve.tensor_copy(part[0][:, :], full[:, :]).then_inc(split, 1)
                ve.wait_ge(split, 1)
                ve.tensor_tensor(rest[:, :], full[:, :], part[0][:, :], ALU.subtract).then_inc(split, 1)
                ve.wait_ge(split, 2)
                ve.tensor_copy(part[1][:, :], rest[:, :]).then_inc(split, 1)
                ve.wait_ge(split, 3)
                ve.tensor_tensor(part[2][:, :], rest[:, :], part[1][:, :], ALU.subtract).then_inc(split, 1)


def route(nc, tag, kit, xn, router_dram, bias_dram, experts, top, mode, gates, gate_dram, total, capacity=None, slots=None):
    E = experts
    tiles = T // P
    with nc.cleanup_on_exit(), ExitStack() as ctx:
        sb = lambda name, shape, dt=F32: ctx.enter_context(nc.sbuf_tensor(f"{tag}_{name}", shape, dt))
        w = sb("w", [P, E])
        bias = sb("bias", [P, E])
        p = sb("p", [P, tiles, E])
        big = [sb(f"big{i}", [P, tiles, E, E]) for i in range(2)]
        col = sb("col", [P, tiles])
        rank = sb("rank", [P, tiles, E])
        out = sb("out", [P, tiles, total])
        ps_l = ctx.enter_context(nc.psum_tensor(f"{tag}_l", [P, tiles, E], F32))
        ps_c = ctx.enter_context(nc.psum_tensor(f"{tag}_c", [P, tiles, E], F32))
        ps_t = [ctx.enter_context(nc.psum_tensor(f"{tag}_t{s}", [total, SL], F32)) for s in range(NS)]
        sem = lambda name: nc.alloc_semaphore(f"{tag}_{name}")
        loaded, logits_ready, shifted, exp_done, chain, gates_ready, turned, gates_in, stored = (sem(n) for n in (
            "loaded", "logits_ready", "shifted", "exp_done", "chain", "gates_ready", "turned", "gates_in", "stored"))
        chosen, counted, filled = sem("chosen"), sem("counted"), sem("filled")

        with nc.Block() as block:

            @block.sync
            def _(sp):
                sp.dma_start(w[:, :], router_dram).then_inc(loaded, 16)
                sp.dma_start(bias[:, :], bias_dram.broadcast_to([P, E])).then_inc(loaded, 16)
                if mode == "capacity":
                    sp.wait_ge(loaded, 32)
                else:
                    sp.wait_ge(gates_in, NS)
                    sp.dma_start(gate_dram, gates[0:total, :]).then_inc(stored, 16)
                    sp.wait_ge(stored, 16)

            @block.tensor
            def _(pe):
                pe.wait_ge(loaded, 32)
                for t in range(tiles):
                    mm = pe.matmul(ps_l[:, t, :], xn[:, t * P:(t + 1) * P], w[:, :], start=True, stop=True)
                mm.then_inc(logits_ready, 1)
                if mode == "capacity":
                    pe.wait_ge(chosen, 1)
                    pe.matmul(ps_c[:, :, :], kit.upto[:, :], rank[:, :, :], start=True, stop=False, skip_group_check=True)
                    for t in range(tiles - 1):
                        mm = pe.matmul(ps_c[:, t + 1:, :], kit.ones[:, :],
                                       rank[:, t, :].unsqueeze(1).broadcast_to([P, tiles - 1 - t, E]), start=False,
                                       stop=t == tiles - 2, skip_group_check=True)
                    mm.then_inc(counted, 1)
                    return
                pe.wait_ge(gates_ready, 1)
                for s in range(NS):
                    for k in range(4):
                        mm = pe.transpose(ps_t[s][:, k * P:(k + 1) * P], out[:, 4 * s + k, :], kit.ident[:, :])
                    mm.then_inc(turned, 1)

            @block.scalar
            def _(ac):
                ac.wait_ge(shifted, 1)
                ac.activation(p[:, :, :], p[:, :, :], ACT.Exp).then_inc(exp_done, 1)
                for s in range(NS if mode != "capacity" else 0):
                    ac.wait_ge(turned, s + 1)
                    ac.activation(gates[0:total, s * SL:(s + 1) * SL], ps_t[s][:, :], ACT.Copy).then_inc(gates_in, 1)

            @block.vector
            def _(ve):
                done = [0]

                def link(ins):
                    done[0] += 1
                    ins.then_inc(chain, 1)
                    ve.wait_ge(chain, done[0])

                def across(a):
                    return a.unsqueeze(2).broadcast_to([P, tiles, E])

                ve.wait_ge(loaded, 32)
                ve.wait_ge(logits_ready, 1)
                link(ve.tensor_tensor(p[:, :, :], ps_l[:, :, :], bias[:, :].unsqueeze(1).broadcast_to([P, tiles, E]), ALU.add))
                link(ve.tensor_reduce(col[:, :], p[:, :, :], AX.X, ALU.max))
                ve.tensor_tensor(p[:, :, :], p[:, :, :], across(col[:, :]), ALU.subtract).then_inc(shifted, 1)
                ve.wait_ge(exp_done, 1)
                link(ve.tensor_reduce(col[:, :], p[:, :, :], AX.X, ALU.add))
                link(ve.reciprocal(col[:, :], col[:, :]))
                link(ve.tensor_tensor(p[:, :, :], p[:, :, :], across(col[:, :]), ALU.mult))
                other = p[:, :, :].unsqueeze(2).broadcast_to([P, tiles, E, E])
                own = p[:, :, :].unsqueeze(3).broadcast_to([P, tiles, E, E])
                ve.tensor_tensor(big[0][:, :, :, :], other, own, ALU.is_gt).then_inc(filled, 1)
                link(ve.tensor_tensor(big[1][:, :, :, :], other, own, ALU.is_equal))
                lower = kit.lower[:, :, :][:, 0:E, 0:E].unsqueeze(1).broadcast_to([P, tiles, E, E])
                link(ve.tensor_tensor(big[1][:, :, :, :], big[1][:, :, :, :], lower, ALU.mult))
                ve.wait_ge(filled, 1)
                link(ve.tensor_tensor(big[0][:, :, :, :], big[0][:, :, :, :], big[1][:, :, :, :], ALU.add))
                link(ve.tensor_reduce(rank[:, :, :], big[0][:, :, :, :], AX.X, ALU.add))
                link(ve.tensor_scalar(rank[:, :, :], rank[:, :, :], top - 0.5, None, ALU.is_lt))
                if mode == "capacity":
                    ve.sem_inc(chosen, 1)
                    ve.wait_ge(counted, 1)
                    link(ve.tensor_scalar(p[:, :, :], ps_c[:, :, :], capacity + 0.5, None, ALU.is_lt))
                    link(ve.tensor_tensor(p[:, :, :], p[:, :, :], rank[:, :, :], ALU.mult))
                    link(ve.tensor_tensor(rank[:, :, :], ps_c[:, :, :], kit.numbers[:, 0:E].unsqueeze(1).broadcast_to([P, tiles, E]), ALU.add))
                    link(ve.tensor_tensor(rank[:, :, :], rank[:, :, :], p[:, :, :], ALU.mult))
                    link(ve.tensor_reduce(col[:, :], p[:, :, :], AX.X, ALU.add))
                    link(ve.tensor_scalar(col[:, :], col[:, :], -1.0, 1.0, ALU.mult, ALU.add))
                    link(ve.tensor_tensor(col[:, :], col[:, :], kit.numbers[:, E:E + tiles], ALU.mult))
                    link(ve.tensor_reduce(out[:, :, 0:1], rank[:, :, :], AX.X, ALU.add))
                    link(ve.tensor_tensor(col[:, :], col[:, :], out[:, :, 0], ALU.add))
                    ve.tensor_copy(slots[:, :], col[:, :]).then_inc(gates_ready, 1)
                elif mode == "share":
                    link(ve.tensor_tensor(p[:, :, :], p[:, :, :], rank[:, :, :], ALU.mult))
                    link(ve.tensor_reduce(col[:, :], p[:, :, :], AX.X, ALU.add))
                    link(ve.reciprocal(col[:, :], col[:, :]))
                    ve.tensor_tensor(out[:, :, :], p[:, :, :], across(col[:, :]), ALU.mult).then_inc(gates_ready, 1)
                else:
                    link(ve.memset(out[:, :, E:E + 1], 1.0))
                    ve.tensor_tensor(out[:, :, 0:E], p[:, :, :], rank[:, :, :], ALU.mult).then_inc(gates_ready, 1)


def residual(nc, tag, x, s_out, result, plus=None):
    with nc.cleanup_on_exit(), ExitStack() as ctx:
        sem = lambda name: nc.alloc_semaphore(f"{tag}_{name}")
        complete, silu_done, multiplied, updated = (sem(n) for n in ("complete", "silu_done", "multiplied", "updated"))
        with nc.Block() as block:

            @block.scalar
            def _(ac):
                for s in range(NS):
                    part = slice(s * SL, (s + 1) * SL)
                    if plus is not None:
                        ac.wait_ge(complete, s + 1)
                    ac.activation(result[:, part], result[:, part], ACT.Silu).then_inc(silu_done, 1)

            @block.vector
            def _(ve):
                for s in range(NS if plus is not None else 0):
                    part = slice(s * SL, (s + 1) * SL)
                    ve.tensor_tensor(result[:, part], result[:, part], plus[:, part], ALU.add).then_inc(complete, 1)
                for s in range(NS):
                    part = slice(s * SL, (s + 1) * SL)
                    ve.wait_ge(silu_done, s + 1)
                    ve.tensor_tensor(s_out[:, part], s_out[:, part], result[:, part], ALU.mult).then_inc(multiplied, 1)
                    ve.wait_ge(multiplied, s + 1)
                    ve.tensor_tensor(x[:, part], x[:, part], s_out[:, part], ALU.add).then_inc(updated, 1)


def add_to(nc, tag, a, b, out):
    with nc.cleanup_on_exit():
        added = nc.alloc_semaphore(f"{tag}_added")
        with nc.Block() as block:

            @block.vector
            def _(ve):
                for s in range(NS):
                    part = slice(s * SL, (s + 1) * SL)
                    ve.tensor_tensor(out[:, part], a[:, part], b[:, part], ALU.add).then_inc(added, 1)


def linear_attention(nc, tag, kit, xin, w_dram, cols_dram, v_all, out_all):
    chunks = N // P
    with nc.cleanup_on_exit(), ExitStack() as ctx:
        sb = lambda name, shape, dt=F32: ctx.enter_context(nc.sbuf_tensor(f"{tag}_{name}", shape, dt))
        w = sb("w", [P, 2, P])
        cols = sb("cols", [P, 2])
        qk = [sb(f"qk{i}", [P, T]) for i in range(2)]
        low = sb("low", [P, T])
        qm = [sb(f"qm{i}", [P, 4, P]) for i in range(2)]
        a_sb = [sb(f"weights{i}", [P, 4, 4, P]) for i in range(2)]
        ktok = [sb(f"ktok{i}", [P, P]) for i in range(2)]
        state = [sb(f"state{i}", [P, 4, P]) for i in range(2)]
        upd = sb("upd", [P, 4, P])
        ps_a = [ctx.enter_context(nc.psum_tensor(f"{tag}_a{g}", [P, 4, P], F32)) for g in range(4)]
        ps_o = [ctx.enter_context(nc.psum_tensor(f"{tag}_o{i}", [P, 4, P], F32)) for i in range(2)]
        ps_u = ctx.enter_context(nc.psum_tensor(f"{tag}_u", [P, 4, P], F32))
        ps_k = ctx.enter_context(nc.psum_tensor(f"{tag}_k", [P, P], F32))
        sem = lambda name: nc.alloc_semaphore(f"{tag}_{name}")
        loaded, product_ready, biased, clipped, exp_done, feature = (sem(n) for n in (
            "loaded", "product_ready", "biased", "clipped", "exp_done", "feature"))
        split_ready, a_ready, masked, turned, ktok_in, num_ready, num_in, u_ready, state_ready = (
            sem(n) for n in ("split_ready", "a_ready", "masked", "turned", "ktok_in", "num_ready", "num_in",
                             "u_ready", "state_ready"))
        clipped_high, updated = sem("clipped_high"), sem("updated")
        last = 2 * chunks - 1
        with nc.Block() as block:

            @block.sync
            def _(sp):
                sp.dma_start(w[:, :, :], w_dram).then_inc(loaded, 16)
                sp.dma_start(cols[:, :], cols_dram).then_inc(loaded, 16)
                sp.wait_ge(loaded, 32)

            @block.tensor
            def _(pe):
                pe.wait_ge(loaded, 32)
                for k in range(2):
                    for s in range(NS):
                        if k:
                            pe.wait_ge(biased, s + 1)
                        pe.matmul(ps_a[s][:, :, :], w[:, k, :], xin[:, s * SL:(s + 1) * SL], start=True, stop=True).then_inc(product_ready, 1)
                pe.wait_ge(feature, 2)

                def scores(t):
                    tok = slice(t * P, (t + 1) * P)
                    pe.wait_ge(split_ready, t + 1)
                    if t:
                        pe.wait_ge(masked, t)
                    for g in range(4):
                        r = slice(32 * g, 32 * g + 32)
                        mm = pe.matmul(ps_a[g][:, :, :], qk[1][r, tok], qm[t % 2][r, :, :], start=True, stop=True, tile_position=(32 * g, 0))
                    mm.then_inc(a_ready, 1)
                    if t:
                        pe.wait_ge(ktok_in, t)
                    pe.transpose(ps_k[:, :], qk[1][:, tok], kit.ident[:, :]).then_inc(turned, 1)

                scores(0)
                for t in range(last + 1):
                    b, kt = t // chunks, t % chunks
                    tok = slice(t * P, (t + 1) * P)
                    if t < last:
                        scores(t + 1)
                    pe.wait_ge(ktok_in, t + 1)
                    if t:
                        pe.wait_ge(updated, t)
                    pe.matmul(ps_u[:, :, :], ktok[t % 2][:, :], v_all[:, b * 4:b * 4 + 4, kt, :, :].rearrange("p g h c -> p g (h c)"),
                              start=True, stop=True).then_inc(u_ready, 1)
                    pe.wait_ge(masked, t + 1)
                    pe.wait_ge(state_ready, t + 1)
                    if t >= 2:
                        pe.wait_ge(num_in, t - 1)
                    for g in range(4):
                        pe.matmul(ps_o[t % 2][:, g, :], state[t % 2][:, g, :], qk[0][:, tok], start=True, stop=False, skip_group_check=True)
                        for j in range(4):
                            mm = pe.matmul(ps_o[t % 2][32 * j:32 * j + 32, g, :], v_all[:, b * 4 + g, kt, j, :], a_sb[t % 2][:, g, j, :],
                                           start=False, stop=True, skip_group_check=True)
                    mm.then_inc(num_ready, 1)

            @block.scalar
            def _(ac):
                ac.wait_ge(loaded, 32)
                for k in range(2):
                    for s in range(NS):
                        ac.wait_ge(product_ready, k * NS + s + 1)
                        ac.activation(qk[k][:, s * SL:(s + 1) * SL], ps_a[s][:, :, :].rearrange("p a n -> p (a n)"), ACT.Identity,
                                      bias=cols[:, k:k + 1]).then_inc(biased, 1)
                for k in range(2):
                    ac.wait_ge(clipped, k + 1)
                    ac.activation(low[:, :], low[:, :], ACT.Exp).then_inc(exp_done, 1)
                for t in range(last + 2):
                    if t <= last:
                        ac.wait_ge(turned, t + 1)
                        if t >= 2:
                            ac.wait_ge(u_ready, t - 1)
                        ac.activation(ktok[t % 2][:, :], ps_k[:, :], ACT.Copy).then_inc(ktok_in, 1)
                    if t:
                        b, kt = (t - 1) // chunks, (t - 1) % chunks
                        ac.wait_ge(num_ready, t)
                        ac.activation(out_all[:, b * 4:b * 4 + 4, kt * P:(kt + 1) * P], ps_o[(t - 1) % 2][:, :, :], ACT.Copy).then_inc(num_in, 1)

            @block.vector
            def _(ve):
                for k in range(2):
                    ve.wait_ge(biased, NS * (k + 1))
                    if k:
                        ve.wait_ge(feature, 1)
                    ve.tensor_scalar(low[:, :], qk[k][:, :], 0.0, E8 ** -0.5 if k == 0 else 1.0, ALU.min, ALU.mult).then_inc(clipped, 1)
                    ve.wait_ge(clipped, k + 1)
                    ve.tensor_scalar(qk[k][:, :], qk[k][:, :], 0.0, E8 ** -0.5 if k == 0 else 1.0, ALU.max, ALU.mult).then_inc(clipped_high, 1)
                    ve.wait_ge(exp_done, k + 1)
                    ve.wait_ge(clipped_high, k + 1)
                    ve.scalar_tensor_tensor(qk[k][:, :], low[:, :], 1.0001 - 1.0, qk[k][:, :], ALU.add, ALU.add).then_inc(feature, 1)
                ve.wait_ge(feature, 2)

                def split(t):
                    ve.tensor_tensor(qm[t % 2][:, :, :], qk[0][:, t * P:(t + 1) * P].unsqueeze(1).broadcast_to([P, 4, P]),
                                     kit.head4[:, :].unsqueeze(2).broadcast_to([P, 4, P]), ALU.mult).then_inc(split_ready, 1)

                split(0)
                split(1)
                ve.memset(state[0][:, :, :], 0.0).then_inc(state_ready, 1)
                for t in range(last + 1):
                    ve.wait_ge(a_ready, t + 1)
                    if t >= 2:
                        ve.wait_ge(num_ready, t - 1)
                    for g in range(4):
                        mk = ve.tensor_tensor(a_sb[t % 2][:, g, :, :], ps_a[g][:, :, :], kit.upto[:, :].unsqueeze(1).broadcast_to([P, 4, P]), ALU.mult)
                    mk.then_inc(masked, 1)
                    if t + 2 <= last:
                        split(t + 2)
                    ve.wait_ge(u_ready, t + 1)
                    if t < last:
                        if t:
                            ve.wait_ge(num_ready, t)
                        if t % chunks == chunks - 1:
                            ve.sem_inc(updated, 1)
                            ve.memset(state[(t + 1) % 2][:, :, :], 0.0).then_inc(state_ready, 1)
                        else:
                            ve.tensor_tensor(upd[:, :, :], ps_u[:, :, :], kit.blocks[:, :, :], ALU.mult).then_inc(updated, 1)
                            ve.wait_ge(updated, t + 1)
                            ve.wait_ge(state_ready, t + 1)
                            ve.tensor_tensor(state[(t + 1) % 2][:, :, :], state[t % 2][:, :, :], upd[:, :, :], ALU.add).then_inc(state_ready, 1)


def mixture(nc, tag, xn, gates, w1_dram, w2_dram, b2_dram, gate_dram, result, experts, chunks, act,
            act_scale=1.0, group=2, gated_unit=False):
    step_count = group * NS * chunks
    ring = 2 if gated_unit else 4
    lag = 1 if gated_unit else 2
    kinds = 2 if gated_unit else 1
    turns = experts // group
    F = chunks * P
    with nc.cleanup_on_exit(), ExitStack() as ctx:
        sb = lambda name, shape, dt=F32: ctx.enter_context(nc.sbuf_tensor(f"{tag}_{name}", shape, dt))
        w1 = [sb(f"w1_{u}", [P, kinds * F + (0 if gated_unit else chunks)]) for u in range(group)]
        w2 = [sb(f"w2_{u}", [P, F]) for u in range(group)]
        gate = [sb(f"gate_{u}", [P, T]) for u in range(group)]
        b2 = sb("b2", [experts, P])
        hidden = sb("hidden", [P, ring, SL])
        ps_h = [ctx.enter_context(nc.psum_tensor(f"{tag}_psh{r}", [P, SL], F32)) for r in range(4)]
        ps_o = [ctx.enter_context(nc.psum_tensor(f"{tag}_pso{s}", [P, SL], F32)) for s in range(NS)]
        sem = lambda name: nc.alloc_semaphore(f"{tag}_{name}")
        expert_in = [sem(f"expert_in{u}") for u in range(group)]
        b2_in = sem("b2_in")
        scaled = sem("scaled")
        h_ready = sem("h_ready")
        act_done = sem("act_done")
        lifted = sem("lifted")
        gated = sem("gated")
        added = sem("added")
        evacuated = sem("evacuated")
        passed = sem("passed")
        steps = [(u, s, c) for u in range(group) for s in range(NS) for c in range(chunks)]
        per = NS * chunks
        with nc.Block() as block:

            def load(sp, u, e):
                sp.dma_start(w1[u][:, :], w1_dram[bass.ds(e, 1), :, :].rearrange("e p n -> (e p) n")).then_inc(expert_in[u], 16)
                sp.dma_start(w2[u][:, :], w2_dram[bass.ds(e, 1), :, :].rearrange("e p n -> (e p) n")).then_inc(expert_in[u], 16)
                sp.dma_start(gate[u][:, :], gate_dram[bass.ds(e, 1), :].broadcast_to([P, T])).then_inc(expert_in[u], 16)

            @block.sync
            def _(sp):
                sp.dma_start(b2[:, :], b2_dram).then_inc(b2_in, 16)
                for u in range(group):
                    load(sp, u, u)
                if turns > 1:
                    with sp.Fori(0, turns - 1) as it:
                        for u in range(group):
                            sp.wait_ge(added, it * step_count + ((u + 1) * per + 1))
                            load(sp, u, it * group + (u + group))
                sp.wait_ge(b2_in, 16)
                for u in range(group):
                    sp.wait_ge(expert_in[u], 48 * turns)

            @block.tensor
            def _(pe):
                pe.wait_ge(b2_in, 16)
                for s in range(NS):
                    mm = pe.matmul(ps_o[s][:, :], b2[:, :], gates[0:experts, s * SL:(s + 1) * SL], start=True, stop=False, skip_group_check=True)
                mm.then_inc(added, 1)
                with pe.Fori(0, turns) as it:
                    for k in range(step_count + lag):
                        if k < step_count:
                            u, s, c = steps[k]
                            if s == 0 and c == 0:
                                pe.wait_ge(expert_in[u], it * 48 + 48)
                            if k >= ring:
                                pe.wait_ge(lifted if gated_unit else act_done, it * step_count + (k - ring + 1))
                            elif gated_unit:
                                pe.wait_ge(added, it * step_count + 1)
                            for m in range(kinds):
                                mm = pe.matmul(ps_h[(k % ring) * kinds + m][:, :], w1[u][:, m * F + c * P:m * F + (c + 1) * P],
                                               xn[:, s * SL:(s + 1) * SL], start=True, stop=True)
                            mm.then_inc(h_ready, 1)
                        if k >= lag:
                            u, s, c = steps[k - lag]
                            pe.wait_ge(gated, it * step_count + (k - lag + 1))
                            pe.matmul(ps_o[s][:, :], w2[u][:, c * P:(c + 1) * P], hidden[:, (k - lag) % ring, :],
                                      start=False, stop=False, skip_group_check=True).then_inc(added, 1)

            @block.scalar
            def _(ac):
                with ac.Fori(0, turns) as it:
                    for k, (u, s, c) in enumerate(steps):
                        ac.wait_ge(h_ready, it * step_count + (k + 1))
                        if act_scale != 1.0 and s == 0 and c == 0:
                            ac.wait_ge(scaled, it * (2 * group) + (2 * u + 1))
                        ac.wait_ge(added, it * step_count + (max(k - ring + 1, 0) + 1))
                        out, src = hidden[:, k % ring, :], ps_h[(k % ring) * kinds][:, :]
                        if gated_unit:
                            ac.activation(out, src, act).then_inc(act_done, 1)
                        else:
                            ac.activation(out, src, act, bias=w1[u][:, F + c:F + c + 1], scale=act_scale).then_inc(act_done, 1)

            if act_scale != 1.0:
                @block.gpsimd
                def _(po):
                    with po.Fori(0, turns) as it:
                        for u in range(group):
                            po.wait_ge(expert_in[u], it * 48 + 48)
                            po.sem_inc(passed, 1)
                            po.tensor_scalar(w1[u][:, F:F + chunks], w1[u][:, F:F + chunks], act_scale, None, ALU.mult).then_inc(scaled, 1)
                            po.tensor_scalar(gate[u][:, :], gate[u][:, :], 1.0 / act_scale, None, ALU.mult).then_inc(scaled, 1)

            @block.vector
            def _(ve):
                with ve.Fori(0, turns) as it:
                    for k, (u, s, c) in enumerate(steps):
                        ve.wait_ge(act_done, it * step_count + (k + 1))
                        if act_scale != 1.0 and s == 0 and c == 0:
                            ve.wait_ge(scaled, it * (2 * group) + (2 * u + 2))
                        part = hidden[:, k % ring, :]
                        if gated_unit:
                            ve.tensor_tensor(part, ps_h[(k % ring) * kinds + 1][:, :], part, ALU.mult).then_inc(lifted, 1)
                            ve.wait_ge(lifted, it * step_count + (k + 1))
                        ve.tensor_tensor(part, part, gate[u][:, s * SL:(s + 1) * SL], ALU.mult).then_inc(gated, 1)
                ve.wait_ge(added, turns * step_count + 1)
                for s in range(NS):
                    ve.tensor_copy(result[:, s * SL:(s + 1) * SL], ps_o[s][:, :]).then_inc(evacuated, 1)


def slot_rows(dram, first):
    return dram[first:first + T, :].rearrange("(t p) f -> p t f", p=P)


def send_tokens(nc, tag, kit, xn, slots, x_rows, y_rows, x_slots):
    tiles = T // P
    with nc.cleanup_on_exit(), ExitStack() as ctx:
        by_token = ctx.enter_context(nc.sbuf_tensor(f"{tag}_token", [P, tiles, P], F32))
        by_slot = ctx.enter_context(nc.sbuf_tensor(f"{tag}_slot", [P, tiles, P], F32))
        ps = [ctx.enter_context(nc.psum_tensor(f"{tag}_ps{i}", [P, SL], F32)) for i in range(8)]
        sem = lambda name: nc.alloc_semaphore(f"{tag}_{name}")
        zeroed, emptied, turned, copied, kept, sent, back, turned_slots, placed = (sem(n) for n in (
            "zeroed", "emptied", "turned", "copied", "kept", "sent", "back", "turned_slots", "placed"))
        with nc.Block() as block:

            @block.vector
            def _(ve):
                ve.memset(by_slot[:, :, :], 0.0).then_inc(zeroed, 1)

            @block.sync
            def _(sp):
                sp.wait_ge(zeroed, 1)
                sp.dma_start(slot_rows(x_rows, 0), by_slot[:, :, :]).then_inc(emptied, 16)
                sp.wait_ge(copied, 4)
                sp.dma_start(slot_rows(y_rows, T), by_token[:, :, :]).then_inc(kept, 16)
                sp.wait_ge(emptied, 16)
                sp.wait_ge(sent, 16 * tiles)
                sp.dma_start(by_slot[:, :, :], slot_rows(x_rows, 0)).then_inc(back, 16)
                sp.wait_ge(kept, 16)
                sp.wait_ge(back, 16)

            @block.gpsimd
            def _(po):
                po.wait_ge(emptied, 16)
                for t in range(tiles):
                    if t % 4 == 0:
                        po.wait_ge(copied, t // 4 + 1)
                    po.indirect_dma_start(x_rows, bass.IndirectOffsetOnAxis(ap=slots[:, t:t + 1], axis=0),
                                          by_token[:, t, :], None).then_inc(sent, 16)
                po.wait_ge(sent, 16 * tiles)

            @block.tensor
            def _(pe):
                for s in range(4):
                    for k in range(4):
                        t = 4 * s + k
                        mm = pe.transpose(ps[s][:, k * P:(k + 1) * P], xn[:, t * P:(t + 1) * P], kit.ident[:, :])
                    mm.then_inc(turned, 1)
                pe.wait_ge(back, 16)
                for s in range(4):
                    for k in range(4):
                        mm = pe.transpose(ps[4 + s][:, k * P:(k + 1) * P], by_slot[:, 4 * s + k, :], kit.ident[:, :])
                    mm.then_inc(turned_slots, 1)

            @block.scalar
            def _(ac):
                for s in range(4):
                    ac.wait_ge(turned, s + 1)
                    ac.activation(by_token[:, 4 * s:4 * s + 4, :].rearrange("p t f -> p (t f)"), ps[s][:, :], ACT.Copy).then_inc(copied, 1)
                for s in range(4):
                    ac.wait_ge(turned_slots, s + 1)
                    ac.activation(x_slots[:, s * SL:(s + 1) * SL], ps[4 + s][:, :], ACT.Copy).then_inc(placed, 1)


def slot_experts(nc, tag, x_slots, w1_dram, w2_dram, y_slots, experts, chunks, act, act_scale):
    F = chunks * P
    cap = T // experts
    group, ring, lag = 2, 4, 2
    turns = experts // group
    n = group * chunks
    with nc.cleanup_on_exit(), ExitStack() as ctx:
        sb = lambda name, shape: ctx.enter_context(nc.sbuf_tensor(f"{tag}_{name}", shape, F32))
        w1 = [sb(f"w1_{u}", [P, F + chunks + 1]) for u in range(group)]
        w2 = [sb(f"w2_{u}", [P, F]) for u in range(group)]
        hidden = sb("hidden", [P, ring, cap])
        ps_h = [ctx.enter_context(nc.psum_tensor(f"{tag}_h{r}", [P, cap], F32)) for r in range(ring)]
        ps_o = [ctx.enter_context(nc.psum_tensor(f"{tag}_o{u}", [P, cap], F32)) for u in range(group)]
        sem = lambda name: nc.alloc_semaphore(f"{tag}_{name}")
        expert_in = [sem(f"expert_in{u}") for u in range(group)]
        scaled, passed, h_ready, act_done, added = (sem(x) for x in ("scaled", "passed", "h_ready", "act_done", "added"))
        finished = sem("finished")
        with nc.Block() as block:

            def load(sp, u, e):
                sp.dma_start(w1[u][:, :], w1_dram[bass.ds(e, 1), :, :].rearrange("e p n -> (e p) n")).then_inc(expert_in[u], 16)
                sp.dma_start(w2[u][:, :], w2_dram[bass.ds(e, 1), :, :].rearrange("e p n -> (e p) n")).then_inc(expert_in[u], 16)

            @block.sync
            def _(sp):
                for u in range(group):
                    load(sp, u, u)
                with sp.Fori(0, turns - 1) as it:
                    for u in range(group):
                        sp.wait_ge(finished, it * group + (u + 1 + 2))
                        load(sp, u, it * group + (u + group))
                for u in range(group):
                    sp.wait_ge(expert_in[u], 32 * turns)

            @block.gpsimd
            def _(po):
                with po.Fori(0, turns) as it:
                    for u in range(group):
                        po.wait_ge(expert_in[u], it * 32 + 32)
                        po.sem_inc(passed, 1)
                        po.tensor_scalar(w1[u][:, F:F + chunks], w1[u][:, F:F + chunks], act_scale, None, ALU.mult).then_inc(scaled, 1)

            @block.tensor
            def _(pe):
                with pe.Fori(0, turns) as it:
                    for k in range(n + lag):
                        if k < n:
                            u, c = k // chunks, k % chunks
                            if c == 0:
                                pe.wait_ge(expert_in[u], it * 32 + 32)
                            if k >= ring:
                                pe.wait_ge(act_done, it * n + (k - ring + 1))
                            pe.matmul(ps_h[k % ring][:, :], w1[u][:, c * P:(c + 1) * P],
                                      x_slots[:, bass.ds((it * group + u) * cap, cap)], start=True, stop=True).then_inc(h_ready, 1)
                        if k >= lag:
                            m = k - lag
                            u, c = m // chunks, m % chunks
                            if c == 0:
                                pe.wait_ge(finished, it * group + (u + 1))
                            pe.wait_ge(act_done, it * n + (m + 1))
                            pe.matmul(ps_o[u][:, :], w2[u][:, c * P:(c + 1) * P], hidden[:, m % ring, :],
                                      start=c == 0, stop=c == chunks - 1).then_inc(added, 1)

            @block.scalar
            def _(ac):
                with ac.Fori(0, turns) as it:
                    for k in range(n):
                        u, c = k // chunks, k % chunks
                        ac.wait_ge(h_ready, it * n + (k + 1))
                        if c == 0:
                            ac.wait_ge(scaled, it * group + (u + 1))
                        if k >= ring:
                            ac.wait_ge(added, it * n + (k - ring + 1))
                        ac.activation(hidden[:, k % ring, :], ps_h[k % ring][:, :], act, bias=w1[u][:, F + c:F + c + 1],
                                      scale=act_scale).then_inc(act_done, 1)

            @block.vector
            def _(ve):
                ve.sem_inc(finished, 2)
                with ve.Fori(0, turns) as it:
                    for u in range(group):
                        ve.wait_ge(added, it * n + (u + 1) * chunks)
                        ve.tensor_scalar(y_slots[:, bass.ds((it * group + u) * cap, cap)], ps_o[u][:, :], 1.0 / act_scale,
                                         w1[u][:, F + chunks:F + chunks + 1], ALU.mult, ALU.add).then_inc(finished, 1)


def fetch_results(nc, tag, kit, y_slots, slots, y_rows, result):
    tiles = T // P
    with nc.cleanup_on_exit(), ExitStack() as ctx:
        by_slot = ctx.enter_context(nc.sbuf_tensor(f"{tag}_slot", [P, tiles, P], F32))
        by_token = ctx.enter_context(nc.sbuf_tensor(f"{tag}_token", [P, tiles, P], F32))
        ps = [ctx.enter_context(nc.psum_tensor(f"{tag}_ps{i}", [P, SL], F32)) for i in range(8)]
        sem = lambda name: nc.alloc_semaphore(f"{tag}_{name}")
        turned, copied, stored, turned_tokens, placed = (sem(n) for n in ("turned", "copied", "stored", "turned_tokens", "placed"))
        fetched = [sem(f"fetched{i}") for i in range(4)]
        with nc.Block() as block:

            @block.sync
            def _(sp):
                sp.wait_ge(copied, 4)
                sp.dma_start(slot_rows(y_rows, 0), by_slot[:, :, :]).then_inc(stored, 16)
                sp.wait_ge(stored, 16)

            @block.gpsimd
            def _(po):
                po.wait_ge(stored, 16)
                for t in range(tiles):
                    po.indirect_dma_start(by_token[:, t, :], None, y_rows,
                                          bass.IndirectOffsetOnAxis(ap=slots[:, t:t + 1], axis=0)).then_inc(fetched[t // 4], 16)
                for i in range(4):
                    po.wait_ge(fetched[i], 64)

            @block.tensor
            def _(pe):
                for s in range(4):
                    for k in range(4):
                        t = 4 * s + k
                        mm = pe.transpose(ps[s][:, k * P:(k + 1) * P], y_slots[:, t * P:(t + 1) * P], kit.ident[:, :])
                    mm.then_inc(turned, 1)
                for s in range(4):
                    pe.wait_ge(fetched[s], 64)
                    for k in range(4):
                        mm = pe.transpose(ps[4 + s][:, k * P:(k + 1) * P], by_token[:, 4 * s + k, :], kit.ident[:, :])
                    mm.then_inc(turned_tokens, 1)

            @block.scalar
            def _(ac):
                for s in range(4):
                    ac.wait_ge(turned, s + 1)
                    ac.activation(by_slot[:, 4 * s:4 * s + 4, :].rearrange("p t f -> p (t f)"), ps[s][:, :], ACT.Copy).then_inc(copied, 1)
                for s in range(4):
                    ac.wait_ge(turned_tokens, s + 1)
                    ac.activation(result[:, s * SL:(s + 1) * SL], ps[4 + s][:, :], ACT.Copy).then_inc(placed, 1)


GH = 4
E8 = 8
ROWS = 48
PARTS_Q = (0, 0, 1, 1, 0, 2)
PARTS_K = (0, 1, 0, 1, 2, 0)


def score_steps(mode):
    out = []
    for s in range(N // SL):
        if mode == "full":
            out += [(s, kt, 0, SL, None) for kt in range(8)]
        elif mode == "causal":
            for kt in range(4 * (s + 1)):
                off = max(0, kt * P - s * SL)
                out.append((s, kt, off, SL - off, (0, P) if kt >= 4 * s else None))
        else:
            for kt in range(max(0, 4 * s - 1), 4 * s + 4):
                if kt == 4 * s - 1:
                    out.append((s, kt, 0, P, (P, P)))
                elif kt == 4 * s + 3:
                    out.append((s, kt, kt * P - s * SL, P, (0, P)))
                else:
                    out.append((s, kt, kt * P - s * SL, 2 * P, (0, 2 * P)))
    return out


def max_uses(mode):
    out = []
    for h in range(GH):
        for qt in range(8):
            if mode == "full":
                out += [[(h, qt, c * SL, SL, None, c)] for c in range(2)]
            elif mode == "causal":
                keys = (qt + 1) * P
                for c in range((keys + SL - 1) // SL):
                    n = min(SL, keys - c * SL)
                    last = (c + 1) * SL >= keys
                    out.append([(h, qt, c * SL, n, (P, P) if last else None, c)])
    if mode == "window":
        for h in range(GH):
            for qt in range(0, 8, 2):
                out.append([(h, q, max(0, q - 1) * P, P if q == 0 else 2 * P, (P, P) if q == 0 else (0, 2 * P), 0)
                            for q in (qt, qt + 1)])
    return out


def attend(nc, tag, mode, scale, q_dram, k_dram, v_all, key_heads, out_all, kit, slots=4):
    groups = 8
    nparts = 1 if mode == "window" else 2
    hw = 4 if mode == "window" else 2
    width = 1024 // hw
    steps = score_steps(mode)
    uses = max_uses(mode)
    blocks = GH // hw
    nst = len(steps)
    nexp = nst * blocks
    small = len(uses) + 1
    start = len(uses) + 1
    slice_end = [max(k for k, st in enumerate(steps) if st[0] == s) for s in range(2)]
    spread = max(1, int(nst * 0.85))
    plan, given = [], 0
    for k in range(nst):
        upto = min(len(uses), (len(uses) * (k + 1) + spread - 1) // spread)
        row = [("max", i) for i in range(given, upto)]
        given = upto
        if k == spread:
            row.append(("turn", 0))
        plan.append(row)
    order = [x for row in plan for x in row]
    turn_at = order.index(("turn", 0))
    assert len(order) == small

    with nc.cleanup_on_exit(), ExitStack() as ctx:
        sb = lambda name, shape, dt=F32: ctx.enter_context(nc.sbuf_tensor(f"{tag}_{name}", shape, dt))
        sem = lambda name: nc.alloc_semaphore(f"{tag}_{name}")
        qst = [sb(f"qst{u}", [P, GH * N], BF16) for u in range(slots)]
        kst = [sb(f"kst{u}", [P, key_heads, N], BF16) for u in range(slots)]
        val = [sb(f"val{u}", [P, 8, key_heads, 32]) for u in range(slots)]
        prob = [sb(f"prob{r}", [P, GH, width]) for r in range(2)]
        mpart = sb("mpart", [P, GH * 8, nparts])
        mcol = sb("mcol", [P, GH * 8])
        mhl = sb("mhl", [GH * 8, 2, P], BF16)
        ps_st = [ctx.enter_context(nc.psum_tensor(f"{tag}_st{r}", [P, hw, width], F32)) for r in range(2)]
        ps_o = ctx.enter_context(nc.psum_tensor(f"{tag}_o", [P, SL], F32))
        ps_s = [ctx.enter_context(nc.psum_tensor(f"{tag}_s{r}", [P, SL], F32)) for r in range(3)]
        cleared = [sem(f"cleared{u}") for u in range(slots)]
        staged = [sem(f"staged{u}") for u in range(slots)]
        shift_in = [sem(f"shift_in{u}") for u in range(slots)]
        small_ready = sem("small_ready")
        small_free = sem("small_free")
        hi_done = sem("hi_done")
        column_done = sem("column_done")
        scores_ready = sem("scores_ready")
        probs_ready = sem("probs_ready")
        probs_used = sem("probs_used")
        o_copied = sem("o_copied")

        def small_of(it, u, n):
            return it * (slots * small) + (start + u * small + n)

        def small_bank(pe, it, u, n):
            pe.wait_ge(small_free, small_of(it, u, n - 2 if n >= 3 else 0))
            return n % 3

        def steps_of(it, u, k):
            return it * (slots * nst) + (u * nst + k)

        def exps_of(it, u, e):
            return it * (slots * nexp) + (u * nexp + e)

        def slices_of(it, u, s):
            return it * (slots * 2) + (u * 2 + s)

        with nc.Block() as block:

            def load(sp, u, b):
                sp.dma_start(qst[u][0:ROWS, :].rearrange("r (h n) -> r h n", h=GH),
                             q_dram[bass.ds(b, 1), :, GH * u:GH * u + GH, :].rearrange("b r h n -> (b r) h n")).then_inc(staged[u], 16)
                sp.dma_start(kst[u][0:ROWS, :, :],
                             k_dram[bass.ds(b, 1), :, key_heads * u:key_heads * (u + 1), :].rearrange("b r h n -> (b r) h n")).then_inc(staged[u], 16)
                sp.dma_start(val[u][:, :, :, :], v_all[:, bass.ds(b * 4 + u, 1), :, :, :].rearrange("p g t h c -> p (g t) h c")).then_inc(staged[u], 16)

            def shift(sp, u, count):
                sp.wait_ge(small_free, count)
                for part in range(2):
                    sp.dma_start(qst[u][ROWS + part:ROWS + part + 1, :], mhl[:, part, :]).then_inc(shift_in[u], 16)

            @block.sync
            def _(sp):
                for u in range(slots):
                    sp.wait_ge(cleared[u], 3)
                    load(sp, u, 0)
                shift(sp, 0, start)
                with sp.Fori(0, groups // slots) as it:
                    for u in range(slots):
                        shift(sp, (u + 1) % slots, small_of(it, u, turn_at + 1))
                        sp.wait_ge(probs_used, steps_of(it, u, nst + 2))
                        load(sp, u, (it + 1) % 2)
                for u in range(slots):
                    sp.wait_ge(staged[u], 48 * (groups // slots + 1))
                    sp.wait_ge(shift_in[u], 32 * (groups // slots + (u == 0)))

            def clear(eng, u):
                eng.memset(qst[u][:, :], 0.0).then_inc(cleared[u], 1)
                eng.memset(kst[u][:, :, :], 0.0).then_inc(cleared[u], 1)
                eng.wait_ge(cleared[u], 2)
                eng.memset(kst[u][32:64, :, :], 1.0).then_inc(cleared[u], 1)
                eng.wait_ge(cleared[u], 3)

            @block.gpsimd
            def _(po):
                for u in range(2, slots):
                    clear(po, u)

            def max_matmuls(pe, u, use, bank):
                col = 0
                for h, qt, k0, nk, mask, part in use:
                    kh = h if key_heads == GH else 0
                    mm = pe.matmul(ps_s[bank][:, col:col + nk], qst[u][0:ROWS, h * N + qt * P:h * N + (qt + 1) * P],
                                   kst[u][0:ROWS, kh, k0:k0 + nk], start=True, stop=mask is None, skip_group_check=True)
                    if mask is not None:
                        mm = pe.matmul(ps_s[bank][:, col + nk - mask[1]:col + nk], kit.ident_bf[:, :],
                                       kit.mask_qk[:, mask[0]:mask[0] + mask[1]], start=False, stop=True,
                                       skip_group_check=True)
                    col += 2 * P
                return mm

            @block.tensor
            def _(pe):
                pe.sem_inc(probs_used, 2)
                pe.wait_ge(staged[0], 48)
                for n, use in enumerate(uses):
                    if n >= 3:
                        pe.wait_ge(small_free, n - 2)
                    max_matmuls(pe, 0, use, n % 3).then_inc(small_ready, 1)
                pe.wait_ge(column_done, 1)
                pe.transpose(ps_s[len(uses) % 3][0:GH * 8, 0:P], mcol[:, :], kit.ident[:, :]).then_inc(small_ready, 1)
                with pe.Fori(0, groups // slots) as it:
                    for u in range(slots):
                        nu = (u + 1) % slots
                        pe.wait_ge(staged[nu], it * 48 + (96 if nu == 0 else 48))
                        pe.wait_ge(shift_in[u], it * 32 + 32)
                        e = n = 0

                        def fill(row):
                            nonlocal n
                            for what, i in row:
                                bank = small_bank(pe, it, u, n)
                                if what == "max":
                                    max_matmuls(pe, nu, uses[i], bank).then_inc(small_ready, 1)
                                else:
                                    pe.wait_ge(column_done, it * slots + (u + 2))
                                    pe.transpose(ps_s[bank][0:GH * 8, 0:P], mcol[:, :], kit.ident[:, :]).then_inc(small_ready, 1)
                                n += 1

                        for k in range(nst + 1):
                            row = plan[k] if k < nst else []
                            cuts = [len(row) * c // (blocks + 1) for c in range(blocks + 2)]
                            if k < nst:
                                s, kt, off, w, mask = steps[k]
                                c0 = 0 if mode == "window" else off
                                for blk in range(blocks):
                                    if e == 0:
                                        pe.wait_ge(probs_ready, exps_of(it, u, 1))
                                    elif e >= 2:
                                        pe.wait_ge(probs_ready, exps_of(it, u, e))
                                    for jj in range(hw):
                                        j = blk * hw + jj
                                        kh = j if key_heads == GH else 0
                                        mm = pe.matmul(ps_st[e % 2][:, jj, c0:c0 + w], kst[u][:, kh, kt * P:(kt + 1) * P],
                                                       qst[u][:, j * N + s * SL + off:j * N + s * SL + off + w],
                                                       start=True, stop=mask is None, skip_group_check=True)
                                        if mask is not None:
                                            mm = pe.matmul(ps_st[e % 2][:, jj, c0:c0 + mask[1]], kit.ident_bf[:, :],
                                                           kit.mask_kq[:, mask[0]:mask[0] + mask[1]], start=False,
                                                           stop=True, skip_group_check=True)
                                    mm.then_inc(scores_ready, 1)
                                    e += 1
                                    fill(row[cuts[blk]:cuts[blk + 1]])
                            if k >= 1:
                                s, kt, off, w, mask = steps[k - 1]
                                c0 = 0 if mode == "window" else off
                                first = k == 1 or steps[k - 2][0] != s
                                if first:
                                    pe.wait_ge(o_copied, slices_of(it, u, s + 1))
                                pe.wait_ge(probs_ready, exps_of(it, u, k * blocks + 1))
                                for j in range(GH):
                                    kh = j if key_heads == GH else 0
                                    mm = pe.matmul(ps_o[32 * j:32 * j + 32, off:off + w], val[u][:, kt, kh, :],
                                                   prob[(k - 1) % 2][:, j, c0:c0 + w], start=first,
                                                   stop=k - 1 in slice_end, skip_group_check=True)
                                mm.then_inc(probs_used, 1)
                            fill(row[cuts[blocks]:])

            @block.scalar
            def _(ac):
                ac.sem_inc(probs_ready, 1)
                ac.sem_inc(o_copied, 1)

                def copy_out(it, u, s):
                    ac.wait_ge(probs_used, steps_of(it, u, slice_end[s] + 3))
                    ac.activation(out_all[:, bass.ds(it * slots + u, 1), s * SL:(s + 1) * SL].rearrange("p g n -> p (g n)"),
                                  ps_o[:, :], ACT.Copy).then_inc(o_copied, 1)

                with ac.Fori(0, groups // slots) as it:
                    for u in range(slots):
                        e = 0
                        for k, (s, kt, off, w, mask) in enumerate(steps):
                            c0 = 0 if mode == "window" else off
                            for blk in range(blocks):
                                ac.wait_ge(scores_ready, exps_of(it, u, e + 1))
                                if blk == 0 and k == 0:
                                    ac.wait_ge(probs_used, steps_of(it, u, 2))
                                elif blk == 0 and k >= 2:
                                    ac.wait_ge(probs_used, steps_of(it, u, k + 1))
                                ac.activation(prob[k % 2][:, blk * hw:(blk + 1) * hw, c0:c0 + w],
                                              ps_st[e % 2][:, :, c0:c0 + w], ACT.Exp, scale=scale).then_inc(probs_ready, 1)
                                e += 1
                            if k == slice_end[0] + 1:
                                copy_out(it, u, 0)
                        copy_out(it, u, 1)

            def reduce_use(ve, use, bank):
                h, qt, k0, nk, mask, part = use[0]
                i = h * 8 + qt
                if len(use) == 1:
                    return ve.tensor_reduce(mpart[:, i, part:part + 1], ps_s[bank][:, 0:nk], AX.X, ALU.max)
                if qt == 0:
                    ve.tensor_reduce(mpart[:, i, 0:1], ps_s[bank][:, 0:P], AX.X, ALU.max)
                    return ve.tensor_reduce(mpart[:, i + 1, 0:1], ps_s[bank][:, 2 * P:4 * P], AX.X, ALU.max)
                return ve.tensor_reduce(mpart[:, i:i + 2, 0], ps_s[bank][:, :].rearrange("p (a k) -> p a k", a=2), AX.X, ALU.max)

            def split_max(ve, bank, hi_count):
                ve.tensor_scalar(mhl[:, 0, :], ps_s[bank][0:GH * 8, 0:P], -1.0, None, ALU.mult).then_inc(hi_done, 1)
                ve.wait_ge(hi_done, hi_count)
                ve.scalar_tensor_tensor(mhl[:, 1, :], ps_s[bank][0:GH * 8, 0:P], -1.0, mhl[:, 0, :], ALU.mult,
                                        ALU.subtract).then_inc(small_free, 1)

            @block.vector
            def _(ve):
                clear(ve, 0)
                clear(ve, 1)
                ve.memset(mpart[:, :, :], -3.0e38).then_inc(hi_done, 1)
                ve.wait_ge(hi_done, 1)
                for n, use in enumerate(uses):
                    ve.wait_ge(small_ready, n + 1)
                    reduce_use(ve, use, n % 3).then_inc(small_free, 1)
                ve.wait_ge(small_free, len(uses))
                ve.tensor_reduce(mcol[:, :], mpart[:, :, :], AX.X, ALU.max).then_inc(column_done, 1)
                ve.wait_ge(small_ready, start)
                split_max(ve, len(uses) % 3, 2)
                with ve.Fori(0, groups // slots) as it:
                    for u in range(slots):
                        for n, (what, i) in enumerate(order):
                            bank = n % 3
                            ve.wait_ge(small_ready, small_of(it, u, n + 1))
                            if what == "max":
                                reduce_use(ve, uses[i], bank).then_inc(small_free, 1)
                                if i == len(uses) - 1:
                                    ve.wait_ge(small_free, small_of(it, u, n + 1))
                                    ve.tensor_reduce(mcol[:, :], mpart[:, :, :], AX.X, ALU.max).then_inc(column_done, 1)
                            elif what == "turn":
                                ve.wait_ge(shift_in[u], it * 32 + 32)
                                split_max(ve, bank, it * slots + (u + 3))


def normalise(nc, tag, kit, out_all, extra=0.0):
    blocks, tiles, ring = 8 * N // SL, SL // P, 3
    with nc.cleanup_on_exit(), ExitStack() as ctx:
        sb = lambda name, shape: ctx.enter_context(nc.sbuf_tensor(f"{tag}_{name}", shape, F32))
        rec = [sb(f"rec{i}", [P, tiles, GH]) for i in range(2)]
        quotient = [sb(f"quotient{i}", [P, tiles * GH, 32]) for i in range(ring)]
        ps_tok = [ctx.enter_context(nc.psum_tensor(f"{tag}_tok{i}", [P, tiles, GH, 32], F32)) for i in range(ring)]
        ps_back = [ctx.enter_context(nc.psum_tensor(f"{tag}_back{i}", [P, SL], F32)) for i in range(ring)]
        sem = lambda name: nc.alloc_semaphore(f"{tag}_{name}")
        turned, summed, inverted, divided, turned_back, stored = (sem(n) for n in (
            "turned", "summed", "inverted", "divided", "turned_back", "stored"))

        def block_of(k):
            return out_all[:, k // 2, (k % 2) * SL:(k % 2 + 1) * SL]

        with nc.Block() as block:

            @block.tensor
            def _(pe):
                for k in range(blocks + 2):
                    if k < blocks:
                        if k >= ring:
                            pe.wait_ge(divided, k - ring + 1)
                        for t in range(tiles):
                            mm = pe.transpose(ps_tok[k % ring][:, t, :, :].rearrange("p j c -> p (j c)"),
                                              block_of(k)[:, t * P:(t + 1) * P], kit.ident[:, :])
                        mm.then_inc(turned, 1)
                    if k >= 2:
                        m = k - 2
                        pe.wait_ge(divided, m + 1)
                        if m >= ring:
                            pe.wait_ge(stored, m - ring + 1)
                        for t in range(tiles):
                            mm = pe.transpose(ps_back[m % ring][:, t * P:(t + 1) * P],
                                              quotient[m % ring][:, t * GH:(t + 1) * GH, :].rearrange("p j c -> p (j c)"), kit.ident[:, :])
                        mm.then_inc(turned_back, 1)

            @block.scalar
            def _(ac):
                for k in range(blocks):
                    ac.wait_ge(turned_back, k + 1)
                    ac.activation(block_of(k), ps_back[k % ring][:, :], ACT.Copy).then_inc(stored, 1)

            @block.vector
            def _(ve):
                for k in range(blocks):
                    ve.wait_ge(turned, k + 1)
                    sums = ps_tok[k % ring][:, :, :, E8]
                    if extra:
                        ve.tensor_scalar(rec[k % 2][:, :, :], sums, extra, None, ALU.add).then_inc(summed, 1)
                        ve.wait_ge(summed, k + 1)
                        sums = rec[k % 2][:, :, :]
                    ve.reciprocal(rec[k % 2][:, :, :], sums).then_inc(inverted, 1)
                    ve.wait_ge(inverted, k + 1)
                    if k >= ring:
                        ve.wait_ge(turned_back, k - ring + 1)
                    ve.tensor_tensor(quotient[k % ring][:, :, :], ps_tok[k % ring][:, :, :, :].rearrange("p t j c -> p (t j) c"),
                                     rec[k % 2][:, :, :].rearrange("p t j -> p (t j)").unsqueeze(2).broadcast_to([P, tiles * GH, 32]),
                                     ALU.mult).then_inc(divided, 1)


CH = 64
NC = N // CH
HP = 8
F = 64


def fast_weights(nc, tag, xn, wqk, wv, wo, win0, wout0, woutT0, decay_in, decay_out, rate_in, rate_out, y, ident):
    with nc.cleanup_on_exit(), ExitStack() as ctx:
        sb = lambda name, shape, dt=F32: ctx.enter_context(nc.sbuf_tensor(f"{tag}_{name}", shape, dt))
        sem = lambda name: nc.alloc_semaphore(f"{tag}_{name}")
        win, wout, woutT = (win0, wout0, woutT0)
        qk = [sb(f"qk{i}", [P, HP, 2, 2, CH]) for i in range(2)]
        vT = [sb(f"vT{i}", [P, HP, 2, CH]) for i in range(2)]
        ktok = [sb(f"ktok{i}", [P, HP, 2, F]) for i in range(2)]
        vtok = [sb(f"vtok{i}", [P, HP, 2, F]) for i in range(2)]
        prob = [sb(f"prob{g}", [P, 4, 2, 2, CH]) for g in range(2)]
        mx = [sb(f"mx{g}", [P, 16]) for g in range(2)]
        sm = [sb(f"sm{g}", [P, 16]) for g in range(2)]
        ptok = [sb(f"ptok{g}", [P, 4, 2, F]) for g in range(2)]
        pa = [sb(f"pa{g}", [P, 4, 2, F]) for g in range(2)]
        ssum = [sb(f"ssum{g}", [P, 2, 4]) for g in range(2)]
        oT = [sb(f"oT{g}", [P, 4, 2, CH]) for g in range(2)]
        ps_z = [ctx.enter_context(nc.psum_tensor(f"{tag}_z{g}", [P, 2, 512], F32)) for g in range(2)]
        ps_g = ctx.enter_context(nc.psum_tensor(f"{tag}_g", [P, 2, 512], F32))
        ps_m = [ctx.enter_context(nc.psum_tensor(f"{tag}_m{g}", [P, 512], F32)) for g in range(2)]
        z_ready, a_ready, go_ready, gi_ready = sem("z_ready"), sem("a_ready"), sem("go_ready"), sem("gi_ready")
        misc_ready = sem("misc_ready")
        act_free = sem("act_free")
        ve_free = sem("ve_free")
        shifted = sem("shifted")
        exp_done = sem("exp_done")
        normed = sem("normed")
        gz_done = sem("gz_done")
        win_new, wout_new = sem("win_new"), sem("wout_new")
        win_decayed, wout_decayed = sem("win_decayed"), sem("wout_decayed")
        ve_chain = sem("ve_chain")
        passed = sem("passed")

        next_qkv = [("qk", i, "act") for i in range(4)] + [("v", i, "act") for i in range(2)]
        next_tok = [("kt", i, "ve") for i in range(2)] + [("vt", i, "ve") for i in range(2)]
        chunk = (next_qkv + [("pt", 0, "act"), ("ot", 0, "act"), ("pt", 1, "act"), ("ot", 1, "act")]
                 + next_tok + [("y", 0, "act")])
        lead = next_qkv + next_tok
        nm = len(chunk)
        na = sum(w == "act" for *_, w in chunk)
        nv = nm - na
        la, lv = 6, 4

        def reads_before(n, who):
            return sum(w == who for *_, w in (chunk + chunk)[:n])

        def misc_wait(pe, it, n):
            if n < 2:
                pe.wait_ge(act_free, it * 2 * na + la)
                pe.wait_ge(ve_free, it * 2 * nv + lv)
            else:
                who = (chunk + chunk)[n - 2][2]
                if who == "act":
                    pe.wait_ge(act_free, it * 2 * na + (la + reads_before(n - 1, "act")))
                else:
                    pe.wait_ge(ve_free, it * 2 * nv + (lv + reads_before(n - 1, "ve")))
            return ps_m[n % 2]

        def misc_at(it, n):
            return it * 2 * nm + (len(lead) + n + 1)

        with nc.Block() as block:

            def tokens(c):
                return xn.rearrange("p (b n) -> p b n", b=2)[:, :, bass.ds(c * CH, CH)]

            def project_qk(pe, bank, i, c):
                for j in range(2):
                    for w in range(2):
                        mm = pe.matmul(bank[:, j * 256 + w * 128:j * 256 + w * 128 + 128].rearrange("p (b n) -> p b n", b=2),
                                       wqk[:, w, 2 * i + j, :], tokens(c), start=True, stop=True)
                return mm

            def project_v(pe, bank, i, c):
                for j in range(4):
                    mm = pe.matmul(bank[:, j * 128:(j + 1) * 128].rearrange("p (b n) -> p b n", b=2),
                                   wv[:, 4 * i + j, :], tokens(c), start=True, stop=True)
                return mm

            def turn(pe, bank, sources):
                for j, src in enumerate(sources):
                    mm = pe.transpose(bank[:, j * 128:(j + 1) * 128], src, ident[:, :])
                return mm

            def make(pe, what, i, bank, nxt, cn, cur, it):
                if what == "qk":
                    return project_qk(pe, bank, i, cn)
                if what == "v":
                    return project_v(pe, bank, i, cn)
                if what == "kt":
                    return turn(pe, bank, [qk[nxt][:, 4 * i + j, 1, :, :].rearrange("p b n -> p (b n)") for j in range(4)])
                if what == "vt":
                    return turn(pe, bank, [vT[nxt][:, 4 * i + j, :, :].rearrange("p b n -> p (b n)") for j in range(4)])
                if what == "pt":
                    return turn(pe, bank, [prob[i][:, j, 1, :, :].rearrange("p b n -> p (b n)") for j in range(4)])
                if what == "ot":
                    for j in range(4):
                        for b in range(2):
                            for h in range(2):
                                r = slice(64 * h, 64 * h + 64)
                                mm = pe.matmul(bank[r, (j * 2 + b) * 64:(j * 2 + b + 1) * 64], wout[r, 4 * i + j, b, :],
                                               prob[i][r, j, 0, b, :], start=True, stop=True, skip_group_check=True)
                    return mm
                if what == "y":
                    for j in range(HP):
                        mm = pe.matmul(bank[:, 0:128], wo[:, j, :], oT[j // 4][:, j % 4, :, :].rearrange("p b n -> p (b n)"),
                                       start=j == 0, stop=j == HP - 1)
                    return mm

            @block.tensor
            def _(pe):
                for n, (what, i, who) in enumerate(lead):
                    if n >= 2:
                        w2 = lead[n - 2][2]
                        pe.wait_ge(act_free if w2 == "act" else ve_free, sum(x[2] == w2 for x in lead[:n - 1]))
                    if n == 6:
                        pe.wait_ge(act_free, 6)
                    make(pe, what, i, ps_m[n % 2], 0, 0, 0, None).then_inc(misc_ready, 1)
                with pe.Fori(0, NC // 2) as it:
                    n = 0
                    for cc in range(2):
                        cur, nxt = cc, 1 - cc
                        cn = (it * 2 + (cc + 1)) % NC
                        act0 = la + cc * na
                        ve0 = lv + cc * nv
                        for g in range(2):
                            pe.wait_ge(win_new, it * 4 + (2 * cc + g + 1))
                            if g == 0:
                                pe.wait_ge(act_free, it * 2 * na + act0)
                            pe.sem_inc(passed, 1)
                            for j in range(4):
                                for b in range(2):
                                    for h in range(2):
                                        r = slice(64 * h, 64 * h + 64)
                                        mm = pe.matmul(ps_z[g][r, j // 2, (j % 2) * 256:(j % 2) * 256 + 256].rearrange("p (w b n) -> p w b n", w=2, b=2)[:, :, b, :],
                                                       win[r, 4 * g + j, b, :], qk[cur][r, 4 * g + j, :, b, :],
                                                       start=True, stop=True, skip_group_check=True)
                            mm.then_inc(z_ready, 1)

                        def misc(what, i):
                            nonlocal n
                            bank = misc_wait(pe, it, n)
                            if what == "ot":
                                pe.sem_inc(passed, 1)
                            make(pe, what, i, bank, nxt, cn, cur, it).then_inc(misc_ready, 1)
                            n += 1

                        for i in range(4):
                            misc("qk", i)
                        for i in range(2):
                            misc("v", i)
                        for g in range(2):
                            pe.wait_ge(normed, it * 4 + (2 * cc + g + 1))
                            if g == 0:
                                pe.wait_ge(wout_new, it * 4 + (2 * cc + 2))
                            misc("pt", g)
                            misc("ot", g)
                            for j in range(4):
                                for h in range(2):
                                    for b in range(2):
                                        r = slice(64 * h, 64 * h + 64)
                                        mm = pe.matmul(ps_z[g][64 * b:64 * b + 64, h, j * 64:(j + 1) * 64], vT[cur][r, 4 * g + j, b, :],
                                                       woutT[r, 4 * g + j, b, :], start=True, stop=True, skip_group_check=True)
                            mm.then_inc(a_ready, 1)

                        def grad_out(g):
                            pe.wait_ge(act_free, it * 2 * na + (act0 + 6 + 2 * g + 1))
                            if g == 0:
                                pe.wait_ge(ve_free, it * 2 * nv + ve0)
                            pe.wait_ge(wout_new, it * 4 + (2 * cc + g + 2))
                            pe.sem_inc(passed, 1)
                            for j in range(4):
                                for b in range(2):
                                    r = slice(64 * b, 64 * b + 64)
                                    for h in range(2):
                                        pe.matmul(ps_g[64 * h:64 * h + 64, b, j * 64:(j + 1) * 64], ptok[g][r, j, h, :],
                                                  vtok[cur][r, 4 * g + j, h, :], start=True, stop=True, skip_group_check=True)
                                    for h in range(2):
                                        mm = pe.matmul(ps_g[64 * h:64 * h + 64, b, 256 + j * 64:256 + (j + 1) * 64],
                                                       vtok[cur][r, 4 * g + j, h, :], ptok[g][r, j, h, :],
                                                       start=True, stop=True, skip_group_check=True)
                            mm.then_inc(go_ready, 1)

                        def grad_in(g):
                            pe.wait_ge(gz_done, it * 4 + (2 * cc + g + 1))
                            pe.sem_inc(passed, 1)
                            for j in range(4):
                                for b in range(2):
                                    r = slice(64 * b, 64 * b + 64)
                                    for h in range(2):
                                        mm = pe.matmul(ps_z[g][64 * h:64 * h + 64, b, j * 64:(j + 1) * 64], ktok[cur][r, 4 * g + j, h, :],
                                                       pa[g][r, j, h, :], start=True, stop=True, skip_group_check=True)
                            mm.then_inc(gi_ready, 1)

                        grad_out(0)
                        pe.wait_ge(act_free, it * 2 * na + (act0 + 6))
                        for i in range(2):
                            misc("kt", i)
                        for i in range(2):
                            misc("vt", i)
                        grad_in(0)
                        grad_out(1)
                        pe.wait_ge(act_free, it * 2 * na + (act0 + 10))
                        misc("y", 0)
                        grad_in(1)

            def read_act(ac, what, i, bank, nxt, c, cur):
                if what == "qk":
                    return ac.activation(qk[nxt][:, 2 * i:2 * i + 2, :, :, :].rearrange("p a b w n -> p (a b w n)"), bank[:, :], ACT.Silu)
                if what == "v":
                    return ac.activation(vT[nxt][:, 4 * i:4 * i + 4, :, :].rearrange("p a b n -> p (a b n)"), bank[:, :], ACT.Copy)
                if what == "pt":
                    return ac.activation(ptok[i][:, :, :, :].rearrange("p a h n -> p (a h n)"), bank[:, :], ACT.Copy)
                if what == "ot":
                    return ac.activation(oT[i][:, :, :, :].rearrange("p a h n -> p (a h n)"), bank[:, :], ACT.Copy)
                if what == "y":
                    return ac.activation(y.rearrange("p (b n) -> p b n", b=2)[:, :, bass.ds(c * CH, CH)],
                                         bank[:, 0:128].rearrange("p (b n) -> p b n", b=2), ACT.Copy)

            @block.scalar
            def _(ac):
                for n, (what, i, who) in enumerate(lead):
                    if who == "act":
                        ac.wait_ge(misc_ready, n + 1)
                        read_act(ac, what, i, ps_m[n % 2], 0, 0, 0).then_inc(act_free, 1)
                with ac.Fori(0, NC // 2) as it:
                    for cc in range(2):
                        cur, nxt = cc, 1 - cc
                        for k, (what, i, who) in enumerate(chunk):
                            n = cc * nm + k
                            if k == 0:
                                if cc:
                                    ac.wait_ge(gi_ready, it * 4 + 2 * cc)
                            if k == 6:
                                for g in range(2):
                                    ac.wait_ge(shifted, it * 4 + (2 * cc + g + 1))
                                    ac.activation(prob[g][:, :, :, :, :].rearrange("p a b w n -> p (a b w n)"),
                                                  prob[g][:, :, :, :, :].rearrange("p a b w n -> p (a b w n)"), ACT.Exp).then_inc(exp_done, 1)
                            if who == "act":
                                ac.wait_ge(misc_ready, misc_at(it, n))
                                read_act(ac, what, i, ps_m[n % 2], nxt, it * 2 + cc, cur).then_inc(act_free, 1)

            def segments(t):
                return t[:, :, :, :, :].rearrange("p a b w n -> p (a b w) n")

            def read_ve(ve, what, i, bank, nxt, cn):
                dst = (ktok if what == "kt" else vtok)[nxt][:, 4 * i:4 * i + 4, :, :].rearrange("p a h d -> p (a h) d")
                rate = (rate_in if what == "kt" else rate_out)[:, bass.ds(cn, 1), 8 * i:8 * i + 8].rearrange("p c h -> p (c h)")
                return ve.tensor_tensor(dst, bank[:, :].rearrange("p (a d) -> p a d", d=F),
                                        rate.unsqueeze(2).broadcast_to([P, 8, F]), ALU.mult)

            @block.vector
            def _(ve):
                ve.sem_inc(win_new, 2)
                ve.sem_inc(wout_new, 2)
                for n, (what, i, who) in enumerate(lead):
                    if who == "ve":
                        ve.wait_ge(misc_ready, n + 1)
                        read_ve(ve, what, i, ps_m[n % 2], 0, 0).then_inc(ve_free, 1)
                links = 12
                with ve.Fori(0, NC // 2) as it:
                    done = [0]

                    def link(ins):
                        done[0] += 1
                        ins.then_inc(ve_chain, 1)
                        ve.wait_ge(ve_chain, it * 2 * links + done[0])

                    for cc in range(2):
                        cur, nxt = cc, 1 - cc
                        cn = (it * 2 + (cc + 1)) % NC
                        for g in range(2):
                            ve.wait_ge(z_ready, it * 4 + (2 * cc + g + 1))
                            z = ps_z[g][:, :, :].rearrange("p k (s n) -> p (k s) n", n=CH)
                            link(ve.tensor_reduce(mx[g][:, :], z, AX.X, ALU.max))
                            ve.tensor_tensor(segments(prob[g]), z, mx[g][:, :].unsqueeze(2).broadcast_to([P, 16, CH]),
                                             ALU.subtract).then_inc(shifted, 1)
                        for g in range(2):
                            ve.wait_ge(exp_done, it * 4 + (2 * cc + g + 1))
                            link(ve.tensor_reduce(sm[g][:, :], segments(prob[g]), AX.X, ALU.add))
                            link(ve.reciprocal(mx[g][:, :], sm[g][:, :]))
                            ve.tensor_tensor(segments(prob[g]), segments(prob[g]), mx[g][:, :].unsqueeze(2).broadcast_to([P, 16, CH]),
                                             ALU.mult).then_inc(normed, 1)
                        for g in range(2):
                            ve.wait_ge(a_ready, it * 4 + (2 * cc + g + 1))
                            ve.wait_ge(act_free, it * 2 * na + (la + cc * na + 6 + 2 * g + 1))
                            a = ps_z[g][:, :, 0:256].rearrange("p h (a d) -> p h a d", d=F)
                            pt = ptok[g][:, :, :, :].rearrange("p a h d -> p h a d")
                            out = pa[g][:, :, :, :].rearrange("p a h d -> p h a d")
                            link(ve.tensor_tensor(out, a, pt, ALU.mult))
                            link(ve.tensor_reduce(ssum[g][:, :, :], out, AX.X, ALU.add))
                            link(ve.tensor_tensor(out, a, ssum[g][:, :, :].unsqueeze(3).broadcast_to([P, 2, 4, F]), ALU.subtract))
                            ve.tensor_tensor(pa[g][:, :, :, :], pa[g][:, :, :, :], ptok[g][:, :, :, :], ALU.mult).then_inc(gz_done, 1)

                        def update_out(g):
                            ve.wait_ge(go_ready, it * 4 + (2 * cc + g + 1))
                            ve.wait_ge(wout_decayed, it * 8 + (4 * cc + 2 * g + 2))
                            for m, w in enumerate((wout, woutT)):
                                wv_ = w[:, 4 * g:4 * g + 4, :, :].rearrange("p a b d -> p b a d")
                                ins = ve.tensor_tensor(wv_, ps_g[:, :, 256 * m:256 * m + 256].rearrange("p b (a d) -> p b a d", d=F), wv_, ALU.add)
                            ins.then_inc(wout_new, 1)

                        def update_in(g):
                            ve.wait_ge(gi_ready, it * 4 + (2 * cc + g + 1))
                            ve.wait_ge(win_decayed, it * 4 + (2 * cc + g + 1))
                            wv_ = win[:, 4 * g:4 * g + 4, :, :].rearrange("p a b d -> p b a d")
                            ve.tensor_tensor(wv_, ps_z[g][:, :, 0:256].rearrange("p b (a d) -> p b a d", d=F), wv_, ALU.add).then_inc(win_new, 1)

                        update_out(0)
                        for k, (what, i, who) in enumerate(chunk):
                            if who == "ve":
                                ve.wait_ge(misc_ready, misc_at(it, cc * nm + k))
                                read_ve(ve, what, i, ps_m[(cc * nm + k) % 2], nxt, cn).then_inc(ve_free, 1)
                        update_in(0)
                        update_out(1)
                        update_in(1)
                    assert done[0] == 2 * links, done

            @block.gpsimd
            def _(po):
                def decay(w, g, d, c):
                    v = w[:, 4 * g:4 * g + 4, :, :].rearrange("p a b d -> p (a b) d")
                    k = d[:, bass.ds(c, 1), 4 * g:4 * g + 4, :].rearrange("p c a b -> p (c a b)")
                    return po.tensor_tensor(v, v, k.unsqueeze(2).broadcast_to([P, 8, F]), ALU.mult)

                with po.Fori(0, NC // 2) as it:
                    for cc in range(2):
                        c = it * 2 + cc
                        for g in range(2):
                            po.wait_ge(z_ready, it * 4 + (2 * cc + g + 1))
                            decay(win, g, decay_in, c).then_inc(win_decayed, 1)
                        for g in range(2):
                            po.wait_ge(a_ready, it * 4 + (2 * cc + g + 1))
                            decay(wout, g, decay_out, c).then_inc(wout_decayed, 1)
                            decay(woutT, g, decay_out, c).then_inc(wout_decayed, 1)


SHIFTS = [0] + [2 << j for j in range(9)] + [1] + [3 << j for j in range(9)]
PAIRED = 9
ZERO_TAPS = 11
FAR_TAPS = 5
PAD = 768


def dilated_attention(nc, tag, kit, xin, w_dram, cols_dram, taps_dram, y):
    n_in = len(SHIFTS)
    n_slots = n_in + 1
    H = 16
    taps = ZERO_TAPS + 2 * PAIRED + 1 + 9 + FAR_TAPS
    with nc.cleanup_on_exit(), ExitStack() as ctx:
        sb = lambda name, shape, dt=F32: ctx.enter_context(nc.sbuf_tensor(f"{tag}_{name}", shape, dt))
        w = sb("w", [P, 5, P])
        cols = sb("cols", [P, 5])
        q = sb("q", [P, T])
        kpad = sb("kpad", [P, 2, PAD + N])
        vpad = sb("vpad", [P, 2, PAD + N])
        pb = sb("pb", [P, taps, H])
        pbm = sb("pbm", [P, n_slots, H])
        bias = sb("bias", [P, n_slots, H])
        prod = [sb(f"prod{i}", [P, SL]) for i in range(8)]
        sc_t = sb("sc_t", [P, 5, SL])
        att = sb("att", [P, 4, n_slots, H])
        stat = sb("stat", [P, 4, H])
        attT = sb("attT", [P, 3, SL])
        wv = [sb(f"wv{i}", [P, SL]) for i in range(2)]
        acc = sb("acc", [P, SL])
        gate = sb("gate", [P, SL])
        ps_sc = [ctx.enter_context(nc.psum_tensor(f"{tag}_sc{i}", [P, SL], F32)) for i in range(2)]
        ps_tok = [ctx.enter_context(nc.psum_tensor(f"{tag}_tok{i}", [P, SL], F32)) for i in range(2)]
        ps_w = [ctx.enter_context(nc.psum_tensor(f"{tag}_w{i}", [P, SL], F32)) for i in range(2)]
        ps_x = [ctx.enter_context(nc.psum_tensor(f"{tag}_x{i}", [P, SL], F32)) for i in range(2)]
        sem = lambda name: nc.alloc_semaphore(f"{tag}_{name}")
        loaded, padded, projected, placed = sem("loaded"), sem("padded"), sem("projected"), sem("placed")
        chain, tap_shifted, tap_exp, tap_sum, tap_ln = (sem(n) for n in ("chain", "tap_shifted", "tap_exp", "tap_sum", "tap_ln"))
        multiplied, used, scores_ready, shifted, exp_done, probs_ready = (sem(n) for n in (
            "multiplied", "used", "scores_ready", "shifted", "exp_done", "probs_ready"))
        turned, turned_in, spread, weighted, added, gate_ready, gated, out_ready, out_in = (sem(n) for n in (
            "turned", "turned_in", "spread", "weighted", "added", "gate_ready", "gated", "out_ready", "out_in"))
        gate_in, copied, sc_turned, tile_in = sem("gate_in"), sem("copied"), sem("sc_turned"), sem("tile_in")
        n_four = n_in // 4
        groups = ((0, 0, 1, ZERO_TAPS), (ZERO_TAPS, 1, PAIRED, 2), (taps - FAR_TAPS, n_in, 1, FAR_TAPS))
        singles = (ZERO_TAPS + 2 * PAIRED, 1 + PAIRED, 10)
        rows3 = (P, P, 5 * H)
        with nc.Block() as block:

            @block.sync
            def _(sp):
                sp.dma_start(w[:, :, :], w_dram).then_inc(loaded, 16)
                sp.dma_start(cols[:, :], cols_dram).then_inc(loaded, 16)
                sp.dma_start(pb[:, :, :], taps_dram.broadcast_to([P, taps, H])).then_inc(loaded, 16)
                sp.wait_ge(loaded, 48)

            @block.gpsimd
            def _(po):
                po.memset(kpad[:, :, 0:PAD], 0.0).then_inc(padded, 1)
                po.memset(vpad[:, :, 0:PAD], 0.0).then_inc(padded, 1)
                for s in range(NS):
                    for i in range(n_in):
                        k = s * n_in + i
                        po.wait_ge(weighted, k + 1)
                        if i == 0:
                            if s:
                                po.wait_ge(gated, s)
                            po.tensor_copy(acc[:, :], wv[k % 2][:, :]).then_inc(added, 1)
                        else:
                            po.wait_ge(added, k)
                            po.tensor_tensor(acc[:, :], acc[:, :], wv[k % 2][:, :], ALU.add).then_inc(added, 1)

            @block.tensor
            def _(pe):
                pe.wait_ge(loaded, 48)
                banks = ps_sc + ps_tok
                for n in range(12):
                    k, s = n // NS, n % NS
                    if n >= 4:
                        pe.wait_ge(placed, n - 3)
                    pe.matmul(banks[s][:, :], w[:, k, :], xin[:, s * SL:(s + 1) * SL], start=True, stop=True).then_inc(projected, 1)

                def score_four(n):
                    pe.wait_ge(multiplied, 4 * n + 4)
                    if n >= 2:
                        pe.wait_ge(copied, n - 1)
                    else:
                        pe.wait_ge(placed, 12)
                    for j in range(4):
                        mm = pe.matmul(ps_sc[n % 2][32 * j:32 * j + 32, :], kit.heads[:, :], prod[(4 * n + j) % 8][:, :],
                                       start=True, stop=True, skip_group_check=True)
                    mm.then_inc(used, 1)

                def turn_scores(s):
                    pe.wait_ge(copied, n_four * (s + 1))
                    for t in range(4):
                        if s or t:
                            pe.wait_ge(tile_in, 4 * s + t)
                        for g in range(n_four):
                            mm = pe.transpose(ps_tok[g // 4][:, (g % 4) * P:(g % 4 + 1) * P], sc_t[:, g, t * P:(t + 1) * P], kit.ident[:, :])
                        mm.then_inc(sc_turned, 1)

                for g in range(n_four):
                    score_four(g)
                turn_scores(0)
                for s in range(NS):
                    pe.wait_ge(probs_ready, s + 1)
                    for g in range(3):
                        n = 3 * s + g
                        if n >= 2:
                            pe.wait_ge(turned_in, n - 1)
                        if s and g < 2:
                            pe.wait_ge(out_in, s)
                            pe.wait_ge(gate_in, s)
                        for t in range(4):
                            mm = pe.transpose(ps_x[n % 2][0:rows3[g], t * P:(t + 1) * P],
                                              att[:, t, :, :].rearrange("p s h -> p (s h)")[:, g * P:g * P + rows3[g]], kit.ident[:, :])
                        mm.then_inc(turned, 1)
                    pe.wait_ge(turned_in, 3 * s + 3)
                    for i in range(n_in):
                        k = s * n_in + i
                        if k >= 2:
                            pe.wait_ge(weighted, k - 1)
                        r = rows3[i // 8]
                        pe.matmul(ps_w[k % 2][:, :], kit.spread[0:r, i % 8, :], attT[0:r, i // 8, :], start=True, stop=True).then_inc(spread, 1)
                        if i % 4 == 3 and s + 1 < NS:
                            score_four((s + 1) * n_four + i // 4)
                    pe.matmul(ps_x[0][:, :], w[:, 3, :], xin[:, s * SL:(s + 1) * SL], start=True, stop=True).then_inc(gate_ready, 1)
                    if s + 1 < NS:
                        turn_scores(s + 1)
                    pe.wait_ge(gated, s + 1)
                    pe.matmul(ps_x[1][:, :], w[:, 4, :], wv[0][:, :], start=True, stop=True).then_inc(out_ready, 1)

            @block.scalar
            def _(ac):
                ac.wait_ge(tap_shifted, 1)
                ac.activation(pb[:, :, :], pb[:, :, :], ACT.Exp).then_inc(tap_exp, 1)
                ac.wait_ge(tap_sum, 1)
                ac.activation(bias[:, :, :], bias[:, :, :], ACT.Ln).then_inc(tap_ln, 1)
                ac.wait_ge(loaded, 48)
                for n in range(12):
                    k, s = n // NS, n % NS
                    ac.wait_ge(projected, n + 1)
                    b, c = s // 2, (s % 2) * SL
                    dst = q[:, s * SL:(s + 1) * SL] if k == 0 else (kpad if k == 1 else vpad)[:, b, PAD + c:PAD + c + SL]
                    ac.activation(dst, (ps_sc + ps_tok)[s][:, :], ACT.Identity, bias=cols[:, k:k + 1]).then_inc(placed, 1)

                def copy_scores(s):
                    for g in range(n_four):
                        ac.wait_ge(used, s * n_four + g + 1)
                        if s:
                            ac.wait_ge(sc_turned, 4 * s)
                        ac.activation(sc_t[:, g, :], ps_sc[(s * n_four + g) % 2][:, :], ACT.Copy).then_inc(copied, 1)

                copy_scores(0)
                for s in range(NS):
                    ac.wait_ge(shifted, s + 1)
                    ac.activation(att[:, :, :, :], att[:, :, :, :], ACT.Exp).then_inc(exp_done, 1)
                    for g in range(3):
                        n = 3 * s + g
                        ac.wait_ge(turned, n + 1)
                        if s:
                            ac.wait_ge(spread, s * n_in)
                        ac.activation(attT[0:rows3[g], g, :], ps_x[n % 2][0:rows3[g], :], ACT.Copy).then_inc(turned_in, 1)
                    if s + 1 < NS:
                        copy_scores(s + 1)
                    ac.wait_ge(gate_ready, s + 1)
                    if s:
                        ac.wait_ge(gated, s)
                    ac.activation(gate[:, :], ps_x[0][:, :], ACT.Sigmoid, bias=cols[:, 3:4]).then_inc(gate_in, 1)
                    ac.wait_ge(out_ready, s + 1)
                    ac.activation(y[:, s * SL:(s + 1) * SL], ps_x[1][:, :], ACT.Identity, bias=cols[:, 4:5]).then_inc(out_in, 1)

            @block.vector
            def _(ve):
                done = [0]

                def link(ins):
                    done[0] += 1
                    ins.then_inc(chain, 1)
                    ve.wait_ge(chain, done[0])

                ve.wait_ge(loaded, 48)
                f0, s0, m0 = singles
                for a, slot, n, each in groups:
                    link(ve.tensor_reduce(pbm[:, slot:slot + n, :], pb[:, a:a + n * each, :].rearrange("p (n k) h -> p n h k", k=each), AX.X, ALU.max))
                link(ve.tensor_copy(pbm[:, s0:s0 + m0, :], pb[:, f0:f0 + m0, :]))
                for a, slot, n, each in groups:
                    view = pb[:, a:a + n * each, :].rearrange("p (n k) h -> p n k h", k=each)
                    link(ve.tensor_tensor(view, view, pbm[:, slot:slot + n, :].unsqueeze(2).broadcast_to([P, n, each, H]), ALU.subtract))
                ve.tensor_tensor(pb[:, f0:f0 + m0, :], pb[:, f0:f0 + m0, :], pbm[:, s0:s0 + m0, :], ALU.subtract).then_inc(tap_shifted, 1)
                ve.wait_ge(tap_exp, 1)
                for a, slot, n, each in groups:
                    link(ve.tensor_reduce(bias[:, slot:slot + n, :], pb[:, a:a + n * each, :].rearrange("p (n k) h -> p n h k", k=each), AX.X, ALU.add))
                ve.tensor_copy(bias[:, s0:s0 + m0, :], pb[:, f0:f0 + m0, :]).then_inc(tap_sum, 1)
                ve.wait_ge(tap_ln, 1)
                link(ve.tensor_tensor(bias[:, :, :], bias[:, :, :], pbm[:, :, :], ALU.add))
                ve.wait_ge(padded, 2)
                ve.wait_ge(placed, 12)

                def product(s, i):
                    k, c, off = s * n_in + i, (s % 2) * SL, SHIFTS[i]
                    if k >= 8:
                        ve.wait_ge(used, k // 4 - 1)
                    ve.tensor_tensor(prod[k % 8][:, :], q[:, s * SL:(s + 1) * SL], kpad[:, s // 2, PAD + c - off:PAD + c - off + SL],
                                     ALU.mult).then_inc(multiplied, 1)

                def softmax(s):
                    if s:
                        ve.wait_ge(turned, 3 * s)
                    ve.tensor_copy(att[:, :, n_in, :], bias[:, n_in, :].unsqueeze(1).broadcast_to([P, 4, H])).then_inc(scores_ready, 1)
                    for t in range(4):
                        ve.wait_ge(sc_turned, 4 * s + t + 1)
                        ve.tensor_tensor(att[:, t, 0:16, :], ps_tok[0][:, :].rearrange("p (s c) -> p s c", c=32)[:, :, 0:H],
                                         bias[:, 0:16, :], ALU.add).then_inc(scores_ready, 1)
                        ve.tensor_tensor(att[:, t, 16:n_in, :], ps_tok[1][:, 0:P].rearrange("p (s c) -> p s c", c=32)[:, :, 0:H],
                                         bias[:, 16:n_in, :], ALU.add).then_inc(tile_in, 1)
                    ve.wait_ge(scores_ready, 5 * s + 5)
                    ve.wait_ge(tile_in, 4 * s + 4)
                    by_head = att[:, :, :, :].rearrange("p t s h -> p t h s")
                    across = stat[:, :, :].unsqueeze(2).broadcast_to([P, 4, n_slots, H])
                    link(ve.tensor_reduce(stat[:, :, :], by_head, AX.X, ALU.max))
                    ve.tensor_tensor(att[:, :, :, :], att[:, :, :, :], across, ALU.subtract).then_inc(shifted, 1)
                    ve.wait_ge(exp_done, s + 1)
                    link(ve.tensor_reduce(stat[:, :, :], by_head, AX.X, ALU.add))
                    link(ve.reciprocal(stat[:, :, :], stat[:, :, :]))
                    ve.tensor_tensor(att[:, :, :, :], att[:, :, :, :], across, ALU.mult).then_inc(probs_ready, 1)

                for i in range(n_in):
                    product(0, i)
                softmax(0)
                for s in range(NS):
                    b, c = s // 2, (s % 2) * SL
                    for i, off in enumerate(SHIFTS):
                        k = s * n_in + i
                        if s + 1 < NS:
                            product(s + 1, i)
                        ve.wait_ge(spread, k + 1)
                        if i >= 2:
                            ve.wait_ge(added, k - 1)
                        elif s:
                            ve.wait_ge(out_ready, s)
                            ve.wait_ge(added, k - 1)
                        ve.tensor_tensor(wv[k % 2][:, :], ps_w[k % 2][:, :], vpad[:, b, PAD + c - off:PAD + c - off + SL],
                                         ALU.mult).then_inc(weighted, 1)
                    ve.wait_ge(added, (s + 1) * n_in)
                    ve.wait_ge(gate_in, s + 1)
                    ve.tensor_tensor(wv[0][:, :], acc[:, :], gate[:, :], ALU.mult).then_inc(gated, 1)
                    if s + 1 < NS:
                        softmax(s + 1)


def chunk_rates(nc, tag, kit, xin, w_dram, rate_dram, decay_dram, decay_in, decay_out, rate_in, rate_out):
    K4 = 64
    chunks = N // 64
    with nc.cleanup_on_exit(), ExitStack() as ctx:
        sb = lambda name, shape, dt=F32: ctx.enter_context(nc.sbuf_tensor(f"{tag}_{name}", shape, dt))
        w = sb("w", [P, K4])
        sig = sb("sig", [K4, T])
        mean = sb("mean", [K4, 2, chunks])
        ps = [ctx.enter_context(nc.psum_tensor(f"{tag}_ps{s}", [K4, SL], F32)) for s in range(NS)]
        sem = lambda name: nc.alloc_semaphore(f"{tag}_{name}")
        loaded, ready, sigmoid_done, summed, scaled, stored, spread = (sem(n) for n in (
            "loaded", "ready", "sigmoid_done", "summed", "scaled", "stored", "spread"))
        with nc.Block() as block:

            @block.sync
            def _(sp):
                sp.dma_start(w[:, :], w_dram).then_inc(loaded, 16)
                sp.wait_ge(scaled, 1)
                with nc.allow_non_contiguous_dma(reason="one small array is stored in another order"):
                    for kind in range(2):
                        for b in range(2):
                            sp.dma_start(rate_dram[kind, b].rearrange("c h -> h c"), mean[16 * kind:16 * kind + 16, b, :]).then_inc(stored, 16)
                            for par in range(2):
                                r = 32 + kind * 16 + par * 8
                                sp.dma_start(decay_dram[kind, par, :, :, b].rearrange("c a -> a c"), mean[r:r + 8, b, :]).then_inc(stored, 16)
                sp.wait_ge(stored, 16 * 12)
                for kind in range(2):
                    rate, decay = ((rate_in, decay_in), (rate_out, decay_out))[kind]
                    for half in range(2):
                        r = slice(64 * half, 64 * half + 64)
                        sp.dma_start(rate[r, :, :], rate_dram[kind, half:half + 1].broadcast_to([64, chunks, 16])).then_inc(spread, 16)
                        sp.dma_start(decay[r, :, :, :], decay_dram[kind, half:half + 1].broadcast_to([64, chunks, 8, 2])).then_inc(spread, 16)
                sp.wait_ge(spread, 16 * 8)

            @block.tensor
            def _(pe):
                pe.wait_ge(loaded, 16)
                for s in range(NS):
                    pe.matmul(ps[s][:, :], w[:, :], xin[:, s * SL:(s + 1) * SL], start=True, stop=True).then_inc(ready, 1)

            @block.scalar
            def _(ac):
                for s in range(NS):
                    ac.wait_ge(ready, s + 1)
                    ac.activation(sig[:, s * SL:(s + 1) * SL], ps[s][:, :], ACT.Sigmoid).then_inc(sigmoid_done, 1)

            @block.vector
            def _(ve):
                ve.wait_ge(sigmoid_done, NS)
                ve.tensor_reduce(mean[:, :, :], sig[:, :].rearrange("p (b c n) -> p b c n", b=2, c=chunks), AX.X, ALU.add).then_inc(summed, 1)
                ve.wait_ge(summed, 1)
                ve.tensor_scalar(mean[:, :, :], mean[:, :, :], kit.columns[0:K4, 2:3], None, ALU.mult).then_inc(scaled, 1)


def load_constants(nc, ctx, kit, a):
    sb = lambda name, shape, dt=F32: ctx.enter_context(nc.sbuf_tensor(f"const_{name}", shape, dt))
    kit.ident, kit.den_sel, kit.mean, kit.ones, kit.upto = (sb(n, [P, P]) for n in ("ident", "den_sel", "mean", "ones", "upto"))
    kit.blocks, kit.head4, kit.heads = sb("blocks", [P, 4, P]), sb("head4", [P, 4]), sb("heads", [P, 32])
    kit.numbers = sb("numbers", [P, 8 + T // P])
    kit.columns, kit.lower = sb("columns", [P, 3]), sb("lower", [P, 16, 16])
    kit.ident_bf, kit.mask_kq, kit.mask_qk = sb("ident_bf", [P, P], BF16), sb("mask_kq", [P, 2 * P], BF16), sb("mask_qk", [P, 2 * P], BF16)
    loads = dict(ident=kit.ident, den_sel=kit.den_sel, mean=kit.mean, ones=kit.ones, upto=kit.upto, blocks=kit.blocks,
                 head4=kit.head4, numbers=kit.numbers, heads=kit.heads, columns=kit.columns, lower=kit.lower)
    with nc.cleanup_on_exit(), ExitStack() as inner:
        masks = inner.enter_context(nc.sbuf_tensor("const_masks", [P, 4 * P], F32))
        loaded, converted = nc.alloc_semaphore("const_loaded"), nc.alloc_semaphore("const_converted")
        with nc.Block() as block:

            @block.sync
            def _(sp):
                for name, tile in loads.items():
                    sp.dma_start(tile[:], a["c_" + name]).then_inc(loaded, 16)
                sp.dma_start(masks[:, :], a["c_masks"]).then_inc(loaded, 16)
                sp.wait_ge(loaded, 16 * (len(loads) + 1))

            @block.vector
            def _(ve):
                ve.wait_ge(loaded, 16 * (len(loads) + 1))
                ve.tensor_copy(kit.ident_bf[:, :], kit.ident[:, :]).then_inc(converted, 1)
                ve.tensor_copy(kit.mask_kq[:, :], masks[:, 0:2 * P]).then_inc(converted, 1)
                ve.tensor_copy(kit.mask_qk[:, :], masks[:, 2 * P:4 * P]).then_inc(converted, 1)


def move(nc, tag, pairs):
    with nc.cleanup_on_exit():
        moved = nc.alloc_semaphore(f"{tag}_moved")
        with nc.Block() as block:

            @block.sync
            def _(sp):
                for dst, src in pairs:
                    sp.dma_start(dst, src).then_inc(moved, 16)
                sp.wait_ge(moved, 16 * len(pairs))


class Buffers:
    pass


def layer0_attention(nc, kit, a, m):
    h = m.g
    layer_norm(nc, "l0n1", kit, m.xn, h, a["l0_ln1"])
    with ExitStack() as ctx:
        v_all = ctx.enter_context(nc.sbuf_tensor("l0_v", [P, 8, 8, GH, 32], F32))
        out_all = ctx.enter_context(nc.sbuf_tensor("l0_out", [P, 8, N], F32))
        query_parts(nc, "l0q", kit, h, a["l0_wq"], a["l0_bq"], P, PARTS_Q, kit.q_dram)
        query_parts(nc, "l0k", kit, h, a["l0_wk"], a["l0_bk"], P, PARTS_K, kit.k_dram)
        values(nc, "l0v", kit, h, a["l0_wv"], a["l0_bv"], GH, v_all)
        attend(nc, "l0a", "window", E8 ** -0.5, kit.q_dram, kit.k_dram, v_all, GH, out_all, kit)
        normalise(nc, "l0d", kit, out_all)
        outs = [heads_of(out_all, g) for g in range(4)]
        terms = [(g, g) for g in range(4)]
        project(nc, "l0p", [(terms, 0, None, P, m.s, False)], outs, a["l0_wp"], a["l0_bp"])
        values(nc, "l0sv", kit, h, a["l0_wsv"], a["l0_bsv"], GH, v_all)
        linear_attention(nc, "l0s", kit, h, a["l0_wsqk"], a["l0_bsqk"], v_all, out_all)
        normalise(nc, "l0sd", kit, out_all, extra=1e-6)
        project(nc, "l0sp", [(terms, 0, None, P, m.s, True)], outs, a["l0_wos"], a["l0_bos"])
    project(nc, "l0m", [([(0, 0)], 0, None, P, m.g, False)], [slices_of(m.s)], a["l0_wo"], a["l0_bo"])
    add_to(nc, "l0x", m.g, m.xn, m.s)
    layer_norm(nc, "l0n2", kit, m.s, m.g, a["l0_ln2"])
    with ExitStack() as ctx:
        mlp = ctx.enter_context(nc.sbuf_tensor("l0_mlp", [P, T], F32))
        one = ctx.enter_context(nc.sbuf_tensor("l0_one", [1, T], F32))
        move(nc, "l0one", [(one[:, :], a["c_one_row"])])
        mixture(nc, "l0mlp", m.g, one, a["l0_w1"], a["l0_w2"], a["l0_b2"], a["c_one_row"], mlp, 1, 4, ACT.Gelu, group=1)
        add_to(nc, "l0y", m.s, mlp, m.s)


def layer0_ffn(nc, kit, a, m):
    with ExitStack() as ctx:
        gates = ctx.enter_context(nc.sbuf_tensor("f0_gates", [16, T], F32))
        route(nc, "f0r", kit, m.xn, a["f0_router"], a["f0_router_b"], 8, 2, "share", gates, kit.gate_dram[0:8, :], 8)
        mixture(nc, "f0", m.xn, gates, a["f0_w1"], a["f0_w2"], a["f0_b2"], kit.gate_dram, m.g, 8, 4, ACT.Gelu)
    residual(nc, "f0x", m.x, m.s, m.g)


def layer1_attention(nc, kit, a, m):
    with ExitStack() as ctx:
        sb = lambda name, shape: ctx.enter_context(nc.sbuf_tensor(f"l1_{name}", shape, F32))
        decay_in, decay_out = (sb(f"decay_{n}", [P, NC, HP, 2]) for n in ("in", "out"))
        rate_in, rate_out = (sb(f"rate_{n}", [P, NC, 2 * HP]) for n in ("in", "out"))
        wqk, wv, wo = sb("wqk", [P, 2, HP, P]), sb("wv", [P, HP, P]), sb("wo", [P, HP, P])
        win, wout, wout_t = (sb(n, [P, HP, 2, F]) for n in ("win", "wout", "wout_t"))
        chunk_rates(nc, "l1r", kit, m.xn, a["l1_wrates"], kit.rate_dram, kit.decay_dram, decay_in, decay_out, rate_in, rate_out)
        move(nc, "l1w", [(wqk[:, :, :, :], a["l1_wqk"]), (wv[:, :, :], a["l1_wv"]), (wo[:, :, :], a["l1_wo"]),
                         (win[:, :, :, :], a["l1_win"]), (wout[:, :, :, :], a["l1_wout"]), (wout_t[:, :, :, :], a["l1_wout_t"])])
        fast_weights(nc, "l1", m.xn[:, :], wqk, wv, wo, win, wout, wout_t, decay_in, decay_out, rate_in, rate_out, m.s[:, :], kit.ident)


def layer1_ffn(nc, kit, a, m):
    with ExitStack() as ctx:
        slots = ctx.enter_context(nc.sbuf_tensor("f1_slots", [P, T // P], mybir.dt.uint32))
        x_slots, y_slots = (ctx.enter_context(nc.sbuf_tensor(f"f1_{n}", [P, T], F32)) for n in ("x_slots", "y_slots"))
        route(nc, "f1r", kit, m.xn, a["f1_router"], a["f1_router_b"], 8, 1, "capacity", None, None, 1, T // 8, slots)
        send_tokens(nc, "f1s", kit, m.xn, slots, kit.x_rows, kit.y_rows, x_slots)
        slot_experts(nc, "f1", x_slots, a["f1_w1"], a["f1_w2"], y_slots, 8, 4, ACT.Gelu, 2.0 ** 0.5 / 1.41421)
        fetch_results(nc, "f1t", kit, y_slots, slots, kit.y_rows, m.g)
    residual(nc, "f1x", m.x, m.s, m.g)


def layer2_attention(nc, kit, a, m):
    with ExitStack() as ctx:
        kit.spread = ctx.enter_context(nc.sbuf_tensor("l2_spread", [P, 8, P], F32))
        move(nc, "l2c", [(kit.spread[:, :, :], a["c_spread"])])
        dilated_attention(nc, "l2", kit, m.xn, a["l2_w"], a["l2_cols"], a["l2_taps"], m.s)


def layer2_ffn(nc, kit, a, m):
    layer_norm(nc, "f2n1", kit, m.xn, m.g, a["f2_g1"], rms=True)
    with ExitStack() as ctx:
        v_all = ctx.enter_context(nc.sbuf_tensor("f2_v", [P, 8, 8, 1, 32], F32))
        out_all = ctx.enter_context(nc.sbuf_tensor("f2_out", [P, 8, N], F32))
        query_parts(nc, "f2q", kit, m.g, a["f2_wq"], None, P, PARTS_Q, kit.q_dram, a["c_rope_q"])
        query_parts(nc, "f2k", kit, m.g, a["f2_wk"], None, 32, PARTS_K, kit.k4_dram, a["c_rope_k"])
        values(nc, "f2v", kit, m.g, a["f2_wv"], a["c_zero_row"][:, 0:32], 1, v_all)
        attend(nc, "f2a", "causal", E8 ** -0.5, kit.q_dram, kit.k4_dram, v_all, 1, out_all, kit)
        normalise(nc, "f2d", kit, out_all)
        project(nc, "f2p", [([(g, g) for g in range(4)], 0, None, P, m.g, False)], [heads_of(out_all, g) for g in range(4)],
                a["f2_wo"], a["c_zero_col"])
    add_to(nc, "f2x", m.g, m.xn, m.g)
    with ExitStack() as ctx:
        norm = ctx.enter_context(nc.sbuf_tensor("f2_norm", [P, T], F32))
        moe = ctx.enter_context(nc.sbuf_tensor("f2_moe", [P, T], F32))
        gates = ctx.enter_context(nc.sbuf_tensor("f2_gates", [16, T], F32))
        layer_norm(nc, "f2n2", kit, m.g, norm, a["f2_g2"], rms=True)
        route(nc, "f2r", kit, norm, a["f2_router"], a["c_zero_row"][:, 0:4], 4, 2, "share", gates, kit.gate_dram[0:4, :], 4)
        mixture(nc, "f2", norm, gates, a["f2_w13"], a["f2_w2"], a["c_zero_4"], kit.gate_dram, moe, 4, 3, ACT.Silu, gated_unit=True)
        residual(nc, "f2y", m.x, m.s, moe, plus=m.g)


def layer3_attention(nc, kit, a, m):
    with ExitStack() as ctx:
        v_all = ctx.enter_context(nc.sbuf_tensor("l3_v", [P, 8, 8, GH, 32], F32))
        out_all = ctx.enter_context(nc.sbuf_tensor("l3_out", [P, 8, N], F32))
        query_parts(nc, "l3q", kit, m.xn, a["l3_wq"], None, P, PARTS_Q, kit.q_dram)
        query_parts(nc, "l3k", kit, m.xn, a["l3_wk"], None, P, PARTS_K, kit.k_dram)
        values(nc, "l3v", kit, m.xn, a["l3_wv"], a["c_zero_row"][:, 0:P], GH, v_all)
        attend(nc, "l3a", "full", P ** -0.5, kit.q_dram, kit.k_dram, v_all, GH, out_all, kit)
        normalise(nc, "l3d", kit, out_all)
        project(nc, "l3p", [([(g, g) for g in range(4)], 0, None, P, m.s, False)], [heads_of(out_all, g) for g in range(4)],
                a["l3_wu"], a["l3_bu"])


def layer3_ffn(nc, kit, a, m):
    with ExitStack() as ctx:
        gates = ctx.enter_context(nc.sbuf_tensor("f3_gates", [16, T], F32))
        route(nc, "f3r", kit, m.xn, a["f3_router"], a["f3_router_b"], 15, 3, "plain", gates, kit.gate_dram[0:16, :], 16)
        mixture(nc, "f3", m.xn, gates, a["f3_w1"], a["f3_w2"], a["f3_b2"], kit.gate_dram, m.g, 16, 1, ACT.Relu)
    residual(nc, "f3x", m.x, m.s, m.g)


LAYERS = ((layer0_attention, layer0_ffn), (layer1_attention, layer1_ffn), (layer2_attention, layer2_ffn),
          (layer3_attention, layer3_ffn))


def network(nc, a, out, layers=(0, 1, 2, 3), s_out=None):
    kit, m = Kit(), Buffers()
    scratch = lambda name, shape, dt: nc.dram_tensor(name, shape, dt).ap()
    kit.q_dram = scratch("q_parts", [2, ROWS, 16, N], BF16)
    kit.k_dram = scratch("k_parts", [2, ROWS, 16, N], BF16)
    kit.k4_dram = scratch("k4_parts", [2, ROWS, 4, N], BF16)
    kit.gate_dram = scratch("gate_rows", [16, T], F32)
    kit.x_rows, kit.y_rows = scratch("x_rows", [2 * T, P], F32), scratch("y_rows", [2 * T, P], F32)
    kit.rate_dram = scratch("rates", [2, 2, NC, 2 * HP], F32)
    kit.decay_dram = scratch("decays", [2, 2, NC, HP, 2], F32)
    with ExitStack() as ctx:
        m.x, m.xn, m.s, m.g = (ctx.enter_context(nc.sbuf_tensor(n, [P, T], F32)) for n in ("resid", "normed", "mixer_out", "ffn_out"))
        load_constants(nc, ctx, kit, a)
        move(nc, "x", [(m.x[:, :], a["x"])])
        for i in layers:
            attention, ffn = LAYERS[i]
            layer_norm(nc, f"n{i}", kit, m.x, m.xn)
            attention(nc, kit, a, m)
            if s_out is not None:
                move(nc, f"dbg{i}", [(s_out, m.s[:, :])])
            ffn(nc, kit, a, m)
        move(nc, "y", [(out, m.x[:, :])])



def shape_constants():
    f = np.float32
    c = {}
    c["ident"] = np.eye(P, dtype=f)
    p = np.arange(P)
    c["den_sel"] = (p[:, None] == 32 * (p[None] // 32) + E8).astype(f)
    c["numbers"] = np.concatenate([np.broadcast_to(np.arange(8) * (T // 8) - 1, (P, 8)), T + p[:, None] + P * np.arange(T // P)[None]], 1)
    c["mean"] = np.full((P, P), 1.0 / P, f)
    c["ones"] = np.ones((P, P), f)
    c["upto"] = (p[:, None] <= p[None]).astype(f)
    col = p[None, None]
    head = 4 * np.arange(4)[None, :, None] + col // 32
    c["blocks"] = ((p[:, None, None] // E8 == head) & (col % 32 <= E8)).astype(f)
    c["head4"] = ((p[:, None] // E8) % 4 == np.arange(4)[None]).astype(f)
    c["heads"] = ((p[:, None] // E8 == np.arange(32)[None]) * f(E8 ** -0.5)).astype(f)
    scale = np.where(p < 32, 0.001 / 64, 0.9 / 64)
    c["columns"] = np.stack([np.full(P, 1e-5), np.full(P, 1.1920928955078125e-07), scale], 1).astype(f)
    lower = np.arange(16)[None, :] < np.arange(16)[:, None]
    c["lower"] = np.broadcast_to(lower.astype(f), (P, 16, 16))
    diag = np.where(p[:, None] <= p[None], 0, -1e30)
    prev = np.where(p[:, None] > p[None], 0, -1e30)
    c["masks"] = np.concatenate([diag, prev, prev.T, diag.T], 1).astype(f)
    k = np.arange(8)[None, :, None]
    c["spread"] = ((p[:, None, None] // 16 == k) & (p[:, None, None] % 16 == col // E8)).astype(f)
    inv_freq = (1.0 / 10000.0 ** (np.arange(0, E8, 2, dtype=f) / f(E8))).astype(f)
    freqs = np.arange(N, dtype=f)[:, None] * inv_freq[None]
    emb = np.concatenate([freqs, freqs], 1).astype(f)
    sign = np.where(np.arange(E8) < E8 // 2, -1.0, 1.0)[:, None]
    cos, sin = np.cos(emb).T.astype(f), (np.sin(emb).T * sign).astype(f)
    c["rope_q"] = np.stack([np.repeat(cos, 16, 0), np.repeat(sin, 16, 0)])
    c["rope_k"] = np.stack([np.repeat(cos, 4, 0), np.repeat(sin, 4, 0)])
    c["one_row"] = np.ones((1, T), f)
    c["zero_row"] = np.zeros((1, P), f)
    c["zero_col"] = np.zeros((P, 1), f)
    c["zero_4"] = np.zeros((4, P), f)
    return {"c_" + n: np.ascontiguousarray(v, dtype=f) for n, v in c.items()}


def lay_out(i):
    a = shape_constants()
    col = lambda *v: np.stack(v, 1)

    def by_dim(w, heads=16):
        return w.reshape(w.shape[:-1] + (heads, E8)).swapaxes(-1, -2).reshape(w.shape)

    def rotated(w, heads=16):
        r = w.reshape(w.shape[:-1] + (heads, E8))
        return np.concatenate([r[..., E8 // 2:], r[..., :E8 // 2]], -1).reshape(w.shape)

    def from_heads(w):
        out = np.zeros((4, 32, 4, P), w.dtype)
        out[:, :E8] = w.reshape(4, 4, E8, P).transpose(1, 2, 0, 3)
        return out.reshape(P, 4, P)

    def experts1(w, b):
        e, _, f = w.shape
        return np.concatenate([w, b.reshape(e, f // P, P).transpose(0, 2, 1)], 2)

    def experts2(w):
        e, f, _ = w.shape
        return w.reshape(e, f // P, P, P).transpose(0, 2, 1, 3).reshape(e, P, f)

    a["x"] = i["L0_attn_x"].reshape(T, P).T
    g = lambda n: i["L0_attn_" + n]
    a["l0_ln1"], a["l0_ln2"] = col(g("g1"), g("b1")), col(g("gm"), g("bm"))
    wq, wk, wv = np.split(g("Wqkv_a"), 3, 1)
    bq, bk, bv = np.split(g("bqkv_a"), 3)
    sq, sk, sv = np.split(g("Wqkv_s"), 3, 1)
    cq, ck, cv = np.split(g("bqkv_s"), 3)
    a["l0_wq"], a["l0_wk"], a["l0_wv"], a["l0_bv"] = by_dim(wq), by_dim(wk), wv, bv[None]
    a["l0_bq"], a["l0_bk"], a["l0_bsqk"] = by_dim(bq)[:, None], by_dim(bk)[:, None], col(cq, ck)
    a["l0_wp"], a["l0_bp"] = from_heads(g("Wp_a")), g("bp_a")[:, None]
    a["l0_wsv"], a["l0_bsv"], a["l0_wsqk"] = sv, cv[None], np.stack([sq, sk], 1)
    a["l0_wos"], a["l0_bos"] = from_heads(g("Wo_s")), g("bo_s")[:, None]
    a["l0_wo"], a["l0_bo"] = g("Wo")[:, None], g("bo")[:, None]
    a["l0_w1"], a["l0_w2"] = experts1(g("W1")[None], g("b1m")[None]), experts2(g("W2")[None])
    a["l0_b2"] = g("b2m")[None]
    g = lambda n: i["L0_ffn_" + n]
    a["f0_router"], a["f0_router_b"] = g("router_w"), g("router_b")[None]
    a["f0_w1"], a["f0_w2"], a["f0_b2"] = experts1(g("w1"), g("b1")), experts2(g("w2")), g("b2")
    g = lambda n: i["L1_attn_" + n]
    a["l1_wqk"] = np.stack([g("Wq").T.reshape(P, HP, P), g("Wk").T.reshape(P, HP, P)], 1)
    a["l1_wv"] = g("Wv").T.reshape(P, HP, P)
    a["l1_wo"] = g("Wo").T.reshape(HP, P, P).transpose(1, 0, 2)

    def pairs(w):
        return np.broadcast_to(w.reshape(HP, 2, F, F).transpose(1, 2, 0, 3).reshape(P, HP, 1, F), (P, HP, 2, F))
    a["l1_win"] = pairs(g("W_in_init")[0].transpose(1, 2, 0))
    a["l1_wout"] = pairs(g("W_out_init")[0].transpose(1, 0, 2))
    a["l1_wout_t"] = pairs(g("W_out_init")[0].transpose(1, 2, 0))
    by_parity = lambda w: w.reshape(2, HP, 2, P).transpose(0, 2, 1, 3).reshape(32, P)
    a["l1_wrates"] = np.concatenate([g("Wlr"), by_parity(g("Wbeta"))], 0).T
    g = lambda n: i["L1_ffn_" + n]
    a["f1_router"], a["f1_router_b"] = g("W_sw"), g("b_sw")[None]
    a["f1_w1"] = np.concatenate([experts1(g("W1"), g("b1")), g("b2")[:, :, None]], 2)
    a["f1_w2"] = experts2(g("W2"))
    g = lambda n: i["L2_attn_" + n]
    a["l2_w"] = np.stack(np.split(g("w_qkv"), 3, 1) + [g("w_gate"), g("w_out")], 1)
    a["l2_cols"] = col(*np.split(g("b_qkv"), 3), g("b_gate"), g("b_out"))
    offsets = [(1 << j) * tap for j in range(11) for tap in range(4)]
    order = [t for s in SHIFTS for t in range(44) if offsets[t] == s] + [t for t in range(44) if offsets[t] >= N]
    a["l2_taps"] = g("pos_bias")[order][None]
    g = lambda n: i["L2_ffn_" + n]
    a["f2_g1"], a["f2_g2"] = g("g1")[:, None], g("g2")[:, None]
    a["f2_wq"] = np.concatenate([by_dim(g("wq")), by_dim(rotated(g("wq")))], 1)
    a["f2_wk"] = np.concatenate([by_dim(g("wk"), 4), by_dim(rotated(g("wk"), 4), 4)], 1)
    a["f2_wv"], a["f2_wo"], a["f2_router"] = g("wv"), from_heads(g("wo")), g("gate")
    a["f2_w13"], a["f2_w2"] = np.concatenate([g("w1"), g("w3")], 2), experts2(g("w2"))
    g = lambda n: i["L3_attn_" + n]
    a["l3_wq"], a["l3_wk"], a["l3_wv"] = by_dim(g("Wq").T), by_dim(g("Wk").T), g("Wv").T
    a["l3_wu"], a["l3_bu"] = from_heads(g("Wu").T), g("bu")[:, None]
    g = lambda n: i["L3_ffn_" + n]
    a["f3_router"], a["f3_router_b"] = g("router_W"), g("router_b")[None]
    a["f3_w1"] = experts1(np.concatenate([g("eW1"), g("sW1")[None]]), np.concatenate([g("eb1"), g("sb1")[None]]))
    a["f3_w2"] = experts2(np.concatenate([g("eW2"), g("sW2")[None]]))
    a["f3_b2"] = np.concatenate([g("eb2"), g("sb2")[None]])
    return {n: np.ascontiguousarray(v) for n, v in a.items()}



def kernel(**inputs):
    import concourse.bacc as _bacc
    from concourse.bass_utils import run_bass_kernel_spmd as _run

    nc = _bacc.Bacc("TRN2", target_bir_lowering=False, num_devices=1)
    laid = lay_out({name: np.asarray(v) for name, v in inputs.items()})
    arrays, a = {}, {}
    for name, v in laid.items():
        arrays[f"in_{name}_dram"] = v
        a[name] = nc.dram_tensor(f"in_{name}_dram", v.shape, mybir.dt.from_np(v.dtype), kind="ExternalInput").ap()
    out = nc.dram_tensor("out_dram", (P, T), F32, kind="ExternalOutput").ap()
    network(nc, a, out)
    r = _run(nc, [arrays], core_ids=[0])
    return np.ascontiguousarray(r.results[0]["out_dram"].T).reshape(2, N, P)
```

```python
from contextlib import ExitStack
import numpy as np
import concourse.bass as bass
from concourse import mybir

F32 = mybir.dt.float32
BF16 = mybir.dt.bfloat16
ACT = mybir.ActivationFunctionType
ALU = mybir.AluOpType
AX = mybir.AxisListType

P = 128
T = 2048
SL = 512
NS = T // SL
N = 1024


class Kit:
    pass


def layer_norm(nc, tag, kit, src, dst, gain_dram=None, rms=False):
    tiles = T // P
    with nc.cleanup_on_exit(), ExitStack() as ctx:
        sb = lambda name, shape: ctx.enter_context(nc.sbuf_tensor(f"{tag}_{name}", shape, F32))
        sq = sb("sq", [P, T])
        gain = sb("gain", [P, 2])
        var, inv, tmp = (sb(n, [P, tiles]) for n in ("var", "inv", "tmp"))
        diag = sb("diag", [P, tiles, P])
        ps = [ctx.enter_context(nc.psum_tensor(f"{tag}_ps{s}", [P, SL], F32)) for s in range(NS)]
        ps_var = ctx.enter_context(nc.psum_tensor(f"{tag}_psvar", [P, tiles], F32))
        sem = lambda name: nc.alloc_semaphore(f"{tag}_{name}")
        loaded, mean_ready, centered, squared, var_ready = (sem(n) for n in ("loaded", "mean_ready", "centered", "squared", "var_ready"))
        chain, var_in, std_ready, diag_ready, spread, scaled = (sem(n) for n in (
            "chain", "var_in", "std_ready", "diag_ready", "spread", "scaled"))
        loads = int(gain_dram is not None)
        n_gain = gain_dram.shape[1] if loads else 0
        base = src if rms else dst
        eps = 1.1920928955078125e-07 if rms else 1e-5
        with nc.Block() as block:

            if loads:
                @block.sync
                def _(sp):
                    sp.dma_start(gain[:, 0:n_gain], gain_dram).then_inc(loaded, 16)
                    sp.wait_ge(loaded, 16)

            @block.tensor
            def _(pe):
                if not rms:
                    for s in range(NS):
                        pe.matmul(ps[s][:, :], kit.mean[:, :], src[:, s * SL:(s + 1) * SL], start=True, stop=True).then_inc(mean_ready, 1)
                for t in range(tiles):
                    if t % 4 == 0:
                        pe.wait_ge(squared, t // 4 + 1)
                    mm = pe.matmul(ps_var[:, t:t + 1], sq[:, t * P:(t + 1) * P], kit.mean[:, 0:1], start=True, stop=True)
                mm.then_inc(var_ready, 1)
                for s in range(NS):
                    pe.wait_ge(diag_ready, s + 1)
                    pe.matmul(ps[s][:, :], kit.ones[:, :], diag[:, 4 * s:4 * s + 4, :], start=True, stop=True).then_inc(spread, 1)

            @block.scalar
            def _(ac):
                for s in range(NS):
                    if not rms:
                        ac.wait_ge(centered, s + 1)
                    ac.activation(sq[:, s * SL:(s + 1) * SL], base[:, s * SL:(s + 1) * SL], ACT.Square).then_inc(squared, 1)
                ac.wait_ge(var_in, 1)
                ac.activation(inv[:, :], var[:, :], ACT.Sqrt).then_inc(std_ready, 1)

            @block.vector
            def _(ve):
                done = [0]

                def link(ins):
                    done[0] += 1
                    ins.then_inc(chain, 1)
                    ve.wait_ge(chain, done[0])

                if not rms:
                    for s in range(NS):
                        ve.wait_ge(mean_ready, s + 1)
                        ve.tensor_tensor(dst[:, s * SL:(s + 1) * SL], src[:, s * SL:(s + 1) * SL], ps[s][:, :], ALU.subtract).then_inc(centered, 1)
                ve.wait_ge(var_ready, 1)
                ve.tensor_scalar(var[:, :], ps_var[:, :], eps, None, ALU.add).then_inc(var_in, 1)
                ve.wait_ge(std_ready, 1)
                link(ve.reciprocal(inv[:, :], inv[:, :]))
                link(ve.tensor_tensor(tmp[:, :], inv[:, :], inv[:, :], ALU.mult))
                link(ve.tensor_tensor(tmp[:, :], tmp[:, :], var[:, :], ALU.mult))
                link(ve.tensor_scalar(tmp[:, :], tmp[:, :], -0.5, 1.5, ALU.mult, ALU.add))
                link(ve.tensor_tensor(inv[:, :], inv[:, :], tmp[:, :], ALU.mult))
                for s in range(NS):
                    ve.tensor_tensor(diag[:, 4 * s:4 * s + 4, :], kit.ident[:, :].unsqueeze(1).broadcast_to([P, 4, P]),
                                     inv[:, 4 * s:4 * s + 4].unsqueeze(2).broadcast_to([P, 4, P]), ALU.mult).then_inc(diag_ready, 1)
                if loads:
                    ve.wait_ge(loaded, 16)
                for s in range(NS):
                    part = slice(s * SL, (s + 1) * SL)
                    ve.wait_ge(spread, s + 1)
                    if gain_dram is None:
                        ve.tensor_tensor(dst[:, part], base[:, part], ps[s][:, :], ALU.mult).then_inc(scaled, 1)
                    else:
                        ve.scalar_tensor_tensor(dst[:, part], base[:, part], gain[:, 0:1], ps[s][:, :], ALU.mult, ALU.mult).then_inc(scaled, 1)
                    if n_gain == 2:
                        ve.wait_ge(scaled, s + 1)
                        ve.tensor_scalar(dst[:, part], dst[:, part], gain[:, 1:2], None, ALU.add).then_inc(centered, 1)


def project(nc, ctx, block, tag, jobs, ins, w_dram, columns_dram):
    n_w = w_dram.shape[1]
    w = ctx.enter_context(nc.sbuf_tensor(f"{tag}_w", [P, n_w, P], F32))
    cols = ctx.enter_context(nc.sbuf_tensor(f"{tag}_cols", [P, columns_dram.shape[1]], F32))
    ps = [ctx.enter_context(nc.psum_tensor(f"{tag}_ps{s}", [P, SL], F32)) for s in range(NS)]
    sem = lambda name: nc.alloc_semaphore(f"{tag}_{name}")
    loaded, product_ready, emptied, added = sem("loaded"), sem("product_ready"), sem("emptied"), sem("added")

    @block.sync
    def _(sp):
        sp.dma_start(w[:, :, :], w_dram).then_inc(loaded, 16)
        sp.dma_start(cols[:, :], columns_dram).then_inc(loaded, 16)
        sp.wait_ge(loaded, 32)

    @block.tensor
    def _(pe):
        pe.wait_ge(loaded, 32)
        for n, (terms, bias, act, rows, out, add) in enumerate(jobs):
            for s in range(NS):
                if n:
                    pe.wait_ge(emptied, (n - 1) * NS + s + 1)
                for i, (k, src) in enumerate(terms):
                    mm = pe.matmul(ps[s][0:rows, :], w[:, k, 0:rows], ins[src](s),
                                   start=i == 0, stop=i == len(terms) - 1)
                mm.then_inc(product_ready, 1)

    @block.scalar
    def _(ac):
        ac.wait_ge(loaded, 32)
        for n, (terms, bias, act, rows, out, add) in enumerate(jobs):
            for s in range(NS):
                ac.wait_ge(product_ready, n * NS + s + 1)
                target = ps[s][0:rows, :] if add else out[:, s * SL:(s + 1) * SL]
                if bias is None:
                    ins_ = ac.activation(target, ps[s][0:rows, :], ACT.Copy if act is None else act)
                else:
                    ins_ = ac.activation(target, ps[s][0:rows, :], ACT.Identity if act is None else act,
                                         bias=cols[0:rows, bias:bias + 1])
                ins_.then_inc(added if add else emptied, 1)

    if any(j[5] for j in jobs):
        @block.vector
        def _(ve):
            k = 0
            for n, (terms, bias, act, rows, out, add) in enumerate(jobs):
                if add:
                    for s in range(NS):
                        k += 1
                        ve.wait_ge(added, k)
                        part = out[:, s * SL:(s + 1) * SL]
                        ve.tensor_tensor(part, ps[s][0:rows, :], part, ALU.add).then_inc(emptied, 1)


def slices_of(a):
    return lambda s: a[:, s * SL:(s + 1) * SL]


def heads_of(out_all, g):
    return lambda s: out_all[:, (s // 2) * 4 + g, (s % 2) * SL:(s % 2 + 1) * SL]


def values(nc, ctx, block, tag, kit, xin, wv_dram, bias_dram, key_heads, v_all):
    nv = 4 * key_heads * E8
    w = ctx.enter_context(nc.sbuf_tensor(f"{tag}_w", [P, nv], F32))
    bias = ctx.enter_context(nc.sbuf_tensor(f"{tag}_b", [P, nv], F32))
    ps = [ctx.enter_context(nc.psum_tensor(f"{tag}_ps{i}", [P, 4, nv], F32)) for i in range(2)]
    sem = lambda name: nc.alloc_semaphore(f"{tag}_{name}")
    loaded, filled, product_ready, placed = sem("loaded"), sem("filled"), sem("product_ready"), sem("placed")

    @block.sync
    def _(sp):
        sp.dma_start(w[:, :], wv_dram).then_inc(loaded, 16)
        sp.dma_start(bias[:, :], bias_dram.broadcast_to([P, nv])).then_inc(loaded, 16)
        sp.wait_ge(loaded, 32)

    @block.gpsimd
    def _(po):
        po.memset(v_all[:, :, :, :, 9:32], 0.0).then_inc(filled, 1)
        po.memset(v_all[:, :, :, :, 8:9], 1.0).then_inc(filled, 1)

    @block.tensor
    def _(pe):
        pe.wait_ge(loaded, 32)
        for i in range(4):
            if i >= 2:
                pe.wait_ge(placed, 4 * (i - 1))
            for k in range(4):
                t = 4 * i + k
                mm = pe.matmul(ps[i % 2][:, k, :], xin[:, t * P:(t + 1) * P], w[:, :], start=True, stop=True)
            mm.then_inc(product_ready, 1)

    @block.vector
    def _(ve):
        ve.wait_ge(loaded, 32)
        for t in range(16):
            if t % 4 == 0:
                ve.wait_ge(product_ready, t // 4 + 1)
            b, kt = t // 8, t % 8
            ve.tensor_tensor(v_all[:, b * 4:b * 4 + 4, kt, :, 0:8],
                             ps[t // 4 % 2][:, t % 4, :].rearrange("p (g h e) -> p g h e", g=4, h=key_heads),
                             bias[:, :].rearrange("p (g h e) -> p g h e", g=4, h=key_heads), ALU.add).then_inc(placed, 1)


def query_parts(nc, ctx, block, tag, kit, xin, w_dram, bias_dram, rows, slots, dest, rope_dram=None):
    nw = 2 if rope_dram is not None else 1
    ring = 2 // nw
    sb = lambda name, shape, dt=F32: ctx.enter_context(nc.sbuf_tensor(f"{tag}_{name}", shape, dt))
    w = sb("w", [P, nw * rows])
    bias = sb("bias", [rows, 1])
    full = sb("full", [rows, T])
    rest = sb("rest", [rows, T])
    part = [sb(f"part{i}", [rows, T], BF16) for i in range(3)]
    rope = [sb(f"rope{i}", [rows, N]) for i in range(2)] if nw == 2 else []
    ps = [ctx.enter_context(nc.psum_tensor(f"{tag}_ps{s}", [rows, SL], F32)) for s in range(2)]
    sem = lambda name: nc.alloc_semaphore(f"{tag}_{name}")
    loaded, product_ready, whole, stored, turned = (sem(n) for n in ("loaded", "product_ready", "whole", "stored", "turned"))
    part_ready = [sem(f"part{i}_ready") for i in range(3)]
    rest_ready = sem("rest_ready")
    loads = 1 + (2 if nw == 2 else 0) + (bias_dram is not None)

    @block.sync
    def _(sp):
        sp.dma_start(w[:, :], w_dram).then_inc(loaded, 16)
        if bias_dram is not None:
            sp.dma_start(bias[:, :], bias_dram).then_inc(loaded, 16)
        for i, r in enumerate(rope):
            sp.dma_start(r[:, :], rope_dram[i, 0:rows]).then_inc(loaded, 16)

    @block.tensor
    def _(pe):
        pe.wait_ge(loaded, 16 * loads)
        for s in range(NS):
            if s >= ring:
                pe.wait_ge(whole, s - ring + 1)
            for k in range(nw):
                mm = pe.matmul(ps[k if nw == 2 else s % 2][:, :], w[:, k * rows:(k + 1) * rows], xin[:, s * SL:(s + 1) * SL],
                               start=True, stop=True)
            mm.then_inc(product_ready, 1)

    @block.scalar
    def _(ac):
        for s in range(NS if nw == 1 else 0):
            ac.wait_ge(product_ready, s + 1)
            if bias_dram is None:
                ac.activation(full[:, s * SL:(s + 1) * SL], ps[s % 2][:, :], ACT.Copy).then_inc(whole, 1)
            else:
                ac.activation(full[:, s * SL:(s + 1) * SL], ps[s % 2][:, :], ACT.Identity, bias=bias[:, 0:1]).then_inc(whole, 1)

    @block.vector
    def _(ve):
        for s in range(NS if nw == 2 else 0):
            ve.wait_ge(product_ready, s + 1)
            a, r = slice(s * SL, (s + 1) * SL), slice((s % 2) * SL, (s % 2 + 1) * SL)
            ve.tensor_tensor(full[:, a], ps[0][:, :], rope[0][:, r], ALU.mult).then_inc(turned, 1)
            ve.tensor_tensor(rest[:, a], ps[1][:, :], rope[1][:, r], ALU.mult).then_inc(turned, 1)
            ve.wait_ge(turned, 2 * s + 2)
            ve.tensor_tensor(full[:, a], full[:, a], rest[:, a], ALU.add).then_inc(whole, 1)

    def split_copy(ac, step):
        if step == 0:
            ac.wait_ge(whole, NS)
            ac.activation(part[0][:, :], full[:, :], ACT.Copy).then_inc(part_ready[0], 1)
        else:
            ac.wait_ge(rest_ready, 1)
            ac.activation(part[1][:, :], rest[:, :], ACT.Copy).then_inc(part_ready[1], 1)

    def split_rest(ve, step):
        if step == 0:
            ve.wait_ge(part_ready[0], 1)
            ve.tensor_tensor(rest[:, :], full[:, :], part[0][:, :], ALU.subtract).then_inc(rest_ready, 1)
        else:
            ve.wait_ge(part_ready[1], 1)
            ve.tensor_tensor(part[2][:, :], rest[:, :], part[1][:, :], ALU.subtract).then_inc(part_ready[2], 1)

    def store(sp):
        for p in range(3):
            sp.wait_ge(part_ready[p], 1)
            for i in range(len(slots)):
                if slots[i] == p:
                    sp.dma_start(dest[:, i * E8:(i + 1) * E8, :, :].rearrange("b e h n -> (e h) b n"),
                                 part[p][:, :].rearrange("r (b n) -> r b n", b=2)).then_inc(stored, 16)
        return stored, 16 * len(slots)

    return split_copy, split_rest, store


def split_parts(block, first, second):

    @block.scalar
    def _(ac):
        for step in range(2):
            for split_copy, _, _ in (first, second):
                split_copy(ac, step)

    @block.vector
    def _(ve):
        for step in range(2):
            for _, split_rest, _ in (first, second):
                split_rest(ve, step)

    return first[2], second[2]


def route(nc, ctx, block, tag, kit, xn, router_dram, bias_dram, experts, top, mode, gate_dram, total, capacity=None, slots=None):
    E = experts
    tiles = T // P
    sb = lambda name, shape, dt=F32: ctx.enter_context(nc.sbuf_tensor(f"{tag}_{name}", shape, dt))
    w = sb("w", [P, E])
    bias = sb("bias", [P, E])
    p = sb("p", [P, tiles, E])
    big = [sb(f"big{i}", [P, tiles, E, E]) for i in range(2)]
    col = sb("col", [P, tiles])
    rank = sb("rank", [P, tiles, E])
    out = sb("out", [P, tiles, total])
    gates = sb("gates", [total, T]) if mode != "capacity" else None
    ps_l = ctx.enter_context(nc.psum_tensor(f"{tag}_l", [P, tiles, E], F32))
    ps_c = ctx.enter_context(nc.psum_tensor(f"{tag}_c", [P, SL], F32))
    counts = ps_c[:, 0:tiles * E].rearrange("p (t e) -> p t e", e=E)
    sem = lambda name: nc.alloc_semaphore(f"{tag}_{name}")
    loaded, logits_ready, shifted, exp_done, chain, gates_ready, turned, gates_in, stored = (sem(n) for n in (
        "loaded", "logits_ready", "shifted", "exp_done", "chain", "gates_ready", "turned", "gates_in", "stored"))
    chosen, counted, filled = sem("chosen"), sem("counted"), sem("filled")


    @block.gpsimd
    def _(po):
        po.dma_start(w[:, :], router_dram).then_inc(loaded, 16)
        po.dma_start(bias[:, :], bias_dram.broadcast_to([P, E])).then_inc(loaded, 16)
        po.wait_ge(loaded, 32)
        if mode != "capacity":
            po.wait_ge(gates_in, NS)
            po.dma_start(gate_dram, gates[0:total, :]).then_inc(stored, 16)
            po.wait_ge(stored, 16)

    @block.tensor
    def _(pe):
        pe.wait_ge(loaded, 32)
        for t in range(tiles):
            mm = pe.matmul(ps_l[:, t, :], xn[:, t * P:(t + 1) * P], w[:, :], start=True, stop=True)
        mm.then_inc(logits_ready, 1)
        if mode == "capacity":
            pe.wait_ge(chosen, 1)
            pe.matmul(counts, kit.upto[:, :], rank[:, :, :], start=True, stop=False, skip_group_check=True)
            for t in range(tiles - 1):
                mm = pe.matmul(counts[:, t + 1:, :], kit.ones[:, :],
                               rank[:, t, :].unsqueeze(1).broadcast_to([P, tiles - 1 - t, E]), start=False,
                               stop=t == tiles - 2, skip_group_check=True)
            mm.then_inc(counted, 1)
            return
        pe.wait_ge(gates_ready, 1)
        for s in range(NS):
            if s:
                pe.wait_ge(gates_in, s)
            for k in range(4):
                mm = pe.transpose(ps_c[0:total, k * P:(k + 1) * P], out[:, 4 * s + k, :], kit.ident[:, :])
            mm.then_inc(turned, 1)

    @block.scalar
    def _(ac):
        ac.wait_ge(shifted, 1)
        ac.activation(p[:, :, :], p[:, :, :], ACT.Exp).then_inc(exp_done, 1)
        for s in range(NS if mode != "capacity" else 0):
            ac.wait_ge(turned, s + 1)
            ac.activation(gates[0:total, s * SL:(s + 1) * SL], ps_c[0:total, :], ACT.Copy).then_inc(gates_in, 1)

    @block.vector
    def _(ve):
        done = [0]

        def link(ins):
            done[0] += 1
            ins.then_inc(chain, 1)
            ve.wait_ge(chain, done[0])

        def across(a):
            return a.unsqueeze(2).broadcast_to([P, tiles, E])

        ve.wait_ge(loaded, 32)
        ve.wait_ge(logits_ready, 1)
        link(ve.tensor_tensor(p[:, :, :], ps_l[:, :, :], bias[:, :].unsqueeze(1).broadcast_to([P, tiles, E]), ALU.add))
        link(ve.tensor_reduce(col[:, :], p[:, :, :], AX.X, ALU.max))
        ve.tensor_tensor(p[:, :, :], p[:, :, :], across(col[:, :]), ALU.subtract).then_inc(shifted, 1)
        ve.wait_ge(exp_done, 1)
        link(ve.tensor_reduce(col[:, :], p[:, :, :], AX.X, ALU.add))
        link(ve.reciprocal(col[:, :], col[:, :]))
        link(ve.tensor_tensor(p[:, :, :], p[:, :, :], across(col[:, :]), ALU.mult))
        other = p[:, :, :].unsqueeze(2).broadcast_to([P, tiles, E, E])
        own = p[:, :, :].unsqueeze(3).broadcast_to([P, tiles, E, E])
        ve.tensor_tensor(big[0][:, :, :, :], other, own, ALU.is_gt).then_inc(filled, 1)
        link(ve.tensor_tensor(big[1][:, :, :, :], other, own, ALU.is_equal))
        lower = kit.lower[:, :, :][:, 0:E, 0:E].unsqueeze(1).broadcast_to([P, tiles, E, E])
        link(ve.tensor_tensor(big[1][:, :, :, :], big[1][:, :, :, :], lower, ALU.mult))
        ve.wait_ge(filled, 1)
        link(ve.tensor_tensor(big[0][:, :, :, :], big[0][:, :, :, :], big[1][:, :, :, :], ALU.add))
        link(ve.tensor_reduce(rank[:, :, :], big[0][:, :, :, :], AX.X, ALU.add))
        link(ve.tensor_scalar(rank[:, :, :], rank[:, :, :], top - 0.5, None, ALU.is_lt))
        if mode == "capacity":
            ve.sem_inc(chosen, 1)
            ve.wait_ge(counted, 1)
            link(ve.tensor_scalar(p[:, :, :], counts, capacity + 0.5, None, ALU.is_lt))
            link(ve.tensor_tensor(p[:, :, :], p[:, :, :], rank[:, :, :], ALU.mult))
            link(ve.tensor_tensor(rank[:, :, :], counts, kit.numbers[:, 0:E].unsqueeze(1).broadcast_to([P, tiles, E]), ALU.add))
            link(ve.tensor_tensor(rank[:, :, :], rank[:, :, :], p[:, :, :], ALU.mult))
            link(ve.tensor_reduce(col[:, :], p[:, :, :], AX.X, ALU.add))
            link(ve.tensor_scalar(col[:, :], col[:, :], -1.0, 1.0, ALU.mult, ALU.add))
            link(ve.tensor_tensor(col[:, :], col[:, :], kit.numbers[:, E:E + tiles], ALU.mult))
            link(ve.tensor_reduce(out[:, :, 0:1], rank[:, :, :], AX.X, ALU.add))
            link(ve.tensor_tensor(col[:, :], col[:, :], out[:, :, 0], ALU.add))
            ve.tensor_copy(slots[:, :], col[:, :]).then_inc(gates_ready, 1)
        elif mode == "share":
            link(ve.tensor_tensor(p[:, :, :], p[:, :, :], rank[:, :, :], ALU.mult))
            link(ve.tensor_reduce(col[:, :], p[:, :, :], AX.X, ALU.add))
            link(ve.reciprocal(col[:, :], col[:, :]))
            ve.tensor_tensor(out[:, :, :], p[:, :, :], across(col[:, :]), ALU.mult).then_inc(gates_ready, 1)
        else:
            link(ve.memset(out[:, :, E:E + 1], 1.0))
            ve.tensor_tensor(out[:, :, 0:E], p[:, :, :], rank[:, :, :], ALU.mult).then_inc(gates_ready, 1)


def residual(nc, tag, x, s_out, result, plus=None):
    with nc.cleanup_on_exit():
        sem = lambda name: nc.alloc_semaphore(f"{tag}_{name}")
        complete, silu_done, multiplied, updated = (sem(n) for n in ("complete", "silu_done", "multiplied", "updated"))
        with nc.Block() as block:

            @block.scalar
            def _(ac):
                for s in range(NS):
                    part = slice(s * SL, (s + 1) * SL)
                    if plus is not None:
                        ac.wait_ge(complete, s + 1)
                    ac.activation(result[:, part], result[:, part], ACT.Silu).then_inc(silu_done, 1)

            @block.vector
            def _(ve):
                for s in range(NS if plus is not None else 0):
                    part = slice(s * SL, (s + 1) * SL)
                    ve.tensor_tensor(result[:, part], result[:, part], plus[:, part], ALU.add).then_inc(complete, 1)
                for s in range(NS):
                    part = slice(s * SL, (s + 1) * SL)
                    ve.wait_ge(silu_done, s + 1)
                    ve.tensor_tensor(s_out[:, part], s_out[:, part], result[:, part], ALU.mult).then_inc(multiplied, 1)
                    ve.wait_ge(multiplied, s + 1)
                    ve.tensor_tensor(x[:, part], x[:, part], s_out[:, part], ALU.add).then_inc(updated, 1)


def add_to(nc, tag, a, b, out):
    with nc.cleanup_on_exit():
        added = nc.alloc_semaphore(f"{tag}_added")
        with nc.Block() as block:

            @block.vector
            def _(ve):
                for s in range(NS):
                    part = slice(s * SL, (s + 1) * SL)
                    ve.tensor_tensor(out[:, part], a[:, part], b[:, part], ALU.add).then_inc(added, 1)


def linear_attention(nc, tag, kit, xin, w_dram, cols_dram, v_all, out_all):
    chunks = N // P
    with nc.cleanup_on_exit(), ExitStack() as ctx:
        sb = lambda name, shape, dt=F32: ctx.enter_context(nc.sbuf_tensor(f"{tag}_{name}", shape, dt))
        w = sb("w", [P, 2, P])
        cols = sb("cols", [P, 2])
        qk = [sb(f"qk{i}", [P, T]) for i in range(2)]
        low = sb("low", [P, T])
        qm = [sb(f"qm{i}", [P, 16, P]) for i in range(3)]
        a_sb = [sb(f"weights{i}", [P, 4, 4, P]) for i in range(2)]
        ktok = [sb(f"ktok{i}", [P, P]) for i in range(2)]
        state = [sb(f"state{i}", [P, 4, P]) for i in range(2)]
        upd = sb("upd", [P, 4, P])
        ps_a = [ctx.enter_context(nc.psum_tensor(f"{tag}_a{g}", [P, 4, P], F32)) for g in range(4)]
        ps_o = [ctx.enter_context(nc.psum_tensor(f"{tag}_o{i}", [P, 4, P], F32)) for i in range(2)]
        ps_u = ctx.enter_context(nc.psum_tensor(f"{tag}_u", [P, 4, P], F32))
        ps_k = ctx.enter_context(nc.psum_tensor(f"{tag}_k", [P, P], F32))
        sem = lambda name: nc.alloc_semaphore(f"{tag}_{name}")
        loaded, product_ready, biased, clipped, exp_done, feature = (sem(n) for n in (
            "loaded", "product_ready", "biased", "clipped", "exp_done", "feature"))
        split_ready, a_ready, masked, turned, ktok_in, num_ready, num_in, u_ready, state_ready = (
            sem(n) for n in ("split_ready", "a_ready", "masked", "turned", "ktok_in", "num_ready", "num_in",
                             "u_ready", "state_ready"))
        clipped_high, updated = sem("clipped_high"), sem("updated")
        last = 2 * chunks - 1
        with nc.Block() as block:

            @block.sync
            def _(sp):
                sp.dma_start(w[:, :, :], w_dram).then_inc(loaded, 16)
                sp.dma_start(cols[:, :], cols_dram).then_inc(loaded, 16)
                sp.wait_ge(loaded, 32)

            @block.gpsimd
            def _(po):
                po.wait_ge(feature, 1)
                for t in range(last + 1):
                    if t >= 3:
                        po.wait_ge(a_ready, 4 * (t - 2))
                    po.tensor_tensor(qm[t % 3][:, :, :], qk[0][:, t * P:(t + 1) * P].unsqueeze(1).broadcast_to([P, 16, P]),
                                     kit.head16[:, :].unsqueeze(2).broadcast_to([P, 16, P]), ALU.mult).then_inc(split_ready, 1)

            @block.tensor
            def _(pe):
                pe.wait_ge(loaded, 32)
                for k in range(2):
                    for s in range(NS):
                        if k:
                            pe.wait_ge(biased, s + 1)
                        pe.matmul(ps_a[s][:, :, :], w[:, k, :], xin[:, s * SL:(s + 1) * SL], start=True, stop=True).then_inc(product_ready, 1)
                pe.wait_ge(feature, 2)

                def scores(t):
                    tok = slice(t * P, (t + 1) * P)
                    pe.wait_ge(split_ready, t + 1)
                    for g in range(4):
                        if t:
                            pe.wait_ge(masked, 4 * (t - 1) + g + 1)
                        pe.matmul(ps_a[g][:, :, :], qk[1][:, tok], qm[t % 3][:, 4 * g:4 * g + 4, :], start=True, stop=True).then_inc(a_ready, 1)
                    if t:
                        pe.wait_ge(ktok_in, t)
                    pe.transpose(ps_k[:, :], qk[1][:, tok], kit.ident[:, :]).then_inc(turned, 1)

                scores(0)
                for t in range(last + 1):
                    b, kt = t // chunks, t % chunks
                    tok = slice(t * P, (t + 1) * P)
                    if t < last:
                        scores(t + 1)
                    pe.wait_ge(ktok_in, t + 1)
                    if t:
                        pe.wait_ge(updated, t)
                    pe.matmul(ps_u[:, :, :], ktok[t % 2][:, :], v_all[:, b * 4:b * 4 + 4, kt, :, :].rearrange("p g h c -> p g (h c)"),
                              start=True, stop=True).then_inc(u_ready, 1)
                    pe.wait_ge(state_ready, t + 1)
                    if t >= 2:
                        pe.wait_ge(num_in, t - 1)
                    for g in range(4):
                        pe.wait_ge(masked, 4 * t + g + 1)
                        pe.matmul(ps_o[t % 2][:, g, :], state[t % 2][:, g, :], qk[0][:, tok], start=True, stop=False, skip_group_check=True)
                        for j in range(4):
                            mm = pe.matmul(ps_o[t % 2][32 * j:32 * j + 32, g, :], v_all[:, b * 4 + g, kt, j, :], a_sb[t % 2][:, g, j, :],
                                           start=False, stop=True, skip_group_check=True)
                    mm.then_inc(num_ready, 1)

            @block.scalar
            def _(ac):
                ac.wait_ge(loaded, 32)
                for k in range(2):
                    for s in range(NS):
                        ac.wait_ge(product_ready, k * NS + s + 1)
                        ac.activation(qk[k][:, s * SL:(s + 1) * SL], ps_a[s][:, :, :].rearrange("p a n -> p (a n)"), ACT.Identity,
                                      bias=cols[:, k:k + 1]).then_inc(biased, 1)
                for k in range(2):
                    ac.wait_ge(clipped, k + 1)
                    ac.activation(low[:, :], low[:, :], ACT.Exp).then_inc(exp_done, 1)
                for t in range(last + 2):
                    if t <= last:
                        ac.wait_ge(turned, t + 1)
                        if t >= 2:
                            ac.wait_ge(u_ready, t - 1)
                        ac.activation(ktok[t % 2][:, :], ps_k[:, :], ACT.Copy).then_inc(ktok_in, 1)
                    if t:
                        b, kt = (t - 1) // chunks, (t - 1) % chunks
                        ac.wait_ge(num_ready, t)
                        ac.activation(out_all[:, b * 4:b * 4 + 4, kt * P:(kt + 1) * P], ps_o[(t - 1) % 2][:, :, :], ACT.Copy).then_inc(num_in, 1)

            @block.vector
            def _(ve):
                for k in range(2):
                    ve.wait_ge(biased, NS * (k + 1))
                    if k:
                        ve.wait_ge(feature, 1)
                    ve.tensor_scalar(low[:, :], qk[k][:, :], 0.0, E8 ** -0.5 if k == 0 else 1.0, ALU.min, ALU.mult).then_inc(clipped, 1)
                    ve.wait_ge(clipped, k + 1)
                    ve.tensor_scalar(qk[k][:, :], qk[k][:, :], 0.0, E8 ** -0.5 if k == 0 else 1.0, ALU.max, ALU.mult).then_inc(clipped_high, 1)
                    ve.wait_ge(exp_done, k + 1)
                    ve.wait_ge(clipped_high, k + 1)
                    ve.scalar_tensor_tensor(qk[k][:, :], low[:, :], 1.0001 - 1.0, qk[k][:, :], ALU.add, ALU.add).then_inc(feature, 1)
                ve.wait_ge(feature, 2)
                ve.memset(state[0][:, :, :], 0.0).then_inc(state_ready, 1)
                for t in range(last + 1):
                    if t >= 2:
                        ve.wait_ge(num_ready, t - 1)
                    for g in range(4):
                        ve.wait_ge(a_ready, 4 * t + g + 1)
                        ve.tensor_tensor(a_sb[t % 2][:, g, :, :], ps_a[g][:, :, :], kit.upto[:, :].unsqueeze(1).broadcast_to([P, 4, P]), ALU.mult).then_inc(masked, 1)
                    ve.wait_ge(u_ready, t + 1)
                    if t < last:
                        if t:
                            ve.wait_ge(num_ready, t)
                        if t % chunks == chunks - 1:
                            ve.sem_inc(updated, 1)
                            ve.memset(state[(t + 1) % 2][:, :, :], 0.0).then_inc(state_ready, 1)
                        else:
                            ve.tensor_tensor(upd[:, :, :], ps_u[:, :, :], kit.blocks[:, :, :], ALU.mult).then_inc(updated, 1)
                            ve.wait_ge(updated, t + 1)
                            ve.wait_ge(state_ready, t + 1)
                            ve.tensor_tensor(state[(t + 1) % 2][:, :, :], state[t % 2][:, :, :], upd[:, :, :], ALU.add).then_inc(state_ready, 1)


def mixture(nc, tag, xn, w1_dram, w2_dram, b2_dram, gate_dram, result, experts, chunks, act,
            act_scale=1.0, group=2, gated_unit=False):
    step_count = group * NS * chunks
    ring = 2 if gated_unit else 4
    lag = 1 if gated_unit else 2
    kinds = 2 if gated_unit else 1
    turns = experts // group
    F = chunks * P
    with nc.cleanup_on_exit(), ExitStack() as ctx:
        sb = lambda name, shape, dt=F32: ctx.enter_context(nc.sbuf_tensor(f"{tag}_{name}", shape, dt))
        w1 = [sb(f"w1_{u}", [P, kinds * F + (0 if gated_unit else chunks)]) for u in range(group)]
        w2 = [sb(f"w2_{u}", [P, F]) for u in range(group)]
        gate = [sb(f"gate_{u}", [P, T]) for u in range(group)]
        b2 = sb("b2", [experts, P])
        gates = sb("gates", [experts, T])
        hidden = sb("hidden", [P, ring, SL])
        ps_h = [ctx.enter_context(nc.psum_tensor(f"{tag}_psh{r}", [P, SL], F32)) for r in range(4)]
        ps_o = [ctx.enter_context(nc.psum_tensor(f"{tag}_pso{s}", [P, SL], F32)) for s in range(NS)]
        sem = lambda name: nc.alloc_semaphore(f"{tag}_{name}")
        expert_in = [sem(f"expert_in{u}") for u in range(group)]
        b2_in = sem("b2_in")
        scaled = sem("scaled")
        h_ready = sem("h_ready")
        act_done = sem("act_done")
        lifted = sem("lifted")
        gated = sem("gated")
        added = sem("added")
        evacuated = sem("evacuated")
        passed = sem("passed")
        steps = [(u, s, c) for u in range(group) for s in range(NS) for c in range(chunks)]
        per = NS * chunks
        with nc.Block() as block:

            def load(sp, u, e):
                sp.dma_start(w1[u][:, :], w1_dram[bass.ds(e, 1), :, :].rearrange("e p n -> (e p) n")).then_inc(expert_in[u], 16)
                sp.dma_start(w2[u][:, :], w2_dram[bass.ds(e, 1), :, :].rearrange("e p n -> (e p) n")).then_inc(expert_in[u], 16)
                sp.dma_start(gate[u][:, :], gate_dram[bass.ds(e, 1), :].broadcast_to([P, T])).then_inc(expert_in[u], 16)

            @block.sync
            def _(sp):
                sp.dma_start(b2[:, :], b2_dram).then_inc(b2_in, 16)
                sp.dma_start(gates[:, :], gate_dram[0:experts, :]).then_inc(b2_in, 16)
                for u in range(group):
                    load(sp, u, u)
                if turns > 1:
                    with sp.Fori(0, turns - 1) as it:
                        for u in range(group):
                            sp.wait_ge(added, it * step_count + ((u + 1) * per + 1))
                            load(sp, u, it * group + (u + group))
                sp.wait_ge(b2_in, 32)
                for u in range(group):
                    sp.wait_ge(expert_in[u], 48 * turns)

            @block.tensor
            def _(pe):
                pe.wait_ge(b2_in, 32)
                for s in range(NS):
                    mm = pe.matmul(ps_o[s][:, :], b2[:, :], gates[0:experts, s * SL:(s + 1) * SL], start=True, stop=False, skip_group_check=True)
                mm.then_inc(added, 1)
                with pe.Fori(0, turns) as it:
                    for k in range(step_count + lag):
                        if k < step_count:
                            u, s, c = steps[k]
                            if s == 0 and c == 0:
                                pe.wait_ge(expert_in[u], it * 48 + 48)
                            if k >= ring:
                                pe.wait_ge(lifted if gated_unit else act_done, it * step_count + (k - ring + 1))
                            elif gated_unit:
                                pe.wait_ge(added, it * step_count + 1)
                            for m in range(kinds):
                                mm = pe.matmul(ps_h[(k % ring) * kinds + m][:, :], w1[u][:, m * F + c * P:m * F + (c + 1) * P],
                                               xn[:, s * SL:(s + 1) * SL], start=True, stop=True)
                            mm.then_inc(h_ready, 1)
                        if k >= lag:
                            u, s, c = steps[k - lag]
                            pe.wait_ge(gated, it * step_count + (k - lag + 1))
                            pe.matmul(ps_o[s][:, :], w2[u][:, c * P:(c + 1) * P], hidden[:, (k - lag) % ring, :],
                                      start=False, stop=False, skip_group_check=True).then_inc(added, 1)

            @block.scalar
            def _(ac):
                with ac.Fori(0, turns) as it:
                    for k, (u, s, c) in enumerate(steps):
                        ac.wait_ge(h_ready, it * step_count + (k + 1))
                        if act_scale != 1.0 and s == 0 and c == 0:
                            ac.wait_ge(scaled, it * (2 * group) + (2 * u + 1))
                        ac.wait_ge(added, it * step_count + (max(k - ring + 1, 0) + 1))
                        out, src = hidden[:, k % ring, :], ps_h[(k % ring) * kinds][:, :]
                        if gated_unit:
                            ac.activation(out, src, act).then_inc(act_done, 1)
                        else:
                            ac.activation(out, src, act, bias=w1[u][:, F + c:F + c + 1], scale=act_scale).then_inc(act_done, 1)

            if act_scale != 1.0:
                @block.gpsimd
                def _(po):
                    with po.Fori(0, turns) as it:
                        for u in range(group):
                            po.wait_ge(expert_in[u], it * 48 + 48)
                            po.sem_inc(passed, 1)
                            po.tensor_scalar(w1[u][:, F:F + chunks], w1[u][:, F:F + chunks], act_scale, None, ALU.mult).then_inc(scaled, 1)
                            po.tensor_scalar(gate[u][:, :], gate[u][:, :], 1.0 / act_scale, None, ALU.mult).then_inc(scaled, 1)

            @block.vector
            def _(ve):
                with ve.Fori(0, turns) as it:
                    for k, (u, s, c) in enumerate(steps):
                        ve.wait_ge(act_done, it * step_count + (k + 1))
                        if act_scale != 1.0 and s == 0 and c == 0:
                            ve.wait_ge(scaled, it * (2 * group) + (2 * u + 2))
                        part = hidden[:, k % ring, :]
                        if gated_unit:
                            ve.tensor_tensor(part, ps_h[(k % ring) * kinds + 1][:, :], part, ALU.mult).then_inc(lifted, 1)
                            ve.wait_ge(lifted, it * step_count + (k + 1))
                        ve.tensor_tensor(part, part, gate[u][:, s * SL:(s + 1) * SL], ALU.mult).then_inc(gated, 1)
                ve.wait_ge(added, turns * step_count + 1)
                for s in range(NS):
                    ve.tensor_copy(result[:, s * SL:(s + 1) * SL], ps_o[s][:, :]).then_inc(evacuated, 1)


def slot_rows(dram, first):
    return dram[first:first + T, :].rearrange("(t p) f -> p t f", p=P)


def send_tokens(nc, tag, kit, xn, slots, x_rows, y_rows, x_slots):
    tiles = T // P
    with nc.cleanup_on_exit(), ExitStack() as ctx:
        by_token = ctx.enter_context(nc.sbuf_tensor(f"{tag}_token", [P, tiles, P], F32))
        by_slot = ctx.enter_context(nc.sbuf_tensor(f"{tag}_slot", [P, tiles, P], F32))
        ps = [ctx.enter_context(nc.psum_tensor(f"{tag}_ps{i}", [P, SL], F32)) for i in range(8)]
        sem = lambda name: nc.alloc_semaphore(f"{tag}_{name}")
        zeroed, emptied, turned, copied, kept, sent, back, turned_slots, placed = (sem(n) for n in (
            "zeroed", "emptied", "turned", "copied", "kept", "sent", "back", "turned_slots", "placed"))
        with nc.Block() as block:

            @block.vector
            def _(ve):
                ve.memset(by_slot[:, :, :], 0.0).then_inc(zeroed, 1)

            @block.sync
            def _(sp):
                sp.wait_ge(zeroed, 1)
                sp.dma_start(slot_rows(x_rows, 0), by_slot[:, :, :]).then_inc(emptied, 16)
                sp.wait_ge(copied, 4)
                sp.dma_start(slot_rows(y_rows, T), by_token[:, :, :]).then_inc(kept, 16)
                sp.wait_ge(emptied, 16)
                sp.wait_ge(sent, 16 * tiles)
                sp.dma_start(by_slot[:, :, :], slot_rows(x_rows, 0)).then_inc(back, 16)
                sp.wait_ge(kept, 16)
                sp.wait_ge(back, 16)

            @block.gpsimd
            def _(po):
                po.wait_ge(emptied, 16)
                for t in range(tiles):
                    if t % 4 == 0:
                        po.wait_ge(copied, t // 4 + 1)
                    po.indirect_dma_start(x_rows, bass.IndirectOffsetOnAxis(ap=slots[:, t:t + 1], axis=0),
                                          by_token[:, t, :], None).then_inc(sent, 16)
                po.wait_ge(sent, 16 * tiles)

            @block.tensor
            def _(pe):
                for s in range(4):
                    for k in range(4):
                        t = 4 * s + k
                        mm = pe.transpose(ps[s][:, k * P:(k + 1) * P], xn[:, t * P:(t + 1) * P], kit.ident[:, :])
                    mm.then_inc(turned, 1)
                pe.wait_ge(back, 16)
                for s in range(4):
                    for k in range(4):
                        mm = pe.transpose(ps[4 + s][:, k * P:(k + 1) * P], by_slot[:, 4 * s + k, :], kit.ident[:, :])
                    mm.then_inc(turned_slots, 1)

            @block.scalar
            def _(ac):
                for s in range(4):
                    ac.wait_ge(turned, s + 1)
                    ac.activation(by_token[:, 4 * s:4 * s + 4, :].rearrange("p t f -> p (t f)"), ps[s][:, :], ACT.Copy).then_inc(copied, 1)
                for s in range(4):
                    ac.wait_ge(turned_slots, s + 1)
                    ac.activation(x_slots[:, s * SL:(s + 1) * SL], ps[4 + s][:, :], ACT.Copy).then_inc(placed, 1)


def slot_experts(nc, tag, x_slots, w1_dram, w2_dram, y_slots, experts, chunks, act, act_scale):
    F = chunks * P
    cap = T // experts
    group, ring, lag = 2, 4, 2
    turns = experts // group
    n = group * chunks
    with nc.cleanup_on_exit(), ExitStack() as ctx:
        sb = lambda name, shape: ctx.enter_context(nc.sbuf_tensor(f"{tag}_{name}", shape, F32))
        w1 = [sb(f"w1_{u}", [P, F + chunks + 1]) for u in range(group)]
        w2 = [sb(f"w2_{u}", [P, F]) for u in range(group)]
        hidden = sb("hidden", [P, ring, cap])
        ps_h = [ctx.enter_context(nc.psum_tensor(f"{tag}_h{r}", [P, cap], F32)) for r in range(ring)]
        ps_o = [ctx.enter_context(nc.psum_tensor(f"{tag}_o{u}", [P, cap], F32)) for u in range(group)]
        sem = lambda name: nc.alloc_semaphore(f"{tag}_{name}")
        expert_in = [sem(f"expert_in{u}") for u in range(group)]
        scaled, passed, h_ready, act_done, added = (sem(x) for x in ("scaled", "passed", "h_ready", "act_done", "added"))
        finished = sem("finished")
        with nc.Block() as block:

            def load(sp, u, e):
                sp.dma_start(w1[u][:, :], w1_dram[bass.ds(e, 1), :, :].rearrange("e p n -> (e p) n")).then_inc(expert_in[u], 16)
                sp.dma_start(w2[u][:, :], w2_dram[bass.ds(e, 1), :, :].rearrange("e p n -> (e p) n")).then_inc(expert_in[u], 16)

            @block.sync
            def _(sp):
                for u in range(group):
                    load(sp, u, u)
                with sp.Fori(0, turns - 1) as it:
                    for u in range(group):
                        sp.wait_ge(finished, it * group + (u + 1 + 2))
                        load(sp, u, it * group + (u + group))
                for u in range(group):
                    sp.wait_ge(expert_in[u], 32 * turns)

            @block.gpsimd
            def _(po):
                with po.Fori(0, turns) as it:
                    for u in range(group):
                        po.wait_ge(expert_in[u], it * 32 + 32)
                        po.sem_inc(passed, 1)
                        po.tensor_scalar(w1[u][:, F:F + chunks], w1[u][:, F:F + chunks], act_scale, None, ALU.mult).then_inc(scaled, 1)

            @block.tensor
            def _(pe):
                with pe.Fori(0, turns) as it:
                    for k in range(n + lag):
                        if k < n:
                            u, c = k // chunks, k % chunks
                            if c == 0:
                                pe.wait_ge(expert_in[u], it * 32 + 32)
                            if k >= ring:
                                pe.wait_ge(act_done, it * n + (k - ring + 1))
                            pe.matmul(ps_h[k % ring][:, :], w1[u][:, c * P:(c + 1) * P],
                                      x_slots[:, bass.ds((it * group + u) * cap, cap)], start=True, stop=True).then_inc(h_ready, 1)
                        if k >= lag:
                            m = k - lag
                            u, c = m // chunks, m % chunks
                            if c == 0:
                                pe.wait_ge(finished, it * group + (u + 1))
                            pe.wait_ge(act_done, it * n + (m + 1))
                            pe.matmul(ps_o[u][:, :], w2[u][:, c * P:(c + 1) * P], hidden[:, m % ring, :],
                                      start=c == 0, stop=c == chunks - 1).then_inc(added, 1)

            @block.scalar
            def _(ac):
                with ac.Fori(0, turns) as it:
                    for k in range(n):
                        u, c = k // chunks, k % chunks
                        ac.wait_ge(h_ready, it * n + (k + 1))
                        if c == 0:
                            ac.wait_ge(scaled, it * group + (u + 1))
                        if k >= ring:
                            ac.wait_ge(added, it * n + (k - ring + 1))
                        ac.activation(hidden[:, k % ring, :], ps_h[k % ring][:, :], act, bias=w1[u][:, F + c:F + c + 1],
                                      scale=act_scale).then_inc(act_done, 1)

            @block.vector
            def _(ve):
                ve.sem_inc(finished, 2)
                with ve.Fori(0, turns) as it:
                    for u in range(group):
                        ve.wait_ge(added, it * n + (u + 1) * chunks)
                        ve.tensor_scalar(y_slots[:, bass.ds((it * group + u) * cap, cap)], ps_o[u][:, :], 1.0 / act_scale,
                                         w1[u][:, F + chunks:F + chunks + 1], ALU.mult, ALU.add).then_inc(finished, 1)


def fetch_results(nc, tag, kit, y_slots, slots, y_rows, result):
    tiles = T // P
    with nc.cleanup_on_exit(), ExitStack() as ctx:
        by_slot = ctx.enter_context(nc.sbuf_tensor(f"{tag}_slot", [P, tiles, P], F32))
        by_token = ctx.enter_context(nc.sbuf_tensor(f"{tag}_token", [P, tiles, P], F32))
        ps = [ctx.enter_context(nc.psum_tensor(f"{tag}_ps{i}", [P, SL], F32)) for i in range(8)]
        sem = lambda name: nc.alloc_semaphore(f"{tag}_{name}")
        turned, copied, stored, turned_tokens, placed = (sem(n) for n in ("turned", "copied", "stored", "turned_tokens", "placed"))
        fetched = [sem(f"fetched{i}") for i in range(4)]
        with nc.Block() as block:

            @block.sync
            def _(sp):
                sp.wait_ge(copied, 4)
                sp.dma_start(slot_rows(y_rows, 0), by_slot[:, :, :]).then_inc(stored, 16)
                sp.wait_ge(stored, 16)

            @block.gpsimd
            def _(po):
                po.wait_ge(stored, 16)
                for t in range(tiles):
                    po.indirect_dma_start(by_token[:, t, :], None, y_rows,
                                          bass.IndirectOffsetOnAxis(ap=slots[:, t:t + 1], axis=0)).then_inc(fetched[t // 4], 16)
                for i in range(4):
                    po.wait_ge(fetched[i], 64)

            @block.tensor
            def _(pe):
                for s in range(4):
                    for k in range(4):
                        t = 4 * s + k
                        mm = pe.transpose(ps[s][:, k * P:(k + 1) * P], y_slots[:, t * P:(t + 1) * P], kit.ident[:, :])
                    mm.then_inc(turned, 1)
                for s in range(4):
                    pe.wait_ge(fetched[s], 64)
                    for k in range(4):
                        mm = pe.transpose(ps[4 + s][:, k * P:(k + 1) * P], by_token[:, 4 * s + k, :], kit.ident[:, :])
                    mm.then_inc(turned_tokens, 1)

            @block.scalar
            def _(ac):
                for s in range(4):
                    ac.wait_ge(turned, s + 1)
                    ac.activation(by_slot[:, 4 * s:4 * s + 4, :].rearrange("p t f -> p (t f)"), ps[s][:, :], ACT.Copy).then_inc(copied, 1)
                for s in range(4):
                    ac.wait_ge(turned_tokens, s + 1)
                    ac.activation(result[:, s * SL:(s + 1) * SL], ps[4 + s][:, :], ACT.Copy).then_inc(placed, 1)


GH = 4
E8 = 8
ROWS = 48
PARTS_Q = (0, 0, 1, 1, 0, 2)
PARTS_K = (0, 1, 0, 1, 2, 0)


def score_steps(mode):
    out = []
    for s in range(N // SL):
        if mode == "full":
            out += [(s, kt, 0, SL, None) for kt in range(8)]
        elif mode == "causal":
            for kt in range(4 * (s + 1)):
                off = max(0, kt * P - s * SL)
                out.append((s, kt, off, SL - off, (0, P) if kt >= 4 * s else None))
        else:
            for kt in range(max(0, 4 * s - 1), 4 * s + 4):
                if kt == 4 * s - 1:
                    out.append((s, kt, 0, P, (P, P)))
                elif kt == 4 * s + 3:
                    out.append((s, kt, kt * P - s * SL, P, (0, P)))
                else:
                    out.append((s, kt, kt * P - s * SL, 2 * P, (0, 2 * P)))
    return out


def max_uses(mode):
    out = []
    for h in range(GH):
        for qt in range(8):
            if mode == "full":
                out += [[(h, qt, c * SL, SL, None, c)] for c in range(2)]
            elif mode == "causal":
                keys = (qt + 1) * P
                for c in range((keys + SL - 1) // SL):
                    n = min(SL, keys - c * SL)
                    last = (c + 1) * SL >= keys
                    out.append([(h, qt, c * SL, n, (P, P) if last else None, c)])
    if mode == "window":
        for h in range(GH):
            for qt in range(0, 8, 2):
                out.append([(h, q, max(0, q - 1) * P, P if q == 0 else 2 * P, (P, P) if q == 0 else (0, 2 * P), 0)
                            for q in (qt, qt + 1)])
    return out


def attend(nc, tag, mode, scale, q_dram, k_dram, v_all, key_heads, out_all, kit, slots=4):
    groups = 8
    nparts = 1 if mode == "window" else 2
    hw = 4 if mode == "window" else 2
    width = 1024 // hw
    steps = score_steps(mode)
    uses = max_uses(mode)
    blocks = GH // hw
    nst = len(steps)
    nexp = nst * blocks
    small = len(uses) + 1
    start = len(uses) + 1
    slice_end = [max(k for k, st in enumerate(steps) if st[0] == s) for s in range(2)]
    spread = max(1, int(nst * 0.85))
    plan, given = [], 0
    for k in range(nst):
        upto = min(len(uses), (len(uses) * (k + 1) + spread - 1) // spread)
        row = [("max", i) for i in range(given, upto)]
        given = upto
        if k == spread:
            row.append(("turn", 0))
        plan.append(row)
    order = [x for row in plan for x in row]
    turn_at = order.index(("turn", 0))
    assert len(order) == small

    with nc.cleanup_on_exit(), ExitStack() as ctx:
        sb = lambda name, shape, dt=F32: ctx.enter_context(nc.sbuf_tensor(f"{tag}_{name}", shape, dt))
        sem = lambda name: nc.alloc_semaphore(f"{tag}_{name}")
        qst = [sb(f"qst{u}", [P, GH * N], BF16) for u in range(slots)]
        kst = [sb(f"kst{u}", [P, key_heads, N], BF16) for u in range(slots)]
        val = [sb(f"val{u}", [P, 8, key_heads, 32]) for u in range(slots)]
        prob = [sb(f"prob{r}", [P, GH, width]) for r in range(2)]
        mpart = sb("mpart", [P, GH * 8, nparts])
        mcol = sb("mcol", [P, GH * 8])
        mhl = sb("mhl", [GH * 8, 2, P], BF16)
        ps_st = [ctx.enter_context(nc.psum_tensor(f"{tag}_st{r}", [P, hw, width], F32)) for r in range(2)]
        ps_o = ctx.enter_context(nc.psum_tensor(f"{tag}_o", [P, SL], F32))
        ps_s = [ctx.enter_context(nc.psum_tensor(f"{tag}_s{r}", [P, SL], F32)) for r in range(3)]
        cleared = [sem(f"cleared{u}") for u in range(slots)]
        ones_set = [sem(f"ones_set{u}") for u in range(slots)]
        staged = [sem(f"staged{u}") for u in range(slots)]
        shift_in = [sem(f"shift_in{u}") for u in range(slots)]
        small_ready = sem("small_ready")
        small_free = sem("small_free")
        hi_done = sem("hi_done")
        column_done = sem("column_done")
        scores_ready = sem("scores_ready")
        probs_ready = sem("probs_ready")
        probs_used = sem("probs_used")
        o_copied = sem("o_copied")

        def small_of(it, u, n):
            return it * (slots * small) + (start + u * small + n)

        def small_bank(pe, it, u, n):
            pe.wait_ge(small_free, small_of(it, u, n - 2 if n >= 3 else 0))
            return n % 3

        def steps_of(it, u, k):
            return it * (slots * nst) + (u * nst + k)

        def exps_of(it, u, e):
            return it * (slots * nexp) + (u * nexp + e)

        def slices_of(it, u, s):
            return it * (slots * 2) + (u * 2 + s)

        with nc.Block() as block:

            def load(sp, u, b):
                sp.dma_start(qst[u][0:ROWS, :].rearrange("r (h n) -> r h n", h=GH),
                             q_dram[bass.ds(b, 1), :, GH * u:GH * u + GH, :].rearrange("b r h n -> (b r) h n")).then_inc(staged[u], 16)
                sp.dma_start(kst[u][0:ROWS, :, :],
                             k_dram[bass.ds(b, 1), :, key_heads * u:key_heads * (u + 1), :].rearrange("b r h n -> (b r) h n")).then_inc(staged[u], 16)
                sp.dma_start(val[u][:, :, :, :], v_all[:, bass.ds(b * 4 + u, 1), :, :, :].rearrange("p g t h c -> p (g t) h c")).then_inc(staged[u], 16)

            def shift(sp, u, count):
                sp.wait_ge(small_free, count)
                for part in range(2):
                    sp.dma_start(qst[u][ROWS + part:ROWS + part + 1, :], mhl[:, part, :]).then_inc(shift_in[u], 16)

            @block.sync
            def _(sp):
                for u in range(slots):
                    sp.wait_ge(cleared[u], 2)
                    sp.wait_ge(ones_set[u], 1)
                    load(sp, u, 0)
                    if u == 1:
                        shift(sp, 0, start)
                with sp.Fori(0, groups // slots) as it:
                    for u in range(slots):
                        shift(sp, (u + 1) % slots, small_of(it, u, turn_at + 1))
                        sp.wait_ge(probs_used, steps_of(it, u, nst + 2))
                        load(sp, u, (it + 1) % 2)
                for u in range(slots):
                    sp.wait_ge(staged[u], 48 * (groups // slots + 1))
                    sp.wait_ge(shift_in[u], 32 * (groups // slots + (u == 0)))

            def clear(eng, u):
                eng.memset(kst[u][:, :, :], 0.0).then_inc(cleared[u], 1)
                eng.memset(qst[u][:, :], 0.0).then_inc(cleared[u], 1)

            def set_ones(eng, u):
                eng.memset(kst[u][32:64, :, :], 1.0).then_inc(ones_set[u], 1)
                eng.wait_ge(ones_set[u], 1)

            @block.gpsimd
            def _(po):
                po.wait_ge(cleared[0], 1)
                set_ones(po, 0)
                for u in range(1, slots):
                    clear(po, u)
                    po.wait_ge(cleared[u], 2)
                    set_ones(po, u)

            def max_matmuls(pe, u, use, bank):
                col = 0
                for h, qt, k0, nk, mask, part in use:
                    kh = h if key_heads == GH else 0
                    mm = pe.matmul(ps_s[bank][:, col:col + nk], qst[u][0:ROWS, h * N + qt * P:h * N + (qt + 1) * P],
                                   kst[u][0:ROWS, kh, k0:k0 + nk], start=True, stop=mask is None, skip_group_check=True)
                    if mask is not None:
                        mm = pe.matmul(ps_s[bank][:, col + nk - mask[1]:col + nk], kit.ident_bf[:, :],
                                       kit.mask_qk[:, mask[0]:mask[0] + mask[1]], start=False, stop=True,
                                       skip_group_check=True)
                    col += 2 * P
                return mm

            @block.tensor
            def _(pe):
                pe.sem_inc(probs_used, 2)
                pe.wait_ge(staged[0], 48)
                for n, use in enumerate(uses):
                    if n >= 3:
                        pe.wait_ge(small_free, n - 2)
                    max_matmuls(pe, 0, use, n % 3).then_inc(small_ready, 1)
                pe.wait_ge(column_done, 1)
                pe.transpose(ps_s[len(uses) % 3][0:GH * 8, 0:P], mcol[:, :], kit.ident[:, :]).then_inc(small_ready, 1)
                with pe.Fori(0, groups // slots) as it:
                    for u in range(slots):
                        nu = (u + 1) % slots
                        pe.wait_ge(staged[nu], it * 48 + (96 if nu == 0 else 48))
                        pe.wait_ge(shift_in[u], it * 32 + 32)
                        e = n = 0

                        def fill(row):
                            nonlocal n
                            for what, i in row:
                                bank = small_bank(pe, it, u, n)
                                if what == "max":
                                    max_matmuls(pe, nu, uses[i], bank).then_inc(small_ready, 1)
                                else:
                                    pe.wait_ge(column_done, it * slots + (u + 2))
                                    pe.transpose(ps_s[bank][0:GH * 8, 0:P], mcol[:, :], kit.ident[:, :]).then_inc(small_ready, 1)
                                n += 1

                        for k in range(nst + 1):
                            row = plan[k] if k < nst else []
                            cuts = [len(row) * c // (blocks + 1) for c in range(blocks + 2)]
                            if k < nst:
                                s, kt, off, w, mask = steps[k]
                                c0 = 0 if mode == "window" else off
                                for blk in range(blocks):
                                    if e == 0:
                                        pe.wait_ge(probs_ready, exps_of(it, u, 1))
                                    elif e >= 2:
                                        pe.wait_ge(probs_ready, exps_of(it, u, e))
                                    for jj in range(hw):
                                        j = blk * hw + jj
                                        kh = j if key_heads == GH else 0
                                        mm = pe.matmul(ps_st[e % 2][:, jj, c0:c0 + w], kst[u][:, kh, kt * P:(kt + 1) * P],
                                                       qst[u][:, j * N + s * SL + off:j * N + s * SL + off + w],
                                                       start=True, stop=mask is None, skip_group_check=True)
                                        if mask is not None:
                                            mm = pe.matmul(ps_st[e % 2][:, jj, c0:c0 + mask[1]], kit.ident_bf[:, :],
                                                           kit.mask_kq[:, mask[0]:mask[0] + mask[1]], start=False,
                                                           stop=True, skip_group_check=True)
                                    mm.then_inc(scores_ready, 1)
                                    e += 1
                                    fill(row[cuts[blk]:cuts[blk + 1]])
                            if k >= 1:
                                s, kt, off, w, mask = steps[k - 1]
                                c0 = 0 if mode == "window" else off
                                first = k == 1 or steps[k - 2][0] != s
                                if first:
                                    pe.wait_ge(o_copied, slices_of(it, u, s + 1))
                                pe.wait_ge(probs_ready, exps_of(it, u, k * blocks + 1))
                                for j in range(GH):
                                    kh = j if key_heads == GH else 0
                                    mm = pe.matmul(ps_o[32 * j:32 * j + 32, off:off + w], val[u][:, kt, kh, :],
                                                   prob[(k - 1) % 2][:, j, c0:c0 + w], start=first,
                                                   stop=k - 1 in slice_end, skip_group_check=True)
                                mm.then_inc(probs_used, 1)
                            fill(row[cuts[blocks]:])

            @block.scalar
            def _(ac):
                ac.sem_inc(probs_ready, 1)
                ac.sem_inc(o_copied, 1)

                def copy_out(it, u, s):
                    ac.wait_ge(probs_used, steps_of(it, u, slice_end[s] + 3))
                    ac.activation(out_all[:, bass.ds(it * slots + u, 1), s * SL:(s + 1) * SL].rearrange("p g n -> p (g n)"),
                                  ps_o[:, :], ACT.Copy).then_inc(o_copied, 1)

                with ac.Fori(0, groups // slots) as it:
                    for u in range(slots):
                        e = 0
                        for k, (s, kt, off, w, mask) in enumerate(steps):
                            c0 = 0 if mode == "window" else off
                            for blk in range(blocks):
                                ac.wait_ge(scores_ready, exps_of(it, u, e + 1))
                                if blk == 0 and k == 0:
                                    ac.wait_ge(probs_used, steps_of(it, u, 2))
                                elif blk == 0 and k >= 2:
                                    ac.wait_ge(probs_used, steps_of(it, u, k + 1))
                                ac.activation(prob[k % 2][:, blk * hw:(blk + 1) * hw, c0:c0 + w],
                                              ps_st[e % 2][:, :, c0:c0 + w], ACT.Exp, scale=scale).then_inc(probs_ready, 1)
                                e += 1
                            if k == slice_end[0] + 1:
                                copy_out(it, u, 0)
                        copy_out(it, u, 1)

            def reduce_use(ve, use, bank):
                h, qt, k0, nk, mask, part = use[0]
                i = h * 8 + qt
                if len(use) == 1:
                    return ve.tensor_reduce(mpart[:, i, part:part + 1], ps_s[bank][:, 0:nk], AX.X, ALU.max)
                if qt == 0:
                    ve.tensor_reduce(mpart[:, i, 0:1], ps_s[bank][:, 0:P], AX.X, ALU.max)
                    return ve.tensor_reduce(mpart[:, i + 1, 0:1], ps_s[bank][:, 2 * P:4 * P], AX.X, ALU.max)
                return ve.tensor_reduce(mpart[:, i:i + 2, 0], ps_s[bank][:, :].rearrange("p (a k) -> p a k", a=2), AX.X, ALU.max)

            def split_max(ve, bank, hi_count):
                ve.tensor_scalar(mhl[:, 0, :], ps_s[bank][0:GH * 8, 0:P], -1.0, None, ALU.mult).then_inc(hi_done, 1)
                ve.wait_ge(hi_done, hi_count)
                ve.scalar_tensor_tensor(mhl[:, 1, :], ps_s[bank][0:GH * 8, 0:P], -1.0, mhl[:, 0, :], ALU.mult,
                                        ALU.subtract).then_inc(small_free, 1)

            @block.vector
            def _(ve):
                clear(ve, 0)
                ve.memset(mpart[:, :, :], -3.0e38).then_inc(hi_done, 1)
                ve.wait_ge(hi_done, 1)
                for n, use in enumerate(uses):
                    ve.wait_ge(small_ready, n + 1)
                    reduce_use(ve, use, n % 3).then_inc(small_free, 1)
                ve.wait_ge(small_free, len(uses))
                ve.tensor_reduce(mcol[:, :], mpart[:, :, :], AX.X, ALU.max).then_inc(column_done, 1)
                ve.wait_ge(small_ready, start)
                split_max(ve, len(uses) % 3, 2)
                with ve.Fori(0, groups // slots) as it:
                    for u in range(slots):
                        for n, (what, i) in enumerate(order):
                            bank = n % 3
                            ve.wait_ge(small_ready, small_of(it, u, n + 1))
                            if what == "max":
                                reduce_use(ve, uses[i], bank).then_inc(small_free, 1)
                                if i == len(uses) - 1:
                                    ve.wait_ge(small_free, small_of(it, u, n + 1))
                                    ve.tensor_reduce(mcol[:, :], mpart[:, :, :], AX.X, ALU.max).then_inc(column_done, 1)
                            elif what == "turn":
                                ve.wait_ge(shift_in[u], it * 32 + 32)
                                split_max(ve, bank, it * slots + (u + 3))


def normalise(nc, tag, kit, out_all, extra=0.0):
    blocks, tiles, ring = 8 * N // SL, SL // P, 3
    with nc.cleanup_on_exit(), ExitStack() as ctx:
        sb = lambda name, shape: ctx.enter_context(nc.sbuf_tensor(f"{tag}_{name}", shape, F32))
        rec = [sb(f"rec{i}", [P, tiles, GH]) for i in range(2)]
        quotient = [sb(f"quotient{i}", [P, tiles * GH, 32]) for i in range(ring)]
        ps_tok = [ctx.enter_context(nc.psum_tensor(f"{tag}_tok{i}", [P, tiles, GH, 32], F32)) for i in range(ring)]
        ps_back = [ctx.enter_context(nc.psum_tensor(f"{tag}_back{i}", [P, SL], F32)) for i in range(ring)]
        sem = lambda name: nc.alloc_semaphore(f"{tag}_{name}")
        turned, summed, inverted, divided, turned_back, stored = (sem(n) for n in (
            "turned", "summed", "inverted", "divided", "turned_back", "stored"))

        def block_of(k):
            return out_all[:, k // 2, (k % 2) * SL:(k % 2 + 1) * SL]

        with nc.Block() as block:

            @block.tensor
            def _(pe):
                for k in range(blocks + 2):
                    if k < blocks:
                        if k >= ring:
                            pe.wait_ge(divided, k - ring + 1)
                        for t in range(tiles):
                            mm = pe.transpose(ps_tok[k % ring][:, t, :, :].rearrange("p j c -> p (j c)"),
                                              block_of(k)[:, t * P:(t + 1) * P], kit.ident[:, :])
                        mm.then_inc(turned, 1)
                    if k >= 2:
                        m = k - 2
                        pe.wait_ge(divided, m + 1)
                        if m >= ring:
                            pe.wait_ge(stored, m - ring + 1)
                        for t in range(tiles):
                            mm = pe.transpose(ps_back[m % ring][:, t * P:(t + 1) * P],
                                              quotient[m % ring][:, t * GH:(t + 1) * GH, :].rearrange("p j c -> p (j c)"), kit.ident[:, :])
                        mm.then_inc(turned_back, 1)

            @block.scalar
            def _(ac):
                for k in range(blocks):
                    ac.wait_ge(turned_back, k + 1)
                    ac.activation(block_of(k), ps_back[k % ring][:, :], ACT.Copy).then_inc(stored, 1)

            @block.vector
            def _(ve):
                for k in range(blocks):
                    ve.wait_ge(turned, k + 1)
                    sums = ps_tok[k % ring][:, :, :, E8]
                    if extra:
                        ve.tensor_scalar(rec[k % 2][:, :, :], sums, extra, None, ALU.add).then_inc(summed, 1)
                        ve.wait_ge(summed, k + 1)
                        sums = rec[k % 2][:, :, :]
                    ve.reciprocal(rec[k % 2][:, :, :], sums).then_inc(inverted, 1)
                    ve.wait_ge(inverted, k + 1)
                    if k >= ring:
                        ve.wait_ge(turned_back, k - ring + 1)
                    ve.tensor_tensor(quotient[k % ring][:, :, :], ps_tok[k % ring][:, :, :, :].rearrange("p t j c -> p (t j) c"),
                                     rec[k % 2][:, :, :].rearrange("p t j -> p (t j)").unsqueeze(2).broadcast_to([P, tiles * GH, 32]),
                                     ALU.mult).then_inc(divided, 1)


CH = 64
NC = N // CH
HP = 8
F = 64


def fast_weights(nc, tag, xn, wqk, wv, wo, win0, wout0, woutT0, decay_in, decay_out, rate_in, rate_out, y, ident):
    with nc.cleanup_on_exit(), ExitStack() as ctx:
        sb = lambda name, shape, dt=F32: ctx.enter_context(nc.sbuf_tensor(f"{tag}_{name}", shape, dt))
        sem = lambda name: nc.alloc_semaphore(f"{tag}_{name}")
        win, wout, woutT = (win0, wout0, woutT0)
        qk = [sb(f"qk{i}", [P, HP, 2, 2, CH]) for i in range(2)]
        vT = [sb(f"vT{i}", [P, HP, 2, CH]) for i in range(2)]
        ktok = [sb(f"ktok{i}", [P, HP, 2, F]) for i in range(2)]
        vtok = [sb(f"vtok{i}", [P, HP, 2, F]) for i in range(2)]
        prob = [sb(f"prob{g}", [P, 4, 2, 2, CH]) for g in range(2)]
        mx = [sb(f"mx{g}", [P, 16]) for g in range(2)]
        sm = [sb(f"sm{g}", [P, 16]) for g in range(2)]
        ptok = [sb(f"ptok{g}", [P, 4, 2, F]) for g in range(2)]
        pa = [sb(f"pa{g}", [P, 4, 2, F]) for g in range(2)]
        ssum = [sb(f"ssum{g}", [P, 2, 4]) for g in range(2)]
        oT = [sb(f"oT{g}", [P, 4, 2, CH]) for g in range(2)]
        ps_z = [ctx.enter_context(nc.psum_tensor(f"{tag}_z{g}", [P, 2, 512], F32)) for g in range(2)]
        ps_g = ctx.enter_context(nc.psum_tensor(f"{tag}_g", [P, 2, 512], F32))
        ps_m = [ctx.enter_context(nc.psum_tensor(f"{tag}_m{g}", [P, 512], F32)) for g in range(2)]
        z_ready, a_ready, go_ready, gi_ready = sem("z_ready"), sem("a_ready"), sem("go_ready"), sem("gi_ready")
        misc_ready = sem("misc_ready")
        act_free = sem("act_free")
        ve_free = sem("ve_free")
        shifted = sem("shifted")
        exp_done = sem("exp_done")
        normed = sem("normed")
        gz_done = sem("gz_done")
        win_new, wout_new = sem("win_new"), sem("wout_new")
        win_decayed, wout_decayed = sem("win_decayed"), sem("wout_decayed")
        ve_chain = sem("ve_chain")
        passed = sem("passed")

        next_qkv = [("qk", i, "act") for i in range(4)] + [("v", i, "act") for i in range(2)]
        next_tok = [("kt", i, "ve") for i in range(2)] + [("vt", i, "ve") for i in range(2)]
        chunk = (next_qkv[4:] + next_qkv[:2] + [("pt", 0, "act"), ("ot", 0, "act"), next_qkv[2], ("pt", 1, "act"),
                 ("ot", 1, "act"), next_qkv[3]] + next_tok + [("y", 0, "act")])
        lead = next_qkv + next_tok
        nm = len(chunk)
        na = sum(w == "act" for *_, w in chunk)
        nv = nm - na
        la, lv = 6, 4

        def act_reads(what, i):
            return sum(w == "act" for *_, w in chunk[:chunk.index((what, i, "act")) + 1])

        def reads_before(n, who):
            return sum(w == who for *_, w in (chunk + chunk)[:n])

        def misc_wait(pe, it, n):
            if n < 2:
                pe.wait_ge(act_free, it * 2 * na + la)
                pe.wait_ge(ve_free, it * 2 * nv + lv)
            else:
                who = (chunk + chunk)[n - 2][2]
                if who == "act":
                    pe.wait_ge(act_free, it * 2 * na + (la + reads_before(n - 1, "act")))
                else:
                    pe.wait_ge(ve_free, it * 2 * nv + (lv + reads_before(n - 1, "ve")))
            return ps_m[n % 2]

        def misc_at(it, n):
            return it * 2 * nm + (len(lead) + n + 1)

        with nc.Block() as block:

            def tokens(c):
                return xn.rearrange("p (b n) -> p b n", b=2)[:, :, bass.ds(c * CH, CH)]

            def project_qk(pe, bank, i, c):
                for j in range(2):
                    for w in range(2):
                        mm = pe.matmul(bank[:, j * 256 + w * 128:j * 256 + w * 128 + 128].rearrange("p (b n) -> p b n", b=2),
                                       wqk[:, w, 2 * i + j, :], tokens(c), start=True, stop=True)
                return mm

            def project_v(pe, bank, i, c):
                for j in range(4):
                    mm = pe.matmul(bank[:, j * 128:(j + 1) * 128].rearrange("p (b n) -> p b n", b=2),
                                   wv[:, 4 * i + j, :], tokens(c), start=True, stop=True)
                return mm

            def turn(pe, bank, sources):
                for j, src in enumerate(sources):
                    mm = pe.transpose(bank[:, j * 128:(j + 1) * 128], src, ident[:, :])
                return mm

            def make(pe, what, i, bank, nxt, cn, cur, it):
                if what == "qk":
                    return project_qk(pe, bank, i, cn)
                if what == "v":
                    return project_v(pe, bank, i, cn)
                if what == "kt":
                    return turn(pe, bank, [qk[nxt][:, 4 * i + j, 1, :, :].rearrange("p b n -> p (b n)") for j in range(4)])
                if what == "vt":
                    return turn(pe, bank, [vT[nxt][:, 4 * i + j, :, :].rearrange("p b n -> p (b n)") for j in range(4)])
                if what == "pt":
                    return turn(pe, bank, [prob[i][:, j, 1, :, :].rearrange("p b n -> p (b n)") for j in range(4)])
                if what == "ot":
                    for j in range(4):
                        for b in range(2):
                            mm = pe.matmul(bank[:, (j * 2 + b) * 64:(j * 2 + b + 1) * 64], wout[:, 4 * i + j, b, :],
                                           prob[i][:, j, 0, b, :], start=True, stop=True, skip_group_check=True)
                    return mm
                if what == "y":
                    for j in range(HP):
                        mm = pe.matmul(bank[:, 0:128], wo[:, j, :], oT[j // 4][:, j % 4, :, :].rearrange("p b n -> p (b n)"),
                                       start=j == 0, stop=j == HP - 1)
                    return mm

            @block.tensor
            def _(pe):
                for n, (what, i, who) in enumerate(lead):
                    if n >= 2:
                        w2 = lead[n - 2][2]
                        pe.wait_ge(act_free if w2 == "act" else ve_free, sum(x[2] == w2 for x in lead[:n - 1]))
                    if n == 6:
                        pe.wait_ge(act_free, 6)
                    make(pe, what, i, ps_m[n % 2], 0, 0, 0, None).then_inc(misc_ready, 1)
                with pe.Fori(0, NC // 2) as it:
                    n = 0
                    for cc in range(2):
                        cur, nxt = cc, 1 - cc
                        cn = (it * 2 + (cc + 1)) % NC
                        act0 = la + cc * na
                        ve0 = lv + cc * nv
                        for g in range(2):
                            pe.wait_ge(win_new, it * 4 + (2 * cc + g + 1))
                            if g == 0:
                                pe.wait_ge(act_free, it * 2 * na + act0)
                            pe.sem_inc(passed, 1)
                            for j in range(4):
                                for b in range(2):
                                    mm = pe.matmul(ps_z[g][:, j // 2, (j % 2) * 256:(j % 2) * 256 + 256].rearrange("p (w b n) -> p w b n", w=2, b=2)[:, :, b, :],
                                                   win[:, 4 * g + j, b, :], qk[cur][:, 4 * g + j, :, b, :],
                                                   start=True, stop=True, skip_group_check=True)
                            mm.then_inc(z_ready, 1)

                        def misc(what, i):
                            nonlocal n
                            bank = misc_wait(pe, it, n)
                            if what == "ot":
                                pe.sem_inc(passed, 1)
                            make(pe, what, i, bank, nxt, cn, cur, it).then_inc(misc_ready, 1)
                            n += 1

                        for what, i in (("v", 0), ("v", 1), ("qk", 0), ("qk", 1)):
                            misc(what, i)
                        for g in range(2):
                            pe.wait_ge(normed, it * 4 + (2 * cc + g + 1))
                            if g == 0:
                                pe.wait_ge(wout_new, it * 4 + (2 * cc + 2))
                            misc("pt", g)
                            misc("ot", g)
                            for j in range(4):
                                for h in range(2):
                                    for b in range(2):
                                        r = slice(64 * h, 64 * h + 64)
                                        mm = pe.matmul(ps_z[g][64 * b:64 * b + 64, h, j * 64:(j + 1) * 64], vT[cur][r, 4 * g + j, b, :],
                                                       woutT[r, 4 * g + j, b, :], start=True, stop=True, skip_group_check=True)
                            mm.then_inc(a_ready, 1)
                            misc("qk", 2 + g)

                        def grad_out(g):
                            pe.wait_ge(act_free, it * 2 * na + (act0 + act_reads("pt", g)))
                            if g == 0:
                                pe.wait_ge(ve_free, it * 2 * nv + ve0)
                            pe.wait_ge(wout_new, it * 4 + (2 * cc + g + 2))
                            pe.sem_inc(passed, 1)
                            for j in range(4):
                                for b in range(2):
                                    r = slice(64 * b, 64 * b + 64)
                                    for h in range(2):
                                        pe.matmul(ps_g[64 * h:64 * h + 64, b, j * 64:(j + 1) * 64], ptok[g][r, j, h, :],
                                                  vtok[cur][r, 4 * g + j, h, :], start=True, stop=True, skip_group_check=True)
                                    for h in range(2):
                                        mm = pe.matmul(ps_g[64 * h:64 * h + 64, b, 256 + j * 64:256 + (j + 1) * 64],
                                                       vtok[cur][r, 4 * g + j, h, :], ptok[g][r, j, h, :],
                                                       start=True, stop=True, skip_group_check=True)
                            mm.then_inc(go_ready, 1)

                        def grad_in(g):
                            pe.wait_ge(gz_done, it * 4 + (2 * cc + g + 1))
                            pe.sem_inc(passed, 1)
                            for j in range(4):
                                for b in range(2):
                                    r = slice(64 * b, 64 * b + 64)
                                    for h in range(2):
                                        mm = pe.matmul(ps_z[g][64 * h:64 * h + 64, b, j * 64:(j + 1) * 64], ktok[cur][r, 4 * g + j, h, :],
                                                       pa[g][r, j, h, :], start=True, stop=True, skip_group_check=True)
                            mm.then_inc(gi_ready, 1)

                        grad_out(0)
                        pe.wait_ge(act_free, it * 2 * na + (act0 + act_reads("qk", 3)))
                        misc("kt", 0)
                        grad_in(0)
                        misc("kt", 1)
                        misc("vt", 0)
                        grad_out(1)
                        misc("vt", 1)
                        pe.wait_ge(act_free, it * 2 * na + (act0 + act_reads("ot", 1)))
                        misc("y", 0)
                        grad_in(1)

            def read_act(ac, what, i, bank, nxt, c, cur):
                if what == "qk":
                    return ac.activation(qk[nxt][:, 2 * i:2 * i + 2, :, :, :].rearrange("p a b w n -> p (a b w n)"), bank[:, :], ACT.Silu)
                if what == "v":
                    return ac.activation(vT[nxt][:, 4 * i:4 * i + 4, :, :].rearrange("p a b n -> p (a b n)"), bank[:, :], ACT.Copy)
                if what == "pt":
                    return ac.activation(ptok[i][:, :, :, :].rearrange("p a h n -> p (a h n)"), bank[:, :], ACT.Copy)
                if what == "ot":
                    return ac.activation(oT[i][:, :, :, :].rearrange("p a h n -> p (a h n)"), bank[:, :], ACT.Copy)
                if what == "y":
                    return ac.activation(y.rearrange("p (b n) -> p b n", b=2)[:, :, bass.ds(c * CH, CH)],
                                         bank[:, 0:128].rearrange("p (b n) -> p b n", b=2), ACT.Copy)

            @block.scalar
            def _(ac):
                for n, (what, i, who) in enumerate(lead):
                    if who == "act":
                        ac.wait_ge(misc_ready, n + 1)
                        read_act(ac, what, i, ps_m[n % 2], 0, 0, 0).then_inc(act_free, 1)
                with ac.Fori(0, NC // 2) as it:
                    for cc in range(2):
                        cur, nxt = cc, 1 - cc
                        for k, (what, i, who) in enumerate(chunk):
                            n = cc * nm + k
                            if k == 0:
                                if cc:
                                    ac.wait_ge(gi_ready, it * 4 + 2 * cc)
                            if (what, i) in (("v", 0), ("qk", 0)):
                                g = 0 if what == "v" else 1
                                ac.wait_ge(shifted, it * 4 + (2 * cc + g + 1))
                                ac.activation(prob[g][:, :, :, :, :].rearrange("p a b w n -> p (a b w n)"),
                                              prob[g][:, :, :, :, :].rearrange("p a b w n -> p (a b w n)"), ACT.Exp).then_inc(exp_done, 1)
                            if who == "act":
                                ac.wait_ge(misc_ready, misc_at(it, n))
                                read_act(ac, what, i, ps_m[n % 2], nxt, it * 2 + cc, cur).then_inc(act_free, 1)

            def own_block(w, g, h):
                return w[64 * h:64 * h + 64, 4 * g:4 * g + 4, :, 64 * h:64 * h + 64]

            def segments(t):
                return t[:, :, :, :, :].rearrange("p a b w n -> p (a b w) n")

            def read_ve(ve, what, i, bank, nxt, cn):
                dst = (ktok if what == "kt" else vtok)[nxt][:, 4 * i:4 * i + 4, :, :].rearrange("p a h d -> p (a h) d")
                rate = (rate_in if what == "kt" else rate_out)[:, bass.ds(cn, 1), 8 * i:8 * i + 8].rearrange("p c h -> p (c h)")
                return ve.tensor_tensor(dst, bank[:, :].rearrange("p (a d) -> p a d", d=F),
                                        rate.unsqueeze(2).broadcast_to([P, 8, F]), ALU.mult)

            @block.vector
            def _(ve):
                ve.sem_inc(win_new, 2)
                ve.sem_inc(wout_new, 2)
                for n, (what, i, who) in enumerate(lead):
                    if who == "ve":
                        ve.wait_ge(misc_ready, n + 1)
                        read_ve(ve, what, i, ps_m[n % 2], 0, 0).then_inc(ve_free, 1)
                links = 12
                with ve.Fori(0, NC // 2) as it:
                    done = [0]

                    def link(ins):
                        done[0] += 1
                        ins.then_inc(ve_chain, 1)
                        ve.wait_ge(ve_chain, it * 2 * links + done[0])

                    for cc in range(2):
                        cur, nxt = cc, 1 - cc
                        cn = (it * 2 + (cc + 1)) % NC
                        for g in range(2):
                            ve.wait_ge(z_ready, it * 4 + (2 * cc + g + 1))
                            z = ps_z[g][:, :, :].rearrange("p k (s n) -> p (k s) n", n=CH)
                            link(ve.tensor_reduce(mx[g][:, :], z, AX.X, ALU.max))
                            ve.tensor_tensor(segments(prob[g]), z, mx[g][:, :].unsqueeze(2).broadcast_to([P, 16, CH]),
                                             ALU.subtract).then_inc(shifted, 1)
                        for g in range(2):
                            ve.wait_ge(exp_done, it * 4 + (2 * cc + g + 1))
                            link(ve.tensor_reduce(sm[g][:, :], segments(prob[g]), AX.X, ALU.add))
                            link(ve.reciprocal(mx[g][:, :], sm[g][:, :]))
                            ve.tensor_tensor(segments(prob[g]), segments(prob[g]), mx[g][:, :].unsqueeze(2).broadcast_to([P, 16, CH]),
                                             ALU.mult).then_inc(normed, 1)
                        for g in range(2):
                            ve.wait_ge(a_ready, it * 4 + (2 * cc + g + 1))
                            ve.wait_ge(act_free, it * 2 * na + (la + cc * na + act_reads("pt", g)))
                            a = ps_z[g][:, :, 0:256].rearrange("p h (a d) -> p h a d", d=F)
                            pt = ptok[g][:, :, :, :].rearrange("p a h d -> p h a d")
                            out = pa[g][:, :, :, :].rearrange("p a h d -> p h a d")
                            link(ve.tensor_tensor(out, a, pt, ALU.mult))
                            link(ve.tensor_reduce(ssum[g][:, :, :], out, AX.X, ALU.add))
                            link(ve.tensor_tensor(out, a, ssum[g][:, :, :].unsqueeze(3).broadcast_to([P, 2, 4, F]), ALU.subtract))
                            ve.tensor_tensor(pa[g][:, :, :, :], pa[g][:, :, :, :], ptok[g][:, :, :, :], ALU.mult).then_inc(gz_done, 1)

                        def update_out(g):
                            ve.wait_ge(go_ready, it * 4 + (2 * cc + g + 1))
                            ve.wait_ge(wout_decayed, it * 8 + (4 * cc + 2 * g + 2))
                            for h in range(2):
                                diagonal = own_block(wout, g, h).rearrange("p a b d -> p b a d")
                                ve.tensor_tensor(diagonal, ps_g[64 * h:64 * h + 64, :, 0:256].rearrange("p b (a d) -> p b a d", d=F), diagonal, ALU.add)
                            turned = woutT[:, 4 * g:4 * g + 4, :, :].rearrange("p a b d -> p b a d")
                            ve.tensor_tensor(turned, ps_g[:, :, 256:512].rearrange("p b (a d) -> p b a d", d=F), turned, ALU.add).then_inc(wout_new, 1)

                        def update_in(g):
                            ve.wait_ge(gi_ready, it * 4 + (2 * cc + g + 1))
                            ve.wait_ge(win_decayed, it * 4 + (2 * cc + g + 1))
                            for h in range(2):
                                diagonal = own_block(win, g, h).rearrange("p a b d -> p b a d")
                                ins = ve.tensor_tensor(diagonal, ps_z[g][64 * h:64 * h + 64, :, 0:256].rearrange("p b (a d) -> p b a d", d=F), diagonal, ALU.add)
                            ins.then_inc(win_new, 1)

                        update_out(0)
                        for k, (what, i, who) in enumerate(chunk):
                            if who == "ve":
                                ve.wait_ge(misc_ready, misc_at(it, cc * nm + k))
                                read_ve(ve, what, i, ps_m[(cc * nm + k) % 2], nxt, cn).then_inc(ve_free, 1)
                        update_in(0)
                        update_out(1)
                        update_in(1)
                    assert done[0] == 2 * links, done

            @block.gpsimd
            def _(po):
                def decay(w, g, d, c):
                    for h in range(2):
                        r = slice(64 * h, 64 * h + 64)
                        v = (w[r, 4 * g:4 * g + 4, :, :] if w is woutT else own_block(w, g, h)).rearrange("p a b d -> p (a b) d")
                        k = d[r, bass.ds(c, 1), 4 * g:4 * g + 4, :].rearrange("p c a b -> p (c a b)")
                        ins = po.tensor_tensor(v, v, k.unsqueeze(2).broadcast_to([64, 8, F]), ALU.mult)
                    return ins

                with po.Fori(0, NC // 2) as it:
                    for cc in range(2):
                        c = it * 2 + cc
                        for g in range(2):
                            po.wait_ge(z_ready, it * 4 + (2 * cc + g + 1))
                            decay(win, g, decay_in, c).then_inc(win_decayed, 1)
                        for g in range(2):
                            po.wait_ge(a_ready, it * 4 + (2 * cc + g + 1))
                            decay(wout, g, decay_out, c).then_inc(wout_decayed, 1)
                            decay(woutT, g, decay_out, c).then_inc(wout_decayed, 1)


SHIFTS = [0] + [2 << j for j in range(9)] + [1] + [3 << j for j in range(9)]
PAIRED = 9
ZERO_TAPS = 11
FAR_TAPS = 5
PAD = 768
TILE_AT = (1, 3, 5, 7)
SHIFT_AT, DIVIDE_AT = 9, 13


def dilated_attention(nc, tag, kit, xin, w_dram, cols_dram, taps_dram, y):
    n_in = len(SHIFTS)
    n_slots = n_in + 1
    H = 16
    taps = ZERO_TAPS + 2 * PAIRED + 1 + 9 + FAR_TAPS
    with nc.cleanup_on_exit(), ExitStack() as ctx:
        sb = lambda name, shape, dt=F32: ctx.enter_context(nc.sbuf_tensor(f"{tag}_{name}", shape, dt))
        w = sb("w", [P, 5, P])
        cols = sb("cols", [P, 5])
        q = sb("q", [P, T])
        kpad = sb("kpad", [P, 2, PAD + N])
        vpad = sb("vpad", [P, 2, PAD + N])
        pb = sb("pb", [P, taps, H])
        pbm = sb("pbm", [P, n_slots, H])
        bias = sb("bias", [P, n_slots, H])
        prod = [sb(f"prod{i}", [P, SL]) for i in range(8)]
        sc_t = [sb(f"sc_t{i}", [P, 5, SL]) for i in range(2)]
        att = sb("att", [P, 4, n_slots, H])
        stat = sb("stat", [P, 4, H])
        attT = sb("attT", [P, 3, SL])
        wv = [sb(f"wv{i}", [P, SL]) for i in range(4)]
        acc = [sb(f"acc{i}", [P, SL]) for i in range(2)]
        mixed = sb("mixed", [P, SL])
        gate = sb("gate", [P, T])
        ps_sc = [ctx.enter_context(nc.psum_tensor(f"{tag}_sc{i}", [P, SL], F32)) for i in range(2)]
        ps_tok = [ctx.enter_context(nc.psum_tensor(f"{tag}_tok{i}", [P, SL], F32)) for i in range(2)]
        ps_w = [ctx.enter_context(nc.psum_tensor(f"{tag}_w{i}", [P, SL], F32)) for i in range(2)]
        ps_x = [ctx.enter_context(nc.psum_tensor(f"{tag}_x{i}", [P, SL], F32)) for i in range(2)]
        sem = lambda name: nc.alloc_semaphore(f"{tag}_{name}")
        loaded, padded, projected, placed = sem("loaded"), sem("padded"), sem("projected"), sem("placed")
        chain, tap_shifted, tap_exp, tap_sum, tap_ln = (sem(n) for n in ("chain", "tap_shifted", "tap_exp", "tap_sum", "tap_ln"))
        multiplied, used, scores_ready, shifted, exp_done, probs_ready = (sem(n) for n in (
            "multiplied", "used", "scores_ready", "shifted", "exp_done", "probs_ready"))
        turned, turned_in, spread, weighted, added, gated, out_ready, out_in = (sem(n) for n in (
            "turned", "turned_in", "spread", "weighted", "added", "gated", "out_ready", "out_in"))
        copied, sc_turned, tile_in = sem("copied"), sem("sc_turned"), sem("tile_in")
        n_four = n_in // 4
        groups = ((0, 0, 1, ZERO_TAPS), (ZERO_TAPS, 1, PAIRED, 2), (taps - FAR_TAPS, n_in, 1, FAR_TAPS))
        singles = (ZERO_TAPS + 2 * PAIRED, 1 + PAIRED, 10)
        rows3 = (P, P, 5 * H)
        with nc.Block() as block:

            @block.sync
            def _(sp):
                sp.dma_start(w[:, :, :], w_dram).then_inc(loaded, 16)
                sp.dma_start(cols[:, :], cols_dram).then_inc(loaded, 16)
                sp.dma_start(pb[:, :, :], taps_dram.broadcast_to([P, taps, H])).then_inc(loaded, 16)
                sp.wait_ge(loaded, 48)

            @block.gpsimd
            def _(po):
                po.memset(kpad[:, :, 0:PAD], 0.0).then_inc(padded, 1)
                po.memset(vpad[:, :, 0:PAD], 0.0).then_inc(padded, 1)
                for s in range(NS):
                    for i in range(n_in):
                        k = s * n_in + i
                        po.wait_ge(weighted, k + 1)
                        if i < 2:
                            if s:
                                po.wait_ge(gated, s)
                            po.tensor_copy(acc[i][:, :], wv[k % 4][:, :]).then_inc(added, 1)
                        else:
                            po.wait_ge(added, k - 1)
                            po.tensor_tensor(acc[i % 2][:, :], acc[i % 2][:, :], wv[k % 4][:, :], ALU.add).then_inc(added, 1)

            @block.tensor
            def _(pe):
                pe.wait_ge(loaded, 48)
                banks = ps_sc + ps_tok
                for n in range(16):
                    k, s = n // NS, n % NS
                    if n >= 4:
                        pe.wait_ge(placed, n - 3)
                    pe.matmul(banks[s][:, :], w[:, k, :], xin[:, s * SL:(s + 1) * SL], start=True, stop=True).then_inc(projected, 1)

                def score_four(n):
                    pe.wait_ge(multiplied, 4 * n + 4)
                    if n >= 2:
                        pe.wait_ge(copied, n - 1)
                    else:
                        pe.wait_ge(placed, 16)
                    for j in range(4):
                        mm = pe.matmul(ps_sc[n % 2][32 * j:32 * j + 32, :], kit.heads[:, :], prod[(4 * n + j) % 8][:, :],
                                       start=True, stop=True, skip_group_check=True)
                    mm.then_inc(used, 1)

                def turn_scores(s, t):
                    pe.wait_ge(copied, n_four * (s + 1))
                    if s or t:
                        pe.wait_ge(tile_in, 4 * s + t)
                    for g in range(n_four):
                        mm = pe.transpose(ps_tok[g // 4][:, (g % 4) * P:(g % 4 + 1) * P], sc_t[s % 2][:, g, t * P:(t + 1) * P], kit.ident[:, :])
                    mm.then_inc(sc_turned, 1)

                def turn_probs(s):
                    pe.wait_ge(probs_ready, s + 1)
                    for g in range(3):
                        n = 3 * s + g
                        if n >= 2:
                            pe.wait_ge(turned_in, n - 1)
                        if s >= 2 and g < 2:
                            pe.wait_ge(out_in, s - 1)
                        for t in range(4):
                            mm = pe.transpose(ps_x[n % 2][0:rows3[g], t * P:(t + 1) * P],
                                              att[:, t, :, :].rearrange("p s h -> p (s h)")[:, g * P:g * P + rows3[g]], kit.ident[:, :])
                        mm.then_inc(turned, 1)

                for g in range(n_four):
                    score_four(g)
                for t in range(4):
                    turn_scores(0, t)
                for g in range(n_four):
                    score_four(n_four + g)
                turn_probs(0)
                for s in range(NS):
                    pe.wait_ge(turned_in, 3 * s + 3)
                    for i in range(n_in):
                        k = s * n_in + i
                        if k >= 2:
                            pe.wait_ge(weighted, k - 1)
                        r = rows3[i // 8]
                        pe.matmul(ps_w[k % 2][:, :], kit.spread[0:r, i % 8, :], attT[0:r, i // 8, :], start=True, stop=True).then_inc(spread, 1)
                        if i in TILE_AT and s + 1 < NS:
                            turn_scores(s + 1, TILE_AT.index(i))
                        if i % 4 == 3 and s + 2 < NS:
                            score_four((s + 2) * n_four + i // 4)
                    if s + 1 < NS:
                        turn_probs(s + 1)
                        pe.wait_ge(turned_in, 3 * s + 6)
                    if s:
                        pe.wait_ge(out_in, s)
                    pe.wait_ge(gated, s + 1)
                    pe.matmul(ps_x[1][:, :], w[:, 4, :], mixed[:, :], start=True, stop=True).then_inc(out_ready, 1)

            @block.scalar
            def _(ac):
                ac.wait_ge(tap_shifted, 1)
                ac.activation(pb[:, :, :], pb[:, :, :], ACT.Exp).then_inc(tap_exp, 1)
                ac.wait_ge(tap_sum, 1)
                ac.activation(bias[:, :, :], bias[:, :, :], ACT.Ln).then_inc(tap_ln, 1)
                ac.wait_ge(loaded, 48)
                for n in range(16):
                    k, s = n // NS, n % NS
                    ac.wait_ge(projected, n + 1)
                    b, c = s // 2, (s % 2) * SL
                    dst = (q if k == 0 else gate)[:, s * SL:(s + 1) * SL] if k in (0, 3) else (kpad if k == 1 else vpad)[:, b, PAD + c:PAD + c + SL]
                    ac.activation(dst, (ps_sc + ps_tok)[s][:, :], ACT.Sigmoid if k == 3 else ACT.Identity, bias=cols[:, k:k + 1]).then_inc(placed, 1)

                def copy_scores(s, fours):
                    for g in fours:
                        ac.wait_ge(used, s * n_four + g + 1)
                        if s >= 2:
                            ac.wait_ge(sc_turned, 4 * (s - 1))
                        ac.activation(sc_t[s % 2][:, g, :], ps_sc[(s * n_four + g) % 2][:, :], ACT.Copy).then_inc(copied, 1)

                def exponentials(s):
                    ac.wait_ge(shifted, s + 1)
                    ac.activation(att[:, :, :, :], att[:, :, :, :], ACT.Exp).then_inc(exp_done, 1)

                def copy_probs(s):
                    for g in range(3):
                        n = 3 * s + g
                        ac.wait_ge(turned, n + 1)
                        if s:
                            ac.wait_ge(spread, s * n_in)
                        ac.activation(attT[0:rows3[g], g, :], ps_x[n % 2][0:rows3[g], :], ACT.Copy).then_inc(turned_in, 1)

                copy_scores(0, range(n_four))
                exponentials(0)
                copy_scores(1, range(n_four))
                copy_probs(0)
                for s in range(NS):
                    if s + 2 < NS:
                        copy_scores(s + 2, range(2))
                    if s + 1 < NS:
                        exponentials(s + 1)
                    if s + 2 < NS:
                        copy_scores(s + 2, range(2, n_four))
                    if s + 1 < NS:
                        copy_probs(s + 1)
                    ac.wait_ge(out_ready, s + 1)
                    ac.activation(y[:, s * SL:(s + 1) * SL], ps_x[1][:, :], ACT.Identity, bias=cols[:, 4:5]).then_inc(out_in, 1)

            @block.vector
            def _(ve):
                done = [0]

                def link(ins):
                    done[0] += 1
                    ins.then_inc(chain, 1)
                    ve.wait_ge(chain, done[0])

                ve.wait_ge(loaded, 48)
                f0, s0, m0 = singles
                for a, slot, n, each in groups:
                    link(ve.tensor_reduce(pbm[:, slot:slot + n, :], pb[:, a:a + n * each, :].rearrange("p (n k) h -> p n h k", k=each), AX.X, ALU.max))
                link(ve.tensor_copy(pbm[:, s0:s0 + m0, :], pb[:, f0:f0 + m0, :]))
                for a, slot, n, each in groups:
                    view = pb[:, a:a + n * each, :].rearrange("p (n k) h -> p n k h", k=each)
                    link(ve.tensor_tensor(view, view, pbm[:, slot:slot + n, :].unsqueeze(2).broadcast_to([P, n, each, H]), ALU.subtract))
                ve.tensor_tensor(pb[:, f0:f0 + m0, :], pb[:, f0:f0 + m0, :], pbm[:, s0:s0 + m0, :], ALU.subtract).then_inc(tap_shifted, 1)
                ve.wait_ge(tap_exp, 1)
                for a, slot, n, each in groups:
                    link(ve.tensor_reduce(bias[:, slot:slot + n, :], pb[:, a:a + n * each, :].rearrange("p (n k) h -> p n h k", k=each), AX.X, ALU.add))
                ve.tensor_copy(bias[:, s0:s0 + m0, :], pb[:, f0:f0 + m0, :]).then_inc(tap_sum, 1)
                ve.wait_ge(tap_ln, 1)
                link(ve.tensor_tensor(bias[:, :, :], bias[:, :, :], pbm[:, :, :], ALU.add))
                ve.wait_ge(padded, 2)
                ve.wait_ge(placed, 16)

                def product(s, i):
                    k, c, off = s * n_in + i, (s % 2) * SL, SHIFTS[i]
                    if k >= 8:
                        ve.wait_ge(used, k // 4 - 1)
                    ve.tensor_tensor(prod[k % 8][:, :], q[:, s * SL:(s + 1) * SL], kpad[:, s // 2, PAD + c - off:PAD + c - off + SL],
                                     ALU.mult).then_inc(multiplied, 1)

                by_head = att[:, :, :, :].rearrange("p t s h -> p t h s")
                across = stat[:, :, :].unsqueeze(2).broadcast_to([P, 4, n_slots, H])

                def add_biases(s, t):
                    if t == 0:
                        if s:
                            ve.wait_ge(turned, 3 * s)
                        ve.tensor_copy(att[:, :, n_in, :], bias[:, n_in, :].unsqueeze(1).broadcast_to([P, 4, H])).then_inc(scores_ready, 1)
                    ve.wait_ge(sc_turned, 4 * s + t + 1)
                    ve.tensor_tensor(att[:, t, 0:16, :], ps_tok[0][:, :].rearrange("p (s c) -> p s c", c=32)[:, :, 0:H],
                                     bias[:, 0:16, :], ALU.add).then_inc(scores_ready, 1)
                    ve.tensor_tensor(att[:, t, 16:n_in, :], ps_tok[1][:, 0:P].rearrange("p (s c) -> p s c", c=32)[:, :, 0:H],
                                     bias[:, 16:n_in, :], ALU.add).then_inc(tile_in, 1)

                def shift(s):
                    ve.wait_ge(scores_ready, 5 * s + 5)
                    ve.wait_ge(tile_in, 4 * s + 4)
                    link(ve.tensor_reduce(stat[:, :, :], by_head, AX.X, ALU.max))
                    ve.tensor_tensor(att[:, :, :, :], att[:, :, :, :], across, ALU.subtract).then_inc(shifted, 1)

                def divide(s):
                    ve.wait_ge(exp_done, s + 1)
                    link(ve.tensor_reduce(stat[:, :, :], by_head, AX.X, ALU.add))
                    link(ve.reciprocal(stat[:, :, :], stat[:, :, :]))
                    ve.tensor_tensor(att[:, :, :, :], att[:, :, :, :], across, ALU.mult).then_inc(probs_ready, 1)

                for i in range(n_in):
                    product(0, i)
                for t in range(4):
                    add_biases(0, t)
                shift(0)
                for i in range(8):
                    product(1, i)
                divide(0)
                for i in range(8, n_in):
                    product(1, i)
                for s in range(NS):
                    b, c = s // 2, (s % 2) * SL
                    for i, off in enumerate(SHIFTS):
                        k = s * n_in + i
                        if s + 2 < NS:
                            product(s + 2, i)
                        ve.wait_ge(spread, k + 1)
                        if k >= 4:
                            ve.wait_ge(added, k - 3)
                        ve.tensor_tensor(wv[k % 4][:, :], ps_w[k % 2][:, :], vpad[:, b, PAD + c - off:PAD + c - off + SL],
                                         ALU.mult).then_inc(weighted, 1)
                        if s + 1 < NS:
                            if i in TILE_AT:
                                add_biases(s + 1, TILE_AT.index(i))
                            if i == SHIFT_AT:
                                shift(s + 1)
                            if i == DIVIDE_AT:
                                divide(s + 1)
                    ve.wait_ge(added, (s + 1) * n_in)
                    if s:
                        ve.wait_ge(out_ready, s)
                    link(ve.tensor_tensor(mixed[:, :], acc[0][:, :], acc[1][:, :], ALU.add))
                    ve.tensor_tensor(mixed[:, :], mixed[:, :], gate[:, s * SL:(s + 1) * SL], ALU.mult).then_inc(gated, 1)


def chunk_rates(nc, ctx, block, tag, kit, xin, w_dram, rate_dram, decay_dram, decay_in, decay_out, rate_in, rate_out):
    K4 = 64
    chunks = NC
    sb = lambda name, shape, dt=F32: ctx.enter_context(nc.sbuf_tensor(f"{tag}_{name}", shape, dt))
    w = sb("w", [P, K4])
    sig = sb("sig", [K4, T])
    mean = sb("mean", [K4, 2, chunks])
    ps = [ctx.enter_context(nc.psum_tensor(f"{tag}_ps{s}", [K4, SL], F32)) for s in range(NS)]
    sem = lambda name: nc.alloc_semaphore(f"{tag}_{name}")
    loaded, ready, sigmoid_done, summed, scaled, stored, spread = (sem(n) for n in (
        "loaded", "ready", "sigmoid_done", "summed", "scaled", "stored", "spread"))

    @block.sync
    def _(sp):
        sp.dma_start(w[:, :], w_dram).then_inc(loaded, 16)
        sp.wait_ge(scaled, 1)
        with nc.allow_non_contiguous_dma(reason="one small array is stored in another order"):
            for kind in range(2):
                for b in range(2):
                    sp.dma_start(rate_dram[kind, b].rearrange("c h -> h c"), mean[16 * kind:16 * kind + 16, b, :]).then_inc(stored, 16)
                    for par in range(2):
                        r = 32 + kind * 16 + par * 8
                        sp.dma_start(decay_dram[kind, par, :, :, b].rearrange("c a -> a c"), mean[r:r + 8, b, :]).then_inc(stored, 16)
        sp.wait_ge(stored, 16 * 12)
        for kind in range(2):
            rate, decay = ((rate_in, decay_in), (rate_out, decay_out))[kind]
            for half in range(2):
                r = slice(64 * half, 64 * half + 64)
                sp.dma_start(rate[r, :, :], rate_dram[kind, half:half + 1].broadcast_to([64, chunks, 16])).then_inc(spread, 16)
                sp.dma_start(decay[r, :, :, :], decay_dram[kind, half:half + 1].broadcast_to([64, chunks, 8, 2])).then_inc(spread, 16)
        sp.wait_ge(spread, 16 * 8)

    @block.tensor
    def _(pe):
        pe.wait_ge(loaded, 16)
        for s in range(NS):
            pe.matmul(ps[s][:, :], w[:, :], xin[:, s * SL:(s + 1) * SL], start=True, stop=True).then_inc(ready, 1)

    @block.scalar
    def _(ac):
        for s in range(NS):
            ac.wait_ge(ready, s + 1)
            ac.activation(sig[:, s * SL:(s + 1) * SL], ps[s][:, :], ACT.Sigmoid).then_inc(sigmoid_done, 1)

    @block.vector
    def _(ve):
        ve.wait_ge(sigmoid_done, NS)
        ve.tensor_reduce(mean[:, :, :], sig[:, :].rearrange("p (b c n) -> p b c n", b=2, c=chunks), AX.X, ALU.add).then_inc(summed, 1)
        ve.wait_ge(summed, 1)
        ve.tensor_scalar(mean[:, :, :], mean[:, :, :], kit.rate_scale[0:K4, 0:1], None, ALU.mult).then_inc(scaled, 1)


def load_constants(nc, ctx, kit, a):
    sb = lambda name, shape, dt=F32: ctx.enter_context(nc.sbuf_tensor(f"const_{name}", shape, dt))
    kit.ident, kit.den_sel, kit.mean, kit.ones, kit.upto = (sb(n, [P, P]) for n in ("ident", "den_sel", "mean", "ones", "upto"))
    kit.blocks, kit.head16, kit.heads = sb("blocks", [P, 4, P]), sb("head16", [P, 16]), sb("heads", [P, 32])
    kit.numbers = sb("numbers", [P, 8 + T // P])
    kit.rate_scale, kit.lower = sb("rate_scale", [P, 1]), sb("lower", [P, 16, 16])
    kit.ident_bf, kit.mask_kq, kit.mask_qk = sb("ident_bf", [P, P], BF16), sb("mask_kq", [P, 2 * P], BF16), sb("mask_qk", [P, 2 * P], BF16)
    loads = dict(ident=kit.ident, den_sel=kit.den_sel, mean=kit.mean, ones=kit.ones, upto=kit.upto, blocks=kit.blocks,
                 head16=kit.head16, numbers=kit.numbers, heads=kit.heads, rate_scale=kit.rate_scale, lower=kit.lower)
    with nc.cleanup_on_exit(), ExitStack() as inner:
        masks = inner.enter_context(nc.sbuf_tensor("const_masks", [P, 4 * P], F32))
        loaded, converted = nc.alloc_semaphore("const_loaded"), nc.alloc_semaphore("const_converted")
        with nc.Block() as block:

            @block.sync
            def _(sp):
                for name, tile in loads.items():
                    sp.dma_start(tile[:], a["c_" + name]).then_inc(loaded, 16)
                sp.dma_start(masks[:, :], a["c_masks"]).then_inc(loaded, 16)
                sp.wait_ge(loaded, 16 * (len(loads) + 1))

            @block.vector
            def _(ve):
                ve.wait_ge(loaded, 16 * (len(loads) + 1))
                ve.tensor_copy(kit.ident_bf[:, :], kit.ident[:, :]).then_inc(converted, 1)
                ve.tensor_copy(kit.mask_kq[:, :], masks[:, 0:2 * P]).then_inc(converted, 1)
                ve.tensor_copy(kit.mask_qk[:, :], masks[:, 2 * P:4 * P]).then_inc(converted, 1)


def move(nc, ctx, block, tag, pairs, beside=False):
    moved = nc.alloc_semaphore(f"{tag}_moved")

    @(block.gpsimd if beside else block.sync)
    def _(eng):
        for dst, src in pairs:
            eng.dma_start(dst, src).then_inc(moved, 16)

    return lambda sp: (moved, 16 * len(pairs))


class Buffers:
    pass


def joint(nc, stages):
    with nc.cleanup_on_exit(), ExitStack() as ctx, nc.Block() as block:
        stores = stages(ctx, block)

        @block.sync
        def _(sp):
            for stored, count in [store(sp) for store in stores]:
                sp.wait_ge(stored, count)


def alone(nc, stage, *arguments):
    def stages(ctx, block):
        store = stage(nc, ctx, block, *arguments)
        return (store,) if store else ()

    joint(nc, stages)


def layer0_attention(nc, kit, a, m):
    h = m.g
    layer_norm(nc, "l0n1", kit, m.xn, h, a["l0_ln1"])
    with ExitStack() as ctx:
        v_all = ctx.enter_context(nc.sbuf_tensor("l0_v", [P, 8, 8, GH, 32], F32))
        out_all = ctx.enter_context(nc.sbuf_tensor("l0_out", [P, 8, N], F32))

        def inputs(c, block):
            q = query_parts(nc, c, block, "l0q", kit, h, a["l0_wq"], a["l0_bq"], P, PARTS_Q, kit.q_dram)
            k = query_parts(nc, c, block, "l0k", kit, h, a["l0_wk"], a["l0_bk"], P, PARTS_K, kit.k_dram)
            values(nc, c, block, "l0v", kit, h, a["l0_wv"], a["l0_bv"], GH, v_all)
            stores = split_parts(block, q, k)
            route(nc, c, block, "f0r", kit, m.xn, a["f0_router"], a["f0_router_b"], 8, 2, "share", kit.gate_dram[0:8, :], 8)
            return stores

        joint(nc, inputs)
        attend(nc, "l0a", "window", E8 ** -0.5, kit.q_dram, kit.k_dram, v_all, GH, out_all, kit)
        normalise(nc, "l0d", kit, out_all)
        outs = [heads_of(out_all, g) for g in range(4)]
        terms = [(g, g) for g in range(4)]
        alone(nc, project, "l0p", [(terms, 0, None, P, m.s, False)], outs, a["l0_wp"], a["l0_bp"])


        def linear_inputs(c, block):
            values(nc, c, block, "l0sv", kit, h, a["l0_wsv"], a["l0_bsv"], GH, v_all)
            return ()

        joint(nc, linear_inputs)
        linear_attention(nc, "l0s", kit, h, a["l0_wsqk"], a["l0_bsqk"], v_all, out_all)
        normalise(nc, "l0sd", kit, out_all, extra=1e-6)
        alone(nc, project, "l0sp", [(terms, 0, None, P, m.s, True)], outs, a["l0_wos"], a["l0_bos"])
    alone(nc, project, "l0m", [([(0, 0)], 0, None, P, m.g, False)], [slices_of(m.s)], a["l0_wo"], a["l0_bo"])
    add_to(nc, "l0x", m.g, m.xn, m.s)
    layer_norm(nc, "l0n2", kit, m.s, m.g, a["l0_ln2"])
    with ExitStack() as ctx:
        mlp = ctx.enter_context(nc.sbuf_tensor("l0_mlp", [P, T], F32))
        mixture(nc, "l0mlp", m.g, a["l0_w1"], a["l0_w2"], a["l0_b2"], a["c_one_row"], mlp, 1, 4, ACT.Gelu, group=1)
        add_to(nc, "l0y", m.s, mlp, m.s)


def layer0_ffn(nc, kit, a, m):
    mixture(nc, "f0", m.xn, a["f0_w1"], a["f0_w2"], a["f0_b2"], kit.gate_dram, m.g, 8, 4, ACT.Gelu)
    residual(nc, "f0x", m.x, m.s, m.g)


def layer1_attention(nc, kit, a, m):
    with ExitStack() as ctx:
        sb = lambda name, shape: ctx.enter_context(nc.sbuf_tensor(f"l1_{name}", shape, F32))
        decay_in, decay_out = (sb(f"decay_{n}", [P, NC, HP, 2]) for n in ("in", "out"))
        rate_in, rate_out = (sb(f"rate_{n}", [P, NC, 2 * HP]) for n in ("in", "out"))
        wqk, wv, wo = sb("wqk", [P, 2, HP, P]), sb("wv", [P, HP, P]), sb("wo", [P, HP, P])
        win, wout, wout_t = sb("win", [P, HP, 2, P]), sb("wout", [P, HP, 2, P]), sb("wout_t", [P, HP, 2, F])

        def weights_and_route(c, block):
            weights = move(nc, c, block, "l1w", [
                (wqk[:, :, :, :], a["l1_wqk"]), (wv[:, :, :], a["l1_wv"]), (wo[:, :, :], a["l1_wo"]),
                (win[:, :, :, :], a["l1_win"]), (wout[:, :, :, :], a["l1_wout"]), (wout_t[:, :, :, :], a["l1_wout_t"])], beside=True)
            chunk_rates(nc, c, block, "l1r", kit, m.xn, a["l1_wrates"], kit.rate_dram, kit.decay_dram, decay_in, decay_out,
                        rate_in, rate_out)
            route(nc, c, block, "f1r", kit, m.xn, a["f1_router"], a["f1_router_b"], 8, 1, "capacity", None, 1, T // 8, m.slots)
            return (weights,)

        joint(nc, weights_and_route)
        fast_weights(nc, "l1", m.xn[:, :], wqk, wv, wo, win, wout, wout_t, decay_in, decay_out, rate_in, rate_out, m.s[:, :], kit.ident)


def layer1_ffn(nc, kit, a, m):
    with ExitStack() as ctx:
        x_slots, y_slots = (ctx.enter_context(nc.sbuf_tensor(f"f1_{n}", [P, T], F32)) for n in ("x_slots", "y_slots"))
        send_tokens(nc, "f1s", kit, m.xn, m.slots, kit.x_rows, kit.y_rows, x_slots)
        slot_experts(nc, "f1", x_slots, a["f1_w1"], a["f1_w2"], y_slots, 8, 4, ACT.Gelu, 2.0 ** 0.5 / 1.41421)
        fetch_results(nc, "f1t", kit, y_slots, m.slots, kit.y_rows, m.g)
    residual(nc, "f1x", m.x, m.s, m.g)


def layer2_attention(nc, kit, a, m):
    with ExitStack() as ctx:
        kit.spread = ctx.enter_context(nc.sbuf_tensor("l2_spread", [P, 8, P], F32))
        alone(nc, move, "l2c", [(kit.spread[:, :, :], a["c_spread"])])
        dilated_attention(nc, "l2", kit, m.xn, a["l2_w"], a["l2_cols"], a["l2_taps"], m.s)


def layer2_ffn(nc, kit, a, m):
    layer_norm(nc, "f2n1", kit, m.xn, m.g, a["f2_g1"], rms=True)
    with ExitStack() as ctx:
        v_all = ctx.enter_context(nc.sbuf_tensor("f2_v", [P, 8, 8, 1, 32], F32))
        out_all = ctx.enter_context(nc.sbuf_tensor("f2_out", [P, 8, N], F32))

        def inputs(c, block):
            q = query_parts(nc, c, block, "f2q", kit, m.g, a["f2_wq"], None, P, PARTS_Q, kit.q_dram, a["c_rope_q"])
            k = query_parts(nc, c, block, "f2k", kit, m.g, a["f2_wk"], None, 32, PARTS_K, kit.k4_dram, a["c_rope_k"])
            values(nc, c, block, "f2v", kit, m.g, a["f2_wv"], a["c_zero_row"][:, 0:32], 1, v_all)
            return split_parts(block, q, k)

        joint(nc, inputs)
        attend(nc, "f2a", "causal", E8 ** -0.5, kit.q_dram, kit.k4_dram, v_all, 1, out_all, kit)
        normalise(nc, "f2d", kit, out_all)
        alone(nc, project, "f2p", [([(g, g) for g in range(4)], 0, None, P, m.g, False)], [heads_of(out_all, g) for g in range(4)],
                a["f2_wo"], a["c_zero_col"])
    add_to(nc, "f2x", m.g, m.xn, m.g)
    with ExitStack() as ctx:
        norm = ctx.enter_context(nc.sbuf_tensor("f2_norm", [P, T], F32))
        moe = ctx.enter_context(nc.sbuf_tensor("f2_moe", [P, T], F32))
        layer_norm(nc, "f2n2", kit, m.g, norm, a["f2_g2"], rms=True)
        alone(nc, route, "f2r", kit, norm, a["f2_router"], a["c_zero_row"][:, 0:4], 4, 2, "share", kit.gate_dram[0:4, :], 4)
        mixture(nc, "f2", norm, a["f2_w13"], a["f2_w2"], a["c_zero_4"], kit.gate_dram, moe, 4, 3, ACT.Silu, gated_unit=True)
        residual(nc, "f2y", m.x, m.s, moe, plus=m.g)


def layer3_attention(nc, kit, a, m):
    with ExitStack() as ctx:
        v_all = ctx.enter_context(nc.sbuf_tensor("l3_v", [P, 8, 8, GH, 32], F32))
        out_all = ctx.enter_context(nc.sbuf_tensor("l3_out", [P, 8, N], F32))

        def inputs(c, block):
            q = query_parts(nc, c, block, "l3q", kit, m.xn, a["l3_wq"], None, P, PARTS_Q, kit.q_dram)
            k = query_parts(nc, c, block, "l3k", kit, m.xn, a["l3_wk"], None, P, PARTS_K, kit.k_dram)
            values(nc, c, block, "l3v", kit, m.xn, a["l3_wv"], a["c_zero_row"][:, 0:P], GH, v_all)
            stores = split_parts(block, q, k)
            route(nc, c, block, "f3r", kit, m.xn, a["f3_router"], a["f3_router_b"], 15, 3, "plain", kit.gate_dram[0:16, :], 16)
            return stores

        joint(nc, inputs)
        attend(nc, "l3a", "full", P ** -0.5, kit.q_dram, kit.k_dram, v_all, GH, out_all, kit)
        normalise(nc, "l3d", kit, out_all)
        alone(nc, project, "l3p", [([(g, g) for g in range(4)], 0, None, P, m.s, False)], [heads_of(out_all, g) for g in range(4)],
              a["l3_wu"], a["l3_bu"])


def layer3_ffn(nc, kit, a, m):
    mixture(nc, "f3", m.xn, a["f3_w1"], a["f3_w2"], a["f3_b2"], kit.gate_dram, m.g, 16, 1, ACT.Relu)
    residual(nc, "f3x", m.x, m.s, m.g)


LAYERS = ((layer0_attention, layer0_ffn), (layer1_attention, layer1_ffn), (layer2_attention, layer2_ffn),
          (layer3_attention, layer3_ffn))


def network(nc, a, out):
    kit, m = Kit(), Buffers()
    scratch = lambda name, shape, dt: nc.dram_tensor(name, shape, dt).ap()
    kit.q_dram = scratch("q_parts", [2, ROWS, 16, N], BF16)
    kit.k_dram = scratch("k_parts", [2, ROWS, 16, N], BF16)
    kit.k4_dram = scratch("k4_parts", [2, ROWS, 4, N], BF16)
    kit.gate_dram = scratch("gate_rows", [16, T], F32)
    kit.x_rows, kit.y_rows = scratch("x_rows", [2 * T, P], F32), scratch("y_rows", [2 * T, P], F32)
    kit.rate_dram = scratch("rates", [2, 2, NC, 2 * HP], F32)
    kit.decay_dram = scratch("decays", [2, 2, NC, HP, 2], F32)
    with ExitStack() as ctx:
        m.x, m.xn, m.s, m.g = (ctx.enter_context(nc.sbuf_tensor(n, [P, T], F32)) for n in ("resid", "normed", "mixer_out", "ffn_out"))
        m.slots = ctx.enter_context(nc.sbuf_tensor("token_slots", [P, T // P], mybir.dt.uint32))
        load_constants(nc, ctx, kit, a)
        alone(nc, move, "x", [(m.x[:, :], a["x"])])
        for i, (attention, ffn) in enumerate(LAYERS):
            layer_norm(nc, f"n{i}", kit, m.x, m.xn)
            attention(nc, kit, a, m)
            ffn(nc, kit, a, m)
        alone(nc, move, "y", [(out, m.x[:, :])])



def shape_constants():
    f = np.float32
    c = {}
    c["ident"] = np.eye(P, dtype=f)
    p = np.arange(P)
    c["den_sel"] = (p[:, None] == 32 * (p[None] // 32) + E8).astype(f)
    c["numbers"] = np.concatenate([np.broadcast_to(np.arange(8) * (T // 8) - 1, (P, 8)), T + p[:, None] + P * np.arange(T // P)[None]], 1)
    c["mean"] = np.full((P, P), 1.0 / P, f)
    c["ones"] = np.ones((P, P), f)
    c["upto"] = (p[:, None] <= p[None]).astype(f)
    col = p[None, None]
    head = 4 * np.arange(4)[None, :, None] + col // 32
    c["blocks"] = ((p[:, None, None] // E8 == head) & (col % 32 <= E8)).astype(f)
    c["head16"] = (p[:, None] // E8 == np.arange(16)[None]).astype(f)
    c["heads"] = ((p[:, None] // E8 == np.arange(32)[None]) * f(E8 ** -0.5)).astype(f)
    c["rate_scale"] = np.where(p < 32, 0.001 / CH, 0.9 / CH)[:, None].astype(f)
    lower = np.arange(16)[None, :] < np.arange(16)[:, None]
    c["lower"] = np.broadcast_to(lower.astype(f), (P, 16, 16))
    diag = np.where(p[:, None] <= p[None], 0, -1e30)
    prev = np.where(p[:, None] > p[None], 0, -1e30)
    c["masks"] = np.concatenate([diag, prev, prev.T, diag.T], 1).astype(f)
    k = np.arange(8)[None, :, None]
    c["spread"] = ((p[:, None, None] // 16 == k) & (p[:, None, None] % 16 == col // E8)).astype(f)
    inv_freq = (1.0 / 10000.0 ** (np.arange(0, E8, 2, dtype=f) / f(E8))).astype(f)
    freqs = np.arange(N, dtype=f)[:, None] * inv_freq[None]
    emb = np.concatenate([freqs, freqs], 1).astype(f)
    sign = np.where(np.arange(E8) < E8 // 2, -1.0, 1.0)[:, None]
    cos, sin = np.cos(emb).T.astype(f), (np.sin(emb).T * sign).astype(f)
    c["rope_q"] = np.stack([np.repeat(cos, 16, 0), np.repeat(sin, 16, 0)])
    c["rope_k"] = np.stack([np.repeat(cos, 4, 0), np.repeat(sin, 4, 0)])
    c["one_row"] = np.ones((1, T), f)
    c["zero_row"] = np.zeros((1, P), f)
    c["zero_col"] = np.zeros((P, 1), f)
    c["zero_4"] = np.zeros((4, P), f)
    return {"c_" + n: np.ascontiguousarray(v, dtype=f) for n, v in c.items()}


def lay_out(i):
    a = shape_constants()
    col = lambda *v: np.stack(v, 1)

    def by_dim(w, heads=16):
        return w.reshape(w.shape[:-1] + (heads, E8)).swapaxes(-1, -2).reshape(w.shape)

    def rotated(w, heads=16):
        r = w.reshape(w.shape[:-1] + (heads, E8))
        return np.concatenate([r[..., E8 // 2:], r[..., :E8 // 2]], -1).reshape(w.shape)

    def from_heads(w):
        out = np.zeros((4, 32, 4, P), w.dtype)
        out[:, :E8] = w.reshape(4, 4, E8, P).transpose(1, 2, 0, 3)
        return out.reshape(P, 4, P)

    def experts1(w, b):
        e, _, f = w.shape
        return np.concatenate([w, b.reshape(e, f // P, P).transpose(0, 2, 1)], 2)

    def experts2(w):
        e, f, _ = w.shape
        return w.reshape(e, f // P, P, P).transpose(0, 2, 1, 3).reshape(e, P, f)

    a["x"] = i["L0_attn_x"].reshape(T, P).T
    g = lambda n: i["L0_attn_" + n]
    a["l0_ln1"], a["l0_ln2"] = col(g("g1"), g("b1")), col(g("gm"), g("bm"))
    wq, wk, wv = np.split(g("Wqkv_a"), 3, 1)
    bq, bk, bv = np.split(g("bqkv_a"), 3)
    sq, sk, sv = np.split(g("Wqkv_s"), 3, 1)
    cq, ck, cv = np.split(g("bqkv_s"), 3)
    a["l0_wq"], a["l0_wk"], a["l0_wv"], a["l0_bv"] = by_dim(wq), by_dim(wk), wv, bv[None]
    a["l0_bq"], a["l0_bk"], a["l0_bsqk"] = by_dim(bq)[:, None], by_dim(bk)[:, None], col(cq, ck)
    a["l0_wp"], a["l0_bp"] = from_heads(g("Wp_a")), g("bp_a")[:, None]
    a["l0_wsv"], a["l0_bsv"], a["l0_wsqk"] = sv, cv[None], np.stack([sq, sk], 1)
    a["l0_wos"], a["l0_bos"] = from_heads(g("Wo_s")), g("bo_s")[:, None]
    a["l0_wo"], a["l0_bo"] = g("Wo")[:, None], g("bo")[:, None]
    a["l0_w1"], a["l0_w2"] = experts1(g("W1")[None], g("b1m")[None]), experts2(g("W2")[None])
    a["l0_b2"] = g("b2m")[None]
    g = lambda n: i["L0_ffn_" + n]
    a["f0_router"], a["f0_router_b"] = g("router_w"), g("router_b")[None]
    a["f0_w1"], a["f0_w2"], a["f0_b2"] = experts1(g("w1"), g("b1")), experts2(g("w2")), g("b2")
    g = lambda n: i["L1_attn_" + n]
    a["l1_wqk"] = np.stack([g("Wq").T.reshape(P, HP, P), g("Wk").T.reshape(P, HP, P)], 1)
    a["l1_wv"] = g("Wv").T.reshape(P, HP, P)
    a["l1_wo"] = g("Wo").T.reshape(HP, P, P).transpose(1, 0, 2)

    def pairs(w):
        return np.broadcast_to(w.reshape(HP, 2, F, F).transpose(1, 2, 0, 3).reshape(P, HP, 1, F), (P, HP, 2, F))

    def on_diagonal(w):
        out = np.zeros((2, F, HP, 2, 2, F), w.dtype)
        for parity in range(2):
            out[parity, :, :, :, parity] = w.reshape(2, F, HP, 2, F)[parity]
        return out.reshape(P, HP, 2, P)

    a["l1_win"] = on_diagonal(pairs(g("W_in_init")[0].transpose(1, 2, 0)))
    a["l1_wout"] = on_diagonal(pairs(g("W_out_init")[0].transpose(1, 0, 2)))
    a["l1_wout_t"] = pairs(g("W_out_init")[0].transpose(1, 2, 0))
    by_parity = lambda w: w.reshape(2, HP, 2, P).transpose(0, 2, 1, 3).reshape(32, P)
    a["l1_wrates"] = np.concatenate([g("Wlr"), by_parity(g("Wbeta"))], 0).T
    g = lambda n: i["L1_ffn_" + n]
    a["f1_router"], a["f1_router_b"] = g("W_sw"), g("b_sw")[None]
    a["f1_w1"] = np.concatenate([experts1(g("W1"), g("b1")), g("b2")[:, :, None]], 2)
    a["f1_w2"] = experts2(g("W2"))
    g = lambda n: i["L2_attn_" + n]
    a["l2_w"] = np.stack(np.split(g("w_qkv"), 3, 1) + [g("w_gate"), g("w_out")], 1)
    a["l2_cols"] = col(*np.split(g("b_qkv"), 3), g("b_gate"), g("b_out"))
    offsets = [(1 << j) * tap for j in range(11) for tap in range(4)]
    order = [t for s in SHIFTS for t in range(44) if offsets[t] == s] + [t for t in range(44) if offsets[t] >= N]
    a["l2_taps"] = g("pos_bias")[order][None]
    g = lambda n: i["L2_ffn_" + n]
    a["f2_g1"], a["f2_g2"] = g("g1")[:, None], g("g2")[:, None]
    a["f2_wq"] = np.concatenate([by_dim(g("wq")), by_dim(rotated(g("wq")))], 1)
    a["f2_wk"] = np.concatenate([by_dim(g("wk"), 4), by_dim(rotated(g("wk"), 4), 4)], 1)
    a["f2_wv"], a["f2_wo"], a["f2_router"] = g("wv"), from_heads(g("wo")), g("gate")
    a["f2_w13"], a["f2_w2"] = np.concatenate([g("w1"), g("w3")], 2), experts2(g("w2"))
    g = lambda n: i["L3_attn_" + n]
    a["l3_wq"], a["l3_wk"], a["l3_wv"] = by_dim(g("Wq").T), by_dim(g("Wk").T), g("Wv").T
    a["l3_wu"], a["l3_bu"] = from_heads(g("Wu").T), g("bu")[:, None]
    g = lambda n: i["L3_ffn_" + n]
    a["f3_router"], a["f3_router_b"] = g("router_W"), g("router_b")[None]
    a["f3_w1"] = experts1(np.concatenate([g("eW1"), g("sW1")[None]]), np.concatenate([g("eb1"), g("sb1")[None]]))
    a["f3_w2"] = experts2(np.concatenate([g("eW2"), g("sW2")[None]]))
    a["f3_b2"] = np.concatenate([g("eb2"), g("sb2")[None]])
    return {n: np.ascontiguousarray(v) for n, v in a.items()}



def kernel(**inputs):
    import concourse.bacc as _bacc
    from concourse.bass_utils import run_bass_kernel_spmd as _run

    nc = _bacc.Bacc("TRN2", target_bir_lowering=False, num_devices=1)
    laid = lay_out({name: np.asarray(v) for name, v in inputs.items()})
    arrays, a = {}, {}
    for name, v in laid.items():
        arrays[f"in_{name}_dram"] = v
        a[name] = nc.dram_tensor(f"in_{name}_dram", v.shape, mybir.dt.from_np(v.dtype), kind="ExternalInput").ap()
    out = nc.dram_tensor("out_dram", (P, T), F32, kind="ExternalOutput").ap()
    network(nc, a, out)
    r = _run(nc, [arrays], core_ids=[0])
    return np.ascontiguousarray(r.results[0]["out_dram"].T).reshape(2, N, P)
```
